# Optimizing a Trainium2 kernel written in Bass

```python
import numpy as np
import jax
import jax.numpy as jnp

def _softmax(x, axis=-1):
    return jax.nn.softmax(x, axis=axis)

def _gelu(x):
    return jax.nn.gelu(x, approximate=True)

def _silu(x):
    return jax.nn.silu(x)

def _sigmoid(x):
    return jax.nn.sigmoid(x)

def _layernorm(x, axis=-1, eps=1e-05):
    m = jnp.mean(x, axis=axis, keepdims=True)
    v = jnp.var(x, axis=axis, keepdims=True)
    return (x - m) / jnp.sqrt(v + eps)

def _scatter_add(tgt, idx, src, axis=0):
    return tgt.at[idx].add(src)

def _segment_sum(src, seg, n):
    return jax.ops.segment_sum(src, seg, n)
kernel_name = 'mk_decoder_postln_d4_seqx_r8_f33938'

def setup_inputs(seed: int=0):
    np.random.seed(seed)
    _w = jnp.asarray

    def _rec_inputs():
        import jax
        import jax.numpy as jnp
        _rk = jax.random.key(seed)
        x = -0.0005207 + 1.001 * jax.random.normal(jax.random.fold_in(_rk, 1), (32, 64, 256), jnp.float32)
        _lenS = 64 - jax.random.randint(jax.random.fold_in(_rk, 7), (32,), 0, max(1, 64 // 4) + 1, jnp.int32)
        _lenS2 = 64 - jax.random.randint(jax.random.fold_in(_rk, 8), (32,), 0, max(1, 64 // 4) + 1, jnp.int32)
        _ctx_2048P = jax.random.normal(jax.random.fold_in(_rk, 11), (32, 16, 256), jnp.float32)
        _ctx_2048c = jax.random.dirichlet(jax.random.fold_in(_rk, 511), 0.3 * jnp.ones((16,), jnp.float32), (32, 64))
        _ctx_2048t = jnp.einsum('bsk,bkd->bsd', _ctx_2048c, _ctx_2048P)
        _ctx_2048t = _ctx_2048t * jax.lax.rsqrt(jnp.mean(jnp.square(_ctx_2048t)) + 1e-12) * 0.953939
        ctx_2048 = -0.000514642 + 1.00011 * (_ctx_2048t + 0.3 * jax.random.normal(jax.random.fold_in(_rk, 611), (32, 64, 256), jnp.float32))
        _validS = jnp.arange(64)[None, :] < _lenS[:, None]
        _validS2 = jnp.arange(64)[None, :] < _lenS2[:, None]
        _causal = jnp.tril(jnp.ones((64, 64), dtype=bool))
        mask_BxS2_bk0 = jnp.logical_not(jnp.broadcast_to(_validS2[:, :], (32, 64)))
        return (x, ctx_2048, mask_BxS2_bk0)
    x, ctx_2048, mask_BxS2_bk0 = _rec_inputs()

    def _L0_attn_setup():
        import jax, jax.numpy as jnp
        import numpy as np
        HID = 256
        H = 16
        D = HID // H
        THETA = 10000.0

        def _rope(q, k):
            T = q.shape[1]
            half = D // 2
            inv_freq = 1.0 / THETA ** (jnp.arange(half, dtype=jnp.float32) / half)
            ang = jnp.arange(T, dtype=jnp.float32)[:, None] * inv_freq[None, :]
            cos = jnp.cos(ang)[None, :, None, :]
            sin = jnp.sin(ang)[None, :, None, :]

            def rot(x):
                x1, x2 = (x[..., :half], x[..., half:])
                return jnp.concatenate([x1 * cos - x2 * sin, x2 * cos + x1 * sin], axis=-1)
            return (rot(q), rot(k))
        key = jax.random.key(seed)
        ks = jax.random.split(key, 7)
        B, T = (1, 256)
        s = 1.0 / np.sqrt(HID)
        return {'hidden_states': jax.random.normal(ks[0], (B, T, HID), dtype=jnp.float32), 'Wq': jax.random.normal(ks[1], (HID, HID), dtype=jnp.float32) * s, 'Wk': jax.random.normal(ks[2], (HID, HID), dtype=jnp.float32) * s, 'Wv': jax.random.normal(ks[3], (HID, HID), dtype=jnp.float32) * s, 'Wb': jax.random.normal(ks[4], (HID, H), dtype=jnp.float32) * s, 'bb': jnp.zeros((H,), dtype=jnp.float32), 'Wo': jax.random.normal(ks[5], (HID, HID), dtype=jnp.float32) * s}
    _L0_attn_all = _L0_attn_setup()
    _L0_attn_in = {k: v for k, v in _L0_attn_all.items() if k in ('Wq', 'Wk', 'Wv', 'Wb', 'bb', 'Wo')}
    del _L0_attn_all

    def _L0_xattn_setup():
        import jax, jax.numpy as jnp
        import numpy as np
        from math import sqrt
        key = jax.random.key(seed)
        kq, kk, kv = jax.random.split(key, 3)
        B, D, N = (8, 128, 256)
        Q = jax.random.normal(kq, (B, D, N), dtype=jnp.float32)
        K = jax.random.normal(kk, (B, D, N), dtype=jnp.float32)
        V = jax.random.normal(kv, (B, D, N), dtype=jnp.float32)
        return {'Q': Q, 'K': K, 'V': V}
    _L0_xattn_all = _L0_xattn_setup()
    _L0_xattn_in = {k: v for k, v in _L0_xattn_all.items() if k in ()}
    del _L0_xattn_all

    def _L0_ffn_setup():
        import jax, jax.numpy as jnp
        import numpy as np
        TOP_K = 2
        key = jax.random.key(seed)
        ks = jax.random.split(key, 6)
        B, S, H, F, E = (1, 256, 256, 176, 8)
        Fs = 2 * F
        std = jnp.float32(0.02)
        return {'hidden_states': jax.random.normal(ks[0], (B, S, H), jnp.float32), 'gate_weight': jax.random.normal(ks[1], (E, H), jnp.float32) * std, 'gate_up_weights': jax.random.normal(ks[2], (E, 2 * F, H), jnp.float32) * std, 'down_weights': jax.random.normal(ks[3], (E, H, F), jnp.float32) * std, 'shared_gate_up': jax.random.normal(ks[4], (2 * Fs, H), jnp.float32) * std, 'shared_down': jax.random.normal(ks[5], (H, Fs), jnp.float32) * std}
    _L0_ffn_all = _L0_ffn_setup()
    _L0_ffn_in = {k: v for k, v in _L0_ffn_all.items() if k in ('gate_weight', 'gate_up_weights', 'down_weights', 'shared_gate_up', 'shared_down')}
    del _L0_ffn_all

    def _L1_attn_setup():
        import jax, jax.numpy as jnp
        import numpy as np
        HIDDEN = 256
        HEADS = 16
        HEAD_DIM = HIDDEN // HEADS
        SCALE = 1.0 / np.sqrt(HEAD_DIM).astype(np.float32)
        key = jax.random.key(seed)
        k1, k2, k3, k4, k5 = jax.random.split(key, 5)
        B, QL = (8, 128)
        NB, BS = (32, 128)
        query = jax.random.normal(k1, (B, QL, HIDDEN), dtype=jnp.float32)
        kv_k = jax.random.normal(k2, (NB, BS, HIDDEN), dtype=jnp.float32)
        kv_v = jax.random.normal(k3, (NB, BS, HIDDEN), dtype=jnp.float32)
        Wq = jax.random.normal(k4, (HIDDEN, HIDDEN), dtype=jnp.float32) * (1.0 / np.sqrt(HIDDEN))
        Wo = jax.random.normal(k5, (HIDDEN, HIDDEN), dtype=jnp.float32) * (1.0 / np.sqrt(HIDDEN))
        return {'query': query, 'kv_k': kv_k, 'kv_v': kv_v, 'Wq': Wq, 'Wo': Wo}
    _L1_attn_all = _L1_attn_setup()
    _L1_attn_in = {k: v for k, v in _L1_attn_all.items() if k in ('kv_k', 'kv_v', 'Wq', 'Wo')}
    del _L1_attn_all

    def _L1_xattn_setup():
        import jax, jax.numpy as jnp
        import numpy as np
        B, S, E, NH = (2, 128, 256, 16)
        DH = E // NH
        EPS = 1e-06

        def _mlstm_forward(q, k, v, Wi, bi, Wf, bf, ln_scale):
            b, s, e = q.shape
            nh = Wi.shape[1]
            dh = e // nh
            x = jnp.concatenate([q, k, v], axis=-1)
            ig = (x @ Wi + bi).transpose(0, 2, 1)[..., None]
            fg = (x @ Wf + bf).transpose(0, 2, 1)[..., None]
            split = lambda t: t.reshape(b, s, nh, dh).transpose(0, 2, 1, 3)
            qh, kh, vh = (split(q), split(k), split(v))
            log_f = jax.nn.log_sigmoid(fg)
            log_f_cum = jnp.concatenate([jnp.zeros((b, nh, 1, 1), q.dtype), jnp.cumsum(log_f, axis=2)], axis=2)
            fg_mat = log_f_cum - jnp.transpose(log_f_cum, (0, 1, 3, 2))
            ltr = jnp.tril(jnp.ones((s, s), dtype=bool))
            log_fg = jnp.where(ltr, fg_mat[:, :, 1:, 1:], -jnp.inf)
            log_D = log_fg + jnp.transpose(ig, (0, 1, 3, 2))
            max_log_D = jnp.max(log_D, axis=-1, keepdims=True)
            D = jnp.exp(log_D - max_log_D)
            qk = jnp.einsum('bhsd,bhtd->bhst', qh, kh) / jnp.sqrt(jnp.asarray(dh, q.dtype))
            C = qk * D
            normalizer = jnp.maximum(jnp.abs(C.sum(-1, keepdims=True)), jnp.exp(-max_log_D))
            Cn = C / (normalizer + EPS)
            h = jnp.einsum('bhst,bhtd->bhsd', Cn, vh)
            mu = h.mean(-1, keepdims=True)
            var = ((h - mu) ** 2).mean(-1, keepdims=True)
            hn = (h - mu) * jax.lax.rsqrt(var + EPS)
            hn = hn * ln_scale.reshape(1, nh, 1, dh)
            return hn.transpose(0, 2, 1, 3).reshape(b, s, e)
        key = jax.random.key(seed)
        ks = jax.random.split(key, 6)
        q = jax.random.normal(ks[0], (B, S, E), dtype=jnp.float32)
        k = jax.random.normal(ks[1], (B, S, E), dtype=jnp.float32)
        v = jax.random.normal(ks[2], (B, S, E), dtype=jnp.float32)
        Wi = jax.random.normal(ks[3], (3 * E, NH), dtype=jnp.float32) * 0.02
        bi = jax.random.normal(ks[4], (NH,), dtype=jnp.float32) * 0.1
        Wf = jax.random.normal(ks[5], (3 * E, NH), dtype=jnp.float32) * 0.02
        bf = jnp.linspace(3.0, 6.0, NH, dtype=jnp.float32)
        ln_scale = jnp.ones((E,), dtype=jnp.float32)
        return {'q': q, 'k': k, 'v': v, 'Wi': Wi, 'bi': bi, 'Wf': Wf, 'bf': bf, 'ln_scale': ln_scale}
    _L1_xattn_all = _L1_xattn_setup()
    _L1_xattn_in = {k: v for k, v in _L1_xattn_all.items() if k in ('Wi', 'bi', 'Wf', 'bf', 'ln_scale')}
    del _L1_xattn_all

    def _L1_ffn_setup():
        import jax, jax.numpy as jnp
        import numpy as np
        TOP_K = 2
        key = jax.random.key(seed)
        ks = jax.random.split(key, 5)
        B, S, D, INTER, E = (4, 256, 256, 256, 8)
        x = jax.random.normal(ks[0], (B, S, D), dtype=jnp.float32)
        w1 = jax.random.normal(ks[1], (INTER, D), dtype=jnp.float32) * (1.0 / np.sqrt(D))
        w3 = jax.random.normal(ks[2], (INTER, INTER), dtype=jnp.float32) * (1.0 / np.sqrt(INTER))
        w2 = jax.random.normal(ks[3], (D, INTER), dtype=jnp.float32) * (1.0 / np.sqrt(INTER))
        wr = jax.random.normal(ks[4], (E, D), dtype=jnp.float32) * (1.0 / np.sqrt(D))
        return {'x': x, 'w1': w1, 'w3': w3, 'w2': w2, 'wr': wr}
    _L1_ffn_all = _L1_ffn_setup()
    _L1_ffn_in = {k: v for k, v in _L1_ffn_all.items() if k in ('w1', 'w3', 'w2', 'wr')}
    del _L1_ffn_all

    def _L2_attn_setup():
        import jax, jax.numpy as jnp
        import numpy as np
        H = 256
        NH = 16
        HD = H // NH
        NB = 8
        INTER = 2 * H
        EPS = 1e-05
        THETA = 10000.0

        def rmsnorm(x, w):
            return x * jax.lax.rsqrt(jnp.mean(x * x, axis=-1, keepdims=True) + EPS) * w

        def _act_quant(x):
            scale = 127.0 / jnp.maximum(jnp.max(jnp.abs(x), axis=-1, keepdims=True), 1e-05)
            return jnp.clip(jnp.round(x * scale), -128, 127) / scale

        def _weight_quant(w):
            scale = 1.0 / jnp.maximum(jnp.mean(jnp.abs(w)), 1e-05)
            return jnp.clip(jnp.round(w * scale), -1, 1) / scale

        def bitlinear(x, w):
            xq = x + jax.lax.stop_gradient(_act_quant(x) - x)
            wq = w + jax.lax.stop_gradient(_weight_quant(w) - w)
            return xq @ wq.T

        def rope_cache(seq_len, dim, theta):
            inv_freq = 1.0 / theta ** (jnp.arange(0, dim, 2, dtype=jnp.float32) / dim)
            t = jnp.arange(seq_len, dtype=jnp.float32)
            freqs = jnp.outer(t, inv_freq)
            return (jnp.cos(freqs), jnp.sin(freqs))

        def apply_rope(x, cos, sin):
            half = x.shape[-1] // 2
            x1, x2 = (x[..., :half], x[..., half:])
            return jnp.concatenate([x1 * cos - x2 * sin, x2 * cos + x1 * sin], axis=-1)
        key = jax.random.key(seed)
        ks = jax.random.split(key, 7)
        B, S = (2, 512)
        w = lambda k, shp: jax.random.normal(k, shp, dtype=jnp.float32) * 0.02
        return {'x': jax.random.normal(ks[0], (B, S, H), dtype=jnp.float32), 'attn_norm_w': jnp.ones((H,), jnp.float32), 'ffn_norm_w': jnp.ones((H,), jnp.float32), 'qkv_w': w(ks[1], (3 * H, H)), 'o_w': w(ks[2], (H, H)), 'ffn_up_w': w(ks[3], (2 * INTER, H)), 'ffn_down_w': w(ks[4], (H, INTER))}
    _L2_attn_all = _L2_attn_setup()
    _L2_attn_in = {k: v for k, v in _L2_attn_all.items() if k in ('attn_norm_w', 'ffn_norm_w', 'qkv_w', 'o_w', 'ffn_up_w', 'ffn_down_w')}
    del _L2_attn_all

    def _L2_xattn_setup():
        import jax, jax.numpy as jnp
        import numpy as np
        N_HEAD = 8
        ALPHA = 5.0
        EPS = 1e-12

        def _l2norm(x, axis):
            n = jnp.sqrt(jnp.sum(x * x, axis=axis, keepdims=True))
            return x / jnp.maximum(n, EPS)
        key = jax.random.key(seed)
        kq, kk, kv = jax.random.split(key, 3)
        B, D, T = (4, 128, 256)
        q = jax.random.normal(kq, (B, D, T), dtype=jnp.float32)
        k = jax.random.normal(kk, (B, D, T), dtype=jnp.float32)
        v = jax.random.normal(kv, (B, D, T), dtype=jnp.float32)
        return {'q': q, 'k': k, 'v': v}
    _L2_xattn_all = _L2_xattn_setup()
    _L2_xattn_in = {k: v for k, v in _L2_xattn_all.items() if k in ()}
    del _L2_xattn_all

    def _L2_ffn_setup():
        import jax, jax.numpy as jnp
        import numpy as np
        B, L, D = (2, 128, 256)
        E, K = (8, 2)
        H, HS = (176, 352)
        key = jax.random.key(seed)
        ks = jax.random.split(key, 9)
        s = 0.02
        return {'x': jax.random.normal(ks[0], (B, L, D), dtype=jnp.float32), 'gate_w': jax.random.normal(ks[1], (E, D), dtype=jnp.float32) * s, 'w_gate': jax.random.normal(ks[2], (E, D, H), dtype=jnp.float32) * s, 'w_up': jax.random.normal(ks[3], (E, D, H), dtype=jnp.float32) * s, 'w_down': jax.random.normal(ks[4], (E, H, D), dtype=jnp.float32) * s, 'shgate_w': jax.random.normal(ks[5], (D,), dtype=jnp.float32) * s, 'shw_gate': jax.random.normal(ks[6], (D, HS), dtype=jnp.float32) * s, 'shw_up': jax.random.normal(ks[7], (D, HS), dtype=jnp.float32) * s, 'shw_down': jax.random.normal(ks[8], (HS, D), dtype=jnp.float32) * s}
    _L2_ffn_all = _L2_ffn_setup()
    _L2_ffn_in = {k: v for k, v in _L2_ffn_all.items() if k in ('gate_w', 'w_gate', 'w_up', 'w_down', 'shgate_w', 'shw_gate', 'shw_up', 'shw_down')}
    del _L2_ffn_all

    def _L3_attn_setup():
        import jax, jax.numpy as jnp
        import numpy as np
        B, S, E, H = (2, 256, 256, 16)
        HD = E // H
        INIT_LAMBDA = 0.8

        def rope_cos_sin(seqlen, head_dim, dtype):
            inv = 1.0 / 10000.0 ** (jnp.arange(0, head_dim, 2, dtype=jnp.float32) / head_dim)
            ang = jnp.arange(seqlen, dtype=jnp.float32)[:, None] * inv[None, :]
            ang = jnp.concatenate([ang, ang], axis=-1)
            return (jnp.cos(ang).astype(dtype), jnp.sin(ang).astype(dtype))

        def apply_rope(x, cos, sin):
            d = x.shape[-1]
            x1, x2 = (x[..., :d // 2], x[..., d // 2:])
            rot = jnp.concatenate([-x2, x1], axis=-1)
            return x * cos + rot * sin
        key = jax.random.key(seed)
        ks = jax.random.split(key, 9)
        return {'x': jax.random.normal(ks[0], (B, S, E), jnp.float32), 'w_qkv': jax.random.normal(ks[1], (3 * E, E), jnp.float32) * 0.02, 'wo': jax.random.normal(ks[2], (E, E), jnp.float32) * 0.02, 'lambda_q1': jax.random.normal(ks[3], (HD,), jnp.float32) * 0.1, 'lambda_q2': jax.random.normal(ks[4], (HD,), jnp.float32) * 0.1, 'lambda_k1': jax.random.normal(ks[5], (HD,), jnp.float32) * 0.1, 'lambda_k2': jax.random.normal(ks[6], (HD,), jnp.float32) * 0.1, 'gamma': jnp.ones((E,), jnp.float32), 'beta': jnp.zeros((E,), jnp.float32)}
    _L3_attn_all = _L3_attn_setup()
    _L3_attn_in = {k: v for k, v in _L3_attn_all.items() if k in ('w_qkv', 'wo', 'lambda_q1', 'lambda_q2', 'lambda_k1', 'lambda_k2', 'gamma', 'beta')}
    del _L3_attn_all

    def _L3_xattn_setup():
        import jax, jax.numpy as jnp
        import numpy as np
        key = jax.random.key(seed)
        k1, k2, k3 = jax.random.split(key, 3)
        B, S, D, M = (8, 256, 256, 128)
        hidden_states = jax.random.normal(k1, (B, S, D), dtype=jnp.float32)
        memory_tokens = jax.random.normal(k2, (B, M, D), dtype=jnp.float32)
        memory_mask = jax.random.randint(k3, (B, M), 0, 2).astype(jnp.bool_)
        return {'hidden_states': hidden_states, 'memory_tokens': memory_tokens, 'memory_mask': memory_mask}
    _L3_xattn_all = _L3_xattn_setup()
    _L3_xattn_in = {k: v for k, v in _L3_xattn_all.items() if k in ()}
    del _L3_xattn_all

    def _L3_ffn_setup():
        import jax, jax.numpy as jnp
        import numpy as np
        TOP_K = 4
        key = jax.random.key(seed)
        ks = jax.random.split(key, 8)
        B, S, D, E, H, HS = (2, 256, 256, 16, 128, 512)
        scaled = lambda k, shape, fan: jax.random.normal(k, shape, jnp.float32) * fan ** (-0.5)
        return {'x': jax.random.normal(ks[0], (B, S, D), jnp.float32), 'w_router': scaled(ks[1], (D, E), D), 'we1': scaled(ks[2], (E, D, H), D), 'we3': scaled(ks[3], (E, D, H), D), 'we2': scaled(ks[4], (E, H, D), H), 'ws1': scaled(ks[5], (D, HS), D), 'ws3': scaled(ks[6], (D, HS), D), 'ws2': scaled(ks[7], (HS, D), HS)}
    _L3_ffn_all = _L3_ffn_setup()
    _L3_ffn_in = {k: v for k, v in _L3_ffn_all.items() if k in ('w_router', 'we1', 'we3', 'we2', 'ws1', 'ws3', 'ws2')}
    del _L3_ffn_all
    return {'x': x, 'ctx_2048': ctx_2048, 'mask_BxS2_bk0': mask_BxS2_bk0, 'L0_attn_Wq': _L0_attn_in['Wq'], 'L0_attn_Wk': _L0_attn_in['Wk'], 'L0_attn_Wv': _L0_attn_in['Wv'], 'L0_attn_Wb': _L0_attn_in['Wb'], 'L0_attn_bb': _L0_attn_in['bb'], 'L0_attn_Wo': _L0_attn_in['Wo'], 'L0_ffn_gate_weight': _L0_ffn_in['gate_weight'], 'L0_ffn_gate_up_weights': _L0_ffn_in['gate_up_weights'], 'L0_ffn_down_weights': _L0_ffn_in['down_weights'], 'L0_ffn_shared_gate_up': _L0_ffn_in['shared_gate_up'], 'L0_ffn_shared_down': _L0_ffn_in['shared_down'], 'L1_attn_kv_k': _L1_attn_in['kv_k'], 'L1_attn_kv_v': _L1_attn_in['kv_v'], 'L1_attn_Wq': _L1_attn_in['Wq'], 'L1_attn_Wo': _L1_attn_in['Wo'], 'L1_xattn_Wi': _L1_xattn_in['Wi'], 'L1_xattn_bi': _L1_xattn_in['bi'], 'L1_xattn_Wf': _L1_xattn_in['Wf'], 'L1_xattn_bf': _L1_xattn_in['bf'], 'L1_xattn_ln_scale': _L1_xattn_in['ln_scale'], 'L1_ffn_w1': _L1_ffn_in['w1'], 'L1_ffn_w3': _L1_ffn_in['w3'], 'L1_ffn_w2': _L1_ffn_in['w2'], 'L1_ffn_wr': _L1_ffn_in['wr'], 'L2_attn_attn_norm_w': _L2_attn_in['attn_norm_w'], 'L2_attn_ffn_norm_w': _L2_attn_in['ffn_norm_w'], 'L2_attn_qkv_w': _L2_attn_in['qkv_w'], 'L2_attn_o_w': _L2_attn_in['o_w'], 'L2_attn_ffn_up_w': _L2_attn_in['ffn_up_w'], 'L2_attn_ffn_down_w': _L2_attn_in['ffn_down_w'], 'L2_ffn_gate_w': _L2_ffn_in['gate_w'], 'L2_ffn_w_gate': _L2_ffn_in['w_gate'], 'L2_ffn_w_up': _L2_ffn_in['w_up'], 'L2_ffn_w_down': _L2_ffn_in['w_down'], 'L2_ffn_shgate_w': _L2_ffn_in['shgate_w'], 'L2_ffn_shw_gate': _L2_ffn_in['shw_gate'], 'L2_ffn_shw_up': _L2_ffn_in['shw_up'], 'L2_ffn_shw_down': _L2_ffn_in['shw_down'], 'L3_attn_w_qkv': _L3_attn_in['w_qkv'], 'L3_attn_wo': _L3_attn_in['wo'], 'L3_attn_lambda_q1': _L3_attn_in['lambda_q1'], 'L3_attn_lambda_q2': _L3_attn_in['lambda_q2'], 'L3_attn_lambda_k1': _L3_attn_in['lambda_k1'], 'L3_attn_lambda_k2': _L3_attn_in['lambda_k2'], 'L3_attn_gamma': _L3_attn_in['gamma'], 'L3_attn_beta': _L3_attn_in['beta'], 'L3_ffn_w_router': _L3_ffn_in['w_router'], 'L3_ffn_we1': _L3_ffn_in['we1'], 'L3_ffn_we3': _L3_ffn_in['we3'], 'L3_ffn_we2': _L3_ffn_in['we2'], 'L3_ffn_ws1': _L3_ffn_in['ws1'], 'L3_ffn_ws3': _L3_ffn_in['ws3'], 'L3_ffn_ws2': _L3_ffn_in['ws2']}

def reference(x, ctx_2048, mask_BxS2_bk0, L0_attn_Wq, L0_attn_Wk, L0_attn_Wv, L0_attn_Wb, L0_attn_bb, L0_attn_Wo, L0_ffn_gate_weight, L0_ffn_gate_up_weights, L0_ffn_down_weights, L0_ffn_shared_gate_up, L0_ffn_shared_down, L1_attn_kv_k, L1_attn_kv_v, L1_attn_Wq, L1_attn_Wo, L1_xattn_Wi, L1_xattn_bi, L1_xattn_Wf, L1_xattn_bf, L1_xattn_ln_scale, L1_ffn_w1, L1_ffn_w3, L1_ffn_w2, L1_ffn_wr, L2_attn_attn_norm_w, L2_attn_ffn_norm_w, L2_attn_qkv_w, L2_attn_o_w, L2_attn_ffn_up_w, L2_attn_ffn_down_w, L2_ffn_gate_w, L2_ffn_w_gate, L2_ffn_w_up, L2_ffn_w_down, L2_ffn_shgate_w, L2_ffn_shw_gate, L2_ffn_shw_up, L2_ffn_shw_down, L3_attn_w_qkv, L3_attn_wo, L3_attn_lambda_q1, L3_attn_lambda_q2, L3_attn_lambda_k1, L3_attn_lambda_k2, L3_attn_gamma, L3_attn_beta, L3_ffn_w_router, L3_ffn_we1, L3_ffn_we3, L3_ffn_we2, L3_ffn_ws1, L3_ffn_ws3, L3_ffn_ws2):
    import jax
    import jax.numpy as jnp

    def _L0_attn_ref(hidden_states, Wq, Wk, Wv, Wb, bb, Wo):
        import jax, jax.numpy as jnp
        import numpy as np
        HID = 256
        H = 16
        D = HID // H
        THETA = 10000.0

        def _rope(q, k):
            T = q.shape[1]
            half = D // 2
            inv_freq = 1.0 / THETA ** (jnp.arange(half, dtype=jnp.float32) / half)
            ang = jnp.arange(T, dtype=jnp.float32)[:, None] * inv_freq[None, :]
            cos = jnp.cos(ang)[None, :, None, :]
            sin = jnp.sin(ang)[None, :, None, :]

            def rot(x):
                x1, x2 = (x[..., :half], x[..., half:])
                return jnp.concatenate([x1 * cos - x2 * sin, x2 * cos + x1 * sin], axis=-1)
            return (rot(q), rot(k))
        B, T, _ = hidden_states.shape
        scale = 1.0 / np.sqrt(D)
        q = (hidden_states @ Wq).reshape(B, T, H, D)
        k = (hidden_states @ Wk).reshape(B, T, H, D)
        v = (hidden_states @ Wv).reshape(B, T, H, D)
        beta = hidden_states @ Wb + bb
        q, k = _rope(q, k)
        s = jnp.einsum('bihd,bjhd->bhij', k, k) * scale
        idx = jnp.arange(T)
        strict = idx[:, None] > idx[None, :]
        s = jnp.where(strict, s, -jnp.inf)
        m = jnp.max(s, axis=-1, keepdims=True)
        e = jnp.exp(s - jnp.where(jnp.isfinite(m), m, 0.0))
        e = jnp.where(strict, e, 0.0)
        denom = jnp.sum(e, axis=-1, keepdims=True)
        p = e / jnp.where(denom == 0, 1.0, denom)
        L = p * beta.transpose(0, 2, 1)[..., None]
        A = L + jnp.eye(T, dtype=L.dtype)[None, None]
        u = jax.scipy.linalg.solve_triangular(A, v.transpose(0, 2, 1, 3), lower=True)
        sc = jnp.einsum('bihd,bjhd->bhij', q, k) * scale
        causal = idx[:, None] >= idx[None, :]
        sc = jnp.where(causal, sc, -jnp.inf)
        attn = jax.nn.softmax(sc, axis=-1)
        o = jnp.einsum('bhij,bhjd->bihd', attn, u).reshape(B, T, HID)
        return o @ Wo

    def _L0_xattn_ref(Q, K, V):
        import jax, jax.numpy as jnp
        import numpy as np
        from math import sqrt
        dk = Q.shape[1]
        x = jnp.einsum('bdn,bdm->bnm', Q, K) / sqrt(dk)
        score = jax.nn.sigmoid(x)
        out = jnp.einsum('bvn,bnm->bvm', V, score)
        return out

    def _L0_ffn_ref(hidden_states, gate_weight, gate_up_weights, down_weights, shared_gate_up, shared_down):
        import jax, jax.numpy as jnp
        import numpy as np
        TOP_K = 2
        B, S, H = hidden_states.shape
        E, twoF, _ = gate_up_weights.shape
        F = twoF // 2
        T = B * S
        x = hidden_states.reshape(T, H)
        logits = x @ gate_weight.T
        scores = jax.nn.softmax(logits, axis=-1)
        topk_w, topk_idx = jax.lax.top_k(scores, TOP_K)
        combine = jnp.zeros((T, E), x.dtype).at[jnp.arange(T)[:, None], topk_idx].add(topk_w)
        gu = jnp.einsum('th,efh->tef', x, gate_up_weights)
        act = jax.nn.silu(gu[..., :F]) * gu[..., F:]
        y = jnp.einsum('tef,te,ehf->th', act, combine, down_weights)
        Fs = shared_gate_up.shape[0] // 2
        sgu = x @ shared_gate_up.T
        sact = jax.nn.silu(sgu[:, :Fs]) * sgu[:, Fs:]
        y = y + sact @ shared_down.T
        return y.reshape(B, S, H)

    def _L1_attn_ref(query, kv_k, kv_v, Wq, Wo):
        import jax, jax.numpy as jnp
        import numpy as np
        HIDDEN = 256
        HEADS = 16
        HEAD_DIM = HIDDEN // HEADS
        SCALE = 1.0 / np.sqrt(HEAD_DIM).astype(np.float32)
        B, QL, _ = query.shape
        NB, BS, _ = kv_k.shape
        KV = NB * BS
        Q = (query @ Wq.T).reshape(B, QL, HEADS, HEAD_DIM)
        K = kv_k.reshape(KV, HEADS, HEAD_DIM)
        V = kv_v.reshape(KV, HEADS, HEAD_DIM)
        scores = jnp.einsum('bqhd,khd->bhqk', Q, K) * SCALE
        attn = jax.nn.softmax(scores, axis=-1)
        out = jnp.einsum('bhqk,khd->bqhd', attn, V).reshape(B, QL, HIDDEN)
        return out @ Wo.T

    def _L1_xattn_ref(q, k, v, Wi, bi, Wf, bf, ln_scale):
        import jax, jax.numpy as jnp
        import numpy as np
        B, S, E, NH = (2, 128, 256, 16)
        DH = E // NH
        EPS = 1e-06

        def _mlstm_forward(q, k, v, Wi, bi, Wf, bf, ln_scale):
            b, s, e = q.shape
            nh = Wi.shape[1]
            dh = e // nh
            x = jnp.concatenate([q, k, v], axis=-1)
            ig = (x @ Wi + bi).transpose(0, 2, 1)[..., None]
            fg = (x @ Wf + bf).transpose(0, 2, 1)[..., None]
            split = lambda t: t.reshape(b, s, nh, dh).transpose(0, 2, 1, 3)
            qh, kh, vh = (split(q), split(k), split(v))
            log_f = jax.nn.log_sigmoid(fg)
            log_f_cum = jnp.concatenate([jnp.zeros((b, nh, 1, 1), q.dtype), jnp.cumsum(log_f, axis=2)], axis=2)
            fg_mat = log_f_cum - jnp.transpose(log_f_cum, (0, 1, 3, 2))
            ltr = jnp.tril(jnp.ones((s, s), dtype=bool))
            log_fg = jnp.where(ltr, fg_mat[:, :, 1:, 1:], -jnp.inf)
            log_D = log_fg + jnp.transpose(ig, (0, 1, 3, 2))
            max_log_D = jnp.max(log_D, axis=-1, keepdims=True)
            D = jnp.exp(log_D - max_log_D)
            qk = jnp.einsum('bhsd,bhtd->bhst', qh, kh) / jnp.sqrt(jnp.asarray(dh, q.dtype))
            C = qk * D
            normalizer = jnp.maximum(jnp.abs(C.sum(-1, keepdims=True)), jnp.exp(-max_log_D))
            Cn = C / (normalizer + EPS)
            h = jnp.einsum('bhst,bhtd->bhsd', Cn, vh)
            mu = h.mean(-1, keepdims=True)
            var = ((h - mu) ** 2).mean(-1, keepdims=True)
            hn = (h - mu) * jax.lax.rsqrt(var + EPS)
            hn = hn * ln_scale.reshape(1, nh, 1, dh)
            return hn.transpose(0, 2, 1, 3).reshape(b, s, e)
        return _mlstm_forward(q, k, v, Wi, bi, Wf, bf, ln_scale)

    def _L1_ffn_ref(x, w1, w3, w2, wr):
        import jax, jax.numpy as jnp
        import numpy as np
        TOP_K = 2
        B, S, D = x.shape
        xr = x.reshape(-1, D)
        route_probs = jax.nn.softmax(xr @ wr.T, axis=-1)
        routes_k, indices_k = jax.lax.top_k(route_probs, TOP_K)
        gates = routes_k / jnp.sum(routes_k, axis=-1, keepdims=True)
        h = jax.nn.silu(xr @ w1.T)
        h = jax.nn.silu(h @ w3.T)
        h = h @ w2.T
        out = jnp.zeros_like(xr)
        for k in range(TOP_K):
            out = out.at[indices_k[:, k]].add(gates[:, k:k + 1] * h)
        return out.reshape(B, S, D)

    def _L2_attn_ref(x, attn_norm_w, ffn_norm_w, qkv_w, o_w, ffn_up_w, ffn_down_w):
        import jax, jax.numpy as jnp
        import numpy as np
        H = 256
        NH = 16
        HD = H // NH
        NB = 8
        INTER = 2 * H
        EPS = 1e-05
        THETA = 10000.0

        def rmsnorm(x, w):
            return x * jax.lax.rsqrt(jnp.mean(x * x, axis=-1, keepdims=True) + EPS) * w

        def _act_quant(x):
            scale = 127.0 / jnp.maximum(jnp.max(jnp.abs(x), axis=-1, keepdims=True), 1e-05)
            return jnp.clip(jnp.round(x * scale), -128, 127) / scale

        def _weight_quant(w):
            scale = 1.0 / jnp.maximum(jnp.mean(jnp.abs(w)), 1e-05)
            return jnp.clip(jnp.round(w * scale), -1, 1) / scale

        def bitlinear(x, w):
            xq = x + jax.lax.stop_gradient(_act_quant(x) - x)
            wq = w + jax.lax.stop_gradient(_weight_quant(w) - w)
            return xq @ wq.T

        def rope_cache(seq_len, dim, theta):
            inv_freq = 1.0 / theta ** (jnp.arange(0, dim, 2, dtype=jnp.float32) / dim)
            t = jnp.arange(seq_len, dtype=jnp.float32)
            freqs = jnp.outer(t, inv_freq)
            return (jnp.cos(freqs), jnp.sin(freqs))

        def apply_rope(x, cos, sin):
            half = x.shape[-1] // 2
            x1, x2 = (x[..., :half], x[..., half:])
            return jnp.concatenate([x1 * cos - x2 * sin, x2 * cos + x1 * sin], axis=-1)
        B, S, _ = x.shape
        bt = S // NB
        h = rmsnorm(x, attn_norm_w)
        qkv = bitlinear(h, qkv_w).reshape(B, S, 3, NH, HD)
        q = jnp.transpose(qkv[:, :, 0], (0, 2, 1, 3))
        k = jnp.transpose(qkv[:, :, 1], (0, 2, 1, 3))
        v = jnp.transpose(qkv[:, :, 2], (0, 2, 1, 3))
        cos, sin = rope_cache(S, HD, THETA)
        q = apply_rope(q, cos, sin)
        k = apply_rope(k, cos, sin)
        blk = lambda t: jnp.transpose(t.reshape(B, NH, NB, bt, HD), (0, 2, 1, 3, 4))
        qb, kb, vb = (blk(q), blk(k), blk(v))
        scale = HD ** (-0.5)
        scores = jnp.einsum('bnhqd,bnhkd->bnhqk', qb, kb) * scale
        causal = jnp.triu(jnp.ones((bt, bt), bool), 1)
        scores = jnp.where(causal, jnp.finfo(scores.dtype).min, scores)
        attn = jax.nn.softmax(scores, axis=-1)
        ctx = jnp.einsum('bnhqk,bnhkd->bnhqd', attn, vb)
        ctx = jnp.transpose(ctx, (0, 2, 1, 3, 4)).reshape(B, NH, S, HD)
        ctx = jnp.transpose(ctx, (0, 2, 1, 3)).reshape(B, S, H)
        x1 = x + bitlinear(ctx, o_w)
        hn = rmsnorm(x1, ffn_norm_w)
        gv = hn @ ffn_up_w.T
        gate, val = jnp.split(gv, 2, axis=-1)
        return x1 + bitlinear(jax.nn.silu(gate) * val, ffn_down_w)

    def _L2_xattn_ref(q, k, v):
        import jax, jax.numpy as jnp
        import numpy as np
        N_HEAD = 8
        ALPHA = 5.0
        EPS = 1e-12

        def _l2norm(x, axis):
            n = jnp.sqrt(jnp.sum(x * x, axis=axis, keepdims=True))
            return x / jnp.maximum(n, EPS)
        B, D, Tq = q.shape
        Tk = k.shape[-1]
        Dv = v.shape[-2]
        h = N_HEAD
        d = D // h
        dv = Dv // h
        qh = q.reshape(B, h, d, Tq)
        kh = k.reshape(B, h, d, Tk)
        vh = v.reshape(B, h, dv, Tk)
        qn = _l2norm(qh, axis=-2)
        kn = _l2norm(kh, axis=-2)
        qk = ALPHA * jnp.einsum('bhdq,bhdk->bhqk', qn, kn)
        sm = jax.nn.softmax(qk, axis=-1)
        out = jnp.einsum('bhqk,bhdk->bhdq', sm, vh)
        return out.reshape(B, Dv, Tq)

    def _L2_ffn_ref(x, gate_w, w_gate, w_up, w_down, shgate_w, shw_gate, shw_up, shw_down):
        import jax, jax.numpy as jnp
        import numpy as np
        B, L, D = (2, 128, 256)
        E, K = (8, 2)
        H, HS = (176, 352)
        b, l, d = x.shape
        xf = x.reshape(-1, d)
        logits = jnp.einsum('td,ed->te', xf.astype(jnp.float32), gate_w)
        probs = jax.nn.softmax(logits.astype(jnp.float32), axis=-1)
        weights, indices = jax.lax.top_k(probs, K)
        weights = (weights / weights.sum(-1, keepdims=True)).astype(x.dtype)
        onehot = jax.nn.one_hot(indices, E, dtype=x.dtype)
        combine = jnp.einsum('tk,tke->te', weights, onehot)
        g = jnp.einsum('td,edh->teh', xf, w_gate)
        u = jnp.einsum('td,edh->teh', xf, w_up)
        h = jax.nn.silu(g) * u
        out = jnp.einsum('teh,ehd,te->td', h.astype(jnp.float32), w_down.astype(jnp.float32), combine.astype(jnp.float32))
        sgate = jax.nn.sigmoid(xf @ shgate_w)[:, None]
        sh = jax.nn.silu(xf @ shw_gate) * (xf @ shw_up) @ shw_down
        out = out + (sgate * sh).astype(jnp.float32)
        return out.astype(x.dtype).reshape(b, l, d)

    def _L3_attn_ref(x, w_qkv, wo, lambda_q1, lambda_q2, lambda_k1, lambda_k2, gamma, beta):
        import jax, jax.numpy as jnp
        import numpy as np
        B, S, E, H = (2, 256, 256, 16)
        HD = E // H
        INIT_LAMBDA = 0.8

        def rope_cos_sin(seqlen, head_dim, dtype):
            inv = 1.0 / 10000.0 ** (jnp.arange(0, head_dim, 2, dtype=jnp.float32) / head_dim)
            ang = jnp.arange(seqlen, dtype=jnp.float32)[:, None] * inv[None, :]
            ang = jnp.concatenate([ang, ang], axis=-1)
            return (jnp.cos(ang).astype(dtype), jnp.sin(ang).astype(dtype))

        def apply_rope(x, cos, sin):
            d = x.shape[-1]
            x1, x2 = (x[..., :d // 2], x[..., d // 2:])
            rot = jnp.concatenate([-x2, x1], axis=-1)
            return x * cos + rot * sin
        b, s, e = x.shape
        hd = e // H
        scaler = hd ** (-0.5)
        qkv = x @ w_qkv.T
        q, k, v = jnp.split(qkv, 3, axis=-1)
        to_heads = lambda t: t.reshape(b, s, H, hd).transpose(0, 2, 1, 3)
        q, k, v = (to_heads(q), to_heads(k), to_heads(v))
        cos, sin = rope_cos_sin(s, hd, x.dtype)
        q = apply_rope(q, cos, sin)
        k = apply_rope(k, cos, sin)
        q1, q2 = jnp.split(q, 2, axis=-1)
        k1, k2 = jnp.split(k, 2, axis=-1)
        lam = (jnp.exp(jnp.sum(lambda_q1 * lambda_k1)) - jnp.exp(jnp.sum(lambda_q2 * lambda_k2)) + INIT_LAMBDA).astype(x.dtype)
        add_mask = jnp.triu(jnp.ones((s, s), x.dtype), k=1)

        def sdpa(qh, kh):
            scores = jnp.einsum('bhqd,bhkd->bhqk', qh, kh) * scaler + add_mask
            p = jax.nn.softmax(scores, axis=-1)
            return jnp.einsum('bhqk,bhkd->bhqd', p, v)
        out = sdpa(q1, k1) - lam * sdpa(q2, k2)
        y = out.transpose(0, 2, 1, 3).reshape(b, e, s)
        yg = y.reshape(b, H, e // H * s)
        mean = jnp.mean(yg, axis=-1, keepdims=True)
        var = jnp.var(yg, axis=-1, keepdims=True)
        yn = ((yg - mean) * jax.lax.rsqrt(var + 1e-05)).reshape(b, e, s)
        yn = yn * gamma[None, :, None] + beta[None, :, None]
        y = (yn * (1.0 - INIT_LAMBDA)).reshape(b, s, e)
        return y @ wo.T

    def _L3_xattn_ref(hidden_states, memory_tokens, memory_mask):
        import jax, jax.numpy as jnp
        import numpy as np
        B, S, D = hidden_states.shape
        scale = 1.0 / jnp.sqrt(jnp.asarray(D, hidden_states.dtype))
        scores = jnp.einsum('bsd,bmd->bsm', hidden_states, memory_tokens) * scale
        neg_inf = jnp.asarray(-1e+30, scores.dtype)
        scores = jnp.where(memory_mask[:, None, :], scores, neg_inf)
        attn = jax.nn.softmax(scores, axis=-1)
        readout = jnp.einsum('bsm,bmd->bsd', attn, memory_tokens)
        valid_b = jnp.any(memory_mask, axis=-1)
        out = jnp.where(valid_b[:, None, None], readout, jnp.zeros_like(readout))
        return out

    def _L3_ffn_ref(x, w_router, we1, we3, we2, ws1, ws3, ws2):
        import jax, jax.numpy as jnp
        import numpy as np
        TOP_K = 4
        B, S, D = x.shape
        T = B * S
        E = w_router.shape[1]
        xt = x.reshape(T, D)
        probs = jax.nn.softmax(xt @ w_router, axis=-1)
        top_w, top_i = jax.lax.top_k(probs, TOP_K)
        top_w = top_w / jnp.sum(top_w, axis=-1, keepdims=True)
        cw = jnp.zeros((T, E), xt.dtype).at[jnp.arange(T)[:, None], top_i].add(top_w)
        g = jax.nn.silu(jnp.einsum('td,edh->teh', xt, we1)) * jnp.einsum('td,edh->teh', xt, we3)
        g = g * cw[:, :, None]
        moe_out = jnp.einsum('teh,ehd->td', g, we2)
        shared = jax.nn.silu(xt @ ws1) * (xt @ ws3) @ ws2
        k = TOP_K
        out = shared / (k + 1) + moe_out * (k / (k + 1))
        return out.reshape(B, S, D)
    x = _layernorm(x + _L0_attn_ref(x, L0_attn_Wq, L0_attn_Wk, L0_attn_Wv, L0_attn_Wb, L0_attn_bb, L0_attn_Wo), axis=-1)
    x = _layernorm(x + _L0_xattn_ref(x, ctx_2048, ctx_2048), axis=-1)
    x = _layernorm(x + _L0_ffn_ref(x, L0_ffn_gate_weight, L0_ffn_gate_up_weights, L0_ffn_down_weights, L0_ffn_shared_gate_up, L0_ffn_shared_down), axis=-1)
    x = _layernorm(x + _L1_attn_ref(x, L1_attn_kv_k, L1_attn_kv_v, L1_attn_Wq, L1_attn_Wo), axis=-1)
    x = _layernorm(x + _L1_xattn_ref(x, ctx_2048, ctx_2048, L1_xattn_Wi, L1_xattn_bi, L1_xattn_Wf, L1_xattn_bf, L1_xattn_ln_scale), axis=-1)
    x = _layernorm(x + _L1_ffn_ref(x, L1_ffn_w1, L1_ffn_w3, L1_ffn_w2, L1_ffn_wr), axis=-1)
    x = _layernorm(x + _L2_attn_ref(x, L2_attn_attn_norm_w, L2_attn_ffn_norm_w, L2_attn_qkv_w, L2_attn_o_w, L2_attn_ffn_up_w, L2_attn_ffn_down_w), axis=-1)
    x = _layernorm(x + _L2_xattn_ref(x, ctx_2048, ctx_2048), axis=-1)
    x = _layernorm(x + _L2_ffn_ref(x, L2_ffn_gate_w, L2_ffn_w_gate, L2_ffn_w_up, L2_ffn_w_down, L2_ffn_shgate_w, L2_ffn_shw_gate, L2_ffn_shw_up, L2_ffn_shw_down), axis=-1)
    x = _layernorm(x + _L3_attn_ref(x, L3_attn_w_qkv, L3_attn_wo, L3_attn_lambda_q1, L3_attn_lambda_q2, L3_attn_lambda_k1, L3_attn_lambda_k2, L3_attn_gamma, L3_attn_beta), axis=-1)
    x = _layernorm(x + _L3_xattn_ref(x, ctx_2048, mask_BxS2_bk0), axis=-1)
    x = _layernorm(x + _L3_ffn_ref(x, L3_ffn_w_router, L3_ffn_we1, L3_ffn_we3, L3_ffn_we2, L3_ffn_ws1, L3_ffn_ws3, L3_ffn_ws2), axis=-1)
    return x

_drawn_inputs = setup_inputs


def setup_inputs(seed=0):
    import zlib

    import numpy as np

    out = dict(_drawn_inputs(seed))
    spreads = {'L0_attn_bb': (0.0, 0.1),
     'L1_xattn_ln_scale': (1.0, 0.2),
     'L2_attn_attn_norm_w': (1.0, 0.6),
     'L2_attn_ffn_norm_w': (1.0, 0.6),
     'L3_attn_gamma': (1.0, 0.6),
     'L3_attn_beta': (0.0, 0.579)}
    factors = {'L0_ffn_gate_weight': 7.015,
     'L0_ffn_gate_up_weights': 6.758,
     'L0_ffn_down_weights': 8.0,
     'L1_xattn_bi': 64.0,
     'L1_xattn_Wf': 3.22,
     'L2_attn_ffn_up_w': 3.629,
     'L2_attn_ffn_down_w': 3.579,
     'L2_ffn_gate_w': 4.176,
     'L2_ffn_w_gate': 3.733,
     'L2_ffn_w_up': 3.625,
     'L2_ffn_w_down': 3.617,
     'L2_ffn_shgate_w': 8.0,
     'L2_ffn_shw_gate': 3.607,
     'L2_ffn_shw_up': 3.334,
     'L2_ffn_shw_down': 3.506,
     'L3_attn_lambda_q1': 59.304,
     'L3_attn_lambda_q2': 36.608,
     'L3_attn_lambda_k2': 32.856,
     'L3_attn_lambda_k1': 8.0}
    for name, (base, spread) in spreads.items():
        noise = np.random.default_rng([zlib.crc32(name.encode()), seed]).standard_normal(out[name].shape)
        drawn = base * np.exp(spread * noise) if base else spread * noise
        out[name] = jnp.asarray(drawn.astype(out[name].dtype))
    for name, factor in factors.items():
        out[name] = (out[name] * factor).astype(out[name].dtype)
    return out
```

```python
import numpy as np
from contextlib import ExitStack
import concourse.bass as bass
from concourse import mybir

FIRST, LAST = 0, 11
P, D, S, NB = 128, 256, 64, 32
N = S * NB
T = N // P
G = 4
F32, BF16 = mybir.dt.float32, mybir.dt.bfloat16
ALU, ACT, AX = mybir.AluOpType, mybir.ActivationFunctionType, mybir.AxisListType
LN_EPS = 1e-5
HEADS, HD = 16, 16
KEYS = 4096
NEG = -1e30


def semaphores(nc, ctx, phase, names):
    return [nc.alloc_semaphore(f"{phase}_{n}") for n in names.split()]


def layer_norm(nc, k, name):
    with ExitStack() as ctx:
        def sb(n, shape):
            return ctx.enter_context(nc.sbuf_tensor(name + n, shape, F32))
        LANES = 4
        stats = sb("stats", [P, T, 6])
        MEAN, APART, VAR, APART2, TOTAL, RSTD = range(6)
        mom = sb("mom", [P, 6, T])
        stage = [sb(f"stage{u}", [P, D]) for u in range(LANES)]
        taken, vec, vared, rstd_ready, staged, written, turned, copied = semaphores(
            nc, ctx, name, "taken vec variance rstd staged written turned copied")
        block = ctx.enter_context(nc.Block(name + "_b"))

        @block.vector
        def _(dve):
            with dve.Fori(0, T // LANES) as i:
                for u in range(LANES):
                    dve.bn_stats(stats[:, bass.ds(LANES * i + u, 1), :], k.x[:, bass.ds(LANES * i + u, 1), :]).then_inc(taken, 1)
            dve.wait_ge(taken, T)
            me, mo, ve, vo = stats[:, :, 1], stats[:, :, 4], stats[:, :, 2], stats[:, :, 5]
            dve.tensor_tensor(mom[:, MEAN, :], me, mo, ALU.add).then_inc(vec, 1)
            dve.tensor_tensor(mom[:, APART, :], me, mo, ALU.subtract).then_inc(vec, 1)
            dve.tensor_tensor(mom[:, VAR, :], ve, vo, ALU.add).then_inc(vec, 1)
            dve.wait_ge(vec, 3)
            dve.tensor_tensor(mom[:, APART2, :], mom[:, APART, :], mom[:, APART, :], ALU.mult).then_inc(vec, 1)
            dve.tensor_scalar(mom[:, VAR, :], mom[:, VAR, :], 1.0 / D, LN_EPS, ALU.mult, ALU.add).then_inc(vec, 1)
            dve.tensor_scalar(mom[:, MEAN, :], mom[:, MEAN, :], 0.5, None, ALU.mult).then_inc(vec, 1)
            dve.wait_ge(vec, 6)
            dve.scalar_tensor_tensor(out=mom[:, TOTAL, :], in0=mom[:, APART2, :], scalar=0.25, in1=mom[:, VAR, :],
                                     op0=ALU.mult, op1=ALU.add).then_inc(vared, 1)
            dve.wait_ge(rstd_ready, 1)
            with dve.Fori(0, T // LANES) as i:
                for u in range(LANES):
                    xt, t = k.x[:, bass.ds(LANES * i + u, 1), :], bass.ds(LANES * i + u, 1)
                    dve.wait_ge(turned, LANES * i + u + 1)
                    dve.tensor_scalar(stage[u][:, :], xt, mom[:, MEAN, t], mom[:, RSTD, t], ALU.subtract, ALU.mult).then_inc(staged, 1)
                    dve.tensor_scalar(xt, xt, mom[:, MEAN, t], mom[:, RSTD, t], ALU.subtract, ALU.mult).then_inc(written, 1)

        @block.gpsimd
        def _(pool):
            pool.wait_ge(vared, 1)
            pool.tensor_tensor(mom[:, RSTD, :], mom[:, TOTAL, :], k.minus_half[:, 0:T], ALU.pow).then_inc(rstd_ready, 1)

        @block.tensor
        def _(pe):
            pe.sem_inc(turned, LANES)
            with pe.Fori(0, T // LANES) as i:
                for u in range(LANES):
                    pe.wait_ge(staged, LANES * i + u + 1)
                    pe.wait_ge(copied, LANES * i + u + 1)
                    pe.transpose(k.ps[u][:, 0:128], stage[u][:, 0:128], k.ident[:, :])
                    pe.transpose(k.ps[u][:, 128:256], stage[u][:, 128:256], k.ident[:, :]).then_inc(turned, 1)

        @block.scalar
        def _(act):
            act.sem_inc(copied, LANES)
            with act.Fori(0, T // LANES) as i:
                for u in range(LANES):
                    act.wait_ge(turned, LANES * i + u + 1 + LANES)
                    act.copy(k.xT[:, :, bass.ds((LANES * i + u) * P, P)],
                             k.ps[u][:, 0:256].rearrange("p (c n) -> p c n", c=2)).then_inc(copied, 1)




class Steps:

    def __init__(self, nc, engine, name, steps):
        self.sem = nc.alloc_semaphore(name)
        by = {"pe": nc.tensor, "act": nc.scalar, "dve": nc.vector, "pool": nc.gpsimd}[engine]
        by.sem_inc(self.sem, 1)
        self.names = steps.split()
        self.per = len(self.names)

    def at(self, i, step):
        return self.per * i + self.names.index(step) + 2

    def turns(self, i):
        return self.per * i + 1


def lane_steps(nc, phase, engine, steps, lanes=2):
    return [Steps(nc, engine, f"{phase}_{engine}{u}", steps) for u in range(lanes)]


def heads3(ap):
    return ap.rearrange("p (h j) -> p h j", j=S)


def l0_attention(nc, k):
    delta_scores(nc, k)
    delta_solve(nc, k)
    delta_output(nc, k)


def delta_scores(nc, k):
    SCALE = HD ** -0.5
    with ExitStack() as ctx:
        def sb(name, shape, dt=F32):
            return ctx.enter_context(nc.sbuf_tensor("d0" + name, shape, dt))
        w = sb("w", [P, 2, 784])
        bb = sb("bb", [P, HEADS])
        xs = [sb(f"xs{u}", [P, 2, P]) for u in range(2)]
        qk = [sb(f"qk{u}", [P, 512]) for u in range(2)]
        t1 = [sb(f"t1{u}", [P, 512]) for u in range(2)]
        t2 = [sb(f"t2{u}", [P, 512]) for u in range(2)]
        v = [sb(f"v{u}", [P, D]) for u in range(2)]
        beta = [sb(f"beta{u}", [P, HEADS]) for u in range(2)]
        qkT = [sb(f"qkT{u}", [P, 4, P]) for u in range(2)]
        kexp = [sb(f"kexp{u}", [P, 2, 2, 8, S]) for u in range(2)]
        sc = [[sb(f"sc{u}{n}", [P, HEADS * S]) for n in range(2)] for u in range(2)]
        pT = [sb(f"pT{u}", [P, HEADS * S]) for u in range(2)]
        mx = [[sb(f"mx{u}{n}", [P, HEADS]) for n in range(2)] for u in range(2)]
        den = [[sb(f"den{u}{n}", [P, HEADS]) for n in range(2)] for u in range(2)]
        loaded, = semaphores(nc, ctx, "d0", "loaded")
        stored = [nc.alloc_semaphore(f"d0_stored{u}") for u in range(2)]
        pe_ = lane_steps(nc, "d0", "pe", "QKV TURNED SCORES PT")
        act_ = lane_steps(nc, "d0", "act", "V QKT EXP0 EXP1 PT")
        dve_ = lane_steps(nc, "d0", "dve", "COS SIN ROPED BETA KEXP MASK0 MAX0 SUB0 MASK1 MAX1 SUB1 SUM0 REC0 FAC0 LROW SUM1 REC1 PROW")
        pool_ = lane_steps(nc, "d0", "pool", "XS")
        bank = [[k.ps[4 * u + n] for n in range(4)] for u in range(2)]
        masks = [k.strict, k.causal]
        block = ctx.enter_context(nc.Block("d0_b"))

        @block.sync
        def _(sp):
            sp.dma_start(w[:, :, :], k.a["L0_attn_W"].rearrange("(c p) n -> p c n", p=P)).then_inc(loaded, 16)
            sp.dma_start(bb[:, :], k.a["L0_attn_bb"].partition_broadcast(P)).then_inc(loaded, 16)
            with sp.Fori(0, T // 2) as i:
                for u in range(2):
                    t = 2 * i + u
                    sp.wait_ge(act_[u].sem, act_[u].at(i, "V"))
                    sp.dma_start(k.v_scr[bass.ds(t * P, P), :], v[u][:, :]).then_inc(stored[u], 16)
                for u in range(2):
                    t = 2 * i + u
                    sp.wait_ge(dve_[u].sem, dve_[u].at(i, "LROW"))
                    for b in range(2):
                        sp.dma_start(k.l_scr[bass.ds(2 * t + b, 1), :, :, :].rearrange("b h i j -> (b i) h j"),
                                     heads3(sc[u][0][64 * b:64 * b + 64, :])).then_inc(stored[u], 16)
                for u in range(2):
                    t = 2 * i + u
                    sp.wait_ge(act_[u].sem, act_[u].at(i, "PT"))
                    sp.dma_start(k.p_scr[bass.ds(t, 1), :, :].rearrange("t p n -> (t p) n"),
                                 pT[u][:, :]).then_inc(stored[u], 16)
            for u in range(2):
                sp.wait_ge(stored[u], 64 * (T // 2))

        @block.gpsimd
        def _(pool):
            with pool.Fori(0, T // 2) as i:
                for u in range(2):
                    pool.wait_ge(pe_[u].sem, pe_[u].turns(i))
                    pool.tensor_copy(xs[u][:, :, :], k.xT[:, :, bass.ds((2 * i + u) * P, P)]).then_inc(pool_[u].sem, 1)

        @block.tensor
        def _(pe):
            pe.wait_ge(loaded, 32)
            with pe.Fori(0, T // 2) as i:
                for u in range(2):
                    A, B, C, E = bank[u]
                    pe.wait_ge(pool_[u].sem, pool_[u].at(i, "XS"))
                    pe.wait_ge(act_[u].sem, act_[u].turns(i))
                    for n, (o, lo, hi) in enumerate(((A[:, :], 0, 512), (B[:, 0:272], 512, 784))):
                        for c in range(2):
                            mm = pe.matmul(o, xs[u][:, c, :], w[:, c, lo:hi], start=(c == 0), stop=(c == 1))
                    mm.then_inc(pe_[u].sem, 1)
                for u in range(2):
                    pe.wait_ge(dve_[u].sem, dve_[u].at(i, "ROPED"))
                    for c in range(4):
                        mm = pe.transpose(bank[u][2][:, c * P:(c + 1) * P], qk[u][:, c * P:(c + 1) * P], k.ident[:, :])
                    mm.then_inc(pe_[u].sem, 1)
                for u in range(2):
                    pe.wait_ge(act_[u].sem, act_[u].at(i, "QKT"))
                    pe.wait_ge(dve_[u].sem, dve_[u].at(i, "KEXP"))
                    for n, first in ((0, 2), (1, 0)):
                        for b in range(2):
                            for c in range(2):
                                mm = pe.matmul(bank[u][2 * n + c][64 * b:64 * b + 64, :],
                                               qkT[u][:, first + c, 64 * b:64 * b + 64],
                                               kexp[u][:, c, b, :, :], start=True, stop=True)
                    mm.then_inc(pe_[u].sem, 1)
                for u in range(2):
                    pe.wait_ge(dve_[u].sem, dve_[u].at(i, "PROW"))
                    for c in range(8):
                        mm = pe.transpose(bank[u][c // 4][:, (c % 4) * P:(c % 4 + 1) * P],
                                          sc[u][1][:, c * P:(c + 1) * P], k.ident[:, :])
                    mm.then_inc(pe_[u].sem, 1)

        @block.scalar
        def _(act):
            act.preload_act_table(ACT.Exp)
            with act.Fori(0, T // 2) as i:
                for u in range(2):
                    act.wait_ge(pe_[u].sem, pe_[u].at(i, "QKV"))
                    act.wait_ge(stored[u], 64 * i)
                    act.copy(v[u][:, :], bank[u][1][:, 0:D]).then_inc(act_[u].sem, 1)
                for u in range(2):
                    act.wait_ge(pe_[u].sem, pe_[u].at(i, "TURNED"))
                    act.copy(qkT[u][:, :, :], bank[u][2][:, :].rearrange("p (c n) -> p c n", c=4)).then_inc(act_[u].sem, 1)
                for n in range(2):
                    for u in range(2):
                        act.wait_ge(dve_[u].sem, dve_[u].at(i, f"SUB{n}"))
                        act.activation(sc[u][n][:, :], sc[u][n][:, :], ACT.Exp).then_inc(act_[u].sem, 1)
                for u in range(2):
                    act.wait_ge(pe_[u].sem, pe_[u].at(i, "PT"))
                    act.wait_ge(stored[u], 64 * i)
                    act.copy(pT[u][:, 0:512], bank[u][0][:, :])
                    act.copy(pT[u][:, 512:1024], bank[u][1][:, :]).then_inc(act_[u].sem, 1)

        @block.vector
        def _(dve):
            def wait(u, i, step):
                dve.wait_ge(dve_[u].sem, dve_[u].at(i, step))

            dve.wait_ge(loaded, 32)
            with dve.Fori(0, T // 2) as i:
                for u in range(2):
                    dve.wait_ge(pe_[u].sem, pe_[u].at(i, "QKV"))
                    x4 = bank[u][0][:, :].rearrange("p (n d) -> p n d", d=8)
                    dve.tensor_tensor(t1[u][:, :].rearrange("p (n d) -> p n d", d=8), x4,
                                      k.cos[:, :].unsqueeze(1).to_broadcast([P, 64, 8]), ALU.mult).then_inc(dve_[u].sem, 1)
                    dve.tensor_tensor(t2[u][:, :].rearrange("p (n d) -> p n d", d=8), x4,
                                      k.sin[:, :].unsqueeze(1).to_broadcast([P, 64, 8]), ALU.mult).then_inc(dve_[u].sem, 1)
                    wait(u, i, "SIN")
                    halves = [a[u][:, :].rearrange("p (n f d) -> p n f d", f=2, d=8) for a in (t1, t2, qk)]
                    dve.tensor_tensor(halves[2][:, :, 0, :], halves[0][:, :, 0, :], halves[1][:, :, 1, :], ALU.subtract)
                    dve.tensor_tensor(halves[2][:, :, 1, :], halves[0][:, :, 1, :], halves[1][:, :, 0, :],
                                      ALU.add).then_inc(dve_[u].sem, 1)
                    dve.wait_ge(act_[u].sem, act_[u].at(i, "V"))
                    dve.tensor_tensor(beta[u][:, :], bank[u][1][:, D:D + HEADS], bb[:, :], ALU.add).then_inc(dve_[u].sem, 1)
                for u in range(2):
                    dve.wait_ge(act_[u].sem, act_[u].at(i, "QKT"))
                    for c in range(2):
                        ins = dve.tensor_tensor(
                            kexp[u][:, c, :, :, :],
                            qkT[u][:, 2 + c, :].rearrange("p (b j) -> p b j", b=2).unsqueeze(2).to_broadcast([P, 2, 8, S]),
                            k.head_mask[:, :].unsqueeze(1).unsqueeze(3).to_broadcast([P, 2, 8, S]), ALU.mult)
                    ins.then_inc(dve_[u].sem, 1)
                for n in range(2):
                    for u in range(2):
                        dve.wait_ge(pe_[u].sem, pe_[u].at(i, "SCORES"))
                        if n == 0:
                            dve.wait_ge(stored[u], 64 * i)
                        for c in range(2):
                            ins = dve.scalar_tensor_tensor(
                                out=heads3(sc[u][n][:, c * 512:(c + 1) * 512]), in0=heads3(bank[u][2 * n + c][:, :]), scalar=SCALE,
                                in1=masks[n][:, :].unsqueeze(1).to_broadcast([P, 8, S]), op0=ALU.mult, op1=ALU.add)
                        ins.then_inc(dve_[u].sem, 1)
                        wait(u, i, f"MASK{n}")
                        dve.tensor_reduce(mx[u][n][:, :], heads3(sc[u][n][:, :]), AX.X, ALU.max).then_inc(dve_[u].sem, 1)
                        wait(u, i, f"MAX{n}")
                        dve.tensor_tensor(heads3(sc[u][n][:, :]), heads3(sc[u][n][:, :]),
                                          mx[u][n][:, :].unsqueeze(2).to_broadcast([P, HEADS, S]),
                                          ALU.subtract).then_inc(dve_[u].sem, 1)
                for u in range(2):
                    dve.wait_ge(act_[u].sem, act_[u].at(i, "EXP0"))
                    dve.tensor_reduce(den[u][0][:, :], heads3(sc[u][0][:, :]), AX.X, ALU.add).then_inc(dve_[u].sem, 1)
                    wait(u, i, "SUM0")
                    dve.reciprocal(den[u][0][:, :], den[u][0][:, :]).then_inc(dve_[u].sem, 1)
                    wait(u, i, "REC0")
                    dve.scalar_tensor_tensor(out=den[u][0][:, :], in0=den[u][0][:, :], scalar=k.not_first[:, :],
                                             in1=beta[u][:, :], op0=ALU.mult, op1=ALU.mult).then_inc(dve_[u].sem, 1)
                    wait(u, i, "FAC0")
                    dve.tensor_tensor(heads3(sc[u][0][:, :]), heads3(sc[u][0][:, :]),
                                      den[u][0][:, :].unsqueeze(2).to_broadcast([P, HEADS, S]), ALU.mult).then_inc(dve_[u].sem, 1)
                for u in range(2):
                    dve.wait_ge(act_[u].sem, act_[u].at(i, "EXP1"))
                    dve.tensor_reduce(den[u][1][:, :], heads3(sc[u][1][:, :]), AX.X, ALU.add).then_inc(dve_[u].sem, 1)
                    wait(u, i, "SUM1")
                    dve.reciprocal(den[u][1][:, :], den[u][1][:, :]).then_inc(dve_[u].sem, 1)
                    wait(u, i, "REC1")
                    dve.tensor_tensor(heads3(sc[u][1][:, :]), heads3(sc[u][1][:, :]),
                                      den[u][1][:, :].unsqueeze(2).to_broadcast([P, HEADS, S]), ALU.mult).then_inc(dve_[u].sem, 1)


def delta_solve(nc, k):
    with ExitStack() as ctx:
        def sb(name, shape, dt=F32):
            return ctx.enter_context(nc.sbuf_tensor("ds" + name, shape, dt))
        lm = [sb(f"l{u}", [P, S, S]) for u in range(2)]
        vs = [sb(f"v{u}", [P, S, HD]) for u in range(2)]
        tmp = [sb(f"tmp{u}", [P, S, HD]) for u in range(2)]
        arrived = [nc.alloc_semaphore(f"ds_arrived{u}") for u in range(2)]
        solved = [nc.alloc_semaphore(f"ds_solved{u}") for u in range(2)]
        stored = [nc.alloc_semaphore(f"ds_stored{u}") for u in range(2)]
        chain = [nc.alloc_semaphore(f"ds_chain{u}") for u in range(2)]
        STEPS = 2 * (S - 1)
        block = ctx.enter_context(nc.Block("ds_b"))

        @block.sync
        def _(sp):
            with sp.Fori(0, 2) as i:
                for u in range(2):
                    g = 2 * i + u
                    sp.wait_ge(stored[u], 16 * 8 * i)
                    sp.dma_start(lm[u][:, :, :].rearrange("p i j -> p (i j)"),
                                 k.l_scr[bass.ds(8 * g, 8), :, :, :].rearrange("b h i j -> (b h) (i j)")).then_inc(arrived[u], 16)
                    for b in range(8):
                        sp.dma_start(vs[u][16 * b:16 * b + 16, :, :],
                                     k.v_scr[bass.ds((8 * g + b) * S, S), :].rearrange("j (h d) -> h j d", d=HD)).then_inc(arrived[u], 16)
                for u in range(2):
                    g = 2 * i + u
                    sp.wait_ge(solved[u], i + 1)
                    for b in range(8):
                        sp.dma_start(k.u_scr[bass.ds((8 * g + b) * S, S), :].rearrange("j (h d) -> h j d", d=HD),
                                     vs[u][16 * b:16 * b + 16, :, :]).then_inc(stored[u], 16)
            for u in range(2):
                sp.wait_ge(stored[u], 16 * 8 * 2)

        @block.vector
        def _(dve):
            with dve.Fori(0, 2) as i:
                for u in range(2):
                    dve.wait_ge(arrived[u], 16 * 9 * (i + 1))
                for j in range(S - 1):
                    n = S - 1 - j
                    for u in range(2):
                        if j:
                            dve.wait_ge(chain[u], i * STEPS + 2 * j)
                        dve.tensor_tensor(tmp[u][:, 0:n, :], lm[u][:, j + 1:S, j].unsqueeze(2).to_broadcast([P, n, HD]),
                                          vs[u][:, j, :].unsqueeze(1).to_broadcast([P, n, HD]), ALU.mult).then_inc(chain[u], 1)
                    for u in range(2):
                        dve.wait_ge(chain[u], i * STEPS + 2 * j + 1)
                        dve.tensor_tensor(vs[u][:, j + 1:S, :], vs[u][:, j + 1:S, :], tmp[u][:, 0:n, :],
                                          ALU.subtract).then_inc(chain[u], 1)
                for u in range(2):
                    dve.wait_ge(chain[u], (i + 1) * STEPS)
                    dve.sem_inc(solved[u], 1)


def delta_output(nc, k):
    with ExitStack() as ctx:
        def sb(name, shape, dt=F32):
            return ctx.enter_context(nc.sbuf_tensor("do" + name, shape, dt))
        w = sb("w", [P, 2, D])
        pT = [sb(f"pT{u}", [P, 8, P]) for u in range(2)]
        ud = [sb(f"ud{u}", [P, 2, D]) for u in range(2)]
        o = [sb(f"o{u}", [P, D]) for u in range(2)]
        oT = [sb(f"oT{u}", [P, 2, P]) for u in range(2)]
        loaded, = semaphores(nc, ctx, "do", "loaded")
        arrived = [nc.alloc_semaphore(f"do_arrived{u}") for u in range(2)]
        pe_ = lane_steps(nc, "do", "pe", "O OT Y")
        act_ = lane_steps(nc, "do", "act", "O OT")
        dve_ = lane_steps(nc, "do", "dve", "UBD Y")
        bank = [[k.ps[4 * u + n] for n in range(4)] for u in range(2)]
        block = ctx.enter_context(nc.Block("do_b"))

        @block.sync
        def _(sp):
            sp.dma_start(w[:, :, :], k.a["L0_attn_Wo"].rearrange("(c p) n -> p c n", p=P)).then_inc(loaded, 16)
            with sp.Fori(0, T // 2) as i:
                for u in range(2):
                    t = 2 * i + u
                    sp.wait_ge(pe_[u].sem, pe_[u].turns(i))
                    sp.dma_start(pT[u][:, :, :].rearrange("p c n -> p (c n)"),
                                 k.p_scr[bass.ds(t, 1), :, :].rearrange("t p n -> (t p) n")).then_inc(arrived[u], 16)
                    for r in range(2):
                        sp.dma_start(ud[u][64 * r:64 * r + 64, :, :],
                                     k.u_scr[bass.ds(t * P, P), :].rearrange("(b j) n -> j b n", b=2)).then_inc(arrived[u], 16)

        @block.vector
        def _(dve):
            with dve.Fori(0, T // 2) as i:
                for u in range(2):
                    dve.wait_ge(arrived[u], 48 * (i + 1))
                    dve.tensor_tensor(ud[u][:, :, :].rearrange("p b (h d) -> p b h d", d=HD),
                                      ud[u][:, :, :].rearrange("p b (h d) -> p b h d", d=HD),
                                      k.parity[:, :].unsqueeze(1).unsqueeze(3).to_broadcast([P, 2, HEADS, HD]),
                                      ALU.mult).then_inc(dve_[u].sem, 1)
                for u in range(2):
                    xt = k.x[:, bass.ds(2 * i + u, 1), :].rearrange("p t d -> p (t d)")
                    dve.wait_ge(pe_[u].sem, pe_[u].at(i, "Y"))
                    dve.tensor_tensor(xt, xt, bank[u][2][:, 0:D], ALU.add).then_inc(dve_[u].sem, 1)

        @block.tensor
        def _(pe):
            pe.wait_ge(loaded, 16)
            with pe.Fori(0, T // 2) as i:
                for u in range(2):
                    pe.wait_ge(dve_[u].sem, dve_[u].at(i, "UBD"))
                    for c in range(8):
                        mm = pe.matmul(bank[u][0][:, 64 * c:64 * c + 64].rearrange("p (b n) -> p b n", b=2), pT[u][:, c, :],
                                       ud[u][:, :, 32 * c:32 * c + 32], start=True, stop=True)
                    mm.then_inc(pe_[u].sem, 1)
                for u in range(2):
                    pe.wait_ge(act_[u].sem, act_[u].at(i, "O"))
                    for c in range(2):
                        mm = pe.transpose(bank[u][1][:, c * P:(c + 1) * P], o[u][:, c * P:(c + 1) * P], k.ident[:, :])
                    mm.then_inc(pe_[u].sem, 1)
                for u in range(2):
                    pe.wait_ge(act_[u].sem, act_[u].at(i, "OT"))
                    pe.wait_ge(dve_[u].sem, dve_[u].turns(i))
                    for c in range(2):
                        mm = pe.matmul(bank[u][2][:, 0:D], oT[u][:, c, :], w[:, c, :], start=(c == 0), stop=(c == 1))
                    mm.then_inc(pe_[u].sem, 1)

        @block.scalar
        def _(act):
            with act.Fori(0, T // 2) as i:
                for u in range(2):
                    act.wait_ge(pe_[u].sem, pe_[u].at(i, "O"))
                    for b in range(2):
                        r = slice(64 * b, 64 * b + 64)
                        ins = act.copy(o[u][r, :].rearrange("p (c n) -> p c n", c=8),
                                       bank[u][0][r, :].rearrange("p (c b n) -> p c b n", b=2, n=32)[:, :, b, :])
                    ins.then_inc(act_[u].sem, 1)
                for u in range(2):
                    act.wait_ge(pe_[u].sem, pe_[u].at(i, "OT"))
                    act.copy(oT[u][:, :, :], bank[u][1][:, 0:D].rearrange("p (c n) -> p c n", c=2)).then_inc(act_[u].sem, 1)


def row_slice(b):
    return slice(64 * b, 64 * b + 64)


def tile_rows(ap, t):
    return ap[:, bass.ds(t, 1), :].rearrange("p t d -> p (t d)")


def over_heads(ap, n=HEADS):
    return ap.unsqueeze(1).to_broadcast([P, n, S])


def per_head(ap, n=S):
    return ap.unsqueeze(2).to_broadcast([P, HEADS, n])


def spread_keys(eng, out, keys, head_mask):
    for c in range(2):
        ins = eng.tensor_tensor(
            out[:, c, :, :, :],
            keys[:, c, :].rearrange("p (b j) -> p b j", b=2).unsqueeze(2).to_broadcast([P, 2, 8, S]),
            head_mask.unsqueeze(1).unsqueeze(3).to_broadcast([P, 2, 8, S]), ALU.mult)
    return ins


def score_matmuls(pe, banks, queries, keys):
    for b in range(2):
        for c in range(2):
            mm = pe.matmul(banks[c][row_slice(b), :], queries[:, c, row_slice(b)], keys[:, c, b, :, :],
                           start=True, stop=True)
    return mm


def weight_transposes(pe, banks, weights, ident):
    for c in range(8):
        mm = pe.transpose(banks[c // 4][:, (c % 4) * P:(c % 4 + 1) * P], weights[:, c * P:(c + 1) * P], ident)
    return mm


def value_matmuls(pe, bank, weights_t, values):
    for c in range(8):
        mm = pe.matmul(bank[:, 64 * c:64 * c + 64].rearrange("p (b n) -> p b n", b=2), weights_t[:, c, :],
                       values[:, :, 32 * c:32 * c + 32], start=True, stop=True)
    return mm


def own_batch(bank, b):
    return bank[row_slice(b), :].rearrange("p (c b h d) -> p c b h d", b=2, h=2, d=HD)[:, :, b, :, :]


def values_by_parity(eng, out, values, parity):
    return eng.tensor_tensor(out[:, :, :].rearrange("p b (h d) -> p b h d", d=HD), values.rearrange("p b (h d) -> p b h d", d=HD),
                             parity.unsqueeze(1).unsqueeze(3).to_broadcast([P, 2, HEADS, HD]), ALU.mult)


def rope_sums(eng, out, by_cos, by_sin):
    c, s, o = (a.rearrange("p (n f d) -> p n f d", f=2, d=8) for a in (by_cos, by_sin, out))
    eng.tensor_tensor(o[:, :, 0, :], c[:, :, 0, :], s[:, :, 1, :], ALU.subtract)
    return eng.tensor_tensor(o[:, :, 1, :], c[:, :, 1, :], s[:, :, 0, :], ALU.add)


def angles(table):
    return table[:, :].unsqueeze(1).to_broadcast([P, 64, 8])


def by8(ap):
    return ap.rearrange("p (n d) -> p n d", d=8)


def l0_cross(nc, k):
    with ExitStack() as ctx:
        def sb(name, shape, dt=F32):
            return ctx.enter_context(nc.sbuf_tensor("c0" + name, shape, dt))
        xs = [sb(f"xs{u}", [P, D]) for u in range(2)]
        cs = [sb(f"cs{u}", [P, D]) for u in range(2)]
        cT = [sb(f"cT{u}", [P, 2, P]) for u in range(2)]
        sig = [sb(f"sig{u}", [P, 2, 2, D]) for u in range(2)]
        arrived = [nc.alloc_semaphore(f"c0_arrived{u}") for u in range(2)]
        pe_ = lane_steps(nc, "c0", "pe", "S0 S1 O")
        act_ = lane_steps(nc, "c0", "act", "SIG0 SIG1")
        dve_ = lane_steps(nc, "c0", "dve", "X")
        pool_ = lane_steps(nc, "c0", "pool", "XS")
        bank = [[k.ps[4 * u + n] for n in range(4)] for u in range(2)]
        block = ctx.enter_context(nc.Block("c0_b"))

        @block.sync
        def _(sp):
            with sp.Fori(0, T // 2) as i:
                for u in range(2):
                    t = 2 * i + u
                    sp.wait_ge(pe_[u].sem, pe_[u].turns(i))
                    sp.dma_start(cs[u][:, :], k.ctx_rows[bass.ds(t * P, P), :]).then_inc(arrived[u], 16)
                    sp.dma_start(cT[u][:, :, :], k.a["ctxT"].rearrange("(c p) n -> p c n", p=P)[:, :, bass.ds(t * P, P)]).then_inc(arrived[u], 16)

        @block.gpsimd
        def _(pool):
            with pool.Fori(0, T // 2) as i:
                for u in range(2):
                    pool.wait_ge(pe_[u].sem, pe_[u].turns(i))
                    pool.tensor_copy(xs[u][:, :], k.x[:, bass.ds(2 * i + u, 1), :]).then_inc(pool_[u].sem, 1)

        @block.tensor
        def _(pe):
            with pe.Fori(0, T // 2) as i:
                for u in range(2):
                    pe.wait_ge(arrived[u], 32 * (i + 1))
                    pe.wait_ge(pool_[u].sem, pool_[u].at(i, "XS"))
                    for b in range(2):
                        r = slice(64 * b, 64 * b + 64)
                        if b == 0:
                            pe.wait_ge(act_[u].sem, act_[u].turns(i))
                        for c in range(2):
                            mm = pe.matmul(bank[u][b][:, c * D:(c + 1) * D], xs[u][r, c * P:(c + 1) * P], cs[u][r, :],
                                           start=True, stop=True)
                        mm.then_inc(pe_[u].sem, 1)
                for u in range(2):
                    pe.wait_ge(dve_[u].sem, dve_[u].turns(i))
                    for b in range(2):
                        pe.wait_ge(act_[u].sem, act_[u].at(i, f"SIG{b}"))
                        for c in range(2):
                            mm = pe.matmul(bank[u][2][64 * b:64 * b + 64, 0:D], cT[u][:, c, 64 * b:64 * b + 64], sig[u][:, b, c, :],
                                           start=(c == 0), stop=(c == 1))
                    mm.then_inc(pe_[u].sem, 1)

        @block.scalar
        def _(act):
            act.preload_act_table(ACT.Sigmoid)
            with act.Fori(0, T // 2) as i:
                for u in range(2):
                    act.wait_ge(pe_[u].sem, pe_[u].turns(i))
                    for b in range(2):
                        act.wait_ge(pe_[u].sem, pe_[u].at(i, f"S{b}"))
                        act.activation(sig[u][:, b, :, :].rearrange("p c m -> p (c m)"), bank[u][b][:, :], ACT.Sigmoid,
                                       scale=S ** -0.5).then_inc(act_[u].sem, 1)

        @block.vector
        def _(dve):
            with dve.Fori(0, T // 2) as i:
                for u in range(2):
                    xt = k.x[:, bass.ds(2 * i + u, 1), :].rearrange("p t d -> p (t d)")
                    dve.wait_ge(pe_[u].sem, pe_[u].at(i, "O"))
                    dve.tensor_tensor(xt, xt, bank[u][2][:, 0:D], ALU.add).then_inc(dve_[u].sem, 1)


def moe_route(nc, k, name, router, E, TOP, renorm, times, shared_gate=False, rows=None):
    EC = E + 1 if shared_gate else E
    with ExitStack() as ctx:
        def sb(n, shape, dt=F32):
            return ctx.enter_context(nc.sbuf_tensor(name + n, shape, dt))
        w = sb("w", [P, 2, EC])
        xs = [sb(f"xs{u}", [P, 2, 4 * P]) for u in range(2)]
        pr = [sb(f"pr{u}", [P, 4, EC]) for u in range(2)]
        cb = [sb(f"cb{u}", [P, 4, EC]) for u in range(2)]
        rep = [sb(f"rep{u}", [P, 4, E]) for u in range(2)]
        top = [sb(f"top{u}", [P, 4, 8]) for u in range(2)]
        m4 = [sb(f"m4{u}", [P, 4]) for u in range(2)]
        carrier = sb("carrier", [P, 1])
        loaded, = semaphores(nc, ctx, name, "loaded")
        pe_ = lane_steps(nc, name, "pe", "LOGITS COMBT")
        act_ = lane_steps(nc, name, "act", "EXP COMBT")
        dve_ = lane_steps(nc, name, "dve", "MAX SUB SUM REC PROBS TOP REST REP COMB" + (" WSUM WREC WNORM" if renorm else "")
                          + (" GATE GATED" if shared_gate else "") + (" ROWS" if rows is not None else ""))
        pool_ = lane_steps(nc, name, "pool", "XS")
        bank = [[k.ps[4 * u + n] for n in range(4)] for u in range(2)]
        block = ctx.enter_context(nc.Block(name + "_b"))

        @block.sync
        def _(sp):
            sp.dma_start(w[:, :, :], k.a[router].rearrange("(c p) n -> p c n", p=P)).then_inc(loaded, 16)

        @block.gpsimd
        def _(pool):
            with pool.Fori(0, T // 8) as i:
                for u in range(2):
                    pool.wait_ge(pe_[u].sem, pe_[u].turns(i))
                    pool.tensor_copy(xs[u][:, :, :], k.xT[:, :, bass.ds((2 * i + u) * 4 * P, 4 * P)]).then_inc(pool_[u].sem, 1)

        @block.tensor
        def _(pe):
            pe.wait_ge(loaded, 16)
            with pe.Fori(0, T // 8) as i:
                for u in range(2):
                    pe.wait_ge(pool_[u].sem, pool_[u].at(i, "XS"))
                    pe.wait_ge(dve_[u].sem, dve_[u].turns(i))
                    for t in range(4):
                        for c in range(2):
                            mm = pe.matmul(bank[u][0][:, t * EC:(t + 1) * EC], xs[u][:, c, t * P:(t + 1) * P], w[:, c, :],
                                           start=(c == 0), stop=(c == 1))
                    mm.then_inc(pe_[u].sem, 1)
                for u in range(2):
                    pe.wait_ge(dve_[u].sem, dve_[u].turns(i + 1))
                    pe.wait_ge(act_[u].sem, act_[u].turns(i))
                    for t in range(4):
                        mm = pe.transpose(bank[u][1][0:EC, t * P:(t + 1) * P], cb[u][:, t, :], k.ident[:, :])
                    mm.then_inc(pe_[u].sem, 1)

        @block.scalar
        def _(act):
            act.preload_act_table(ACT.Exp)
            with act.Fori(0, T // 8) as i:
                for u in range(2):
                    act.wait_ge(dve_[u].sem, dve_[u].at(i, "SUB"))
                    act.activation(pr[u][:, :, :], pr[u][:, :, :], ACT.Exp).then_inc(act_[u].sem, 1)
                for u in range(2):
                    act.wait_ge(pe_[u].sem, pe_[u].at(i, "COMBT"))
                    act.copy(k.combT[0:EC, bass.ds((2 * i + u) * 4 * P, 4 * P)], bank[u][1][0:EC, :]).then_inc(act_[u].sem, 1)

        @block.vector
        def _(dve):
            with dve.Fori(0, T // 8) as i:
                for u in range(2):
                    def wait(step, u=u):
                        dve.wait_ge(dve_[u].sem, dve_[u].at(i, step))

                    lg = bank[u][0][:, 0:4 * EC].rearrange("p (t e) -> p t e", e=EC)
                    probs, comb = pr[u][:, :, 0:E], cb[u][:, :, 0:E]
                    spread = m4[u][:, :].unsqueeze(2).to_broadcast([P, 4, E])
                    dve.wait_ge(pe_[u].sem, pe_[u].at(i, "LOGITS"))
                    dve.tensor_reduce(m4[u][:, :], lg[:, :, 0:E], AX.X, ALU.max).then_inc(dve_[u].sem, 1)
                    wait("MAX")
                    if shared_gate:
                        dve.tensor_scalar(pr[u][:, :, E], lg[:, :, E], -1.0, None, ALU.mult)
                    dve.tensor_tensor(probs, lg[:, :, 0:E], spread, ALU.subtract).then_inc(dve_[u].sem, 1)
                for u in range(2):
                    probs, comb = pr[u][:, :, 0:E], cb[u][:, :, 0:E]
                    spread = m4[u][:, :].unsqueeze(2).to_broadcast([P, 4, E])

                    def wait(step, u=u):
                        dve.wait_ge(dve_[u].sem, dve_[u].at(i, step))

                    dve.wait_ge(act_[u].sem, act_[u].at(i, "EXP"))
                    dve.tensor_reduce(m4[u][:, :], probs, AX.X, ALU.add).then_inc(dve_[u].sem, 1)
                    wait("SUM")
                    dve.reciprocal(m4[u][:, :], m4[u][:, :]).then_inc(dve_[u].sem, 1)
                    wait("REC")
                    dve.tensor_tensor(probs, probs, spread, ALU.mult).then_inc(dve_[u].sem, 1)
                    wait("PROBS")
                    dve.memset(carrier[:, :], 0.0)
                    for t in range(4):
                        ins = dve.max(top[u][:, t, :], pr[u][:, t, 0:E])
                    ins.then_inc(dve_[u].sem, 1)
                    wait("TOP")
                    dve.memset(top[u][:, :, TOP:8], -1.0).then_inc(dve_[u].sem, 1)
                    wait("REST")
                    dve.memset(carrier[:, :], 0.0)
                    for t in range(4):
                        ins = dve.match_replace(out=rep[u][:, t, :], in_to_replace=top[u][:, t, :],
                                                in_values=pr[u][:, t, 0:E], imm_value=0.0)
                    ins.then_inc(dve_[u].sem, 1)
                    wait("REP")
                    dve.tensor_tensor(comb, probs, rep[u][:, :, :], ALU.subtract).then_inc(dve_[u].sem, 1)
                    if renorm:
                        wait("COMB")
                        dve.tensor_reduce(m4[u][:, :], comb, AX.X, ALU.add).then_inc(dve_[u].sem, 1)
                        wait("WSUM")
                        dve.reciprocal(m4[u][:, :], m4[u][:, :]).then_inc(dve_[u].sem, 1)
                        wait("WREC")
                        if times != 1.0:
                            for t in range(4):
                                ins = dve.tensor_scalar(cb[u][:, t, 0:E], cb[u][:, t, 0:E], m4[u][:, t:t + 1], times, ALU.mult, ALU.mult)
                            ins.then_inc(dve_[u].sem, 1)
                        else:
                            dve.tensor_tensor(comb, comb, spread, ALU.mult).then_inc(dve_[u].sem, 1)
                    if rows is not None:
                        wait("WNORM")
                        dve.tensor_copy(rows[:, bass.ds(4 * (2 * i + u), 4), :], comb).then_inc(dve_[u].sem, 1)
                    if shared_gate:
                        wait("WNORM")
                        dve.tensor_scalar(pr[u][:, :, E], pr[u][:, :, E], 1.0, None, ALU.add).then_inc(dve_[u].sem, 1)
                        wait("GATE")
                        dve.reciprocal(cb[u][:, :, E], pr[u][:, :, E]).then_inc(dve_[u].sem, 1)


def moe_experts(nc, k, name, weights, n_exp, n_shared, sel_rows, shared_by_row, shared_times):
    gname, uname, dname, sname = weights
    widths = [P] * n_exp + list(n_shared)
    NC = len(widths)
    starts = [sum(widths[:c]) for c in range(NC)]
    H = sum(widths)
    scaled = [c < n_exp or shared_by_row for c in range(NC)]
    GT = 4 * P
    with ExitStack() as ctx:
        def sb(n, shape, dt=F32):
            return ctx.enter_context(nc.sbuf_tensor(name + n, shape, dt))
        wg = sb("wg", [P, 2, H])
        wu = sb("wu", [P, 2, H])
        wd = sb("wd", [P, NC, D])
        sel = sb("sel", [sel_rows, H])
        h = sb("h", [P, NC, GT])
        sg = [sb(f"sg{u}", [P, GT]) for u in range(2)]
        loaded, gated, upped, silu_done, product, h_done, down_done, x_added = semaphores(
            nc, ctx, name, "loaded gated upped silu_done product h_done down_done x_added")
        gbank, ubank, cbank, ybank = k.ps[0:2], k.ps[2:4], k.ps[4:6], k.ps[6:8]
        n_scaled = sum(scaled)
        block = ctx.enter_context(nc.Block(name + "_b"))

        @block.sync
        def _(sp):
            sp.dma_start(wg[:, :, :], k.a[gname].rearrange("(c p) n -> p c n", p=P)).then_inc(loaded, 16)
            sp.dma_start(wu[:, :, :], k.a[uname].rearrange("(c p) n -> p c n", p=P)).then_inc(loaded, 16)
            sp.dma_start(sel[:, :], k.a[sname]).then_inc(loaded, 16)
            full = [c for c in range(NC) if widths[c] == P]
            nf = len(full)
            sp.dma_start(wd[:, 0:nf, :], k.a[dname][0:nf * P, :].rearrange("(c p) n -> p c n", p=P)).then_inc(loaded, 16)
            for c in range(nf, NC):
                sp.dma_start(wd[0:widths[c], c, :], k.a[dname][starts[c]:starts[c] + widths[c], :]).then_inc(loaded, 16)

        nload = 4 + sum(1 for w_ in widths if w_ != P)

        @block.tensor
        def _(pe):
            pe.wait_ge(loaded, 16 * nload)
            with pe.Fori(0, N // GT) as i:
                xg = [k.xT[:, c, bass.ds(i * GT, GT)] for c in range(2)]
                cg = k.combT[0:sel_rows, bass.ds(i * GT, GT)]
                for c in range(NC):
                    w_, s_, u = widths[c], starts[c], c % 2
                    if c >= 2:
                        pe.wait_ge(h_done, NC * i + c - 1)
                    else:
                        pe.wait_ge(h_done, NC * i)
                    for kk in range(2):
                        mm = pe.matmul(gbank[u][0:w_, :], wg[:, kk, s_:s_ + w_], xg[kk], start=(kk == 0), stop=(kk == 1))
                    mm.then_inc(gated, 1)
                    for kk in range(2):
                        mm = pe.matmul(ubank[u][0:w_, :], wu[:, kk, s_:s_ + w_], xg[kk], start=(kk == 0), stop=(kk == 1))
                    if scaled[c]:
                        mm = pe.matmul(cbank[u][0:w_, :], sel[:, s_:s_ + w_], cg, start=True, stop=True)
                    mm.then_inc(upped, 1)
                pe.wait_ge(h_done, NC * (i + 1))
                for t in range(4):
                    if t >= 2:
                        pe.wait_ge(x_added, 4 * i + t - 1)
                    else:
                        pe.wait_ge(x_added, 4 * i)
                    for c in range(NC):
                        mm = pe.matmul(ybank[t % 2][:, 0:D], h[0:widths[c], c, t * P:(t + 1) * P], wd[0:widths[c], c, :],
                                       start=(c == 0), stop=(c == NC - 1))
                    mm.then_inc(down_done, 1)

        @block.scalar
        def _(act):
            act.preload_act_table(ACT.Silu)
            with act.Fori(0, N // GT) as i:
                for c in range(NC):
                    act.wait_ge(gated, NC * i + c + 1)
                    if c >= 2:
                        act.wait_ge(h_done, NC * i + c - 1)
                    else:
                        act.wait_ge(h_done, NC * i)
                    act.activation(sg[c % 2][0:widths[c], :], gbank[c % 2][0:widths[c], :], ACT.Silu).then_inc(silu_done, 1)

        @block.vector
        def _(dve):
            with dve.Fori(0, N // GT) as i:
                dve.wait_ge(down_done, 4 * i)
                for c in range(NC):
                    w_, u = widths[c], c % 2
                    dve.wait_ge(silu_done, NC * i + c + 1)
                    dve.wait_ge(upped, NC * i + c + 1)
                    if scaled[c]:
                        dve.tensor_tensor(sg[u][0:w_, :], sg[u][0:w_, :], ubank[u][0:w_, :], ALU.mult).then_inc(product, 1)
                        dve.wait_ge(product, n_scaled * i + sum(scaled[:c]) + 1)
                        dve.tensor_tensor(h[0:w_, c, :], sg[u][0:w_, :], cbank[u][0:w_, :], ALU.mult).then_inc(h_done, 1)
                    else:
                        dve.scalar_tensor_tensor(out=h[0:w_, c, :], in0=sg[u][0:w_, :], scalar=shared_times, in1=ubank[u][0:w_, :],
                                                 op0=ALU.mult, op1=ALU.mult).then_inc(h_done, 1)
                for t in range(4):
                    xt = k.x[:, bass.ds(4 * i + t, 1), :].rearrange("p t d -> p (t d)")
                    dve.wait_ge(down_done, 4 * i + t + 1)
                    dve.tensor_tensor(xt, xt, ybank[t % 2][:, 0:D], ALU.add).then_inc(x_added, 1)


def l0_ffn(nc, k):
    with nc.sbuf_tensor("f0combT", [8, N], F32) as combT:
        k.combT = combT
        moe_route(nc, k, "r0", "L0_router", 8, 2, False, 1.0)
        moe_experts(nc, k, "f0", ("L0_g", "L0_u", "L0_d", "sel176"), 11, (128, 128, 96), 8, False, 1.0)


def l2_ffn(nc, k):
    with nc.sbuf_tensor("f2combT", [9, N], F32) as combT:
        k.combT = combT
        moe_route(nc, k, "r2", "L2_router", 8, 2, True, 1.0, shared_gate=True)
        moe_experts(nc, k, "f2", ("L2_g", "L2_u", "L2_d", "sel176s"), 11, (128, 128, 96), 9, True, 1.0)


def l3_ffn(nc, k):
    TOP = 4
    with nc.sbuf_tensor("f3combT", [16, N], F32) as combT:
        k.combT = combT
        moe_route(nc, k, "r3", "L3_ffn_w_router", 16, TOP, True, TOP / (TOP + 1))
        moe_experts(nc, k, "f3", ("L3_g", "L3_u", "L3_d", "sel128"), 16, (128,) * 4, 16, False, 1.0 / (TOP + 1))


KT = KEYS // P
QG = 4 * P
STACK = 6 * HD


def l1_attention(nc, k):
    split_to_dram(nc, k)
    with nc.sbuf_tensor("a1o", [P, T, D], F32) as o:
        key_attention(nc, k, o)
        project_add(nc, k, "a1p", o, "L1_Wo")


def split_to_dram(nc, k):
    with ExitStack() as ctx:
        def sb(name, shape, dt=F32):
            return ctx.enter_context(nc.sbuf_tensor("s1" + name, shape, dt))
        CH = 1024
        LANES = range(4)
        w = sb("w", [P, 2, D])
        raw = [sb(f"raw{n}", [P, CH]) for n in LANES]
        part = [[sb(f"part{n}{m}", [P, CH], BF16) for m in range(3)] for n in LANES]
        loaded, = semaphores(nc, ctx, "s1", "loaded")
        arrived = [nc.alloc_semaphore(f"s1_arrived{n}") for n in LANES]
        stored = [nc.alloc_semaphore(f"s1_stored{n}") for n in LANES]
        pe_ = lane_steps(nc, "s1", "pe", "Q", 4)
        act_ = lane_steps(nc, "s1", "act", "HIGH LOW", 4)
        dve_ = lane_steps(nc, "s1", "dve", "REST1 MIDDLE REST2", 4)
        qbank = [k.psum[:, 2 * n:2 * n + 2, :] for n in LANES]
        q = [b.rearrange("p c n -> p (c n)") for b in qbank]
        block = ctx.enter_context(nc.Block("s1_b"))
        NK, NQ = KEYS // CH // 2, N // CH // 2

        def chunk(n, i):
            return bass.ds((2 * i + n // 2) * CH, CH)

        def features(n):
            return slice(n % 2 * P, n % 2 * P + P)

        def store(eng, i, turn, scr):
            for n in LANES:
                for m in range(3):
                    into = scr[m, features(n), chunk(n, i)]
                    eng.wait_ge(act_[n].sem, act_[n].at(turn, "LOW"))
                    eng.dma_start(into, part[n][m][:, :]).then_inc(stored[n], 16)

        @block.sync
        def _(sp):
            sp.dma_start(w[:, :, :], k.a["L1_Wq"].rearrange("(c p) n -> p c n", p=P)).then_inc(loaded, 16)

            def load(n, i):
                sp.dma_start(raw[n][:, :], k.a["L1_kT"][features(n), chunk(n, i)]).then_inc(arrived[n], 16)

            for n in LANES:
                load(n, 0)
            for i in range(NK):
                store(sp, i, i, k.k_scr)
                if i + 1 < NK:
                    for n in LANES:
                        load(n, i + 1)
            for i in range(NQ):
                store(sp, i, i + NK, k.q_scr)
            for n in LANES:
                sp.wait_ge(stored[n], 16 * 3 * (NK + NQ))

        @block.tensor
        def _(pe):
            pe.wait_ge(loaded, 16)
            for i in range(NQ):
                for n in LANES:
                    if i:
                        pe.wait_ge(dve_[n].sem, dve_[n].turns(i + NK))
                    for half in range(2):
                        lo = (2 * i + n // 2) * CH + half * 512
                        for c in range(2):
                            mm = pe.matmul(qbank[n][:, half, :], w[:, c, features(n)], k.xT[:, c, lo:lo + 512],
                                           start=(c == 0), stop=(c == 1))
                    mm.then_inc(pe_[n].sem, 1)

        @block.scalar
        def _(act):
            for i in range(NK + NQ):
                for n in LANES:
                    if i < NK:
                        act.wait_ge(arrived[n], 16 * (i + 1))
                    else:
                        act.wait_ge(pe_[n].sem, pe_[n].at(i - NK, "Q"))
                    if i:
                        act.wait_ge(stored[n], 16 * 3 * i)
                    act.copy(part[n][0][:, :], raw[n][:, :] if i < NK else q[n]).then_inc(act_[n].sem, 1)
                for n in LANES:
                    act.wait_ge(dve_[n].sem, dve_[n].at(i, "REST2"))
                    act.copy(part[n][2][:, :], raw[n][:, :]).then_inc(act_[n].sem, 1)

        @block.vector
        def _(dve):
            for i in range(NK + NQ):
                for n in LANES:
                    dve.wait_ge(act_[n].sem, act_[n].at(i, "HIGH"))
                    dve.tensor_tensor(raw[n][:, :], raw[n][:, :] if i < NK else q[n], part[n][0][:, :], ALU.subtract).then_inc(dve_[n].sem, 1)
                    dve.wait_ge(dve_[n].sem, dve_[n].at(i, "REST1"))
                    dve.tensor_copy(part[n][1][:, :], raw[n][:, :]).then_inc(dve_[n].sem, 1)
                    dve.wait_ge(dve_[n].sem, dve_[n].at(i, "MIDDLE"))
                    dve.tensor_tensor(raw[n][:, :], raw[n][:, :], part[n][1][:, :], ALU.subtract).then_inc(dve_[n].sem, 1)


def key_attention(nc, k, o):
    RING = 4
    AM = 4 * (KEYS // QG)
    LAG = 4
    SUMS_AT, ROWS_AT = 8, 18
    SPLITS = 6
    BODIES = 4 * HEADS
    with ExitStack() as ctx:
        def sb(name, shape, dt=F32):
            return ctx.enter_context(nc.sbuf_tensor("k1" + name, shape, dt))
        identb = sb("identb", [P, P], BF16)
        kst = [sb(f"kst{r}", [STACK + 3, KEYS], BF16) for r in range(RING)]
        qst = [sb(f"qst{r}", [STACK + 3, N], BF16) for r in range(RING)]
        v = sb("v", [P, KT, D])
        vst = [sb(f"vst{u}", [P, KT, 32]) for u in range(2)]
        ex = [sb(f"ex{m}", [P, QG]) for m in range(8)]
        osb = sb("osb", [P, QG])
        pm = sb("pm", [P, 4, KEYS // QG])
        nm = sb("nm", [P, 4])
        rest = sb("rest", [P, 4])
        nm3 = sb("nm3", [P, 4, 3], BF16)
        rec = sb("rec", [P, 4])
        v_loaded, ready, valued, released = semaphores(nc, ctx, "k1", "v_loaded ready valued released")
        stacked = [nc.alloc_semaphore(f"k1_stacked{r}") for r in range(RING)]
        scored, exped, attended, a_scored, a_reduced, reciprocal = semaphores(
            nc, ctx, "k1", "scored exped attended a_scored a_reduced reciprocal")
        o_copied, summed, normed, split, rows_scored, rows_copied = semaphores(
            nc, ctx, "k1", "o_copied summed normed split rows_scored rows_copied")
        abank, sbank = k.ps[0:3], k.ps[3:6]
        obank, mbank = k.ps[6], k.ps[7]
        LOADS = 12 * 16
        EX, SB, AB = 8, 3, 3

        def bank_free(n, a):
            return KT * n + a + (2 if a < KT % 3 else 1)

        block = ctx.enter_context(nc.Block("k1_b"))

        def all_heads(eng, head):
            head(0, 0, True, False)
            with eng.Fori(0, HEADS // RING - 1) as i:
                for u in range(1, RING + 1):
                    head(RING * i + u, u % RING, False, False)
            for h in range(HEADS - RING + 1, HEADS):
                head(h, h % RING, False, h == HEADS - 1)

        def bodies(eng, h, body):
            body(4 * h, 0)
            with eng.Fori(1, 4) as qg:
                body(4 * h + qg, qg)

        def heads_attended(heads):
            return 4 * KT * heads + EX

        def opening(qg):
            return isinstance(qg, int)

        @block.sync
        def _(sp):
            sp.dma_start(v[:, :, :], k.a["L1_v"].rearrange("(t p) d -> p t d", p=P)).then_inc(v_loaded, 16)

            def load(r, h):
                parts = ((0, 0), (1, 0), (2, 0), (0, 1), (1, 1), (0, 2))
                here = slice(h * HD, h * HD + HD) if isinstance(h, int) else bass.ds(h * HD, HD)
                for row, (k_part, q_part) in enumerate(parts):
                    at = slice(HD * row, HD * row + HD)
                    sp.dma_start(kst[r][at, :], k.k_scr[k_part, here, :]).then_inc(stacked[r], 16)
                    sp.dma_start(qst[r][at, :], k.q_scr[q_part, here, :]).then_inc(stacked[r], 16)

            for h in range(RING):
                load(h, h)
            with sp.Fori(0, HEADS // RING - 1) as i:
                for u in range(1, RING + 1):
                    sp.wait_ge(attended, heads_attended(RING * i + u))
                    sp.sem_inc(released, 1)
                    load((u + 3) % RING, RING * i + u + 3)

        @block.gpsimd
        def _(pool):
            for u in range(2):
                pool.memset(vst[u][:, :, HD:HD + 1], 1.0)
                pool.memset(vst[u][:, :, HD + 1:32], 0.0)
            pool.wait_ge(v_loaded, 16)
            for h in range(2):
                pool.tensor_copy(vst[h][:, :, 0:HD], v[:, :, h * HD:(h + 1) * HD]).then_inc(valued, 1)
            with pool.Fori(1, HEADS // 2) as i:
                for u in range(2):
                    h = 2 * i + u
                    pool.wait_ge(attended, heads_attended(h - 1))
                    pool.tensor_copy(vst[u][:, :, 0:HD], v[:, :, bass.ds(h * HD, HD)]).then_inc(valued, 1)

        @block.tensor
        def _(pe):
            pe.sem_inc(attended, EX)
            pe.sem_inc(summed, 1)
            pe.sem_inc(rows_scored, 1)
            pe.wait_ge(ready, 2)

            def maximum_product(r, qg, n, a):
                tile, group = divmod(a, KEYS // QG)
                pe.wait_ge(a_reduced, bank_free(n, a))
                pe.matmul(abank[a % 3], qst[r][0:STACK, bass.ds(qg * QG + tile * P, P)], kst[r][0:STACK, group * QG:(group + 1) * QG],
                          start=True, stop=True).then_inc(a_scored, 1)

            def maximum_rows(n):
                pe.wait_ge(split, SPLITS * (n + 1) + 1)
                for tile in range(4):
                    mm = pe.matmul(mbank[STACK:STACK + 3, tile * P:(tile + 1) * P], nm3[:, tile, :], identb[:, :], start=True, stop=True)
                mm.then_inc(rows_scored, 1)

            def attend(u, n, p):
                pe.wait_ge(exped, KT * n + p + 1 + SB)
                strip = slice(32 * (p % 4), 32 * (p % 4) + 32)
                pe.matmul(obank[strip, :], vst[u % 2][:, p, :], ex[p % EX][:, :],
                          start=(p < 4), stop=(p >= KT - 4)).then_inc(attended, 1)

            def sums(n):
                pe.wait_ge(o_copied, n + 2)
                for tile in range(4):
                    mm = pe.matmul(mbank[:, tile * 17:tile * 17 + 17], osb[:, tile * P:(tile + 1) * P], k.strip_sum[:, :],
                                   start=True, stop=True)
                mm.then_inc(summed, 1)

            pe.wait_ge(stacked[0], LOADS)
            with pe.Fori(0, 4) as qg:
                for a in range(AM):
                    maximum_product(0, qg, qg, a)
                pe.wait_ge(rows_copied, qg + 1)
                maximum_rows(qg)

            def head(h, u, first, last):
                nxt = (u + 1) % RING

                def body(n, qg):
                    started = first and opening(qg)
                    ending = (u - 1) % RING if opening(qg) else u
                    for p in range(KT):
                        if p == SUMS_AT and not started:
                            if last and not opening(qg):
                                pe.wait_ge(normed, n)
                                pe.wait_ge(rows_copied, BODIES + 1)
                            else:
                                pe.wait_ge(rows_copied, n + 4)
                            sums(n - 1)
                        if p == ROWS_AT and not started and not (last and not opening(qg)):
                            pe.wait_ge(normed, n + 1)
                            maximum_rows(n + 3)
                        if p == 0:
                            pe.wait_ge(rows_copied, n + 2)
                        pe.wait_ge(exped, bank_free(n, p))
                        pe.matmul(sbank[p % 3], kst[u][:, p * P:(p + 1) * P], qst[u][:, bass.ds(qg * QG, QG)],
                                  start=True, stop=True).then_inc(scored, 1)
                        if not last:
                            if p == 0 and opening(qg):
                                pe.wait_ge(stacked[nxt], LOADS * ((h + 1 - nxt) // RING + 1) if isinstance(h, int)
                                           else turn_loads(h, u))
                            maximum_product(nxt, qg, n + 4, p)
                        if p >= LAG:
                            if p == LAG:
                                if opening(qg):
                                    pe.wait_ge(valued, h + 1)
                                pe.wait_ge(o_copied, n + 1)
                            attend(u, n, p - LAG)
                        elif not started:
                            attend(ending, n - 1, KT - LAG + p)

                bodies(pe, h, body)

            def turn_loads(h, u):
                following = u + 1 if u else RING + 1
                return (h - (u or RING)) // RING * LOADS + LOADS * (1 + following // RING)

            all_heads(pe, head)
            last = (HEADS - 1) % RING
            for p in range(KT - LAG, KT):
                attend(last, BODIES - 1, p)
            pe.wait_ge(normed, BODIES)
            sums(BODIES - 1)

        @block.scalar
        def _(act):
            act.preload_act_table(ACT.Exp)
            act.sem_inc(exped, SB)
            act.sem_inc(o_copied, 1)
            act.sem_inc(rows_copied, 1)

            def rows(r, qg, n):
                act.wait_ge(rows_scored, n + 2)
                act.copy(qst[r][STACK:STACK + 3, bass.ds(qg * QG, QG)], mbank[STACK:STACK + 3, :]).then_inc(rows_copied, 1)

            def strips(n):
                act.wait_ge(attended, KT * (n + 1) + EX)
                act.wait_ge(summed, n + 1)
                act.copy(osb[:, :], obank).then_inc(o_copied, 1)

            with act.Fori(0, 4) as qg:
                rows(0, qg, qg)

            def head(h, u, first, last):
                def body(n, qg):
                    started = first and opening(qg)
                    for p in range(KT):
                        if p == LAG and not started:
                            strips(n - 1)
                        if p == ROWS_AT + 1 and not started:
                            if opening(qg):
                                rows(u, 3, n + 3)
                            elif not last:
                                rows((u + 1) % RING, qg - 1, n + 3)
                        act.wait_ge(scored, KT * n + p + 1)
                        act.wait_ge(attended, KT * n + p + 1)
                        act.activation(ex[p % EX][:, :], sbank[p % 3], ACT.Exp, scale=HD ** -0.5).then_inc(exped, 1)

                bodies(act, h, body)

            all_heads(act, head)
            strips(BODIES - 1)

        @block.vector
        def _(dve):
            dve.tensor_copy(identb[:, :], k.ident[:, :]).then_inc(ready, 1)
            for r in range(RING):
                ins = dve.memset(kst[r][STACK:STACK + 3, :], 1.0)
            ins.then_inc(ready, 1)
            dve.sem_inc(a_reduced, AB)
            dve.sem_inc(normed, 1)
            dve.sem_inc(split, 1)

            def reduce(n, a):
                tile, group = divmod(a, KEYS // QG)
                if a == 0:
                    dve.wait_ge(split, SPLITS * n + 1)
                dve.wait_ge(a_scored, AM * n + a + 1)
                dve.tensor_reduce(pm[:, tile, group:group + 1], abank[a % 3], AX.X, ALU.max).then_inc(a_reduced, 1)

            def split_maxima(n):
                dve.wait_ge(a_reduced, AM * (n + 1) + AB)
                dve.tensor_reduce(nm[:, :], pm[:, :, :], AX.X, ALU.max, negate=True).then_inc(split, 1)
                dve.wait_ge(rows_scored, n + 1)
                dve.wait_ge(split, SPLITS * n + 2)
                dve.tensor_copy(nm3[:, :, 0], nm[:, :]).then_inc(split, 1)
                dve.wait_ge(split, SPLITS * n + 3)
                dve.tensor_tensor(rest[:, :], nm[:, :], nm3[:, :, 0], ALU.subtract).then_inc(split, 1)
                dve.wait_ge(split, SPLITS * n + 4)
                dve.tensor_copy(nm3[:, :, 1], rest[:, :]).then_inc(split, 1)
                dve.wait_ge(split, SPLITS * n + 5)
                dve.tensor_tensor(rest[:, :], rest[:, :], nm3[:, :, 1], ALU.subtract).then_inc(split, 1)
                dve.wait_ge(split, SPLITS * n + 6)
                dve.tensor_copy(nm3[:, :, 2], rest[:, :]).then_inc(split, 1)

            def divide(n, h, quarter):
                sums = mbank[:, 0:68].rearrange("p (t d) -> p t d", d=17)
                dve.wait_ge(summed, n + 2)
                dve.wait_ge(normed, n + 1)
                dve.reciprocal(rec[:, :], sums[:, :, HD]).then_inc(reciprocal, 1)
                dve.wait_ge(reciprocal, n + 1)
                dve.tensor_tensor(o[:, bass.ds(4 * quarter, 4), bass.ds(h * HD, HD)], sums[:, :, 0:HD],
                                  rec[:, :].unsqueeze(2).to_broadcast([P, 4, HD]), ALU.mult).then_inc(normed, 1)

            with dve.Fori(0, 4) as qg:
                for a in range(AM):
                    reduce(qg, a)
                split_maxima(qg)

            def head(h, u, first, last):
                def body(n, qg):
                    divide_at = SUMS_AT + 2
                    for a in range(AM):
                        if a == divide_at and not (first and opening(qg)):
                            divide(n - 1, h - 1 if opening(qg) else h, 3 if opening(qg) else qg - 1)
                        if not last:
                            reduce(n + 4, a)
                    if not last:
                        split_maxima(n + 4)

                bodies(dve, h, body)

            all_heads(dve, head)
            divide(BODIES - 1, HEADS - 1, 3)


def project_add(nc, k, name, o, weight):
    with ExitStack() as ctx:
        def sb(n, shape, dt=F32):
            return ctx.enter_context(nc.sbuf_tensor(name + n, shape, dt))
        w = sb("w", [P, 2, D])
        os = [sb(f"os{u}", [P, D]) for u in range(2)]
        oT = [sb(f"oT{u}", [P, 2, P]) for u in range(2)]
        loaded, = semaphores(nc, ctx, name, "loaded")
        pe_ = lane_steps(nc, name, "pe", "OT Y")
        act_ = lane_steps(nc, name, "act", "OT")
        dve_ = lane_steps(nc, name, "dve", "PICK X")
        bank = [[k.ps[4 * u + n] for n in range(4)] for u in range(2)]
        block = ctx.enter_context(nc.Block(name + "_b"))

        @block.sync
        def _(sp):
            sp.dma_start(w[:, :, :], k.a[weight].rearrange("(c p) n -> p c n", p=P)).then_inc(loaded, 16)

        @block.tensor
        def _(pe):
            pe.wait_ge(loaded, 16)
            with pe.Fori(0, T // 2) as i:
                for u in range(2):
                    pe.wait_ge(dve_[u].sem, dve_[u].at(i, "PICK"))
                    for c in range(2):
                        mm = pe.transpose(bank[u][0][:, c * P:(c + 1) * P], os[u][:, c * P:(c + 1) * P], k.ident[:, :])
                    mm.then_inc(pe_[u].sem, 1)
                for u in range(2):
                    pe.wait_ge(act_[u].sem, act_[u].at(i, "OT"))
                    for c in range(2):
                        mm = pe.matmul(bank[u][1][:, 0:D], oT[u][:, c, :], w[:, c, :], start=(c == 0), stop=(c == 1))
                    mm.then_inc(pe_[u].sem, 1)

        @block.scalar
        def _(act):
            with act.Fori(0, T // 2) as i:
                for u in range(2):
                    act.wait_ge(pe_[u].sem, pe_[u].at(i, "OT"))
                    act.copy(oT[u][:, :, :], bank[u][0][:, 0:D].rearrange("p (c n) -> p c n", c=2)).then_inc(act_[u].sem, 1)

        @block.vector
        def _(dve):
            with dve.Fori(0, T // 2) as i:
                for u in range(2):
                    dve.tensor_copy(os[u][:, :], tile_rows(o, 2 * i + u)).then_inc(dve_[u].sem, 1)
                for u in range(2):
                    xt = tile_rows(k.x, 2 * i + u)
                    dve.wait_ge(pe_[u].sem, pe_[u].at(i, "Y"))
                    dve.tensor_tensor(xt, xt, bank[u][1][:, 0:D], ALU.add).then_inc(dve_[u].sem, 1)


def l1_cross(nc, k):
    with ExitStack() as outer:
        def sb(name, shape):
            return outer.enter_context(nc.sbuf_tensor("m1" + name, shape, F32))
        cum = sb("cum", [P, T, HEADS])
        inp = sb("inp", [P, T, HEADS])
        centred = sb("centred", [P, T, D])
        var = sb("var", [P, T, HEADS])
        mlstm_gates(nc, k, cum, inp)
        mlstm_attention(nc, k, cum, inp, centred, var)
        mlstm_output(nc, k, centred, var)


def mlstm_gates(nc, k, cum, inp):
    with ExitStack() as ctx:
        def sb(name, shape, dt=F32):
            return ctx.enter_context(nc.sbuf_tensor("mg" + name, shape, dt))
        w = sb("w", [P, 6, 32])
        bias = sb("bias", [P, 32])
        xs = [sb(f"xs{u}", [P, 2, P]) for u in range(2)]
        cT = [sb(f"cT{u}", [P, 2, P]) for u in range(2)]
        gates = sb("gates", [P, T, 32])
        fg = sb("fg", [P, T, HEADS])
        low = sb("low", [P, T, HEADS])
        big = sb("big", [P, T, HEADS])
        loaded, gated, biased, logs, summed, dn = semaphores(nc, ctx, "mg", "loaded gated biased logs summed vec")
        arrived = [nc.alloc_semaphore(f"mg_arrived{u}") for u in range(2)]
        copied, = semaphores(nc, ctx, "mg", "copied")
        block = ctx.enter_context(nc.Block("mg_b"))

        @block.sync
        def _(sp):
            sp.dma_start(w[:, :, :], k.a["L1_gates"].rearrange("(c p) n -> p c n", p=P)).then_inc(loaded, 16)
            sp.dma_start(bias[:, :], k.a["L1_gates_b"].partition_broadcast(P)).then_inc(loaded, 16)
            with sp.Fori(0, T // 2) as i:
                for u in range(2):
                    sp.wait_ge(gated, 2 * i)
                    sp.dma_start(cT[u][:, :, :], k.a["ctxT"].rearrange("(c p) n -> p c n", p=P)[:, :, bass.ds((2 * i + u) * P, P)]).then_inc(arrived[u], 16)

        @block.gpsimd
        def _(pool):
            with pool.Fori(0, T // 2) as i:
                for u in range(2):
                    pool.wait_ge(gated, 2 * i)
                    pool.tensor_copy(xs[u][:, :, :], k.xT[:, :, bass.ds((2 * i + u) * P, P)]).then_inc(copied, 1)

        @block.tensor
        def _(pe):
            pe.wait_ge(loaded, 32)
            with pe.Fori(0, T // 2) as i:
                for u in range(2):
                    pe.wait_ge(arrived[u], 16 * (i + 1))
                    pe.wait_ge(copied, 2 * i + u + 1)
                    pe.wait_ge(biased, 2 * i)
                    for c in range(6):
                        lhs = xs[u] if c < 2 else cT[u]
                        mm = pe.matmul(k.ps[u][:, 0:32], lhs[:, c % 2, :], w[:, c, :], start=(c == 0), stop=(c == 5))
                    mm.then_inc(gated, 1)
            pe.wait_ge(dn, 5)
            pe.matmul(k.ps[2][:, 0:D], k.cumulate[:, :], low[:, :, :].rearrange("p t h -> p (t h)"),
                      start=True, stop=True).then_inc(summed, 1)

        @block.scalar
        def _(act):
            act.preload_act_table_set("natural_log_exp_and_others")
            act.wait_ge(dn, 3)
            act.activation(big[:, :, :], big[:, :, :], ACT.Exp, scale=-1.0).then_inc(logs, 1)
            act.wait_ge(logs, 1)
            act.activation(big[:, :, :], big[:, :, :], ACT.Ln, bias=1.0).then_inc(logs, 1)

        @block.vector
        def _(dve):
            with dve.Fori(0, T // 2) as i:
                for u in range(2):
                    dve.wait_ge(gated, 2 * i + u + 1)
                    dve.tensor_tensor(tile_rows(gates, 2 * i + u), k.ps[u][:, 0:32], bias[:, :], ALU.add).then_inc(biased, 1)
            dve.wait_ge(biased, T)
            dve.tensor_copy(fg[:, :, :], gates[:, :, HEADS:32]).then_inc(dn, 1)
            dve.wait_ge(dn, 1)
            dve.tensor_scalar(low[:, :, :], fg[:, :, :], 0.0, None, ALU.min).then_inc(dn, 1)
            dve.scalar_tensor_tensor(out=big[:, :, :], in0=fg[:, :, :], scalar=-1.0, in1=fg[:, :, :], op0=ALU.mult, op1=ALU.max).then_inc(dn, 1)
            dve.wait_ge(logs, 2)
            dve.tensor_tensor(low[:, :, :], low[:, :, :], big[:, :, :], ALU.subtract).then_inc(dn, 1)
            dve.wait_ge(dn, 4)
            dve.sem_inc(dn, 1)
            dve.wait_ge(summed, 1)
            dve.tensor_copy(cum[:, :, :].rearrange("p t h -> p (t h)"), k.ps[2][:, 0:D]).then_inc(dn, 1)
            dve.wait_ge(dn, 6)
            dve.tensor_tensor(inp[:, :, :], gates[:, :, 0:HEADS], cum[:, :, :], ALU.subtract).then_inc(dn, 1)


def mlstm_attention(nc, k, cum, inp, centred, var):
    with ExitStack() as ctx:
        def sb(name, shape, dt=F32):
            return ctx.enter_context(nc.sbuf_tensor("ma" + name, shape, dt))
        xs = [sb(f"xs{u}", [P, 2, P]) for u in range(2)]
        cT = [sb(f"cT{u}", [P, 2, P]) for u in range(2)]
        vd = [sb(f"vd{u}", [P, 2, D]) for u in range(2)]
        kexp = [sb(f"kexp{u}", [P, 2, 2, 8, S]) for u in range(2)]
        diag = [sb(f"diag{u}", [P, HEADS * S]) for u in range(2)]
        sc = [sb(f"sc{u}", [P, HEADS * S]) for u in range(2)]
        pT = [sb(f"pT{u}", [P, 8, P]) for u in range(2)]
        hd = [sb(f"hd{u}", [P, D]) for u in range(2)]
        m = [sb(f"m{u}", [P, 6, HEADS]) for u in range(2)]
        MAX, SUM, CUMMAX, FLOOR, NORM, MEAN = range(6)
        arrived = [nc.alloc_semaphore(f"ma_arrived{u}") for u in range(2)]
        pe_ = lane_steps(nc, "ma", "pe", "DECAY SCORES PT O")
        act_ = lane_steps(nc, "ma", "act", "EXP FLOOR PT")
        dve_ = lane_steps(nc, "ma", "dve", "DIAG KEXP VBD MASK MAX SUB CUMMAX C SUM ABS NORM EPS REC O MEAN MEAN16 CENTRE SQ VAR")
        pool_ = lane_steps(nc, "ma", "pool", "XS")
        bank = [[k.ps[4 * u + n] for n in range(4)] for u in range(2)]
        block = ctx.enter_context(nc.Block("ma_b"))

        @block.sync
        def _(sp):
            with sp.Fori(0, T // 2) as i:
                for u in range(2):
                    t = 2 * i + u
                    sp.wait_ge(pe_[u].sem, pe_[u].turns(i))
                    sp.dma_start(cT[u][:, :, :], k.a["ctxT"].rearrange("(c p) n -> p c n", p=P)[:, :, bass.ds(t * P, P)]).then_inc(arrived[u], 16)
                    for r in range(2):
                        sp.dma_start(vd[u][row_slice(r), :, :],
                                     k.ctx_rows[bass.ds(t * P, P), :].rearrange("(b j) n -> j b n", b=2)).then_inc(arrived[u], 16)

        @block.gpsimd
        def _(pool):
            with pool.Fori(0, T // 2) as i:
                for u in range(2):
                    pool.wait_ge(pe_[u].sem, pe_[u].turns(i))
                    pool.tensor_copy(xs[u][:, :, :], k.xT[:, :, bass.ds((2 * i + u) * P, P)]).then_inc(pool_[u].sem, 1)

        @block.tensor
        def _(pe):
            with pe.Fori(0, T // 2) as i:
                for u in range(2):
                    pe.wait_ge(dve_[u].sem, dve_[u].at(i, "DIAG"))
                    for c in range(2):
                        mm = pe.matmul(bank[u][c], k.ones64[:, :], diag[u][:, c * 512:(c + 1) * 512], start=True, stop=True)
                    mm.then_inc(pe_[u].sem, 1)
                for u in range(2):
                    pe.wait_ge(dve_[u].sem, dve_[u].at(i, "KEXP"))
                    pe.wait_ge(pool_[u].sem, pool_[u].at(i, "XS"))
                    score_matmuls(pe, bank[u][2:4], xs[u], kexp[u]).then_inc(pe_[u].sem, 1)
                for u in range(2):
                    pe.wait_ge(dve_[u].sem, dve_[u].at(i, "C"))
                    weight_transposes(pe, bank[u][0:2], sc[u], k.ident[:, :]).then_inc(pe_[u].sem, 1)
                for u in range(2):
                    pe.wait_ge(act_[u].sem, act_[u].at(i, "PT"))
                    value_matmuls(pe, bank[u][2], pT[u], vd[u]).then_inc(pe_[u].sem, 1)

        @block.scalar
        def _(act):
            act.preload_act_table(ACT.Exp)
            with act.Fori(0, T // 2) as i:
                for u in range(2):
                    act.wait_ge(dve_[u].sem, dve_[u].at(i, "SUB"))
                    act.activation(sc[u][:, :], sc[u][:, :], ACT.Exp).then_inc(act_[u].sem, 1)
                    act.wait_ge(dve_[u].sem, dve_[u].at(i, "CUMMAX"))
                    act.activation(m[u][:, FLOOR, :], m[u][:, CUMMAX, :], ACT.Exp, scale=-1.0).then_inc(act_[u].sem, 1)
                for u in range(2):
                    act.wait_ge(pe_[u].sem, pe_[u].at(i, "PT"))
                    act.copy(pT[u][:, 0:4, :], bank[u][0].rearrange("p (c n) -> p c n", c=4))
                    act.copy(pT[u][:, 4:8, :], bank[u][1].rearrange("p (c n) -> p c n", c=4)).then_inc(act_[u].sem, 1)

        @block.vector
        def _(dve):
            with dve.Fori(0, T // 2) as i:
                for u in range(2):
                    t = 2 * i + u
                    dve.wait_ge(dve_[u].sem, dve_[u].turns(i))
                    dve.tensor_tensor(heads3(diag[u][:, :]), inp[:, bass.ds(t, 1), :].rearrange("p t h -> p (t h)").unsqueeze(2).to_broadcast([P, HEADS, S]),
                                      over_heads(k.eye64[:, :]), ALU.mult).then_inc(dve_[u].sem, 1)
                    dve.wait_ge(arrived[u], 48 * (i + 1))
                    spread_keys(dve, kexp[u], cT[u], k.head_mask[:, :]).then_inc(dve_[u].sem, 1)
                    values_by_parity(dve, vd[u], vd[u][:, :, :], k.parity[:, :]).then_inc(dve_[u].sem, 1)
                for u in range(2):
                    def wait(name, u=u):
                        dve.wait_ge(dve_[u].sem, dve_[u].at(i, name))

                    t = 2 * i + u
                    dve.wait_ge(pe_[u].sem, pe_[u].at(i, "DECAY"))
                    for c in range(2):
                        ins = dve.tensor_tensor(heads3(sc[u][:, c * 512:(c + 1) * 512]), heads3(bank[u][c]),
                                                over_heads(k.causal[:, :], 8), ALU.add)
                    ins.then_inc(dve_[u].sem, 1)
                    wait("MASK")
                    dve.tensor_reduce(m[u][:, MAX, :], heads3(sc[u][:, :]), AX.X, ALU.max).then_inc(dve_[u].sem, 1)
                    wait("MAX")
                    dve.tensor_tensor(heads3(sc[u][:, :]), heads3(sc[u][:, :]), per_head(m[u][:, MAX, :]), ALU.subtract).then_inc(dve_[u].sem, 1)
                    dve.tensor_tensor(m[u][:, CUMMAX, :], m[u][:, MAX, :], cum[:, bass.ds(t, 1), :].rearrange("p t h -> p (t h)"),
                                      ALU.add).then_inc(dve_[u].sem, 1)
                for u in range(2):
                    def wait(name, u=u):
                        dve.wait_ge(dve_[u].sem, dve_[u].at(i, name))

                    dve.wait_ge(pe_[u].sem, pe_[u].at(i, "SCORES"))
                    dve.wait_ge(act_[u].sem, act_[u].at(i, "EXP"))
                    for c in range(2):
                        half = sc[u][:, c * 512:(c + 1) * 512]
                        ins = dve.scalar_tensor_tensor(out=half, in0=bank[u][2 + c], scalar=HD ** -0.5, in1=half,
                                                       op0=ALU.mult, op1=ALU.mult)
                    ins.then_inc(dve_[u].sem, 1)
                    wait("C")
                    dve.tensor_reduce(m[u][:, SUM, :], heads3(sc[u][:, :]), AX.X, ALU.add).then_inc(dve_[u].sem, 1)
                    wait("SUM")
                    dve.scalar_tensor_tensor(out=m[u][:, NORM, :], in0=m[u][:, SUM, :], scalar=-1.0, in1=m[u][:, SUM, :],
                                             op0=ALU.mult, op1=ALU.max).then_inc(dve_[u].sem, 1)
                    wait("ABS")
                    dve.wait_ge(act_[u].sem, act_[u].at(i, "FLOOR"))
                    dve.tensor_tensor(m[u][:, NORM, :], m[u][:, NORM, :], m[u][:, FLOOR, :], ALU.max).then_inc(dve_[u].sem, 1)
                    wait("NORM")
                    dve.tensor_scalar(m[u][:, NORM, :], m[u][:, NORM, :], 1e-6, None, ALU.add).then_inc(dve_[u].sem, 1)
                    wait("EPS")
                    dve.reciprocal(m[u][:, NORM, :], m[u][:, NORM, :]).then_inc(dve_[u].sem, 1)
                    wait("REC")
                for u in range(2):
                    def wait(name, u=u):
                        dve.wait_ge(dve_[u].sem, dve_[u].at(i, name))

                    t = 2 * i + u
                    h3 = hd[u][:, :].rearrange("p (h d) -> p h d", d=HD)
                    ctile = tile_rows(centred, t).rearrange("p (h d) -> p h d", d=HD)
                    vtile = var[:, bass.ds(t, 1), :].rearrange("p t h -> p (t h)")
                    dve.wait_ge(pe_[u].sem, pe_[u].at(i, "O"))
                    for b in range(2):
                        r = row_slice(b)
                        ins = dve.tensor_tensor(hd[u][r, :].rearrange("p (c h d) -> p c h d", h=2, d=HD), own_batch(bank[u][2], b),
                                                m[u][r, NORM, :].rearrange("p (c h) -> p c h", h=2).unsqueeze(3).to_broadcast([64, 8, 2, HD]),
                                                ALU.mult)
                    ins.then_inc(dve_[u].sem, 1)
                    wait("O")
                    dve.tensor_reduce(m[u][:, MEAN, :], h3, AX.X, ALU.add).then_inc(dve_[u].sem, 1)
                    wait("MEAN")
                    dve.tensor_scalar(m[u][:, MEAN, :], m[u][:, MEAN, :], 1.0 / HD, None, ALU.mult).then_inc(dve_[u].sem, 1)
                    wait("MEAN16")
                    dve.tensor_tensor(h3, h3, per_head(m[u][:, MEAN, :], HD), ALU.subtract).then_inc(dve_[u].sem, 1)
                    wait("CENTRE")
                    dve.tensor_copy(ctile, h3)
                    dve.tensor_tensor(diag[u][:, 0:D], hd[u][:, :], hd[u][:, :], ALU.mult).then_inc(dve_[u].sem, 1)
                    wait("SQ")
                    dve.tensor_reduce(vtile, diag[u][:, 0:D].rearrange("p (h d) -> p h d", d=HD), AX.X, ALU.add).then_inc(dve_[u].sem, 1)


def mlstm_output(nc, k, centred, var):
    with ExitStack() as ctx:
        scale = ctx.enter_context(nc.sbuf_tensor("mo_scale", [P, D], F32))
        loaded, vec, rooted = semaphores(nc, ctx, "mo", "loaded vec rooted")
        chain = [nc.alloc_semaphore(f"mo_chain{u}") for u in range(2)]
        block = ctx.enter_context(nc.Block("mo_b"))

        @block.sync
        def _(sp):
            sp.dma_start(scale[:, :], k.a["L1_xattn_ln_scale"].partition_broadcast(P)).then_inc(loaded, 16)

        @block.scalar
        def _(act):
            act.wait_ge(vec, 1)
            act.activation(var[:, :, :], var[:, :, :], ACT.Sqrt).then_inc(rooted, 1)

        @block.vector
        def _(dve):
            dve.tensor_scalar(var[:, :, :], var[:, :, :], 1.0 / HD, 1e-6, ALU.mult, ALU.add).then_inc(vec, 1)
            dve.wait_ge(vec, 1)
            dve.wait_ge(rooted, 1)
            dve.reciprocal(var[:, :, :], var[:, :, :]).then_inc(vec, 1)
            dve.wait_ge(vec, 2)
            dve.wait_ge(loaded, 16)
            with dve.Fori(0, T // 2) as i:
                for u in range(2):
                    c = tile_rows(centred, 2 * i + u)
                    c3 = c.rearrange("p (h d) -> p h d", d=HD)
                    dve.tensor_tensor(c3, c3, var[:, bass.ds(2 * i + u, 1), :].rearrange("p t h -> p (t h)").unsqueeze(2).to_broadcast([P, HEADS, HD]),
                                      ALU.mult).then_inc(chain[u], 1)
                for u in range(2):
                    c = tile_rows(centred, 2 * i + u)
                    dve.wait_ge(chain[u], 3 * i + 1)
                    dve.tensor_tensor(c, c, scale[:, :], ALU.mult).then_inc(chain[u], 1)
                for u in range(2):
                    c, xt = tile_rows(centred, 2 * i + u), tile_rows(k.x, 2 * i + u)
                    dve.wait_ge(chain[u], 3 * i + 2)
                    dve.tensor_tensor(xt, xt, c, ALU.add).then_inc(chain[u], 1)


def l1_ffn(nc, k):
    with ExitStack() as outer:
        k.combT = outer.enter_context(nc.sbuf_tensor("f1combT", [8, N], F32))
        gates = outer.enter_context(nc.sbuf_tensor("f1gates", [P, T, 8], F32))
        moe_route(nc, k, "r1", "L1_wr", 8, 2, True, 1.0, rows=gates)
        l1_ffn_scatter(nc, k, gates)


def l1_ffn_scatter(nc, k, gates):
    GT, E = 4 * P, 8
    with ExitStack() as ctx:
        def sb(name, shape, dt=F32):
            return ctx.enter_context(nc.sbuf_tensor("f1" + name, shape, dt))
        w1, w3, w2 = (sb(n, [P, 2, D]) for n in ("w1", "w3", "w2"))
        h1 = sb("h1", [P, 2, GT])
        h2 = sb("h2", [P, 4, D])
        gs = sb("gs", [P, 4, E])
        acc = sb("acc", [E, D])
        accT = sb("accT", [P, 2, E])
        loaded, picked, cleared, first, second, summed, act1, act2, added, turned, copied, projected, final = semaphores(
            nc, ctx, "f1", "loaded picked cleared first second summed act1 act2 added turned copied projected final")
        block = ctx.enter_context(nc.Block("f1_b"))

        @block.sync
        def _(sp):
            for t, n in ((w1, "L1_w1"), (w3, "L1_w3"), (w2, "L1_w2")):
                sp.dma_start(t[:, :, :], k.a[n].rearrange("(c p) n -> p c n", p=P)).then_inc(loaded, 16)

        @block.gpsimd
        def _(pool):
            with pool.Fori(0, N // GT) as i:
                pool.wait_ge(summed, i)
                pool.tensor_copy(gs[:, :, :], gates[:, bass.ds(4 * i, 4), :]).then_inc(picked, 1)

        @block.tensor
        def _(pe):
            pe.wait_ge(loaded, 48)
            with pe.Fori(0, N // GT) as i:
                pe.wait_ge(act1, 2 * i)
                for m in range(2):
                    for c in range(2):
                        mm = pe.matmul(k.ps[m], w1[:, c, m * P:(m + 1) * P], k.xT[:, c, bass.ds(i * GT, GT)],
                                       start=(c == 0), stop=(c == 1))
                    mm.then_inc(first, 1)
                pe.wait_ge(act1, 2 * i + 2)
                pe.wait_ge(act2, 2 * i)
                for t in range(4):
                    for c in range(2):
                        mm = pe.matmul(k.ps[2 + t // 2][:, (t % 2) * D:(t % 2 + 1) * D], h1[:, c, t * P:(t + 1) * P], w3[:, c, :],
                                       start=(c == 0), stop=(c == 1))
                    mm.then_inc(second, 1)
                pe.wait_ge(act2, 2 * i + 2)
                pe.wait_ge(picked, i + 1)
                pe.wait_ge(added, i)
                for t in range(4):
                    mm = pe.matmul(k.ps[4][0:E, 0:D], gs[:, t, :], h2[:, t, :], start=(t == 0), stop=(t == 3))
                mm.then_inc(summed, 1)
            pe.wait_ge(added, N // GT)
            for c in range(2):
                mm = pe.transpose(k.ps[5][:, c * E:(c + 1) * E], acc[:, c * P:(c + 1) * P], k.ident[0:E, 0:E])
            mm.then_inc(turned, 1)
            pe.wait_ge(copied, 1)
            for c in range(2):
                mm = pe.matmul(k.ps[6][0:E, 0:D], accT[:, c, :], w2[:, c, :], start=(c == 0), stop=(c == 1))
            mm.then_inc(projected, 1)

        @block.scalar
        def _(act):
            act.preload_act_table(ACT.Silu)
            with act.Fori(0, N // GT) as i:
                act.wait_ge(second, 4 * i)
                for m in range(2):
                    act.wait_ge(first, 2 * i + m + 1)
                    act.activation(h1[:, m, :], k.ps[m], ACT.Silu).then_inc(act1, 1)
                act.wait_ge(summed, i)
                for m in range(2):
                    act.wait_ge(second, 4 * i + 2 * m + 2)
                    act.activation(h2[:, 2 * m:2 * m + 2, :].rearrange("p t d -> p (t d)"), k.ps[2 + m], ACT.Silu).then_inc(act2, 1)
            act.wait_ge(turned, 1)
            act.copy(accT[:, :, :], k.ps[5][:, 0:2 * E].rearrange("p (c e) -> p c e", c=2)).then_inc(copied, 1)

        @block.vector
        def _(dve):
            dve.memset(acc[:, :], 0.0).then_inc(cleared, 1)
            dve.wait_ge(cleared, 1)
            with dve.Fori(0, N // GT) as i:
                dve.wait_ge(added, i)
                dve.wait_ge(summed, i + 1)
                dve.tensor_tensor(acc[:, :], acc[:, :], k.ps[4][0:E, 0:D], ALU.add).then_inc(added, 1)
            dve.wait_ge(projected, 1)
            dve.tensor_tensor(k.x[0:E, 0, :], k.x[0:E, 0, :], k.ps[6][0:E, 0:D], ALU.add).then_inc(final, 1)


MAGIC = 1.5 * 2.0 ** 23


def l2_attention(nc, k):
    with ExitStack() as outer:
        def sb(name, shape, dt=F32):
            return outer.enter_context(nc.sbuf_tensor("b2" + name, shape, dt))
        wq = {n: sb("q_" + n, [P, c, m], BF16) for n, (c, m) in BIT_WEIGHTS.items()}
        wm = {n: sb("m_" + n, [P, 1]) for n in BIT_WEIGHTS}
        x1 = sb("x1", [P, T, D])
        bit_weights(nc, k, wq, wm)
        rs = sb("rs", [P, T])
        rms_scales(nc, k, "b2n1", k.x, rs)
        bit_attention(nc, k, wq, wm, x1, rs)
        rms_scales(nc, k, "b2n2", x1, rs)
        bit_mlp(nc, k, wq, wm, x1, rs)


BIT_WEIGHTS = {"qkv": (2, 768), "o": (2, 256), "down": (4, 256)}


def bit_weights(nc, k, wq, wm):
    with ExitStack() as ctx:
        def sb(name, shape, dt=F32):
            return ctx.enter_context(nc.sbuf_tensor("bw" + name, shape, dt))
        raw = {n: sb("raw_" + n, [P, c, m]) for n, (c, m) in BIT_WEIGHTS.items()}
        part = {n: sb("part_" + n, [P, 1]) for n in BIT_WEIGHTS}
        inv = {n: sb("inv_" + n, [P, 1]) for n in BIT_WEIGHTS}
        loaded, summed, spread, vec = semaphores(nc, ctx, "bw", "loaded summed spread vec")
        block = ctx.enter_context(nc.Block("bw_b"))

        @block.sync
        def _(sp):
            for n in BIT_WEIGHTS:
                sp.dma_start(raw[n][:, :, :], k.a["L2_" + n].rearrange("(c p) n -> p c n", p=P)).then_inc(loaded, 16)

        @block.tensor
        def _(pe):
            for j, n in enumerate(BIT_WEIGHTS):
                pe.wait_ge(summed, j + 1)
                pe.matmul(k.ps[j][:, 0:1], k.ones[:, :], part[n][:, :], start=True, stop=True).then_inc(spread, 1)

        @block.vector
        def _(dve):
            count = [0]

            def link(ins):
                count[0] += 1
                ins.then_inc(vec, 1)
                dve.wait_ge(vec, count[0])

            dve.wait_ge(loaded, 48)
            for n in BIT_WEIGHTS:
                dve.tensor_reduce(part[n][:, :], raw[n][:, :, :].rearrange("p c n -> p (c n)"), AX.X, ALU.add,
                                  apply_absolute_value=True).then_inc(summed, 1)
            for j, (n, (c, m)) in enumerate(BIT_WEIGHTS.items()):
                flat = raw[n][:, :, :].rearrange("p c n -> p (c n)")
                dve.wait_ge(spread, j + 1)
                link(dve.tensor_scalar(wm[n][:, :], k.ps[j][:, 0:1], 1.0 / (c * P * m), 1e-5, ALU.mult, ALU.max))
                link(dve.reciprocal(inv[n][:, :], wm[n][:, :]))
                link(dve.tensor_scalar(flat, flat, inv[n][:, :], MAGIC, ALU.mult, ALU.add))
                link(dve.tensor_scalar(flat, flat, -MAGIC, -1.0, ALU.add, ALU.max))
                link(dve.tensor_scalar(wq[n][:, :, :].rearrange("p c n -> p (c n)"), flat, 1.0, None, ALU.min))


def rms_scales(nc, k, name, x, rs):
    with ExitStack() as ctx:
        junk = [ctx.enter_context(nc.sbuf_tensor(f"{name}junk{u}", [P, D], F32)) for u in range(2)]
        squared, vec, scaled = semaphores(nc, ctx, name, "squared vec scaled")
        block = ctx.enter_context(nc.Block(name + "_b"))

        @block.scalar
        def _(act):
            act.preload_act_table(ACT.Square)
            with act.Fori(0, T // 2) as i:
                for u in range(2):
                    act.wait_ge(squared, 2 * i)
                    act.activation(junk[u][:, :], tile_rows(x, 2 * i + u), ACT.Square,
                                   accum_out=rs[:, bass.ds(2 * i + u, 1)]).then_inc(squared, 1)

        @block.vector
        def _(dve):
            dve.wait_ge(squared, T)
            dve.tensor_scalar(rs[:, :], rs[:, :], 1.0 / D, 1e-5, ALU.mult, ALU.add).then_inc(vec, 1)

        @block.gpsimd
        def _(pool):
            pool.wait_ge(vec, 1)
            pool.tensor_tensor(rs[:, :], rs[:, :], k.minus_half[:, 0:T], ALU.pow).then_inc(scaled, 1)


QUANT = "AMAX CLAMP REC SCALE ROUND INT DEQ"


def quantise(dve, done, wait, tag, row, width, q, rounded, ints, wscale):
    done(dve.tensor_reduce(q[:, 0:1], row, AX.X, ALU.max, apply_absolute_value=True), tag + "AMAX")
    wait(tag + "AMAX")
    done(dve.tensor_scalar(q[:, 0:1], q[:, 0:1], 1e-5, None, ALU.max), tag + "CLAMP")
    wait(tag + "CLAMP")
    done(dve.reciprocal(q[:, 1:2], q[:, 0:1]), tag + "REC")
    wait(tag + "REC")
    done(dve.tensor_scalar(q[:, 2:3], q[:, 1:2], 127.0, None, ALU.mult), tag + "SCALE")
    wait(tag + "SCALE")
    done(dve.tensor_scalar(rounded, row, q[:, 2:3], MAGIC, ALU.mult, ALU.add), tag + "ROUND")
    wait(tag + "ROUND")
    done(dve.tensor_scalar(ints, rounded, -MAGIC, None, ALU.add), tag + "INT")
    done(dve.tensor_scalar(q[:, 3:4], q[:, 0:1], wscale[:, :], 1.0 / 127.0, ALU.mult, ALU.mult), tag + "DEQ")


def tagged(tag):
    return " ".join(tag + n for n in QUANT.split())


def bit_attention(nc, k, wq, wm, x1, rs):
    with ExitStack() as ctx:
        def sb(name, shape, dt=F32):
            return ctx.enter_context(nc.sbuf_tensor("ba" + name, shape, dt))
        norm_w = sb("norm_w", [P, D])
        identb = sb("identb", [P, P], BF16)
        h = [sb(f"h{u}", [P, D]) for u in range(2)]
        hr = [sb(f"hr{u}", [P, D]) for u in range(2)]
        hi = [sb(f"hi{u}", [P, D], BF16) for u in range(2)]
        hiT = [sb(f"hiT{u}", [P, 2, P], BF16) for u in range(2)]
        qa = [sb(f"qa{u}", [P, 4]) for u in range(2)]
        qo = [sb(f"qo{u}", [P, 4]) for u in range(2)]
        t1 = [sb(f"t1{u}", [P, 512]) for u in range(2)]
        t2 = [sb(f"t2{u}", [P, 512]) for u in range(2)]
        qk = [sb(f"qk{u}", [P, 512]) for u in range(2)]
        v = [sb(f"v{u}", [P, D]) for u in range(2)]
        vd = [sb(f"vd{u}", [P, 2, D]) for u in range(2)]
        qkT = [sb(f"qkT{u}", [P, 4, P]) for u in range(2)]
        kexp = [sb(f"kexp{u}", [P, 2, 2, 8, S]) for u in range(2)]
        sc = [sb(f"sc{u}", [P, HEADS * S]) for u in range(2)]
        pT = [sb(f"pT{u}", [P, 8, P]) for u in range(2)]
        mx = [sb(f"mx{u}", [P, HEADS]) for u in range(2)]
        den = [sb(f"den{u}", [P, HEADS]) for u in range(2)]
        loaded, ready = semaphores(nc, ctx, "ba", "loaded ready")
        pe_ = lane_steps(nc, "ba", "pe", "HT QKV TURNED SCORES PT O OT Y")
        act_ = lane_steps(nc, "ba", "act", "HT V QKT EXP PT OT")
        dve_ = lane_steps(nc, "ba", "dve", "H " + tagged("H") + " COS SIN ROPED VBD KEXP MASK MAX SUB SUM REC O "
                          + tagged("O") + " X1")
        bank = [[k.ps[4 * u + n] for n in range(4)] for u in range(2)]
        block = ctx.enter_context(nc.Block("ba_b"))

        @block.sync
        def _(sp):
            sp.dma_start(norm_w[:, :], k.a["L2_norm1"].partition_broadcast(P)).then_inc(loaded, 16)

        @block.tensor
        def _(pe):
            pe.wait_ge(ready, 1)
            with pe.Fori(0, T // 2) as i:
                for u in range(2):
                    pe.wait_ge(dve_[u].sem, dve_[u].at(i, "HINT"))
                    turned = bank[u][0].bitcast(BF16)
                    for c in range(2):
                        mm = pe.transpose(turned[:, c * P:(c + 1) * P], hi[u][:, c * P:(c + 1) * P], identb[:, :])
                    mm.then_inc(pe_[u].sem, 1)
                for u in range(2):
                    pe.wait_ge(act_[u].sem, act_[u].at(i, "HT"))
                    for o, lo, hi_ in ((bank[u][0], 0, 512), (bank[u][1][:, 0:D], 512, 768)):
                        for c in range(2):
                            mm = pe.matmul(o, hiT[u][:, c, :], wq["qkv"][:, c, lo:hi_], start=(c == 0), stop=(c == 1))
                    mm.then_inc(pe_[u].sem, 1)
                for u in range(2):
                    pe.wait_ge(dve_[u].sem, dve_[u].at(i, "ROPED"))
                    pe.wait_ge(act_[u].sem, act_[u].at(i, "V"))
                    for c in range(4):
                        pe.transpose(bank[u][2][:, c * P:(c + 1) * P], qk[u][:, c * P:(c + 1) * P], k.ident[:, :])
                    for b in range(2):
                        mm = pe.matmul(bank[u][3][:, b * D:(b + 1) * D], k.dup[:, b * P:(b + 1) * P], v[u][:, :], start=True, stop=True)
                    mm.then_inc(pe_[u].sem, 1)
                for u in range(2):
                    pe.wait_ge(dve_[u].sem, dve_[u].at(i, "KEXP"))
                    score_matmuls(pe, bank[u][0:2], qkT[u], kexp[u]).then_inc(pe_[u].sem, 1)
                for u in range(2):
                    pe.wait_ge(act_[u].sem, act_[u].at(i, "EXP"))
                    weight_transposes(pe, bank[u][2:4], sc[u], k.ident[:, :]).then_inc(pe_[u].sem, 1)
                for u in range(2):
                    pe.wait_ge(act_[u].sem, act_[u].at(i, "PT"))
                    value_matmuls(pe, bank[u][0], pT[u], vd[u]).then_inc(pe_[u].sem, 1)
                for u in range(2):
                    pe.wait_ge(dve_[u].sem, dve_[u].at(i, "OINT"))
                    turned = bank[u][1].bitcast(BF16)
                    for c in range(2):
                        mm = pe.transpose(turned[:, c * P:(c + 1) * P], hi[u][:, c * P:(c + 1) * P], identb[:, :])
                    mm.then_inc(pe_[u].sem, 1)
                for u in range(2):
                    pe.wait_ge(act_[u].sem, act_[u].at(i, "OT"))
                    for c in range(2):
                        mm = pe.matmul(bank[u][2][:, 0:D], hiT[u][:, c, :], wq["o"][:, c, :], start=(c == 0), stop=(c == 1))
                    mm.then_inc(pe_[u].sem, 1)

        @block.scalar
        def _(act):
            act.preload_act_table(ACT.Exp)

            with act.Fori(0, T // 2) as i:
                for u in range(2):
                    act.wait_ge(pe_[u].sem, pe_[u].at(i, "HT"))
                    act.copy(hiT[u][:, :, :], bank[u][0].bitcast(BF16)[:, 0:D].rearrange("p (c n) -> p c n", c=2)).then_inc(act_[u].sem, 1)
                for u in range(2):
                    act.wait_ge(pe_[u].sem, pe_[u].at(i, "QKV"))
                    act.wait_ge(dve_[u].sem, dve_[u].at(i, "HDEQ"))
                    act.activation(v[u][:, :], bank[u][1][:, 0:D], ACT.Copy, scale=qa[u][:, 3:4]).then_inc(act_[u].sem, 1)
                for u in range(2):
                    act.wait_ge(pe_[u].sem, pe_[u].at(i, "TURNED"))
                    act.copy(qkT[u][:, :, :], bank[u][2].rearrange("p (c n) -> p c n", c=4)).then_inc(act_[u].sem, 1)
                for u in range(2):
                    act.wait_ge(dve_[u].sem, dve_[u].at(i, "SUB"))
                    act.activation(sc[u][:, :], sc[u][:, :], ACT.Exp).then_inc(act_[u].sem, 1)
                for u in range(2):
                    act.wait_ge(pe_[u].sem, pe_[u].at(i, "PT"))
                    act.copy(pT[u][:, 0:4, :], bank[u][2].rearrange("p (c n) -> p c n", c=4))
                    act.copy(pT[u][:, 4:8, :], bank[u][3].rearrange("p (c n) -> p c n", c=4)).then_inc(act_[u].sem, 1)
                for u in range(2):
                    act.wait_ge(pe_[u].sem, pe_[u].at(i, "OT"))
                    act.copy(hiT[u][:, :, :], bank[u][1].bitcast(BF16)[:, 0:D].rearrange("p (c n) -> p c n", c=2)).then_inc(act_[u].sem, 1)

        @block.vector
        def _(dve):
            dve.tensor_copy(identb[:, :], k.ident[:, :]).then_inc(ready, 1)
            dve.wait_ge(loaded, 16)
            with dve.Fori(0, T // 2) as i:
                def done(ins, step, u):
                    ins.then_inc(dve_[u].sem, 1)

                def wait(step, u):
                    dve.wait_ge(dve_[u].sem, dve_[u].at(i, step))

                for u in range(2):
                    t = 2 * i + u
                    dve.scalar_tensor_tensor(out=h[u][:, :], in0=tile_rows(k.x, t), scalar=rs[:, bass.ds(t, 1)], in1=norm_w[:, :],
                                             op0=ALU.mult, op1=ALU.mult).then_inc(dve_[u].sem, 1)
                    wait("H", u)
                    quantise(dve, lambda ins, s, u=u: done(ins, s, u), lambda s, u=u: wait(s, u), "H", h[u][:, :], D,
                             qa[u], hr[u][:, :], hi[u][:, :], wm["qkv"])
                for u in range(2):
                    dve.wait_ge(pe_[u].sem, pe_[u].at(i, "QKV"))
                    wait("HDEQ", u)
                    for o, table in ((t1, k.cos), (t2, k.sin)):
                        dve.scalar_tensor_tensor(out=by8(o[u][:, :]), in0=by8(bank[u][0]), scalar=qa[u][:, 3:4], in1=angles(table),
                                                 op0=ALU.mult, op1=ALU.mult).then_inc(dve_[u].sem, 1)
                    wait("SIN", u)
                    rope_sums(dve, qk[u][:, :], t1[u][:, :], t2[u][:, :]).then_inc(dve_[u].sem, 1)
                for u in range(2):
                    dve.wait_ge(pe_[u].sem, pe_[u].at(i, "TURNED"))
                    values_by_parity(dve, vd[u], bank[u][3].rearrange("p (b n) -> p b n", b=2), k.parity[:, :]).then_inc(dve_[u].sem, 1)
                    dve.wait_ge(act_[u].sem, act_[u].at(i, "QKT"))
                    spread_keys(dve, kexp[u], qkT[u][:, 2:4, :], k.head_mask[:, :]).then_inc(dve_[u].sem, 1)
                for u in range(2):
                    dve.wait_ge(pe_[u].sem, pe_[u].at(i, "SCORES"))
                    for c in range(2):
                        ins = dve.scalar_tensor_tensor(out=heads3(sc[u][:, c * 512:(c + 1) * 512]), in0=heads3(bank[u][c]),
                                                       scalar=HD ** -0.5, in1=over_heads(k.block_causal[:, :], 8), op0=ALU.mult, op1=ALU.add)
                    ins.then_inc(dve_[u].sem, 1)
                    wait("MASK", u)
                    dve.tensor_reduce(mx[u][:, :], heads3(sc[u][:, :]), AX.X, ALU.max).then_inc(dve_[u].sem, 1)
                    wait("MAX", u)
                    dve.tensor_tensor(heads3(sc[u][:, :]), heads3(sc[u][:, :]), per_head(mx[u][:, :]), ALU.subtract).then_inc(dve_[u].sem, 1)
                for u in range(2):
                    dve.wait_ge(act_[u].sem, act_[u].at(i, "EXP"))
                    dve.tensor_reduce(den[u][:, :], heads3(sc[u][:, :]), AX.X, ALU.add).then_inc(dve_[u].sem, 1)
                    wait("SUM", u)
                    dve.reciprocal(den[u][:, :], den[u][:, :]).then_inc(dve_[u].sem, 1)
                for u in range(2):
                    dve.wait_ge(pe_[u].sem, pe_[u].at(i, "O"))
                    wait("REC", u)
                    for b in range(2):
                        r = row_slice(b)
                        ins = dve.tensor_tensor(h[u][r, :].rearrange("p (c h d) -> p c h d", h=2, d=HD), own_batch(bank[u][0], b),
                                                den[u][r, :].rearrange("p (c h) -> p c h", h=2).unsqueeze(3).to_broadcast([64, 8, 2, HD]),
                                                ALU.mult)
                    ins.then_inc(dve_[u].sem, 1)
                    wait("O", u)
                    quantise(dve, lambda ins, s, u=u: done(ins, s, u), lambda s, u=u: wait(s, u), "O", h[u][:, :], D,
                             qo[u], hr[u][:, :], hi[u][:, :], wm["o"])
                for u in range(2):
                    t = 2 * i + u
                    dve.wait_ge(pe_[u].sem, pe_[u].at(i, "Y"))
                    wait("ODEQ", u)
                    dve.scalar_tensor_tensor(out=tile_rows(x1, t), in0=bank[u][2][:, 0:D], scalar=qo[u][:, 3:4], in1=tile_rows(k.x, t),
                                             op0=ALU.mult, op1=ALU.add).then_inc(dve_[u].sem, 1)


def bit_mlp(nc, k, wq, wm, x1, rs):
    with ExitStack() as ctx:
        def sb(name, shape, dt=F32):
            return ctx.enter_context(nc.sbuf_tensor("bm" + name, shape, dt))
        norm_w = sb("norm_w", [P, D])
        identb = sb("identb", [P, P], BF16)
        up = sb("up", [P, 2, 1024])
        h = [sb(f"h{u}", [P, D]) for u in range(2)]
        hT = [sb(f"hT{u}", [P, 2, P]) for u in range(2)]
        sg = [sb(f"sg{u}", [P, 512]) for u in range(2)]
        gv = [sb(f"gv{u}", [P, 512]) for u in range(2)]
        gi = [sb(f"gi{u}", [P, 512], BF16) for u in range(2)]
        giT = [sb(f"giT{u}", [P, 4, P], BF16) for u in range(2)]
        qa = [sb(f"qa{u}", [P, 4]) for u in range(2)]
        loaded, ready = semaphores(nc, ctx, "bm", "loaded ready")
        pe_ = lane_steps(nc, "bm", "pe", "HT GATE VAL GT Y")
        act_ = lane_steps(nc, "bm", "act", "HT SILU GT")
        dve_ = lane_steps(nc, "bm", "dve", "H X GV " + tagged("G") + " Y")
        bank = [[k.ps[4 * u + n] for n in range(4)] for u in range(2)]
        block = ctx.enter_context(nc.Block("bm_b"))

        @block.sync
        def _(sp):
            sp.dma_start(norm_w[:, :], k.a["L2_norm2"].partition_broadcast(P)).then_inc(loaded, 16)
            sp.dma_start(up[:, :, :], k.a["L2_up"].rearrange("(c p) n -> p c n", p=P)).then_inc(loaded, 16)

        @block.tensor
        def _(pe):
            pe.wait_ge(loaded, 32)
            pe.wait_ge(ready, 1)
            with pe.Fori(0, T // 2) as i:
                for u in range(2):
                    pe.wait_ge(dve_[u].sem, dve_[u].at(i, "H"))
                    for c in range(2):
                        mm = pe.transpose(bank[u][0][:, c * P:(c + 1) * P], h[u][:, c * P:(c + 1) * P], k.ident[:, :])
                    mm.then_inc(pe_[u].sem, 1)
                for u in range(2):
                    pe.wait_ge(act_[u].sem, act_[u].at(i, "HT"))
                    for half in range(2):
                        for c in range(2):
                            mm = pe.matmul(bank[u][1 + half], hT[u][:, c, :], up[:, c, half * 512:(half + 1) * 512],
                                           start=(c == 0), stop=(c == 1))
                        mm.then_inc(pe_[u].sem, 1)
                for u in range(2):
                    pe.wait_ge(dve_[u].sem, dve_[u].at(i, "GINT"))
                    turned = bank[u][3].bitcast(BF16)
                    for c in range(4):
                        mm = pe.transpose(turned[:, c * P:(c + 1) * P], gi[u][:, c * P:(c + 1) * P], identb[:, :])
                    mm.then_inc(pe_[u].sem, 1)
                for u in range(2):
                    pe.wait_ge(act_[u].sem, act_[u].at(i, "GT"))
                    for c in range(4):
                        mm = pe.matmul(bank[u][0][:, 0:D], giT[u][:, c, :], wq["down"][:, c, :], start=(c == 0), stop=(c == 3))
                    mm.then_inc(pe_[u].sem, 1)

        @block.scalar
        def _(act):
            act.preload_act_table(ACT.Silu)
            with act.Fori(0, T // 2) as i:
                for u in range(2):
                    act.wait_ge(pe_[u].sem, pe_[u].at(i, "HT"))
                    act.copy(hT[u][:, :, :], bank[u][0][:, 0:D].rearrange("p (c n) -> p c n", c=2)).then_inc(act_[u].sem, 1)
                for u in range(2):
                    act.wait_ge(pe_[u].sem, pe_[u].at(i, "GATE"))
                    act.activation(sg[u][:, :], bank[u][1], ACT.Silu).then_inc(act_[u].sem, 1)
                for u in range(2):
                    act.wait_ge(pe_[u].sem, pe_[u].at(i, "GT"))
                    act.copy(giT[u][:, :, :], bank[u][3].bitcast(BF16)[:, 0:512].rearrange("p (c n) -> p c n", c=4)).then_inc(act_[u].sem, 1)

        @block.vector
        def _(dve):
            dve.tensor_copy(identb[:, :], k.ident[:, :]).then_inc(ready, 1)
            dve.wait_ge(loaded, 32)
            with dve.Fori(0, T // 2) as i:
                def done(ins, step, u):
                    ins.then_inc(dve_[u].sem, 1)

                def wait(step, u):
                    dve.wait_ge(dve_[u].sem, dve_[u].at(i, step))

                for u in range(2):
                    t = 2 * i + u
                    dve.scalar_tensor_tensor(out=h[u][:, :], in0=tile_rows(x1, t), scalar=rs[:, bass.ds(t, 1)], in1=norm_w[:, :],
                                             op0=ALU.mult, op1=ALU.mult).then_inc(dve_[u].sem, 1)
                    dve.tensor_tensor(tile_rows(k.x, t), tile_rows(k.x, t), tile_rows(x1, t), ALU.add).then_inc(dve_[u].sem, 1)
                for u in range(2):
                    dve.wait_ge(pe_[u].sem, pe_[u].at(i, "VAL"))
                    dve.wait_ge(act_[u].sem, act_[u].at(i, "SILU"))
                    dve.tensor_tensor(gv[u][:, :], sg[u][:, :], bank[u][2], ALU.mult).then_inc(dve_[u].sem, 1)
                    wait("GV", u)
                    quantise(dve, lambda ins, s, u=u: done(ins, s, u), lambda s, u=u: wait(s, u), "G", gv[u][:, :], 512,
                             qa[u], sg[u][:, :], gi[u][:, :], wm["down"])
                for u in range(2):
                    t = 2 * i + u
                    dve.wait_ge(pe_[u].sem, pe_[u].at(i, "Y"))
                    wait("GDEQ", u)
                    dve.scalar_tensor_tensor(out=tile_rows(k.x, t), in0=bank[u][0][:, 0:D], scalar=qa[u][:, 3:4], in1=tile_rows(k.x, t),
                                             op0=ALU.mult, op1=ALU.add).then_inc(dve_[u].sem, 1)


def l2_cross(nc, k):
    with ExitStack() as outer:
        xn = outer.enter_context(nc.sbuf_tensor("c2xn", [P, T, D], F32))
        cn = outer.enter_context(nc.sbuf_tensor("c2cn", [P, T, D], F32))
        cosine_norms(nc, k, xn, cn)
        cosine_attention(nc, k, xn, cn)


def cosine_norms(nc, k, xn, cn):
    with ExitStack() as ctx:
        def sb(name, shape, dt=F32):
            return ctx.enter_context(nc.sbuf_tensor("cn" + name, shape, dt))
        cs = [sb(f"cs{u}", [P, D]) for u in range(2)]
        sq = [sb(f"sq{u}", [P, 512]) for u in range(2)]
        nrm = [sb(f"nrm{u}", [P, 512]) for u in range(2)]
        arrived = [nc.alloc_semaphore(f"cn_arrived{u}") for u in range(2)]
        pe_ = lane_steps(nc, "cn", "pe", "SUMS")
        act_ = lane_steps(nc, "cn", "act", "SQRT")
        dve_ = lane_steps(nc, "cn", "dve", "SQ MAX REC")
        pool_ = lane_steps(nc, "cn", "pool", "XN CN")
        block = ctx.enter_context(nc.Block("cn_b"))

        @block.sync
        def _(sp):
            with sp.Fori(0, T // 2) as i:
                for u in range(2):
                    sp.wait_ge(pool_[u].sem, pool_[u].turns(i))
                    sp.dma_start(cs[u][:, :], k.ctx_rows[bass.ds((2 * i + u) * P, P), :]).then_inc(arrived[u], 16)

        @block.tensor
        def _(pe):
            with pe.Fori(0, T // 2) as i:
                for u in range(2):
                    pe.wait_ge(dve_[u].sem, dve_[u].at(i, "SQ"))
                    pe.matmul(k.ps[u], k.ones8[:, :], sq[u][:, :], start=True, stop=True).then_inc(pe_[u].sem, 1)

        @block.scalar
        def _(act):
            act.preload_act_table(ACT.Sqrt)
            with act.Fori(0, T // 2) as i:
                for u in range(2):
                    act.wait_ge(pe_[u].sem, pe_[u].at(i, "SUMS"))
                    act.activation(nrm[u][:, :], k.ps[u], ACT.Sqrt).then_inc(act_[u].sem, 1)

        @block.vector
        def _(dve):
            with dve.Fori(0, T // 2) as i:
                for u in range(2):
                    xt = k.x[:, bass.ds(2 * i + u, 1), :].rearrange("p t d -> p (t d)")
                    dve.wait_ge(arrived[u], 16 * (i + 1))
                    dve.tensor_tensor(sq[u][:, 0:D], xt, xt, ALU.mult)
                    dve.tensor_tensor(sq[u][:, D:2 * D], cs[u][:, :], cs[u][:, :], ALU.mult).then_inc(dve_[u].sem, 1)
                for u in range(2):
                    dve.wait_ge(act_[u].sem, act_[u].at(i, "SQRT"))
                    dve.tensor_scalar(nrm[u][:, :], nrm[u][:, :], 1e-12, None, ALU.max).then_inc(dve_[u].sem, 1)
                    dve.wait_ge(dve_[u].sem, dve_[u].at(i, "MAX"))
                    dve.reciprocal(nrm[u][:, :], nrm[u][:, :]).then_inc(dve_[u].sem, 1)

        @block.gpsimd
        def _(pool):
            with pool.Fori(0, T // 2) as i:
                for u in range(2):
                    t = bass.ds(2 * i + u, 1)
                    flat = "p t d -> p (t d)"
                    pool.wait_ge(dve_[u].sem, dve_[u].at(i, "REC"))
                    pool.tensor_tensor(xn[:, t, :].rearrange(flat), k.x[:, t, :].rearrange(flat), nrm[u][:, 0:D], ALU.mult).then_inc(pool_[u].sem, 1)
                    pool.tensor_tensor(cn[:, t, :].rearrange(flat), cs[u][:, :], nrm[u][:, D:2 * D], ALU.mult).then_inc(pool_[u].sem, 1)


def cosine_attention(nc, k, xn, cn):
    ALPHA, SYS, HD8 = 5.0, 16, 8
    PAIRS = SYS // 2
    with ExitStack() as ctx:
        def sb(name, shape, dt=F32):
            return ctx.enter_context(nc.sbuf_tensor("ca" + name, shape, dt))
        kn = [sb(f"kn{u}", [P, D]) for u in range(2)]
        cT = [sb(f"cT{u}", [P, 2, P]) for u in range(2)]
        qe = [sb(f"qe{u}", [P, SYS, D]) for u in range(2)]
        v1 = [sb(f"v1{u}", [P, 2, SYS, HD8 + 1]) for u in range(2)]
        ex = [sb(f"ex{m}", [P, 2, 2 * D]) for m in range(4)]
        rec = [sb(f"rec{u}", [P, 2, SYS]) for u in range(2)]
        oT = [sb(f"oT{u}", [P, 2, SYS, HD8]) for u in range(2)]
        arrived = [nc.alloc_semaphore(f"ca_arrived{u}") for u in range(2)]
        ones_set, spread, keyed, rec_done = semaphores(nc, ctx, "ca", "ones_set spread keyed rec_done")
        valued, scored, exped, attended, normed, turned, added = semaphores(
            nc, ctx, "ca", "valued scored exped attended normed turned added")
        VALUED, SCORED, EXPED, ATTENDED, NORMED, TURNED, ADDED = 2, 1, 2, 4 + PAIRS, 2, 2, 2
        sbank, obank, tbank = [k.psum[:, 0:2, :], k.psum[:, 2:4, :]], k.ps[4:6], k.ps[6:8]
        block = ctx.enter_context(nc.Block("ca_b"))

        @block.sync
        def _(sp):
            with sp.Fori(0, T // 2) as i:
                for u in range(2):
                    t = 2 * i + u
                    sp.wait_ge(valued, VALUED + t - 1)
                    sp.dma_start(cT[u][:, :, :], k.a["ctxT"].rearrange("(c p) n -> p c n", p=P)[:, :, bass.ds(t * P, P)]).then_inc(arrived[u], 16)

        @block.gpsimd
        def _(pool):
            pool.sem_inc(valued, VALUED)
            with pool.Fori(0, T // 2) as i:
                for u in range(2):
                    t = 2 * i + u
                    pool.wait_ge(attended, ATTENDED + PAIRS * (t - 1))
                    pool.wait_ge(arrived[u], 16 * (i + 1))
                    pool.tensor_copy(kn[u][:, :], cn[:, bass.ds(t, 1), :]).then_inc(keyed, 1)
                    pool.tensor_copy(v1[u][:, :, :, 0:HD8], cT[u][:, :, :].rearrange("p c (s d) -> p c s d", d=HD8)).then_inc(valued, 1)

        @block.tensor
        def _(pe):
            pe.sem_inc(scored, SCORED)
            pe.sem_inc(attended, ATTENDED)
            pe.sem_inc(turned, TURNED)
            pe.wait_ge(ones_set, 2)

            def scores(u, t, m):
                pe.wait_ge(exped, EXPED + PAIRS * t + m - 1)
                for c in range(2):
                    mm = pe.matmul(sbank[m % 2][:, c, :], kn[u][:, c * P:(c + 1) * P],
                                   qe[u][:, 2 * m:2 * m + 2, :].rearrange("p s d -> p (s d)"), start=True, stop=True)
                mm.then_inc(scored, 1)

            def attend(u, t, m):
                if m == 0:
                    pe.wait_ge(valued, VALUED + t + 1)
                    pe.wait_ge(normed, NORMED + t - 1)
                pe.wait_ge(exped, EXPED + PAIRS * t + m + 1)
                for s in range(2):
                    sys_ = 2 * m + s
                    for q in range(2):
                        for c in range(2):
                            mm = pe.matmul(obank[u][:, (q * SYS + sys_) * 9:(q * SYS + sys_) * 9 + 9],
                                           ex[m % 4][:, c, s * D + q * P:s * D + (q + 1) * P], v1[u][:, c, sys_, :],
                                           start=(c == 0), stop=(c == 1))
                mm.then_inc(attended, 1)

            def turn(u, t):
                pe.wait_ge(normed, NORMED + t + 1)
                pe.wait_ge(added, ADDED + t - 1)
                for q in range(2):
                    mm = pe.transpose(tbank[u][:, q * P:(q + 1) * P], oT[u][:, q, :, :].rearrange("p s d -> p (s d)"), k.ident[:, :])
                mm.then_inc(turned, 1)

            def tile(u, t, first):
                pe.wait_ge(spread, t + 1)
                pe.wait_ge(keyed, t + 1)
                for m in range(PAIRS):
                    scores(u, t, m)
                    if m >= 1:
                        attend(u, t, m - 1)
                    if m == 4 and not first:
                        turn(1 - u, t - 1)
                attend(u, t, PAIRS - 1)

            for t in range(2):
                tile(t, t, t == 0)
            with pe.Fori(1, T // 2) as i:
                for u in range(2):
                    tile(u, 2 * i + u, False)
            turn(1, T - 1)

        @block.scalar
        def _(act):
            act.preload_act_table(ACT.Exp)
            act.sem_inc(exped, EXPED)
            with act.Fori(0, T // 2) as i:
                for u in range(2):
                    t = 2 * i + u
                    for m in range(PAIRS):
                        act.wait_ge(scored, SCORED + PAIRS * t + m + 1)
                        act.wait_ge(attended, ATTENDED + PAIRS * t + m - 3)
                        act.activation(ex[m % 4][:, :, :], sbank[m % 2], ACT.Exp, scale=ALPHA).then_inc(exped, 1)

        @block.vector
        def _(dve):
            dve.sem_inc(normed, NORMED)
            dve.sem_inc(added, ADDED)
            for u in range(2):
                dve.memset(v1[u][:, :, :, HD8:HD8 + 1], 1.0).then_inc(ones_set, 1)

            def spread_queries(u, t):
                at = slice(t, t + 1) if isinstance(t, int) else bass.ds(t, 1)
                dve.tensor_tensor(qe[u][:, :, :], xn[:, at, :].to_broadcast([P, SYS, D]),
                                  k.rows_of_unit[:, :].unsqueeze(2).to_broadcast([P, SYS, D]), ALU.mult).then_inc(spread, 1)

            def divide(u, t):
                o4 = obank[u][:, 0:2 * SYS * 9].rearrange("p (q s d) -> p q s d", q=2, d=9)
                dve.wait_ge(attended, ATTENDED + PAIRS * (t + 1))
                dve.reciprocal(rec[u][:, :, :], o4[:, :, :, HD8]).then_inc(rec_done, 1)
                dve.wait_ge(rec_done, t + 1)
                dve.wait_ge(turned, TURNED + t - 1)
                dve.tensor_tensor(oT[u][:, :, :, :], o4[:, :, :, 0:HD8],
                                  rec[u][:, :, :].unsqueeze(3).to_broadcast([P, 2, SYS, HD8]), ALU.mult).then_inc(normed, 1)

            def add(u, t):
                at = slice(t, t + 1) if isinstance(t, int) else bass.ds(t, 1)
                xt = k.x[:, at, :].rearrange("p t d -> p (t d)")
                dve.wait_ge(turned, TURNED + t + 1)
                dve.tensor_tensor(xt, xt, tbank[u][:, 0:D], ALU.add).then_inc(added, 1)

            def tile(u, t, first, last):
                if not first:
                    add(1 - u, t - 1)
                divide(u, t)
                if not last:
                    dve.wait_ge(scored, SCORED + PAIRS * (t + 1))
                    spread_queries(u, t + 2)

            for u in range(2):
                spread_queries(u, u)
            for u in range(2):
                tile(u, u, u == 0, False)
            with dve.Fori(1, T // 2 - 1) as i:
                for u in range(2):
                    tile(u, 2 * i + u, False, False)
            for u in range(2):
                tile(u, T - 2 + u, False, True)
            add(1, T - 1)


def l3_attention(nc, k):
    with ExitStack() as outer:
        def sb(name, shape):
            return outer.enter_context(nc.sbuf_tensor("a3" + name, shape, F32))
        o = sb("o", [P, T, D])
        stats = sb("stats", [P, T, 6])
        diff_attention(nc, k, o, stats)
        group_norm_output(nc, k, o, stats)


def diff_attention(nc, k, o, stats):
    with ExitStack() as ctx:
        def sb(name, shape, dt=F32):
            return ctx.enter_context(nc.sbuf_tensor("d3" + name, shape, dt))
        w = sb("w", [P, 2, 768])
        lams = sb("lams", [P, 4, HD])
        lprod = sb("lprod", [P, 2, HD])
        lsum = sb("lsum", [P, 2])
        lam = sb("lam", [P, 1])
        xs = [sb(f"xs{u}", [P, 2, P]) for u in range(2)]
        t1 = [sb(f"t1{u}", [P, 512]) for u in range(2)]
        t2 = [sb(f"t2{u}", [P, 512]) for u in range(2)]
        qk = [sb(f"qk{u}", [P, 512]) for u in range(2)]
        v = [sb(f"v{u}", [P, D]) for u in range(2)]
        vd = [sb(f"vd{u}", [P, 2, D]) for u in range(2)]
        kT = [sb(f"kT{u}", [P, 2, P]) for u in range(2)]
        qT = [[sb(f"qT{u}{n}", [P, 2, P]) for n in range(2)] for u in range(2)]
        kexp = [sb(f"kexp{u}", [P, 2, 2, 8, S]) for u in range(2)]
        sc = [[sb(f"sc{u}{n}", [P, HEADS * S]) for n in range(2)] for u in range(2)]
        pT = [sb(f"pT{u}", [P, 8, P]) for u in range(2)]
        mx = [[sb(f"mx{u}{n}", [P, HEADS]) for n in range(2)] for u in range(2)]
        den = [[sb(f"den{u}{n}", [P, HEADS]) for n in range(2)] for u in range(2)]
        loaded, vec, lexp = semaphores(nc, ctx, "d3", "loaded vec lexp")
        pe_ = lane_steps(nc, "d3", "pe", "QKV TURNED SCORES0 SCORES1 PT O")
        act_ = lane_steps(nc, "d3", "act", "V QT EXP0 EXP1 PT")
        dve_ = lane_steps(nc, "d3", "dve", "COS SIN ROPED VBD KEXP MASK0 MAX0 SUB0 MASK1 MAX1 SUB1 SUM0 REC0 P0 SUM1 REC1 LREC P1 DIFF O STATS")
        pool_ = lane_steps(nc, "d3", "pool", "XS")
        bank = [[k.ps[4 * u + n] for n in range(4)] for u in range(2)]
        block = ctx.enter_context(nc.Block("d3_b"))

        @block.sync
        def _(sp):
            sp.dma_start(w[:, :, :], k.a["L3_qkv"].rearrange("(c p) n -> p c n", p=P)).then_inc(loaded, 16)
            sp.dma_start(lams[:, :, :], k.a["L3_lambdas"].partition_broadcast(P)).then_inc(loaded, 16)

        @block.gpsimd
        def _(pool):
            with pool.Fori(0, T // 2) as i:
                for u in range(2):
                    pool.wait_ge(pe_[u].sem, pe_[u].turns(i))
                    pool.tensor_copy(xs[u][:, :, :], k.xT[:, :, bass.ds((2 * i + u) * P, P)]).then_inc(pool_[u].sem, 1)

        @block.tensor
        def _(pe):
            pe.wait_ge(loaded, 32)
            with pe.Fori(0, T // 2) as i:
                for u in range(2):
                    pe.wait_ge(pool_[u].sem, pool_[u].at(i, "XS"))
                    for o_, lo, hi in ((bank[u][0], 0, 512), (bank[u][1][:, 0:D], 512, 768)):
                        for c in range(2):
                            mm = pe.matmul(o_, xs[u][:, c, :], w[:, c, lo:hi], start=(c == 0), stop=(c == 1))
                    mm.then_inc(pe_[u].sem, 1)
                for u in range(2):
                    pe.wait_ge(dve_[u].sem, dve_[u].at(i, "ROPED"))
                    pe.wait_ge(act_[u].sem, act_[u].at(i, "V"))
                    pe.wait_ge(dve_[u].sem, dve_[u].turns(i))
                    for c in range(4):
                        pe.transpose(bank[u][2][:, c * P:(c + 1) * P], qk[u][:, c * P:(c + 1) * P], k.ident[:, :])
                    for b in range(2):
                        mm = pe.matmul(bank[u][3][:, b * D:(b + 1) * D], k.dup[:, b * P:(b + 1) * P], v[u][:, :], start=True, stop=True)
                    mm.then_inc(pe_[u].sem, 1)
                for n in range(2):
                    for u in range(2):
                        if n == 0:
                            pe.wait_ge(dve_[u].sem, dve_[u].at(i, "KEXP"))
                        score_matmuls(pe, bank[u][2 * n:2 * n + 2], qT[u][n], kexp[u]).then_inc(pe_[u].sem, 1)
                for u in range(2):
                    pe.wait_ge(dve_[u].sem, dve_[u].at(i, "DIFF"))
                    weight_transposes(pe, bank[u][0:2], sc[u][0], k.ident[:, :]).then_inc(pe_[u].sem, 1)
                for u in range(2):
                    pe.wait_ge(act_[u].sem, act_[u].at(i, "PT"))
                    value_matmuls(pe, bank[u][2], pT[u], vd[u]).then_inc(pe_[u].sem, 1)

        @block.scalar
        def _(act):
            act.preload_act_table(ACT.Exp)
            act.wait_ge(vec, 3)
            act.activation(lsum[:, :], lsum[:, :], ACT.Exp).then_inc(lexp, 1)
            with act.Fori(0, T // 2) as i:
                for u in range(2):
                    act.wait_ge(pe_[u].sem, pe_[u].at(i, "QKV"))
                    act.copy(v[u][:, :], bank[u][1][:, 0:D]).then_inc(act_[u].sem, 1)
                for u in range(2):
                    act.wait_ge(pe_[u].sem, pe_[u].at(i, "TURNED"))
                    for n in range(2):
                        act.activation(qT[u][n][:, :, :], bank[u][2][:, 0:D].rearrange("p (c n) -> p c n", c=2), ACT.Copy,
                                       scale=k.half[:, n:n + 1])
                    act.copy(kT[u][:, :, :], bank[u][2][:, D:2 * D].rearrange("p (c n) -> p c n", c=2)).then_inc(act_[u].sem, 1)
                for n in range(2):
                    for u in range(2):
                        act.wait_ge(dve_[u].sem, dve_[u].at(i, f"SUB{n}"))
                        act.activation(sc[u][n][:, :], sc[u][n][:, :], ACT.Exp).then_inc(act_[u].sem, 1)
                for u in range(2):
                    act.wait_ge(pe_[u].sem, pe_[u].at(i, "PT"))
                    act.copy(pT[u][:, 0:4, :], bank[u][0].rearrange("p (c n) -> p c n", c=4))
                    act.copy(pT[u][:, 4:8, :], bank[u][1].rearrange("p (c n) -> p c n", c=4)).then_inc(act_[u].sem, 1)

        @block.vector
        def _(dve):
            dve.wait_ge(loaded, 32)
            l4 = lams[:, :, :].rearrange("p (n two) d -> p n two d", two=2)
            dve.tensor_tensor(lprod[:, :, :], l4[:, :, 0, :], l4[:, :, 1, :], ALU.mult).then_inc(vec, 1)
            dve.wait_ge(vec, 1)
            dve.tensor_reduce(lsum[:, :], lprod[:, :, :], AX.X, ALU.add).then_inc(vec, 1)
            dve.wait_ge(vec, 2)
            dve.sem_inc(vec, 1)
            dve.wait_ge(lexp, 1)
            dve.tensor_tensor(lam[:, :], lsum[:, 0:1], lsum[:, 1:2], ALU.subtract).then_inc(vec, 1)
            dve.wait_ge(vec, 4)
            dve.tensor_scalar(lam[:, :], lam[:, :], 0.8, None, ALU.add).then_inc(vec, 1)
            dve.wait_ge(vec, 5)
            with dve.Fori(0, T // 2) as i:
                def wait(step, u):
                    dve.wait_ge(dve_[u].sem, dve_[u].at(i, step))

                for u in range(2):
                    dve.wait_ge(pe_[u].sem, pe_[u].at(i, "QKV"))
                    for o_, table in ((t1, k.cos), (t2, k.sin)):
                        dve.tensor_tensor(by8(o_[u][:, :]), by8(bank[u][0]), angles(table), ALU.mult).then_inc(dve_[u].sem, 1)
                    wait("SIN", u)
                    rope_sums(dve, qk[u][:, :], t1[u][:, :], t2[u][:, :]).then_inc(dve_[u].sem, 1)
                for u in range(2):
                    dve.wait_ge(pe_[u].sem, pe_[u].at(i, "TURNED"))
                    values_by_parity(dve, vd[u], bank[u][3].rearrange("p (b n) -> p b n", b=2), k.parity[:, :]).then_inc(dve_[u].sem, 1)
                    dve.wait_ge(act_[u].sem, act_[u].at(i, "QT"))
                    spread_keys(dve, kexp[u], kT[u], k.head_mask[:, :]).then_inc(dve_[u].sem, 1)
                for n in range(2):
                    for u in range(2):
                        dve.wait_ge(pe_[u].sem, pe_[u].at(i, f"SCORES{n}"))
                        for c in range(2):
                            ins = dve.scalar_tensor_tensor(out=heads3(sc[u][n][:, c * 512:(c + 1) * 512]), in0=heads3(bank[u][2 * n + c]),
                                                           scalar=HD ** -0.5, in1=over_heads(k.upper[:, :], 8), op0=ALU.mult, op1=ALU.add)
                        ins.then_inc(dve_[u].sem, 1)
                    for u in range(2):
                        wait(f"MASK{n}", u)
                        dve.tensor_reduce(mx[u][n][:, :], heads3(sc[u][n][:, :]), AX.X, ALU.max).then_inc(dve_[u].sem, 1)
                    for u in range(2):
                        wait(f"MAX{n}", u)
                        dve.tensor_tensor(heads3(sc[u][n][:, :]), heads3(sc[u][n][:, :]), per_head(mx[u][n][:, :]),
                                          ALU.subtract).then_inc(dve_[u].sem, 1)
                for u in range(2):
                    for n in range(2):
                        dve.wait_ge(act_[u].sem, act_[u].at(i, f"EXP{n}"))
                        dve.tensor_reduce(den[u][n][:, :], heads3(sc[u][n][:, :]), AX.X, ALU.add).then_inc(dve_[u].sem, 1)
                        wait(f"SUM{n}", u)
                        dve.reciprocal(den[u][n][:, :], den[u][n][:, :]).then_inc(dve_[u].sem, 1)
                        wait(f"REC{n}", u)
                        if n:
                            dve.tensor_scalar(den[u][1][:, :], den[u][1][:, :], lam[:, :], None, ALU.mult).then_inc(dve_[u].sem, 1)
                            wait("LREC", u)
                        dve.tensor_tensor(heads3(sc[u][n][:, :]), heads3(sc[u][n][:, :]), per_head(den[u][n][:, :]),
                                          ALU.mult).then_inc(dve_[u].sem, 1)
                    wait("P1", u)
                    dve.tensor_tensor(sc[u][0][:, :], sc[u][0][:, :], sc[u][1][:, :], ALU.subtract).then_inc(dve_[u].sem, 1)
                for u in range(2):
                    t = 2 * i + u
                    dve.wait_ge(pe_[u].sem, pe_[u].at(i, "O"))
                    for b in range(2):
                        r = row_slice(b)
                        ins = dve.tensor_copy(o[r, bass.ds(t, 1), :].rearrange("p t (c h d) -> p (t c) h d", h=2, d=HD), own_batch(bank[u][2], b))
                    ins.then_inc(dve_[u].sem, 1)
                    wait("O", u)
                    dve.bn_stats(stats[:, bass.ds(t, 1), :], tile_rows(o, t)).then_inc(dve_[u].sem, 1)


def group_norm_output(nc, k, o, stats):
    with ExitStack() as ctx:
        def sb(name, shape, dt=F32):
            return ctx.enter_context(nc.sbuf_tensor("g3" + name, shape, dt))
        w = sb("w", [P, 2, D])
        gamma, beta = sb("gamma", [P, 4]), sb("beta", [P, 4])
        mom = sb("mom", [P, 4, T])
        pair = sb("pair", [P, 2, T])
        y = [sb(f"y{u}", [P, D]) for u in range(2)]
        yT = [sb(f"yT{u}", [P, 2, P]) for u in range(2)]
        loaded, vec, averaged, rooted = semaphores(nc, ctx, "g3", "loaded vec averaged rooted")
        pe_ = lane_steps(nc, "g3", "pe", "YT OUT")
        act_ = lane_steps(nc, "g3", "act", "YT")
        dve_ = lane_steps(nc, "g3", "dve", "NORM GAMMA BETA X")
        bank = [[k.ps[4 * u + n] for n in range(4)] for u in range(2)]
        block = ctx.enter_context(nc.Block("g3_b"))

        @block.sync
        def _(sp):
            sp.dma_start(w[:, :, :], k.a["L3_wo"].rearrange("(c p) n -> p c n", p=P)).then_inc(loaded, 16)
            for b in range(2):
                sp.dma_start(gamma[row_slice(b), :], k.a["L3_gamma"]).then_inc(loaded, 16)
                sp.dma_start(beta[row_slice(b), :], k.a["L3_beta"]).then_inc(loaded, 16)

        @block.gpsimd
        def _(pool):
            pool.wait_ge(vec, 12)
            pool.tensor_tensor(mom[:, 3, :], mom[:, 2, :], k.minus_half[:, 0:T], ALU.pow).then_inc(rooted, 1)

        @block.tensor
        def _(pe):
            pe.wait_ge(loaded, 80)
            pe.wait_ge(vec, 9)
            pe.matmul(k.ps[7][:, 0:2 * T], k.avg4[:, :], pair[:, :, :].rearrange("p n t -> p (n t)"), start=True, stop=True).then_inc(averaged, 1)
            with pe.Fori(0, T // 2) as i:
                for u in range(2):
                    pe.wait_ge(dve_[u].sem, dve_[u].at(i, "BETA"))
                    for c in range(2):
                        mm = pe.transpose(bank[u][0][:, c * P:(c + 1) * P], y[u][:, c * P:(c + 1) * P], k.ident[:, :])
                    mm.then_inc(pe_[u].sem, 1)
                for u in range(2):
                    pe.wait_ge(act_[u].sem, act_[u].at(i, "YT"))
                    pe.wait_ge(dve_[u].sem, dve_[u].turns(i))
                    for c in range(2):
                        mm = pe.matmul(bank[u][1][:, 0:D], yT[u][:, c, :], w[:, c, :], start=(c == 0), stop=(c == 1))
                    mm.then_inc(pe_[u].sem, 1)

        @block.scalar
        def _(act):
            with act.Fori(0, T // 2) as i:
                for u in range(2):
                    act.wait_ge(pe_[u].sem, pe_[u].at(i, "YT"))
                    act.copy(yT[u][:, :, :], bank[u][0][:, 0:D].rearrange("p (c n) -> p c n", c=2)).then_inc(act_[u].sem, 1)

        @block.vector
        def _(dve):
            count = [0]

            def link(ins):
                count[0] += 1
                ins.then_inc(vec, 1)
                dve.wait_ge(vec, count[0])

            me, mo, ve, vo = stats[:, :, 1], stats[:, :, 4], stats[:, :, 2], stats[:, :, 5]
            link(dve.tensor_tensor(pair[:, 0, :], me, mo, ALU.add))
            link(dve.tensor_scalar(pair[:, 0, :], pair[:, 0, :], 0.5, None, ALU.mult))
            link(dve.tensor_tensor(mom[:, 0, :], me, me, ALU.mult))
            link(dve.tensor_tensor(mom[:, 1, :], mo, mo, ALU.mult))
            link(dve.tensor_tensor(mom[:, 0, :], mom[:, 0, :], mom[:, 1, :], ALU.add))
            link(dve.tensor_scalar(mom[:, 0, :], mom[:, 0, :], 0.5, None, ALU.mult))
            link(dve.tensor_tensor(mom[:, 1, :], ve, vo, ALU.add))
            link(dve.tensor_scalar(mom[:, 1, :], mom[:, 1, :], 1.0 / D, None, ALU.mult))
            link(dve.tensor_tensor(pair[:, 1, :], mom[:, 0, :], mom[:, 1, :], ALU.add))
            dve.wait_ge(averaged, 1)
            link(dve.tensor_copy(pair[:, :, :].rearrange("p n t -> p (n t)"), k.ps[7][:, 0:2 * T]))
            link(dve.tensor_tensor(mom[:, 0, :], pair[:, 0, :], pair[:, 0, :], ALU.mult))
            link(dve.scalar_tensor_tensor(out=mom[:, 2, :], in0=pair[:, 1, :], scalar=1e-5, in1=mom[:, 0, :], op0=ALU.add, op1=ALU.subtract))
            dve.wait_ge(rooted, 1)
            dve.wait_ge(loaded, 80)
            with dve.Fori(0, T // 2) as i:
                for u in range(2):
                    t = 2 * i + u
                    y3 = y[u][:, :].rearrange("p (g d) -> p g d", g=4)
                    dve.tensor_scalar(y[u][:, :], tile_rows(o, t), pair[:, 0, bass.ds(t, 1)], mom[:, 3, bass.ds(t, 1)],
                                      ALU.subtract, ALU.mult).then_inc(dve_[u].sem, 1)
                    dve.wait_ge(dve_[u].sem, dve_[u].at(i, "NORM"))
                    dve.tensor_tensor(y3, y3, gamma[:, :].unsqueeze(2).to_broadcast([P, 4, 64]), ALU.mult).then_inc(dve_[u].sem, 1)
                    dve.wait_ge(dve_[u].sem, dve_[u].at(i, "GAMMA"))
                    dve.tensor_tensor(y3, y3, beta[:, :].unsqueeze(2).to_broadcast([P, 4, 64]), ALU.add).then_inc(dve_[u].sem, 1)
                for u in range(2):
                    xt = tile_rows(k.x, 2 * i + u)
                    dve.wait_ge(pe_[u].sem, pe_[u].at(i, "OUT"))
                    dve.scalar_tensor_tensor(out=xt, in0=bank[u][1][:, 0:D], scalar=1.0 - 0.8, in1=xt, op0=ALU.mult, op1=ALU.add).then_inc(dve_[u].sem, 1)


def l3_cross(nc, k):
    with ExitStack() as ctx:
        def sb(name, shape, dt=F32):
            return ctx.enter_context(nc.sbuf_tensor("c3" + name, shape, dt))
        mk8 = sb("mk8", [P, T, S], mybir.dt.uint8)
        mk = sb("mk", [P, T, S])
        neg = sb("neg", [P, T, S])
        valid = sb("valid", [P, T])
        xs = [sb(f"xs{u}", [P, 2, P]) for u in range(2)]
        cT = [sb(f"cT{u}", [P, 2, P]) for u in range(2)]
        cs = [sb(f"cs{u}", [P, D]) for u in range(2)]
        sc = [sb(f"sc{u}", [P, S]) for u in range(2)]
        nmx = [sb(f"nmx{u}", [P, 1]) for u in range(2)]
        den = [sb(f"den{u}", [P, 1]) for u in range(2)]
        fac = [sb(f"fac{u}", [P, 1]) for u in range(2)]
        pbd = [sb(f"pbd{u}", [P, P]) for u in range(2)]
        pT = [sb(f"pT{u}", [P, P]) for u in range(2)]
        loaded, ready = semaphores(nc, ctx, "c3", "loaded ready")
        arrived = [nc.alloc_semaphore(f"c3_arrived{u}") for u in range(2)]
        pe_ = lane_steps(nc, "c3", "pe", "S PT O")
        act_ = lane_steps(nc, "c3", "act", "EXP PT")
        dve_ = lane_steps(nc, "c3", "dve", "SCALED MASKED MAX REC FAC X")
        pool_ = lane_steps(nc, "c3", "pool", "XS")
        bank = [[k.ps[4 * u + n] for n in range(4)] for u in range(2)]
        block = ctx.enter_context(nc.Block("c3_b"))

        @block.sync
        def _(sp):
            for b in range(2):
                sp.dma_start(mk8[64 * b:64 * b + 64, :, :],
                             k.a["mask"].rearrange("(t b) j -> b t j", b=2)[b].partition_broadcast(64)).then_inc(loaded, 16)
            with sp.Fori(0, T // 2) as i:
                for u in range(2):
                    t = 2 * i + u
                    sp.wait_ge(pe_[u].sem, pe_[u].turns(i))
                    sp.dma_start(cs[u][:, :], k.ctx_rows[bass.ds(t * P, P), :]).then_inc(arrived[u], 16)
                    sp.dma_start(cT[u][:, :, :], k.a["ctxT"].rearrange("(c p) n -> p c n", p=P)[:, :, bass.ds(t * P, P)]).then_inc(arrived[u], 16)

        @block.gpsimd
        def _(pool):
            with pool.Fori(0, T // 2) as i:
                for u in range(2):
                    pool.wait_ge(pe_[u].sem, pe_[u].turns(i))
                    pool.tensor_copy(xs[u][:, :, :], k.xT[:, :, bass.ds((2 * i + u) * P, P)]).then_inc(pool_[u].sem, 1)

        @block.tensor
        def _(pe):
            with pe.Fori(0, T // 2) as i:
                for u in range(2):
                    pe.wait_ge(arrived[u], 32 * (i + 1))
                    pe.wait_ge(pool_[u].sem, pool_[u].at(i, "XS"))
                    pe.wait_ge(dve_[u].sem, dve_[u].turns(i))
                    for c in range(2):
                        mm = pe.matmul(bank[u][0][:, 0:P], xs[u][:, c, :], cT[u][:, c, :], start=(c == 0), stop=(c == 1))
                    mm.then_inc(pe_[u].sem, 1)
                for u in range(2):
                    pe.wait_ge(act_[u].sem, act_[u].at(i, "EXP"))
                    pe.transpose(bank[u][1][:, 0:P], pbd[u][:, :], k.ident[:, :]).then_inc(pe_[u].sem, 1)
                for u in range(2):
                    pe.wait_ge(act_[u].sem, act_[u].at(i, "PT"))
                    pe.matmul(bank[u][2][:, 0:D], pT[u][:, :], cs[u][:, :], start=True, stop=True).then_inc(pe_[u].sem, 1)

        @block.scalar
        def _(act):
            act.preload_act_table(ACT.Exp)
            act.wait_ge(ready, 6)
            with act.Fori(0, T // 2) as i:
                for u in range(2):
                    act.wait_ge(dve_[u].sem, dve_[u].at(i, "MAX"))
                    for b in range(2):
                        r = slice(64 * b, 64 * b + 64)
                        ins = act.activation(pbd[u][r, r], sc[u][r, :], ACT.Exp, bias=nmx[u][r, :], accum_out=den[u][r, :])
                    ins.then_inc(act_[u].sem, 1)
                for u in range(2):
                    act.wait_ge(pe_[u].sem, pe_[u].at(i, "PT"))
                    act.copy(pT[u][:, :], bank[u][1][:, 0:P]).then_inc(act_[u].sem, 1)

        @block.vector
        def _(dve):
            dve.memset(pbd[0][:, :], 0.0).then_inc(ready, 1)
            dve.memset(pbd[1][:, :], 0.0).then_inc(ready, 1)
            dve.wait_ge(loaded, 32)
            dve.tensor_copy(mk[:, :, :], mk8[:, :, :]).then_inc(ready, 1)
            dve.wait_ge(ready, 3)
            dve.tensor_scalar(neg[:, :, :], mk[:, :, :], -1.0, -NEG, ALU.add, ALU.mult).then_inc(ready, 1)
            dve.tensor_reduce(valid[:, :], mk[:, :, :], AX.X, ALU.max).then_inc(ready, 1)
            dve.wait_ge(ready, 5)
            dve.sem_inc(ready, 1)
            with dve.Fori(0, T // 2) as i:
                for u in range(2):
                    def wait(step, u=u):
                        dve.wait_ge(dve_[u].sem, dve_[u].at(i, step))

                    t = bass.ds(2 * i + u, 1)
                    dve.wait_ge(pe_[u].sem, pe_[u].at(i, "S"))
                    for b in range(2):
                        r = slice(64 * b, 64 * b + 64)
                        ins = dve.scalar_tensor_tensor(out=sc[u][r, :], in0=bank[u][0][r, r], scalar=D ** -0.5,
                                                       in1=mk[r, t, :].rearrange("p t j -> p (t j)"), op0=ALU.mult, op1=ALU.mult)
                    ins.then_inc(dve_[u].sem, 1)
                    wait("SCALED")
                    dve.tensor_tensor(sc[u][:, :], sc[u][:, :], neg[:, t, :].rearrange("p t j -> p (t j)"), ALU.add).then_inc(dve_[u].sem, 1)
                    wait("MASKED")
                    dve.tensor_reduce(nmx[u][:, :], sc[u][:, :], AX.X, ALU.max, negate=True).then_inc(dve_[u].sem, 1)
                for u in range(2):
                    t = bass.ds(2 * i + u, 1)
                    dve.wait_ge(act_[u].sem, act_[u].at(i, "EXP"))
                    dve.reciprocal(den[u][:, :], den[u][:, :]).then_inc(dve_[u].sem, 1)
                    dve.wait_ge(dve_[u].sem, dve_[u].at(i, "REC"))
                    dve.tensor_tensor(fac[u][:, :], den[u][:, :], valid[:, t], ALU.mult).then_inc(dve_[u].sem, 1)
                for u in range(2):
                    xt = k.x[:, bass.ds(2 * i + u, 1), :].rearrange("p t d -> p (t d)")
                    dve.wait_ge(pe_[u].sem, pe_[u].at(i, "O"))
                    dve.wait_ge(dve_[u].sem, dve_[u].at(i, "FAC"))
                    dve.scalar_tensor_tensor(out=xt, in0=bank[u][2][:, 0:D], scalar=fac[u][:, :], in1=xt,
                                             op0=ALU.mult, op1=ALU.add).then_inc(dve_[u].sem, 1)


class Shared:
    pass


def build(nc, a, out):
    with ExitStack() as ctx:
        k = Shared()
        k.a = a
        def sb(name, shape, dt=F32):
            return ctx.enter_context(nc.sbuf_tensor(name, shape, dt))
        k.psum = ctx.enter_context(nc.psum_tensor("psum", [P, 8, 512], F32))
        k.ps = [k.psum[:, i, :] for i in range(8)]
        k.x = sb("x", [P, T, D])
        k.xT = sb("xT", [P, 2, N])
        k.consts = {n[2:]: sb(n, list(ap.shape)) for n, ap in a.items() if n.startswith("c_")}
        c = k.consts
        k.ident, k.cos, k.sin, k.head_mask, k.parity = c["ident"], c["cos"], c["sin"], c["head_mask"], c["parity"]
        k.strict, k.causal, k.not_first = c["strict"], c["causal"], c["not_first"]
        k.ones8, k.rows_of_unit = c["ones8"], c["rows_of_unit"]
        k.dup, k.block_causal, k.upper, k.half = c["dup"], c["block_causal"], c["upper"], c["half"]
        k.ones64, k.cumulate, k.eye64, k.avg4, k.ones = c["ones64"], c["cumulate"], c["eye64"], c["avg4"], c["ones"]
        k.minus_half = sb("minus_half", [P, T])
        k.v_scr = nc.dram_tensor("v_scr", (N, D), F32, kind="Internal").ap()
        k.u_scr = nc.dram_tensor("u_scr", (N, D), F32, kind="Internal").ap()
        k.l_scr = nc.dram_tensor("l_scr", (NB, 16, S, S), F32, kind="Internal").ap()
        k.p_scr = nc.dram_tensor("p_scr", (T, P, 1024), F32, kind="Internal").ap()
        k.q_scr = nc.dram_tensor("q_scr", (3, D, N), BF16, kind="Internal").ap()
        k.k_scr = nc.dram_tensor("k_scr", (3, D, KEYS), BF16, kind="Internal").ap()
        k.strip_sum = c["strip_sum"]
        k.ctx_rows = a["ctx"]
        load_phase(nc, k)
        for n, phase in list(enumerate(PHASES))[FIRST:LAST + 1]:
            with nc.cleanup_on_exit():
                phase(nc, k)
                layer_norm(nc, k, f"ln{n}")
        store_phase(nc, k, out)


def load_phase(nc, k):
    with ExitStack() as ctx:
        loaded, const, turned, copied = semaphores(nc, ctx, "load", "loaded const turned copied")
        block = ctx.enter_context(nc.Block("load_b"))

        @block.sync
        def _(sp):
            for b in range(2):
                sp.dma_start(k.x[64 * b:64 * b + 64, :, :],
                             k.a["x"].rearrange("(t c) s d -> c s t d", c=2)[b]).then_inc(loaded, 16)
            for n, tile in k.consts.items():
                sp.dma_start(tile[:, :], k.a["c_" + n]).then_inc(loaded, 16)
            sp.wait_ge(loaded, 32 + 16 * len(k.consts))

        @block.gpsimd
        def _(pool):
            pool.memset(k.minus_half[:, :], -0.5).then_inc(const, 1)
            pool.wait_ge(const, 1)

        @block.tensor
        def _(pe):
            pe.wait_ge(loaded, 32 + 16 * len(k.consts))
            for t in range(T):
                if t >= 8:
                    pe.wait_ge(copied, t - 7)
                pe.transpose(k.ps[t % 8][:, 0:128], k.x[:, t, 0:128], k.ident[:, :])
                pe.transpose(k.ps[t % 8][:, 128:256], k.x[:, t, 128:256], k.ident[:, :]).then_inc(turned, 1)

        @block.scalar
        def _(act):
            for t in range(T):
                act.wait_ge(turned, t + 1)
                act.copy(k.xT[:, :, t * P:(t + 1) * P],
                         k.ps[t % 8][:, 0:256].rearrange("p (c n) -> p c n", c=2)).then_inc(copied, 1)


def store_phase(nc, k, out):
    with ExitStack() as ctx:
        stored, = semaphores(nc, ctx, "store", "stored")
        block = ctx.enter_context(nc.Block("store_b"))

        @block.sync
        def _(sp):
            for b in range(2):
                sp.dma_start(out.rearrange("(t c) s d -> c s t d", c=2)[b], k.x[64 * b:64 * b + 64, :, :]).then_inc(stored, 16)
            sp.wait_ge(stored, 32)


PHASES = [l0_attention, l0_cross, l0_ffn] + [l1_attention, l1_cross, l1_ffn, l2_attention, l2_cross, l2_ffn, l3_attention, l3_cross, l3_ffn]


def shape_constants():
    p = np.arange(P)
    s = p % S
    j = np.arange(S)
    ang = s[:, None].astype(np.float32) * (1.0 / 10000.0 ** (np.arange(8) / 8.0)).astype(np.float32)[None]
    f = lambda m: np.ascontiguousarray(m, dtype=np.float32)
    return {
        "ident": f(np.eye(P)),
        "cos": f(np.cos(ang)), "sin": f(np.sin(ang)),
        "head_mask": f(p[:, None] // HD == np.arange(8)[None]),
        "parity": f(p[:, None] // S == np.arange(HEADS)[None] % 2),
        "strict": f(np.where(s[:, None] > j[None], 0, NEG)),
        "causal": f(np.where(s[:, None] >= j[None], 0, NEG)),
        "not_first": f(s[:, None] > 0),
        "strip_sum": f(p[:, None] % 32 == np.arange(HD + 1)[None]),
        "dup": f(np.concatenate([p[:, None] == b * S + s[None] for b in range(2)], axis=1)),
        "block_causal": f(np.where((s[:, None] >= j[None]) & (s[:, None] // 8 == j[None] // 8), 0, NEG)),
        "upper": f(j[None] > s[:, None]),
        "half": f(p[:, None] % HD // 8 == np.arange(2)[None]),
        "ones64": f(p[:, None] // S == p[None] // S),
        "cumulate": f((p[:, None] // S == p[None] // S) & (p[:, None] <= p[None])),
        "eye64": f(s[:, None] == j[None]),
        "avg4": f((p[:, None] // 4 == p[None] // 4) * 0.25),
        "ones": f(np.ones((P, P))),
        "ones8": f(p[:, None] // 8 == p[None] // 8),
        "rows_of_unit": f(p[:, None] // 8 == np.arange(16)[None]),
    }


def selection(experts, width, hidden, shared_row=False):
    unit = np.arange(hidden)
    owner = np.minimum(unit // width, experts)
    rows = experts + 1 if shared_row else experts
    return (np.arange(rows)[:, None] == owner[None]).astype(np.float32)


def laid_out(i):
    out = {n: np.ascontiguousarray(i[n]) for n in ("x",)}
    out["L0_attn_W"] = np.concatenate([i["L0_attn_Wq"], i["L0_attn_Wk"], i["L0_attn_Wv"], i["L0_attn_Wb"]], axis=1)
    out["L0_attn_bb"] = np.ascontiguousarray(i["L0_attn_bb"])
    out["L0_attn_Wo"] = np.ascontiguousarray(i["L0_attn_Wo"])
    out["mask"] = i["mask_BxS2_bk0"]
    out["L1_wr"], out["L1_w1"], out["L1_w3"], out["L1_w2"] = (i["L1_ffn_" + n].T for n in ("wr", "w1", "w3", "w2"))
    out["L1_gates"] = np.concatenate([i["L1_xattn_Wi"], i["L1_xattn_Wf"]], axis=1)
    out["L1_gates_b"] = np.concatenate([i["L1_xattn_bi"], i["L1_xattn_bf"]])
    out["L1_xattn_ln_scale"] = i["L1_xattn_ln_scale"]
    out["L2_norm1"], out["L2_norm2"] = i["L2_attn_attn_norm_w"], i["L2_attn_ffn_norm_w"]
    out["L2_qkv"], out["L2_o"], out["L2_up"], out["L2_down"] = (i["L2_attn_" + n + "_w"].T for n in ("qkv", "o", "ffn_up", "ffn_down"))
    out["L3_qkv"], out["L3_wo"] = i["L3_attn_w_qkv"].T, i["L3_attn_wo"].T
    out["L3_lambdas"] = np.stack([i["L3_attn_lambda_" + n] for n in ("q1", "k1", "q2", "k2")])
    out["L3_gamma"], out["L3_beta"] = i["L3_attn_gamma"].reshape(S, 4), i["L3_attn_beta"].reshape(S, 4)
    out["L1_kT"] = i["L1_attn_kv_k"].reshape(-1, D).T
    out["L1_v"] = i["L1_attn_kv_v"].reshape(-1, D)
    out["L1_Wq"], out["L1_Wo"] = i["L1_attn_Wq"].T, i["L1_attn_Wo"].T
    out["ctx"] = i["ctx_2048"].reshape(N, D)
    out["ctxT"] = i["ctx_2048"].reshape(N, D).T
    gu, F = i["L0_ffn_gate_up_weights"], i["L0_ffn_gate_up_weights"].shape[1] // 2
    sgu, FS = i["L0_ffn_shared_gate_up"], i["L0_ffn_shared_gate_up"].shape[0] // 2
    out["L0_router"] = i["L0_ffn_gate_weight"].T
    out["L0_g"] = np.concatenate([gu[:, :F].reshape(-1, D), sgu[:FS]]).T
    out["L0_u"] = np.concatenate([gu[:, F:].reshape(-1, D), sgu[FS:]]).T
    out["L0_d"] = np.concatenate([i["L0_ffn_down_weights"].transpose(0, 2, 1).reshape(-1, D), i["L0_ffn_shared_down"].T])
    out["sel176"] = selection(8, F, 8 * F + FS)
    flat = lambda w: w.transpose(1, 0, 2).reshape(D, -1)
    out["L2_router"] = np.concatenate([i["L2_ffn_gate_w"].T, i["L2_ffn_shgate_w"][:, None]], axis=1)
    out["L2_g"] = np.concatenate([flat(i["L2_ffn_w_gate"]), i["L2_ffn_shw_gate"]], axis=1)
    out["L2_u"] = np.concatenate([flat(i["L2_ffn_w_up"]), i["L2_ffn_shw_up"]], axis=1)
    out["L2_d"] = np.concatenate([i["L2_ffn_w_down"].reshape(-1, D), i["L2_ffn_shw_down"]])
    out["sel176s"] = selection(8, F, 8 * F + FS, shared_row=True)
    out["L3_ffn_w_router"] = i["L3_ffn_w_router"]
    out["L3_g"] = np.concatenate([flat(i["L3_ffn_we1"]), i["L3_ffn_ws1"]], axis=1)
    out["L3_u"] = np.concatenate([flat(i["L3_ffn_we3"]), i["L3_ffn_ws3"]], axis=1)
    out["L3_d"] = np.concatenate([i["L3_ffn_we2"].reshape(-1, D), i["L3_ffn_ws2"]])
    out["sel128"] = selection(16, 128, 16 * 128 + 512)
    return {n: np.ascontiguousarray(a) for n, a in out.items()}


def kernel(**inputs):
    import concourse.bacc as _bacc
    from concourse.bass_utils import run_bass_kernel_spmd as _run

    nc = _bacc.Bacc("TRN2", target_bir_lowering=False, num_devices=1)
    arrays, aps = {}, {}
    given = laid_out({n: np.asarray(a) for n, a in inputs.items()})
    for name, a in {**given, **{"c_" + n: c for n, c in shape_constants().items()}}.items():
        arrays[f"in_{name}_dram"] = a
        aps[name] = nc.dram_tensor(f"in_{name}_dram", a.shape, mybir.dt.from_np(a.dtype), kind="ExternalInput").ap()
    out = nc.dram_tensor("out_0_dram", (NB, S, D), F32, kind="ExternalOutput").ap()
    build(nc, aps, out)
    r = _run(nc, [arrays], core_ids=[0])
    return r.results[0]["out_0_dram"]
```

```python
import numpy as np
from contextlib import ExitStack
import concourse.bass as bass
from concourse import mybir

FIRST, LAST = 0, 11
P, D, S, NB = 128, 256, 64, 32
N = S * NB
T = N // P
G = 4
F32, BF16 = mybir.dt.float32, mybir.dt.bfloat16
ALU, ACT, AX = mybir.AluOpType, mybir.ActivationFunctionType, mybir.AxisListType
LN_EPS = 1e-5
HEADS, HD = 16, 16
KEYS = 4096
NEG = -1e30


def semaphores(nc, ctx, phase, names):
    return [nc.alloc_semaphore(f"{phase}_{n}") for n in names.split()]


def layer_norm(nc, k, name):
    with ExitStack() as ctx:
        def sb(n, shape):
            return ctx.enter_context(nc.sbuf_tensor(name + n, shape, F32))
        LANES = 4
        stats = sb("stats", [P, T, 6])
        MEAN, APART, VAR, APART2, TOTAL, RSTD = range(6)
        mom = sb("mom", [P, 6, T])
        stage = [sb(f"stage{u}", [P, D]) for u in range(LANES)]
        taken, vec, vared, rstd_ready, staged, written, turned, copied = semaphores(
            nc, ctx, name, "taken vec variance rstd staged written turned copied")
        block = ctx.enter_context(nc.Block(name + "_b"))

        @block.vector
        def _(dve):
            with dve.Fori(0, T // LANES) as i:
                for u in range(LANES):
                    dve.bn_stats(stats[:, bass.ds(LANES * i + u, 1), :], k.x[:, bass.ds(LANES * i + u, 1), :]).then_inc(taken, 1)
            dve.wait_ge(taken, T)
            me, mo, ve, vo = stats[:, :, 1], stats[:, :, 4], stats[:, :, 2], stats[:, :, 5]
            dve.tensor_tensor(mom[:, MEAN, :], me, mo, ALU.add).then_inc(vec, 1)
            dve.tensor_tensor(mom[:, APART, :], me, mo, ALU.subtract).then_inc(vec, 1)
            dve.tensor_tensor(mom[:, VAR, :], ve, vo, ALU.add).then_inc(vec, 1)
            dve.wait_ge(vec, 3)
            dve.tensor_tensor(mom[:, APART2, :], mom[:, APART, :], mom[:, APART, :], ALU.mult).then_inc(vec, 1)
            dve.tensor_scalar(mom[:, VAR, :], mom[:, VAR, :], 1.0 / D, LN_EPS, ALU.mult, ALU.add).then_inc(vec, 1)
            dve.tensor_scalar(mom[:, MEAN, :], mom[:, MEAN, :], 0.5, None, ALU.mult).then_inc(vec, 1)
            dve.wait_ge(vec, 6)
            dve.scalar_tensor_tensor(out=mom[:, TOTAL, :], in0=mom[:, APART2, :], scalar=0.25, in1=mom[:, VAR, :],
                                     op0=ALU.mult, op1=ALU.add).then_inc(vared, 1)
            dve.wait_ge(rstd_ready, 1)
            with dve.Fori(0, T // LANES) as i:
                for u in range(LANES):
                    xt, t = k.x[:, bass.ds(LANES * i + u, 1), :], bass.ds(LANES * i + u, 1)
                    dve.wait_ge(turned, LANES * i + u + 1)
                    dve.tensor_scalar(stage[u][:, :], xt, mom[:, MEAN, t], mom[:, RSTD, t], ALU.subtract, ALU.mult).then_inc(staged, 1)
                    dve.tensor_scalar(xt, xt, mom[:, MEAN, t], mom[:, RSTD, t], ALU.subtract, ALU.mult).then_inc(written, 1)

        @block.gpsimd
        def _(pool):
            pool.wait_ge(vared, 1)
            pool.tensor_tensor(mom[:, RSTD, :], mom[:, TOTAL, :], k.minus_half[:, 0:T], ALU.pow).then_inc(rstd_ready, 1)

        @block.tensor
        def _(pe):
            pe.sem_inc(turned, LANES)
            with pe.Fori(0, T // LANES) as i:
                for u in range(LANES):
                    pe.wait_ge(staged, LANES * i + u + 1)
                    pe.wait_ge(copied, LANES * i + u + 1)
                    pe.transpose(k.ps[u][:, 0:128], stage[u][:, 0:128], k.ident[:, :])
                    pe.transpose(k.ps[u][:, 128:256], stage[u][:, 128:256], k.ident[:, :]).then_inc(turned, 1)

        @block.scalar
        def _(act):
            act.sem_inc(copied, LANES)
            with act.Fori(0, T // LANES) as i:
                for u in range(LANES):
                    act.wait_ge(turned, LANES * i + u + 1 + LANES)
                    act.copy(k.xT[:, :, bass.ds((LANES * i + u) * P, P)],
                             k.ps[u][:, 0:256].rearrange("p (c n) -> p c n", c=2)).then_inc(copied, 1)




class Steps:

    def __init__(self, nc, engine, name, steps):
        self.sem = nc.alloc_semaphore(name)
        by = {"pe": nc.tensor, "act": nc.scalar, "dve": nc.vector, "pool": nc.gpsimd}[engine]
        by.sem_inc(self.sem, 1)
        self.names = steps.split()
        self.per = len(self.names)

    def at(self, i, step):
        return self.per * i + self.names.index(step) + 2

    def turns(self, i):
        return self.per * i + 1


def lane_steps(nc, phase, engine, steps, lanes=2):
    return [Steps(nc, engine, f"{phase}_{engine}{u}", steps) for u in range(lanes)]


def heads3(ap):
    return ap.rearrange("p (h j) -> p h j", j=S)


def l0_attention(nc, k):
    delta_scores(nc, k)
    delta_solve(nc, k)
    delta_output(nc, k)


def delta_scores(nc, k):
    SCALE = HD ** -0.5
    with ExitStack() as ctx:
        def sb(name, shape, dt=F32):
            return ctx.enter_context(nc.sbuf_tensor("d0" + name, shape, dt))
        w = sb("w", [P, 2, 784])
        bb = sb("bb", [P, HEADS])
        xs = [sb(f"xs{u}", [P, 2, P]) for u in range(2)]
        qk = [sb(f"qk{u}", [P, 512]) for u in range(2)]
        t1 = [sb(f"t1{u}", [P, 512]) for u in range(2)]
        t2 = [sb(f"t2{u}", [P, 512]) for u in range(2)]
        v = [sb(f"v{u}", [P, D]) for u in range(2)]
        beta = [sb(f"beta{u}", [P, HEADS]) for u in range(2)]
        qkT = [sb(f"qkT{u}", [P, 4, P]) for u in range(2)]
        kexp = [sb(f"kexp{u}", [P, 2, 2, 8, S]) for u in range(2)]
        sc = [[sb(f"sc{u}{n}", [P, HEADS * S]) for n in range(2)] for u in range(2)]
        pT = [sb(f"pT{u}", [P, HEADS * S]) for u in range(2)]
        mx = [[sb(f"mx{u}{n}", [P, HEADS]) for n in range(2)] for u in range(2)]
        den = [[sb(f"den{u}{n}", [P, HEADS]) for n in range(2)] for u in range(2)]
        loaded, = semaphores(nc, ctx, "d0", "loaded")
        stored = [nc.alloc_semaphore(f"d0_stored{u}") for u in range(2)]
        pe_ = lane_steps(nc, "d0", "pe", "QKV TURNED SCORES0 SCORES1 PT")
        act_ = lane_steps(nc, "d0", "act", "V QKT EXP0 EXP1 PT")
        dve_ = lane_steps(nc, "d0", "dve", "COS SIN ROPED BETA KEXP MASK0 MAX0 MASK1 MAX1 SUB1 REC0 FAC0 LROW SUM1 REC1 PROW")
        pool_ = lane_steps(nc, "d0", "pool", "XS")
        bank = [[k.ps[4 * u + n] for n in range(4)] for u in range(2)]
        masks = [k.strict, k.causal]
        block = ctx.enter_context(nc.Block("d0_b"))

        @block.sync
        def _(sp):
            sp.dma_start(w[:, :, :], k.a["L0_attn_W"].rearrange("(c p) n -> p c n", p=P)).then_inc(loaded, 16)
            sp.dma_start(bb[:, :], k.a["L0_attn_bb"].partition_broadcast(P)).then_inc(loaded, 16)
            for u in range(2):
                sp.sem_inc(stored[u], 1)

            def store_weights(u, i):
                t = 2 * i + u
                tile_at = slice(t, t + 1) if isinstance(t, int) else bass.ds(t, 1)
                sp.wait_ge(dve_[u].sem, dve_[u].at(i, "LROW"))
                for b in range(2):
                    at = slice(2 * t + b, 2 * t + b + 1) if isinstance(t, int) else bass.ds(2 * t + b, 1)
                    sp.dma_start(k.l_scr[at, :, :, :].rearrange("b h i j -> (b i) h j"),
                                 heads3(sc[u][0][64 * b:64 * b + 64, :])).then_inc(stored[u], 16)
                sp.wait_ge(act_[u].sem, act_[u].at(i, "PT"))
                sp.dma_start(k.p_scr[tile_at, :, :].rearrange("t p n -> (t p) n"), pT[u][:, :]).then_inc(stored[u], 16)

            def tile(u, i, before, after):
                t = 2 * i + u
                rows = slice(t * P, t * P + P) if isinstance(t, int) else bass.ds(t * P, P)
                sp.wait_ge(act_[u].sem, act_[u].at(i, "V"))
                sp.dma_start(k.v_scr[rows, :], v[u][:, :]).then_inc(stored[u], 16)
                if before:
                    store_weights(*before)

            store_weights(*staggered(sp, tile))
            for u in range(2):
                sp.wait_ge(stored[u], 64 * (T // 2) + 1)

        @block.gpsimd
        def _(pool):
            with pool.Fori(0, T // 2) as i:
                for u in range(2):
                    pool.wait_ge(pe_[u].sem, pe_[u].turns(i))
                    pool.tensor_copy(xs[u][:, :, :], k.xT[:, :, bass.ds((2 * i + u) * P, P)]).then_inc(pool_[u].sem, 1)

        @block.tensor
        def _(pe):
            pe.wait_ge(loaded, 32)

            def project(u, i):
                pe.wait_ge(pool_[u].sem, pool_[u].at(i, "XS"))
                pe.wait_ge(act_[u].sem, act_[u].turns(i))
                for o, lo, hi in ((bank[u][0], 0, 512), (bank[u][1][:, 0:272], 512, 784)):
                    for c in range(2):
                        mm = pe.matmul(o, xs[u][:, c, :], w[:, c, lo:hi], start=(c == 0), stop=(c == 1))
                mm.then_inc(pe_[u].sem, 1)

            def turn(u, i):
                pe.wait_ge(dve_[u].sem, dve_[u].at(i, "ROPED"))
                for c in range(4):
                    mm = pe.transpose(bank[u][2][:, c * P:(c + 1) * P], qk[u][:, c * P:(c + 1) * P], k.ident[:, :])
                mm.then_inc(pe_[u].sem, 1)

            def scores(u, i, n):
                if n == 0:
                    pe.wait_ge(act_[u].sem, act_[u].at(i, "QKT"))
                    pe.wait_ge(dve_[u].sem, dve_[u].at(i, "KEXP"))
                queries = qkT[u][:, 2:4, :] if n == 0 else qkT[u][:, 0:2, :]
                score_matmuls(pe, bank[u][2 * n:2 * n + 2], queries, kexp[u]).then_inc(pe_[u].sem, 1)

            def turn_weights(u, i):
                pe.wait_ge(dve_[u].sem, dve_[u].at(i, "PROW"))
                weight_transposes(pe, bank[u][0:2], sc[u][1], k.ident[:, :]).then_inc(pe_[u].sem, 1)

            def tile(u, i, before, after):
                turn(u, i)
                scores(u, i, 0)
                if before:
                    turn_weights(*before)
                scores(u, i, 1)
                if after:
                    project(*after)

            project(0, 0)
            turn_weights(*staggered(pe, tile))

        @block.scalar
        def _(act):
            act.preload_act_table(ACT.Exp)

            def weights_out(u, i):
                act.wait_ge(pe_[u].sem, pe_[u].at(i, "PT"))
                act.copy(pT[u][:, 0:512], bank[u][0])
                act.copy(pT[u][:, 512:1024], bank[u][1]).then_inc(act_[u].sem, 1)

            def tile(u, i, before, after):
                act.wait_ge(pe_[u].sem, pe_[u].at(i, "QKV"))
                act.wait_ge(stored[u], 64 * i + 1)
                act.copy(v[u][:, :], bank[u][1][:, 0:D]).then_inc(act_[u].sem, 1)
                act.wait_ge(pe_[u].sem, pe_[u].at(i, "TURNED"))
                act.copy(qkT[u][:, :, :], bank[u][2].rearrange("p (c n) -> p c n", c=4)).then_inc(act_[u].sem, 1)
                if before:
                    weights_out(*before)
                act.wait_ge(dve_[u].sem, dve_[u].at(i, "MAX0"))
                exponentials(act, sc[u][0], mx[u][0], den[u][0]).then_inc(act_[u].sem, 1)
                act.wait_ge(dve_[u].sem, dve_[u].at(i, "SUB1"))
                act.activation(sc[u][1][:, :], sc[u][1][:, :], ACT.Exp).then_inc(act_[u].sem, 1)

            weights_out(*staggered(act, tile))

        @block.vector
        def _(dve):
            def wait(u, i, step):
                dve.wait_ge(dve_[u].sem, dve_[u].at(i, step))

            dve.wait_ge(loaded, 32)

            def rope(u, i):
                dve.wait_ge(pe_[u].sem, pe_[u].at(i, "QKV"))
                for o, table in ((t1, k.cos), (t2, k.sin)):
                    dve.tensor_tensor(by8(o[u][:, :]), by8(bank[u][0]), angles(table), ALU.mult).then_inc(dve_[u].sem, 1)
                wait(u, i, "SIN")
                rope_sums(dve, qk[u][:, :], t1[u][:, :], t2[u][:, :]).then_inc(dve_[u].sem, 1)
                dve.wait_ge(act_[u].sem, act_[u].at(i, "V"))
                dve.tensor_tensor(beta[u][:, :], bank[u][1][:, D:D + HEADS], bb[:, :], ALU.add).then_inc(dve_[u].sem, 1)

            def mask(u, i, n):
                dve.wait_ge(pe_[u].sem, pe_[u].at(i, f"SCORES{n}"))
                for c in range(2):
                    ins = dve.scalar_tensor_tensor(out=heads3(sc[u][n][:, c * 512:(c + 1) * 512]), in0=heads3(bank[u][2 * n + c]),
                                                   scalar=SCALE, in1=over_heads(masks[n][:, :], 8), op0=ALU.mult, op1=ALU.add)
                ins.then_inc(dve_[u].sem, 1)
                wait(u, i, f"MASK{n}")
                dve.tensor_reduce(mx[u][n][:, :], heads3(sc[u][n][:, :]), AX.X, ALU.max, negate=(n == 0)).then_inc(dve_[u].sem, 1)

            def normalise(u, n):
                dve.tensor_tensor(heads3(sc[u][n][:, :]), heads3(sc[u][n][:, :]), per_head(den[u][n][:, :]), ALU.mult).then_inc(dve_[u].sem, 1)

            def finish_keys(u, i):
                dve.wait_ge(act_[u].sem, act_[u].at(i, "EXP0"))
                dve.reciprocal(den[u][0][:, :], den[u][0][:, :]).then_inc(dve_[u].sem, 1)
                wait(u, i, "REC0")
                dve.scalar_tensor_tensor(out=den[u][0][:, :], in0=den[u][0][:, :], scalar=k.not_first[:, :],
                                         in1=beta[u][:, :], op0=ALU.mult, op1=ALU.mult).then_inc(dve_[u].sem, 1)
                wait(u, i, "FAC0")
                normalise(u, 0)

            def finish_queries(u, i):
                dve.wait_ge(act_[u].sem, act_[u].at(i, "EXP1"))
                dve.tensor_reduce(den[u][1][:, :], heads3(sc[u][1][:, :]), AX.X, ALU.add).then_inc(dve_[u].sem, 1)
                wait(u, i, "SUM1")
                dve.reciprocal(den[u][1][:, :], den[u][1][:, :]).then_inc(dve_[u].sem, 1)
                wait(u, i, "REC1")
                normalise(u, 1)

            def tile(u, i, before, after):
                rope(u, i)
                if before:
                    finish_keys(*before)
                dve.wait_ge(act_[u].sem, act_[u].at(i, "QKT"))
                spread_keys(dve, kexp[u], qkT[u][:, 2:4, :], k.head_mask[:, :]).then_inc(dve_[u].sem, 1)
                if before:
                    finish_queries(*before)
                mask(u, i, 0)
                mask(u, i, 1)
                wait(u, i, "MAX1")
                dve.tensor_tensor(heads3(sc[u][1][:, :]), heads3(sc[u][1][:, :]), per_head(mx[u][1][:, :]), ALU.subtract).then_inc(dve_[u].sem, 1)

            end = staggered(dve, tile)
            finish_keys(*end)
            finish_queries(*end)


def delta_solve(nc, k):
    GROUPS = NB * HEADS // P
    with ExitStack() as ctx:
        def sb(name, shape, dt=F32):
            return ctx.enter_context(nc.sbuf_tensor("ds" + name, shape, dt))
        lm = sb("l", [P, GROUPS, S, S])
        vs = sb("v", [P, GROUPS, S, HD])
        tmp = [sb(f"tmp{u}", [P, S, HD]) for u in range(2)]
        arrived = [nc.alloc_semaphore(f"ds_arrived{u}") for u in range(2)]
        chain = [nc.alloc_semaphore(f"ds_chain{u}") for u in range(2)]
        stored, = semaphores(nc, ctx, "ds", "stored")
        STEPS = 2 * (S - 1)
        block = ctx.enter_context(nc.Block("ds_b"))

        def scratch(scr, b):
            return scr[b * S:(b + 1) * S, :].rearrange("j (h d) -> h j d", d=HD)

        @block.sync
        def _(sp):
            for g in range(GROUPS):
                if g >= 2:
                    sp.wait_ge(arrived[g % 2], 16 * 9)
                sp.dma_start(lm[:, g, :, :].rearrange("p i j -> p (i j)"),
                             k.l_scr[8 * g:8 * g + 8, :, :, :].rearrange("b h i j -> (b h) (i j)")).then_inc(arrived[g % 2], 16)
                for b in range(8):
                    sp.dma_start(vs[16 * b:16 * b + 16, g, :, :], scratch(k.v_scr, 8 * g + b)).then_inc(arrived[g % 2], 16)
            for g in range(GROUPS):
                sp.wait_ge(chain[g % 2], 1 + STEPS * (g // 2 + 1))
                for b in range(8):
                    sp.dma_start(scratch(k.u_scr, 8 * g + b), vs[16 * b:16 * b + 16, g, :, :]).then_inc(stored, 16)
            sp.wait_ge(stored, 16 * 8 * GROUPS)

        @block.vector
        def _(dve):
            for u in range(2):
                dve.sem_inc(chain[u], 1)
            with dve.Fori(0, GROUPS // 2) as i:
                l_, v_ = ([ap[:, bass.ds(2 * i + u, 1), :, :].rearrange("p g i j -> p (g i) j") for u in range(2)] for ap in (lm, vs))
                for u in range(2):
                    dve.wait_ge(arrived[u], 16 * 9 * (i + 1))
                for j in range(S - 1):
                    n = S - 1 - j
                    for u in range(2):
                        dve.wait_ge(chain[u], i * STEPS + 2 * j + 1)
                        dve.tensor_tensor(tmp[u][:, 0:n, :], l_[u][:, j + 1:S, j].unsqueeze(2).to_broadcast([P, n, HD]),
                                          v_[u][:, j, :].unsqueeze(1).to_broadcast([P, n, HD]), ALU.mult).then_inc(chain[u], 1)
                    for u in range(2):
                        dve.wait_ge(chain[u], i * STEPS + 2 * j + 2)
                        dve.tensor_tensor(v_[u][:, j + 1:S, :], v_[u][:, j + 1:S, :], tmp[u][:, 0:n, :],
                                          ALU.subtract).then_inc(chain[u], 1)


def delta_output(nc, k):
    with ExitStack() as ctx:
        def sb(name, shape, dt=F32):
            return ctx.enter_context(nc.sbuf_tensor("do" + name, shape, dt))
        w = sb("w", [P, 2, D])
        pT = [sb(f"pT{u}", [P, 8, P]) for u in range(2)]
        ud = [sb(f"ud{u}", [P, 2, D]) for u in range(2)]
        o = [sb(f"o{u}", [P, D]) for u in range(2)]
        oT = [sb(f"oT{u}", [P, 2, P]) for u in range(2)]
        loaded, = semaphores(nc, ctx, "do", "loaded")
        arrived = [nc.alloc_semaphore(f"do_arrived{u}") for u in range(2)]
        pe_ = lane_steps(nc, "do", "pe", "O OT Y")
        act_ = lane_steps(nc, "do", "act", "O OT")
        dve_ = lane_steps(nc, "do", "dve", "UBD Y")
        bank = [[k.ps[4 * u + n] for n in range(4)] for u in range(2)]
        block = ctx.enter_context(nc.Block("do_b"))

        @block.sync
        def _(sp):
            sp.dma_start(w[:, :, :], k.a["L0_attn_Wo"].rearrange("(c p) n -> p c n", p=P)).then_inc(loaded, 16)
            with sp.Fori(0, T // 2) as i:
                for u in range(2):
                    t = 2 * i + u
                    sp.wait_ge(pe_[u].sem, pe_[u].turns(i))
                    sp.dma_start(pT[u][:, :, :].rearrange("p c n -> p (c n)"),
                                 k.p_scr[bass.ds(t, 1), :, :].rearrange("t p n -> (t p) n")).then_inc(arrived[u], 16)
                    for r in range(2):
                        sp.dma_start(ud[u][64 * r:64 * r + 64, :, :],
                                     k.u_scr[bass.ds(t * P, P), :].rearrange("(b j) n -> j b n", b=2)).then_inc(arrived[u], 16)

        @block.vector
        def _(dve):
            with dve.Fori(0, T // 2) as i:
                for u in range(2):
                    dve.wait_ge(arrived[u], 48 * (i + 1))
                    dve.tensor_tensor(ud[u][:, :, :].rearrange("p b (h d) -> p b h d", d=HD),
                                      ud[u][:, :, :].rearrange("p b (h d) -> p b h d", d=HD),
                                      k.parity[:, :].unsqueeze(1).unsqueeze(3).to_broadcast([P, 2, HEADS, HD]),
                                      ALU.mult).then_inc(dve_[u].sem, 1)
                for u in range(2):
                    xt = k.x[:, bass.ds(2 * i + u, 1), :].rearrange("p t d -> p (t d)")
                    dve.wait_ge(pe_[u].sem, pe_[u].at(i, "Y"))
                    dve.tensor_tensor(xt, xt, bank[u][2][:, 0:D], ALU.add).then_inc(dve_[u].sem, 1)

        @block.tensor
        def _(pe):
            pe.wait_ge(loaded, 16)
            with pe.Fori(0, T // 2) as i:
                for u in range(2):
                    pe.wait_ge(dve_[u].sem, dve_[u].at(i, "UBD"))
                    for c in range(8):
                        mm = pe.matmul(bank[u][0][:, 64 * c:64 * c + 64].rearrange("p (b n) -> p b n", b=2), pT[u][:, c, :],
                                       ud[u][:, :, 32 * c:32 * c + 32], start=True, stop=True)
                    mm.then_inc(pe_[u].sem, 1)
                for u in range(2):
                    pe.wait_ge(act_[u].sem, act_[u].at(i, "O"))
                    for c in range(2):
                        mm = pe.transpose(bank[u][1][:, c * P:(c + 1) * P], o[u][:, c * P:(c + 1) * P], k.ident[:, :])
                    mm.then_inc(pe_[u].sem, 1)
                for u in range(2):
                    pe.wait_ge(act_[u].sem, act_[u].at(i, "OT"))
                    pe.wait_ge(dve_[u].sem, dve_[u].turns(i))
                    for c in range(2):
                        mm = pe.matmul(bank[u][2][:, 0:D], oT[u][:, c, :], w[:, c, :], start=(c == 0), stop=(c == 1))
                    mm.then_inc(pe_[u].sem, 1)

        @block.scalar
        def _(act):
            with act.Fori(0, T // 2) as i:
                for u in range(2):
                    act.wait_ge(pe_[u].sem, pe_[u].at(i, "O"))
                    for b in range(2):
                        r = slice(64 * b, 64 * b + 64)
                        ins = act.copy(o[u][r, :].rearrange("p (c n) -> p c n", c=8),
                                       bank[u][0][r, :].rearrange("p (c b n) -> p c b n", b=2, n=32)[:, :, b, :])
                    ins.then_inc(act_[u].sem, 1)
                for u in range(2):
                    act.wait_ge(pe_[u].sem, pe_[u].at(i, "OT"))
                    act.copy(oT[u][:, :, :], bank[u][1][:, 0:D].rearrange("p (c n) -> p c n", c=2)).then_inc(act_[u].sem, 1)


def row_slice(b):
    return slice(64 * b, 64 * b + 64)


def tile_rows(ap, t):
    at = slice(t, t + 1) if isinstance(t, int) else bass.ds(t, 1)
    return ap[:, at, :].rearrange("p t d -> p (t d)")


def over_heads(ap, n=HEADS):
    return ap.unsqueeze(1).to_broadcast([P, n, S])


def per_head(ap, n=S):
    return ap.unsqueeze(2).to_broadcast([P, HEADS, n])


def spread_keys(eng, out, keys, head_mask):
    for c in range(2):
        ins = eng.tensor_tensor(
            out[:, c, :, :, :],
            keys[:, c, :].rearrange("p (b j) -> p b j", b=2).unsqueeze(2).to_broadcast([P, 2, 8, S]),
            head_mask.unsqueeze(1).unsqueeze(3).to_broadcast([P, 2, 8, S]), ALU.mult)
    return ins


def score_matmuls(pe, banks, queries, keys):
    for b in range(2):
        for c in range(2):
            mm = pe.matmul(banks[c][row_slice(b), :], queries[:, c, row_slice(b)], keys[:, c, b, :, :],
                           start=True, stop=True)
    return mm


def weight_transposes(pe, banks, weights, ident):
    for c in range(8):
        mm = pe.transpose(banks[c // 4][:, (c % 4) * P:(c % 4 + 1) * P], weights[:, c * P:(c + 1) * P], ident)
    return mm


def value_matmuls(pe, bank, weights_t, values):
    for c in range(8):
        mm = pe.matmul(bank[:, 64 * c:64 * c + 64].rearrange("p (b n) -> p b n", b=2), weights_t[:, c, :],
                       values[:, :, 32 * c:32 * c + 32], start=True, stop=True)
    return mm


def own_batch(bank, b):
    return bank[row_slice(b), :].rearrange("p (c b h d) -> p c b h d", b=2, h=2, d=HD)[:, :, b, :, :]


def values_by_parity(eng, out, values, parity):
    return eng.tensor_tensor(out[:, :, :].rearrange("p b (h d) -> p b h d", d=HD), values.rearrange("p b (h d) -> p b h d", d=HD),
                             parity.unsqueeze(1).unsqueeze(3).to_broadcast([P, 2, HEADS, HD]), ALU.mult)


def rope_sums(eng, out, by_cos, by_sin):
    c, s, o = (a.rearrange("p (n f d) -> p n f d", f=2, d=8) for a in (by_cos, by_sin, out))
    eng.tensor_tensor(o[:, :, 0, :], c[:, :, 0, :], s[:, :, 1, :], ALU.subtract)
    return eng.tensor_tensor(o[:, :, 1, :], c[:, :, 1, :], s[:, :, 0, :], ALU.add)


def angles(table):
    return table[:, :].unsqueeze(1).to_broadcast([P, 64, 8])


def by8(ap):
    return ap.rearrange("p (n d) -> p n d", d=8)


def exponentials(act, weights, minus_max, sums):
    for h in range(HEADS):
        here = weights[:, h * S:(h + 1) * S]
        ins = act.activation(here, here, ACT.Exp, bias=minus_max[:, h:h + 1], accum_out=sums[:, h:h + 1])
    return ins


def staggered(eng, tile):
    last = T // 2 - 1
    tile(0, 0, None, (1, 0))
    tile(1, 0, (0, 0), (0, 1))
    with eng.Fori(1, last) as i:
        tile(0, i, (1, i - 1), (1, i))
        tile(1, i, (0, i), (0, i + 1))
    tile(0, last, (1, last - 1), (1, last))
    tile(1, last, (0, last), None)
    return 1, last


def l0_cross(nc, k):
    with ExitStack() as ctx:
        def sb(name, shape, dt=F32):
            return ctx.enter_context(nc.sbuf_tensor("c0" + name, shape, dt))
        xs = [sb(f"xs{u}", [P, D]) for u in range(2)]
        cs = [sb(f"cs{u}", [P, D]) for u in range(2)]
        cT = [sb(f"cT{u}", [P, 2, P]) for u in range(2)]
        sig = [sb(f"sig{u}", [P, 2, 2, D]) for u in range(2)]
        arrived = [nc.alloc_semaphore(f"c0_arrived{u}") for u in range(2)]
        pe_ = lane_steps(nc, "c0", "pe", "S0 S1 O")
        act_ = lane_steps(nc, "c0", "act", "SIG0 SIG1")
        dve_ = lane_steps(nc, "c0", "dve", "X")
        pool_ = lane_steps(nc, "c0", "pool", "XS")
        bank = [[k.ps[4 * u + n] for n in range(4)] for u in range(2)]
        block = ctx.enter_context(nc.Block("c0_b"))

        @block.sync
        def _(sp):
            with sp.Fori(0, T // 2) as i:
                for u in range(2):
                    t = 2 * i + u
                    sp.wait_ge(pe_[u].sem, pe_[u].turns(i))
                    sp.dma_start(cs[u][:, :], k.ctx_rows[bass.ds(t * P, P), :]).then_inc(arrived[u], 16)
                    sp.dma_start(cT[u][:, :, :], k.a["ctxT"].rearrange("(c p) n -> p c n", p=P)[:, :, bass.ds(t * P, P)]).then_inc(arrived[u], 16)

        @block.gpsimd
        def _(pool):
            with pool.Fori(0, T // 2) as i:
                for u in range(2):
                    pool.wait_ge(pe_[u].sem, pe_[u].turns(i))
                    pool.tensor_copy(xs[u][:, :], k.x[:, bass.ds(2 * i + u, 1), :]).then_inc(pool_[u].sem, 1)

        @block.tensor
        def _(pe):
            with pe.Fori(0, T // 2) as i:
                for u in range(2):
                    pe.wait_ge(arrived[u], 32 * (i + 1))
                    pe.wait_ge(pool_[u].sem, pool_[u].at(i, "XS"))
                    for b in range(2):
                        r = slice(64 * b, 64 * b + 64)
                        if b == 0:
                            pe.wait_ge(act_[u].sem, act_[u].turns(i))
                        for c in range(2):
                            mm = pe.matmul(bank[u][b][:, c * D:(c + 1) * D], xs[u][r, c * P:(c + 1) * P], cs[u][r, :],
                                           start=True, stop=True)
                        mm.then_inc(pe_[u].sem, 1)
                for u in range(2):
                    pe.wait_ge(dve_[u].sem, dve_[u].turns(i))
                    for b in range(2):
                        pe.wait_ge(act_[u].sem, act_[u].at(i, f"SIG{b}"))
                        for c in range(2):
                            mm = pe.matmul(bank[u][2][64 * b:64 * b + 64, 0:D], cT[u][:, c, 64 * b:64 * b + 64], sig[u][:, b, c, :],
                                           start=(c == 0), stop=(c == 1))
                    mm.then_inc(pe_[u].sem, 1)

        @block.scalar
        def _(act):
            act.preload_act_table(ACT.Sigmoid)
            with act.Fori(0, T // 2) as i:
                for u in range(2):
                    act.wait_ge(pe_[u].sem, pe_[u].turns(i))
                    for b in range(2):
                        act.wait_ge(pe_[u].sem, pe_[u].at(i, f"S{b}"))
                        act.activation(sig[u][:, b, :, :].rearrange("p c m -> p (c m)"), bank[u][b][:, :], ACT.Sigmoid,
                                       scale=S ** -0.5).then_inc(act_[u].sem, 1)

        @block.vector
        def _(dve):
            with dve.Fori(0, T // 2) as i:
                for u in range(2):
                    xt = k.x[:, bass.ds(2 * i + u, 1), :].rearrange("p t d -> p (t d)")
                    dve.wait_ge(pe_[u].sem, pe_[u].at(i, "O"))
                    dve.tensor_tensor(xt, xt, bank[u][2][:, 0:D], ALU.add).then_inc(dve_[u].sem, 1)


COMB_ROWS = 96


def moe_route(nc, k, name, w, loaded, E, TOP, renorm, times, shared_gate=False, rows=None):
    EC = E + 1 if shared_gate else E
    with ExitStack() as ctx:
        def sb(n, shape, dt=F32):
            return ctx.enter_context(nc.sbuf_tensor(name + n, shape, dt))
        xs = [sb(f"xs{u}", [P, 2, 4 * P]) for u in range(2)]
        pr = [sb(f"pr{u}", [P, 4, EC]) for u in range(2)]
        cb = [sb(f"cb{u}", [P, 4, EC]) for u in range(2)]
        rep = [sb(f"rep{u}", [P, 4, E]) for u in range(2)]
        top = [sb(f"top{u}", [P, 4, 8]) for u in range(2)]
        m4 = [sb(f"m4{u}", [P, 4]) for u in range(2)]
        parts = [sb(f"parts{u}", [P, 4, COMB_ROWS], BF16) for u in range(2)]
        rest = [sb(f"rest{u}", [P, 4, EC]) for u in range(2)]
        identb = sb("identb", [P, P], BF16)
        ready, = semaphores(nc, ctx, name, "ready")
        carrier = sb("carrier", [P, 1])
        pe_ = lane_steps(nc, name, "pe", "LOGITS COMBT")
        act_ = lane_steps(nc, name, "act", "EXP COMBT")
        dve_ = lane_steps(nc, name, "dve", "MAX SUB SUM REC PROBS TOP REST REP COMB" + (" WSUM WREC WNORM" if renorm else "")
                          + (" GATE GATED" if shared_gate else "") + (" ROWS" if rows is not None else "") + " HIGH REST1 MIDDLE REST2 LOW")
        pool_ = lane_steps(nc, name, "pool", "XS")
        bank = [[k.ps[4 * u + n] for n in range(4)] for u in range(2)]
        block = ctx.enter_context(nc.Block(name + "_b"))

        @block.gpsimd
        def _(pool):
            with pool.Fori(0, T // 8) as i:
                for u in range(2):
                    pool.wait_ge(pe_[u].sem, pe_[u].turns(i))
                    pool.tensor_copy(xs[u][:, :, :], k.xT[:, :, bass.ds((2 * i + u) * 4 * P, 4 * P)]).then_inc(pool_[u].sem, 1)

        @block.tensor
        def _(pe):
            pe.wait_ge(loaded, 16)
            pe.wait_ge(ready, 1)
            with pe.Fori(0, T // 8) as i:
                for u in range(2):
                    pe.wait_ge(pool_[u].sem, pool_[u].at(i, "XS"))
                    pe.wait_ge(dve_[u].sem, dve_[u].turns(i))
                    for t in range(4):
                        for c in range(2):
                            mm = pe.matmul(bank[u][0][:, t * EC:(t + 1) * EC], xs[u][:, c, t * P:(t + 1) * P], w[:, c, :],
                                           start=(c == 0), stop=(c == 1))
                    mm.then_inc(pe_[u].sem, 1)
                for u in range(2):
                    pe.wait_ge(dve_[u].sem, dve_[u].turns(i + 1))
                    pe.wait_ge(act_[u].sem, act_[u].turns(i))
                    for t in range(4):
                        mm = pe.transpose(bank[u][1].bitcast(BF16)[0:COMB_ROWS, t * P:(t + 1) * P], parts[u][:, t, :], identb[:, :])
                    mm.then_inc(pe_[u].sem, 1)

        @block.scalar
        def _(act):
            act.preload_act_table(ACT.Exp)
            with act.Fori(0, T // 8) as i:
                for u in range(2):
                    act.wait_ge(dve_[u].sem, dve_[u].at(i, "SUB"))
                    act.activation(pr[u][:, :, :], pr[u][:, :, :], ACT.Exp).then_inc(act_[u].sem, 1)
                for u in range(2):
                    act.wait_ge(pe_[u].sem, pe_[u].at(i, "COMBT"))
                    act.copy(k.combT[:, bass.ds((2 * i + u) * 4 * P, 4 * P)], bank[u][1].bitcast(BF16)[0:COMB_ROWS, 0:4 * P]).then_inc(act_[u].sem, 1)

        @block.vector
        def _(dve):
            dve.tensor_copy(identb[:, :], k.ident[:, :]).then_inc(ready, 1)
            for u in range(2):
                dve.memset(parts[u][:, :, :], 0.0).then_inc(ready, 1)
            dve.wait_ge(ready, 3)
            with dve.Fori(0, T // 8) as i:
                for u in range(2):
                    def wait(step, u=u):
                        dve.wait_ge(dve_[u].sem, dve_[u].at(i, step))

                    lg = bank[u][0][:, 0:4 * EC].rearrange("p (t e) -> p t e", e=EC)
                    probs, comb = pr[u][:, :, 0:E], cb[u][:, :, 0:E]
                    spread = m4[u][:, :].unsqueeze(2).to_broadcast([P, 4, E])
                    dve.wait_ge(pe_[u].sem, pe_[u].at(i, "LOGITS"))
                    dve.tensor_reduce(m4[u][:, :], lg[:, :, 0:E], AX.X, ALU.max).then_inc(dve_[u].sem, 1)
                    wait("MAX")
                    if shared_gate:
                        dve.tensor_scalar(pr[u][:, :, E], lg[:, :, E], -1.0, None, ALU.mult)
                    dve.tensor_tensor(probs, lg[:, :, 0:E], spread, ALU.subtract).then_inc(dve_[u].sem, 1)
                for u in range(2):
                    probs, comb = pr[u][:, :, 0:E], cb[u][:, :, 0:E]
                    spread = m4[u][:, :].unsqueeze(2).to_broadcast([P, 4, E])

                    def wait(step, u=u):
                        dve.wait_ge(dve_[u].sem, dve_[u].at(i, step))

                    dve.wait_ge(act_[u].sem, act_[u].at(i, "EXP"))
                    dve.tensor_reduce(m4[u][:, :], probs, AX.X, ALU.add).then_inc(dve_[u].sem, 1)
                    wait("SUM")
                    dve.reciprocal(m4[u][:, :], m4[u][:, :]).then_inc(dve_[u].sem, 1)
                    wait("REC")
                    dve.tensor_tensor(probs, probs, spread, ALU.mult).then_inc(dve_[u].sem, 1)
                    wait("PROBS")
                    dve.memset(carrier[:, :], 0.0)
                    for t in range(4):
                        ins = dve.max(top[u][:, t, :], pr[u][:, t, 0:E])
                    ins.then_inc(dve_[u].sem, 1)
                    wait("TOP")
                    dve.memset(top[u][:, :, TOP:8], -1.0).then_inc(dve_[u].sem, 1)
                    wait("REST")
                    dve.memset(carrier[:, :], 0.0)
                    for t in range(4):
                        ins = dve.match_replace(out=rep[u][:, t, :], in_to_replace=top[u][:, t, :],
                                                in_values=pr[u][:, t, 0:E], imm_value=0.0)
                    ins.then_inc(dve_[u].sem, 1)
                    wait("REP")
                    dve.tensor_tensor(comb, probs, rep[u][:, :, :], ALU.subtract).then_inc(dve_[u].sem, 1)
                    if renorm:
                        wait("COMB")
                        dve.tensor_reduce(m4[u][:, :], comb, AX.X, ALU.add).then_inc(dve_[u].sem, 1)
                        wait("WSUM")
                        dve.reciprocal(m4[u][:, :], m4[u][:, :]).then_inc(dve_[u].sem, 1)
                        wait("WREC")
                        if times != 1.0:
                            for t in range(4):
                                ins = dve.tensor_scalar(cb[u][:, t, 0:E], cb[u][:, t, 0:E], m4[u][:, t:t + 1], times, ALU.mult, ALU.mult)
                            ins.then_inc(dve_[u].sem, 1)
                        else:
                            dve.tensor_tensor(comb, comb, spread, ALU.mult).then_inc(dve_[u].sem, 1)
                    if rows is not None:
                        wait("WNORM")
                        dve.tensor_copy(rows[:, bass.ds(4 * (2 * i + u), 4), :], comb).then_inc(dve_[u].sem, 1)
                    if shared_gate:
                        wait("WNORM")
                        dve.tensor_scalar(pr[u][:, :, E], pr[u][:, :, E], 1.0, None, ALU.add).then_inc(dve_[u].sem, 1)
                        wait("GATE")
                        dve.reciprocal(cb[u][:, :, E], pr[u][:, :, E]).then_inc(dve_[u].sem, 1)
                    dve.wait_ge(dve_[u].sem, dve_[u].at(i, "HIGH") - 1)
                    high, middle, low = (parts[u][:, :, 32 * n:32 * n + EC] for n in range(3))
                    dve.wait_ge(pe_[u].sem, pe_[u].turns(i))
                    dve.tensor_copy(high, cb[u][:, :, :]).then_inc(dve_[u].sem, 1)
                    wait("HIGH")
                    dve.tensor_tensor(rest[u][:, :, :], cb[u][:, :, :], high, ALU.subtract).then_inc(dve_[u].sem, 1)
                    wait("REST1")
                    dve.tensor_copy(middle, rest[u][:, :, :]).then_inc(dve_[u].sem, 1)
                    wait("MIDDLE")
                    dve.tensor_tensor(rest[u][:, :, :], rest[u][:, :, :], middle, ALU.subtract).then_inc(dve_[u].sem, 1)
                    wait("REST2")
                    dve.tensor_copy(low, rest[u][:, :, :]).then_inc(dve_[u].sem, 1)


class Experts:

    def __init__(self, nc, ctx, k, name, weights, n_exp, n_shared):
        gname, uname, dname, sname = weights
        self.n_exp = n_exp
        self.widths = [P] * n_exp + list(n_shared)
        self.chunks = len(self.widths)
        self.starts = [sum(self.widths[:c]) for c in range(self.chunks)]
        hidden = sum(self.widths)

        def sb(n, shape):
            return ctx.enter_context(nc.sbuf_tensor(name + n, shape, F32))
        self.gate, self.up = sb("wg", [P, 2, hidden]), sb("wu", [P, 2, hidden])
        self.down = sb("wd", [P, self.chunks, D])
        self.sel = sb("sel", [COMB_ROWS, hidden])
        self.selb = ctx.enter_context(nc.sbuf_tensor(name + "selb", [COMB_ROWS, hidden], BF16))
        self.loaded = nc.alloc_semaphore(name + "_loaded")
        halves = "(c p) n -> p c n"
        nc.sync.dma_start(self.gate[:, :, :], k.a[gname].rearrange(halves, p=P)).then_inc(self.loaded, 16)
        nc.sync.dma_start(self.up[:, :, :], k.a[uname].rearrange(halves, p=P)).then_inc(self.loaded, 16)
        self.sel_loaded, self.sel_ready = semaphores(nc, ctx, name, "sel_loaded sel_ready")
        nc.sync.dma_start(self.sel[:, :], k.a[sname]).then_inc(self.sel_loaded, 16)
        full = self.widths.count(P)
        nc.sync.dma_start(self.down[:, 0:full, :], k.a[dname][0:full * P, :].rearrange(halves, p=P)).then_inc(self.loaded, 16)
        for c in range(full, self.chunks):
            rows = slice(self.starts[c], self.starts[c] + self.widths[c])
            nc.sync.dma_start(self.down[0:self.widths[c], c, :], k.a[dname][rows, :]).then_inc(self.loaded, 16)
        self.loads = 16 * (3 + self.chunks - full)


def moe_experts(nc, k, name, experts, shared_by_row, shared_times):
    widths, starts, NC = experts.widths, experts.starts, experts.chunks
    wg, wu, wd, sel = experts.gate, experts.up, experts.down, experts.selb
    scaled = [c < experts.n_exp or shared_by_row for c in range(NC)]
    GT = 4 * P
    with ExitStack() as ctx:
        def sb(n, shape, dt=F32):
            return ctx.enter_context(nc.sbuf_tensor(name + n, shape, dt))
        h = sb("h", [P, NC, GT])
        sg = [sb(f"sg{u}", [P, GT]) for u in range(2)]
        gated, upped, silu_done, product = semaphores(nc, ctx, name, "gated upped silu_done product")
        h_done, down_done, x_added = semaphores(nc, ctx, name, "h_done down_done x_added")
        gbank, ubank, cbank, ybank = k.ps[0:2], k.ps[2:4], k.ps[4:6], k.ps[6:8]
        n_scaled = sum(scaled)
        block = ctx.enter_context(nc.Block(name + "_b"))

        @block.tensor
        def _(pe):
            pe.sem_inc(down_done, 1)
            pe.wait_ge(experts.loaded, experts.loads)
            pe.wait_ge(experts.sel_ready, 1)
            with pe.Fori(0, N // GT) as i:
                xg = [k.xT[:, c, bass.ds(i * GT, GT)] for c in range(2)]
                cg = k.combT[:, bass.ds(i * GT, GT)]
                for c in range(NC):
                    w_, s_, u = widths[c], starts[c], c % 2
                    pe.wait_ge(h_done, NC * i + max(c - 1, 0) + 1)
                    for kk in range(2):
                        mm = pe.matmul(gbank[u][0:w_, :], wg[:, kk, s_:s_ + w_], xg[kk], start=(kk == 0), stop=(kk == 1))
                    mm.then_inc(gated, 1)
                    for kk in range(2):
                        mm = pe.matmul(ubank[u][0:w_, :], wu[:, kk, s_:s_ + w_], xg[kk], start=(kk == 0), stop=(kk == 1))
                    if scaled[c]:
                        mm = pe.matmul(cbank[u][0:w_, :], sel[:, s_:s_ + w_], cg, start=True, stop=True)
                    mm.then_inc(upped, 1)
                for t in range(4):
                    pe.wait_ge(x_added, 4 * i + max(t - 1, 0) + 1)
                    for c in range(NC):
                        if t == 0:
                            pe.wait_ge(h_done, NC * i + c + 2)
                        mm = pe.matmul(ybank[t % 2][:, 0:D], h[0:widths[c], c, t * P:(t + 1) * P], wd[0:widths[c], c, :],
                                       start=(c == 0), stop=(c == NC - 1))
                    mm.then_inc(down_done, 1)

        @block.scalar
        def _(act):
            act.preload_act_table(ACT.Silu)
            act.wait_ge(experts.sel_loaded, 16)
            act.copy(experts.selb[:, :], experts.sel[:, :]).then_inc(experts.sel_ready, 1)
            with act.Fori(0, N // GT) as i:
                for c in range(NC):
                    act.wait_ge(gated, NC * i + c + 1)
                    act.wait_ge(h_done, NC * i + max(c - 1, 0) + 1)
                    act.activation(sg[c % 2][0:widths[c], :], gbank[c % 2][0:widths[c], :], ACT.Silu).then_inc(silu_done, 1)

        @block.vector
        def _(dve):
            dve.sem_inc(h_done, 1)
            dve.sem_inc(x_added, 1)
            with dve.Fori(0, N // GT) as i:
                dve.wait_ge(down_done, 4 * i + 1)
                for c in range(NC):
                    w_, u = widths[c], c % 2
                    dve.wait_ge(silu_done, NC * i + c + 1)
                    dve.wait_ge(upped, NC * i + c + 1)
                    if scaled[c]:
                        dve.tensor_tensor(sg[u][0:w_, :], sg[u][0:w_, :], ubank[u][0:w_, :], ALU.mult).then_inc(product, 1)
                        dve.wait_ge(product, n_scaled * i + sum(scaled[:c]) + 1)
                        dve.tensor_tensor(h[0:w_, c, :], sg[u][0:w_, :], cbank[u][0:w_, :], ALU.mult).then_inc(h_done, 1)
                    else:
                        dve.scalar_tensor_tensor(out=h[0:w_, c, :], in0=sg[u][0:w_, :], scalar=shared_times, in1=ubank[u][0:w_, :],
                                                 op0=ALU.mult, op1=ALU.mult).then_inc(h_done, 1)
                for t in range(4):
                    xt = k.x[:, bass.ds(4 * i + t, 1), :].rearrange("p t d -> p (t d)")
                    dve.wait_ge(down_done, 4 * i + t + 2)
                    dve.tensor_tensor(xt, xt, ybank[t % 2][:, 0:D], ALU.add).then_inc(x_added, 1)


def feed_forward(nc, k, name, router, E, TOP, renorm, times, weights, n_exp, n_shared, shared_gate=False, shared_times=1.0):
    rows = E + 1 if shared_gate else E
    with ExitStack() as ctx:
        k.combT = ctx.enter_context(nc.sbuf_tensor(name + "combT", [COMB_ROWS, N], BF16))
        w = ctx.enter_context(nc.sbuf_tensor(name + "wr", [P, 2, rows], F32))
        loaded, = semaphores(nc, ctx, name, "router_loaded")
        nc.sync.dma_start(w[:, :, :], k.a[router].rearrange("(c p) n -> p c n", p=P)).then_inc(loaded, 16)
        experts = Experts(nc, ctx, k, name, weights, n_exp, n_shared)
        moe_route(nc, k, "r" + name, w, loaded, E, TOP, renorm, times, shared_gate=shared_gate)
        moe_experts(nc, k, name, experts, shared_gate, shared_times)


def l0_ffn(nc, k):
    feed_forward(nc, k, "f0", "L0_router", 8, 2, False, 1.0, ("L0_g", "L0_u", "L0_d", "sel176"), 11, (128, 128, 96))


def l2_ffn(nc, k):
    feed_forward(nc, k, "f2", "L2_router", 8, 2, True, 1.0, ("L2_g", "L2_u", "L2_d", "sel176s"), 11, (128, 128, 96), shared_gate=True)


def l3_ffn(nc, k):
    TOP = 4
    feed_forward(nc, k, "f3", "L3_ffn_w_router", 16, TOP, True, TOP / (TOP + 1), ("L3_g", "L3_u", "L3_d", "sel128"), 16, (128,) * 4,
                 shared_times=1.0 / (TOP + 1))


KT = KEYS // P
QG = 4 * P
STACK = 6 * HD


def l1_attention(nc, k):
    split_to_dram(nc, k)
    with nc.sbuf_tensor("a1o", [P, T, D], F32) as o:
        key_attention(nc, k, o)
        project_add(nc, k, "a1p", o, "L1_Wo")


def split_to_dram(nc, k):
    with ExitStack() as ctx:
        def sb(name, shape, dt=F32):
            return ctx.enter_context(nc.sbuf_tensor("s1" + name, shape, dt))
        CH = 1024
        LANES = range(4)
        w = sb("w", [P, 2, D])
        raw = [sb(f"raw{n}", [P, CH]) for n in LANES]
        part = [[sb(f"part{n}{m}", [P, CH], BF16) for m in range(3)] for n in LANES]
        loaded, = semaphores(nc, ctx, "s1", "loaded")
        arrived = [nc.alloc_semaphore(f"s1_arrived{n}") for n in LANES]
        stored = [nc.alloc_semaphore(f"s1_stored{n}") for n in LANES]
        pe_ = lane_steps(nc, "s1", "pe", "Q", 4)
        act_ = lane_steps(nc, "s1", "act", "HIGH LOW", 4)
        dve_ = lane_steps(nc, "s1", "dve", "REST1 MIDDLE REST2", 4)
        qbank = [k.psum[:, 2 * n:2 * n + 2, :] for n in LANES]
        q = [b.rearrange("p c n -> p (c n)") for b in qbank]
        block = ctx.enter_context(nc.Block("s1_b"))
        NK, NQ = KEYS // CH // 2, N // CH // 2

        def chunk(n, i):
            return bass.ds((2 * i + n // 2) * CH, CH)

        def features(n):
            return slice(n % 2 * P, n % 2 * P + P)

        def store(eng, i, turn, scr):
            for n in LANES:
                for m in range(3):
                    into = scr[m, features(n), chunk(n, i)]
                    eng.wait_ge(act_[n].sem, act_[n].at(turn, "LOW"))
                    eng.dma_start(into, part[n][m][:, :]).then_inc(stored[n], 16)

        @block.sync
        def _(sp):
            sp.dma_start(w[:, :, :], k.a["L1_Wq"].rearrange("(c p) n -> p c n", p=P)).then_inc(loaded, 16)

            def load(n, i):
                sp.dma_start(raw[n][:, :], k.a["L1_kT"][features(n), chunk(n, i)]).then_inc(arrived[n], 16)

            for n in LANES:
                load(n, 0)
            for i in range(NK):
                store(sp, i, i, k.k_scr)
                if i + 1 < NK:
                    for n in LANES:
                        load(n, i + 1)
            for i in range(NQ):
                store(sp, i, i + NK, k.q_scr)
            for n in LANES:
                sp.wait_ge(stored[n], 16 * 3 * (NK + NQ))

        @block.tensor
        def _(pe):
            pe.wait_ge(loaded, 16)
            for i in range(NQ):
                for n in LANES:
                    if i:
                        pe.wait_ge(dve_[n].sem, dve_[n].turns(i + NK))
                    for half in range(2):
                        lo = (2 * i + n // 2) * CH + half * 512
                        for c in range(2):
                            mm = pe.matmul(qbank[n][:, half, :], w[:, c, features(n)], k.xT[:, c, lo:lo + 512],
                                           start=(c == 0), stop=(c == 1))
                    mm.then_inc(pe_[n].sem, 1)

        @block.scalar
        def _(act):
            for i in range(NK + NQ):
                for n in LANES:
                    if i < NK:
                        act.wait_ge(arrived[n], 16 * (i + 1))
                    else:
                        act.wait_ge(pe_[n].sem, pe_[n].at(i - NK, "Q"))
                    if i:
                        act.wait_ge(stored[n], 16 * 3 * i)
                    act.copy(part[n][0][:, :], raw[n][:, :] if i < NK else q[n]).then_inc(act_[n].sem, 1)
                for n in LANES:
                    act.wait_ge(dve_[n].sem, dve_[n].at(i, "REST2"))
                    act.copy(part[n][2][:, :], raw[n][:, :]).then_inc(act_[n].sem, 1)

        @block.vector
        def _(dve):
            for i in range(NK + NQ):
                for n in LANES:
                    dve.wait_ge(act_[n].sem, act_[n].at(i, "HIGH"))
                    dve.tensor_tensor(raw[n][:, :], raw[n][:, :] if i < NK else q[n], part[n][0][:, :], ALU.subtract).then_inc(dve_[n].sem, 1)
                    dve.wait_ge(dve_[n].sem, dve_[n].at(i, "REST1"))
                    dve.tensor_copy(part[n][1][:, :], raw[n][:, :]).then_inc(dve_[n].sem, 1)
                    dve.wait_ge(dve_[n].sem, dve_[n].at(i, "MIDDLE"))
                    dve.tensor_tensor(raw[n][:, :], raw[n][:, :], part[n][1][:, :], ALU.subtract).then_inc(dve_[n].sem, 1)


def key_attention(nc, k, o):
    RING = 4
    AM = 4 * (KEYS // QG)
    LAG = 4
    SUMS_AT, ROWS_AT = 8, 18
    SPLITS = 6
    BODIES = 4 * HEADS
    with ExitStack() as ctx:
        def sb(name, shape, dt=F32):
            return ctx.enter_context(nc.sbuf_tensor("k1" + name, shape, dt))
        identb = sb("identb", [P, P], BF16)
        kst = [sb(f"kst{r}", [STACK + 3, KEYS], BF16) for r in range(RING)]
        qst = [sb(f"qst{r}", [STACK + 3, N], BF16) for r in range(RING)]
        v = sb("v", [P, KT, D])
        vst = [sb(f"vst{u}", [P, KT, 32]) for u in range(2)]
        ex = [sb(f"ex{m}", [P, QG]) for m in range(8)]
        osb = sb("osb", [P, QG])
        pm = sb("pm", [P, 4, KEYS // QG])
        nm = sb("nm", [P, 4])
        rest = sb("rest", [P, 4])
        nm3 = sb("nm3", [P, 4, 3], BF16)
        rec = sb("rec", [P, 4])
        v_loaded, ready, valued, released = semaphores(nc, ctx, "k1", "v_loaded ready valued released")
        stacked = [nc.alloc_semaphore(f"k1_stacked{r}") for r in range(RING)]
        scored, exped, attended, a_scored, a_reduced, reciprocal = semaphores(
            nc, ctx, "k1", "scored exped attended a_scored a_reduced reciprocal")
        o_copied, summed, normed, split, rows_scored, rows_copied = semaphores(
            nc, ctx, "k1", "o_copied summed normed split rows_scored rows_copied")
        abank, sbank = k.ps[0:3], k.ps[3:6]
        obank, mbank = k.ps[6], k.ps[7]
        LOADS = 12 * 16
        EX, SB, AB = 8, 3, 3

        def bank_free(n, a):
            return KT * n + a + (2 if a < KT % 3 else 1)

        block = ctx.enter_context(nc.Block("k1_b"))

        def all_heads(eng, head):
            head(0, 0, True, False)
            with eng.Fori(0, HEADS // RING - 1) as i:
                for u in range(1, RING + 1):
                    head(RING * i + u, u % RING, False, False)
            for h in range(HEADS - RING + 1, HEADS):
                head(h, h % RING, False, h == HEADS - 1)

        def bodies(eng, h, body):
            body(4 * h, 0)
            with eng.Fori(1, 4) as qg:
                body(4 * h + qg, qg)

        def heads_attended(heads):
            return 4 * KT * heads + EX

        def opening(qg):
            return isinstance(qg, int)

        @block.sync
        def _(sp):
            sp.dma_start(v[:, :, :], k.a["L1_v"].rearrange("(t p) d -> p t d", p=P)).then_inc(v_loaded, 16)

            def load(r, h):
                parts = ((0, 0), (1, 0), (2, 0), (0, 1), (1, 1), (0, 2))
                here = slice(h * HD, h * HD + HD) if isinstance(h, int) else bass.ds(h * HD, HD)
                for row, (k_part, q_part) in enumerate(parts):
                    at = slice(HD * row, HD * row + HD)
                    sp.dma_start(kst[r][at, :], k.k_scr[k_part, here, :]).then_inc(stacked[r], 16)
                    sp.dma_start(qst[r][at, :], k.q_scr[q_part, here, :]).then_inc(stacked[r], 16)

            for h in range(RING):
                load(h, h)
            with sp.Fori(0, HEADS // RING - 1) as i:
                for u in range(1, RING + 1):
                    sp.wait_ge(attended, heads_attended(RING * i + u))
                    sp.sem_inc(released, 1)
                    load((u + 3) % RING, RING * i + u + 3)

        @block.gpsimd
        def _(pool):
            for u in range(2):
                pool.memset(vst[u][:, :, HD:HD + 1], 1.0)
                pool.memset(vst[u][:, :, HD + 1:32], 0.0)
            pool.wait_ge(v_loaded, 16)
            for h in range(2):
                pool.tensor_copy(vst[h][:, :, 0:HD], v[:, :, h * HD:(h + 1) * HD]).then_inc(valued, 1)
            with pool.Fori(1, HEADS // 2) as i:
                for u in range(2):
                    h = 2 * i + u
                    pool.wait_ge(attended, heads_attended(h - 1))
                    pool.tensor_copy(vst[u][:, :, 0:HD], v[:, :, bass.ds(h * HD, HD)]).then_inc(valued, 1)

        @block.tensor
        def _(pe):
            pe.sem_inc(attended, EX)
            pe.sem_inc(summed, 1)
            pe.sem_inc(rows_scored, 1)
            pe.wait_ge(ready, 2)

            def maximum_product(r, qg, n, a):
                tile, group = divmod(a, KEYS // QG)
                pe.wait_ge(a_reduced, bank_free(n, a))
                pe.matmul(abank[a % 3], qst[r][0:STACK, bass.ds(qg * QG + tile * P, P)], kst[r][0:STACK, group * QG:(group + 1) * QG],
                          start=True, stop=True).then_inc(a_scored, 1)

            def maximum_rows(n):
                pe.wait_ge(split, SPLITS * (n + 1) + 1)
                for tile in range(4):
                    mm = pe.matmul(mbank[STACK:STACK + 3, tile * P:(tile + 1) * P], nm3[:, tile, :], identb[:, :], start=True, stop=True)
                mm.then_inc(rows_scored, 1)

            def attend(u, n, p):
                pe.wait_ge(exped, KT * n + p + 1 + SB)
                strip = slice(32 * (p % 4), 32 * (p % 4) + 32)
                pe.matmul(obank[strip, :], vst[u % 2][:, p, :], ex[p % EX][:, :],
                          start=(p < 4), stop=(p >= KT - 4)).then_inc(attended, 1)

            def sums(n):
                pe.wait_ge(o_copied, n + 2)
                for tile in range(4):
                    mm = pe.matmul(mbank[:, tile * 17:tile * 17 + 17], osb[:, tile * P:(tile + 1) * P], k.strip_sum[:, :],
                                   start=True, stop=True)
                mm.then_inc(summed, 1)

            pe.wait_ge(stacked[0], LOADS)
            with pe.Fori(0, 4) as qg:
                for a in range(AM):
                    maximum_product(0, qg, qg, a)
                pe.wait_ge(rows_copied, qg + 1)
                maximum_rows(qg)

            def head(h, u, first, last):
                nxt = (u + 1) % RING

                def body(n, qg):
                    started = first and opening(qg)
                    ending = (u - 1) % RING if opening(qg) else u
                    for p in range(KT):
                        if p == SUMS_AT and not started:
                            if last and not opening(qg):
                                pe.wait_ge(normed, n)
                                pe.wait_ge(rows_copied, BODIES + 1)
                            else:
                                pe.wait_ge(rows_copied, n + 4)
                            sums(n - 1)
                        if p == ROWS_AT and not started and not (last and not opening(qg)):
                            pe.wait_ge(normed, n + 1)
                            maximum_rows(n + 3)
                        if p == 0:
                            pe.wait_ge(rows_copied, n + 2)
                        pe.wait_ge(exped, bank_free(n, p))
                        pe.matmul(sbank[p % 3], kst[u][:, p * P:(p + 1) * P], qst[u][:, bass.ds(qg * QG, QG)],
                                  start=True, stop=True).then_inc(scored, 1)
                        if not last:
                            if p == 0 and opening(qg):
                                pe.wait_ge(stacked[nxt], LOADS * ((h + 1 - nxt) // RING + 1) if isinstance(h, int)
                                           else turn_loads(h, u))
                            maximum_product(nxt, qg, n + 4, p)
                        if p >= LAG:
                            if p == LAG:
                                if opening(qg):
                                    pe.wait_ge(valued, h + 1)
                                pe.wait_ge(o_copied, n + 1)
                            attend(u, n, p - LAG)
                        elif not started:
                            attend(ending, n - 1, KT - LAG + p)

                bodies(pe, h, body)

            def turn_loads(h, u):
                following = u + 1 if u else RING + 1
                return (h - (u or RING)) // RING * LOADS + LOADS * (1 + following // RING)

            all_heads(pe, head)
            last = (HEADS - 1) % RING
            for p in range(KT - LAG, KT):
                attend(last, BODIES - 1, p)
            pe.wait_ge(normed, BODIES)
            sums(BODIES - 1)

        @block.scalar
        def _(act):
            act.preload_act_table(ACT.Exp)
            act.sem_inc(exped, SB)
            act.sem_inc(o_copied, 1)
            act.sem_inc(rows_copied, 1)

            def rows(r, qg, n):
                act.wait_ge(rows_scored, n + 2)
                act.copy(qst[r][STACK:STACK + 3, bass.ds(qg * QG, QG)], mbank[STACK:STACK + 3, :]).then_inc(rows_copied, 1)

            def strips(n):
                act.wait_ge(attended, KT * (n + 1) + EX)
                act.wait_ge(summed, n + 1)
                act.copy(osb[:, :], obank).then_inc(o_copied, 1)

            with act.Fori(0, 4) as qg:
                rows(0, qg, qg)

            def head(h, u, first, last):
                def body(n, qg):
                    started = first and opening(qg)
                    for p in range(KT):
                        if p == LAG and not started:
                            strips(n - 1)
                        if p == ROWS_AT + 1 and not started:
                            if opening(qg):
                                rows(u, 3, n + 3)
                            elif not last:
                                rows((u + 1) % RING, qg - 1, n + 3)
                        act.wait_ge(scored, KT * n + p + 1)
                        act.wait_ge(attended, KT * n + p + 1)
                        act.activation(ex[p % EX][:, :], sbank[p % 3], ACT.Exp, scale=HD ** -0.5).then_inc(exped, 1)

                bodies(act, h, body)

            all_heads(act, head)
            strips(BODIES - 1)

        @block.vector
        def _(dve):
            dve.tensor_copy(identb[:, :], k.ident[:, :]).then_inc(ready, 1)
            for r in range(RING):
                ins = dve.memset(kst[r][STACK:STACK + 3, :], 1.0)
            ins.then_inc(ready, 1)
            dve.sem_inc(a_reduced, AB)
            dve.sem_inc(normed, 1)
            dve.sem_inc(split, 1)

            def reduce(n, a):
                tile, group = divmod(a, KEYS // QG)
                if a == 0:
                    dve.wait_ge(split, SPLITS * n + 1)
                dve.wait_ge(a_scored, AM * n + a + 1)
                dve.tensor_reduce(pm[:, tile, group:group + 1], abank[a % 3], AX.X, ALU.max).then_inc(a_reduced, 1)

            def split_maxima(n):
                dve.wait_ge(a_reduced, AM * (n + 1) + AB)
                dve.tensor_reduce(nm[:, :], pm[:, :, :], AX.X, ALU.max, negate=True).then_inc(split, 1)
                dve.wait_ge(rows_scored, n + 1)
                dve.wait_ge(split, SPLITS * n + 2)
                dve.tensor_copy(nm3[:, :, 0], nm[:, :]).then_inc(split, 1)
                dve.wait_ge(split, SPLITS * n + 3)
                dve.tensor_tensor(rest[:, :], nm[:, :], nm3[:, :, 0], ALU.subtract).then_inc(split, 1)
                dve.wait_ge(split, SPLITS * n + 4)
                dve.tensor_copy(nm3[:, :, 1], rest[:, :]).then_inc(split, 1)
                dve.wait_ge(split, SPLITS * n + 5)
                dve.tensor_tensor(rest[:, :], rest[:, :], nm3[:, :, 1], ALU.subtract).then_inc(split, 1)
                dve.wait_ge(split, SPLITS * n + 6)
                dve.tensor_copy(nm3[:, :, 2], rest[:, :]).then_inc(split, 1)

            def divide(n, h, quarter):
                sums = mbank[:, 0:68].rearrange("p (t d) -> p t d", d=17)
                dve.wait_ge(summed, n + 2)
                dve.wait_ge(normed, n + 1)
                dve.reciprocal(rec[:, :], sums[:, :, HD]).then_inc(reciprocal, 1)
                dve.wait_ge(reciprocal, n + 1)
                dve.tensor_tensor(o[:, bass.ds(4 * quarter, 4), bass.ds(h * HD, HD)], sums[:, :, 0:HD],
                                  rec[:, :].unsqueeze(2).to_broadcast([P, 4, HD]), ALU.mult).then_inc(normed, 1)

            with dve.Fori(0, 4) as qg:
                for a in range(AM):
                    reduce(qg, a)
                split_maxima(qg)

            def head(h, u, first, last):
                def body(n, qg):
                    divide_at = SUMS_AT + 2
                    for a in range(AM):
                        if a == divide_at and not (first and opening(qg)):
                            divide(n - 1, h - 1 if opening(qg) else h, 3 if opening(qg) else qg - 1)
                        if not last:
                            reduce(n + 4, a)
                    if not last:
                        split_maxima(n + 4)

                bodies(dve, h, body)

            all_heads(dve, head)
            divide(BODIES - 1, HEADS - 1, 3)


def project_add(nc, k, name, o, weight):
    with ExitStack() as ctx:
        def sb(n, shape, dt=F32):
            return ctx.enter_context(nc.sbuf_tensor(name + n, shape, dt))
        w = sb("w", [P, 2, D])
        os = [sb(f"os{u}", [P, D]) for u in range(2)]
        oT = [sb(f"oT{u}", [P, 2, P]) for u in range(2)]
        loaded, = semaphores(nc, ctx, name, "loaded")
        pe_ = lane_steps(nc, name, "pe", "OT Y")
        act_ = lane_steps(nc, name, "act", "OT")
        dve_ = lane_steps(nc, name, "dve", "PICK X")
        bank = [[k.ps[4 * u + n] for n in range(4)] for u in range(2)]
        block = ctx.enter_context(nc.Block(name + "_b"))

        @block.sync
        def _(sp):
            sp.dma_start(w[:, :, :], k.a[weight].rearrange("(c p) n -> p c n", p=P)).then_inc(loaded, 16)

        @block.tensor
        def _(pe):
            pe.wait_ge(loaded, 16)
            with pe.Fori(0, T // 2) as i:
                for u in range(2):
                    pe.wait_ge(dve_[u].sem, dve_[u].at(i, "PICK"))
                    for c in range(2):
                        mm = pe.transpose(bank[u][0][:, c * P:(c + 1) * P], os[u][:, c * P:(c + 1) * P], k.ident[:, :])
                    mm.then_inc(pe_[u].sem, 1)
                for u in range(2):
                    pe.wait_ge(act_[u].sem, act_[u].at(i, "OT"))
                    for c in range(2):
                        mm = pe.matmul(bank[u][1][:, 0:D], oT[u][:, c, :], w[:, c, :], start=(c == 0), stop=(c == 1))
                    mm.then_inc(pe_[u].sem, 1)

        @block.scalar
        def _(act):
            with act.Fori(0, T // 2) as i:
                for u in range(2):
                    act.wait_ge(pe_[u].sem, pe_[u].at(i, "OT"))
                    act.copy(oT[u][:, :, :], bank[u][0][:, 0:D].rearrange("p (c n) -> p c n", c=2)).then_inc(act_[u].sem, 1)

        @block.vector
        def _(dve):
            with dve.Fori(0, T // 2) as i:
                for u in range(2):
                    dve.tensor_copy(os[u][:, :], tile_rows(o, 2 * i + u)).then_inc(dve_[u].sem, 1)
                for u in range(2):
                    xt = tile_rows(k.x, 2 * i + u)
                    dve.wait_ge(pe_[u].sem, pe_[u].at(i, "Y"))
                    dve.tensor_tensor(xt, xt, bank[u][1][:, 0:D], ALU.add).then_inc(dve_[u].sem, 1)


def l1_cross(nc, k):
    with ExitStack() as outer:
        def sb(name, shape):
            return outer.enter_context(nc.sbuf_tensor("m1" + name, shape, F32))
        cum = sb("cum", [P, T, HEADS])
        inp = sb("inp", [P, T, HEADS])
        centred = sb("centred", [P, T, D])
        var = sb("var", [P, T, HEADS])
        mlstm_gates(nc, k, cum, inp)
        mlstm_attention(nc, k, cum, inp, centred, var)
        mlstm_output(nc, k, centred, var)


def mlstm_gates(nc, k, cum, inp):
    with ExitStack() as ctx:
        def sb(name, shape, dt=F32):
            return ctx.enter_context(nc.sbuf_tensor("mg" + name, shape, dt))
        LANES = 4
        w = sb("w", [P, 6, 32])
        bias = sb("bias", [P, 32])
        xs = [sb(f"xs{u}", [P, 2, P]) for u in range(LANES)]
        cT = [sb(f"cT{u}", [P, 2, P]) for u in range(LANES)]
        gates = sb("gates", [P, T, 32])
        fg = sb("fg", [P, T, HEADS])
        low = sb("low", [P, T, HEADS])
        big = sb("big", [P, T, HEADS])
        loaded, gated, biased, logs, summed, dn = semaphores(nc, ctx, "mg", "loaded gated biased logs summed vec")
        arrived = [nc.alloc_semaphore(f"mg_arrived{u}") for u in range(LANES)]
        copied, = semaphores(nc, ctx, "mg", "copied")
        block = ctx.enter_context(nc.Block("mg_b"))

        @block.sync
        def _(sp):
            sp.dma_start(w[:, :, :], k.a["L1_gates"].rearrange("(c p) n -> p c n", p=P)).then_inc(loaded, 16)
            sp.dma_start(bias[:, :], k.a["L1_gates_b"].partition_broadcast(P)).then_inc(loaded, 16)
            with sp.Fori(0, T // LANES) as i:
                for u in range(LANES):
                    sp.wait_ge(gated, LANES * i + 1)
                    sp.dma_start(cT[u][:, :, :], k.a["ctxT"].rearrange("(c p) n -> p c n", p=P)[:, :, bass.ds((LANES * i + u) * P, P)]).then_inc(arrived[u], 16)

        @block.gpsimd
        def _(pool):
            with pool.Fori(0, T // LANES) as i:
                for u in range(LANES):
                    pool.wait_ge(gated, LANES * i + 1)
                    pool.tensor_copy(xs[u][:, :, :], k.xT[:, :, bass.ds((LANES * i + u) * P, P)]).then_inc(copied, 1)

        @block.tensor
        def _(pe):
            pe.sem_inc(gated, 1)
            pe.wait_ge(loaded, 32)
            with pe.Fori(0, T // LANES) as i:
                for u in range(LANES):
                    pe.wait_ge(arrived[u], 16 * (i + 1))
                    pe.wait_ge(copied, LANES * i + u + 1)
                    pe.wait_ge(biased, LANES * i + 1)
                    for c in range(6):
                        lhs = xs[u] if c < 2 else cT[u]
                        mm = pe.matmul(k.ps[u][:, 0:32], lhs[:, c % 2, :], w[:, c, :], start=(c == 0), stop=(c == 5))
                    mm.then_inc(gated, 1)
            pe.wait_ge(dn, 5)
            pe.matmul(k.ps[LANES][:, 0:D], k.cumulate[:, :], low[:, :, :].rearrange("p t h -> p (t h)"),
                      start=True, stop=True).then_inc(summed, 1)

        @block.scalar
        def _(act):
            act.preload_act_table_set("natural_log_exp_and_others")
            act.wait_ge(dn, 3)
            act.activation(big[:, :, :], big[:, :, :], ACT.Exp, scale=-1.0).then_inc(logs, 1)
            act.wait_ge(logs, 1)
            act.activation(big[:, :, :], big[:, :, :], ACT.Ln, bias=1.0).then_inc(logs, 1)

        @block.vector
        def _(dve):
            dve.sem_inc(biased, 1)
            with dve.Fori(0, T // LANES) as i:
                for u in range(LANES):
                    dve.wait_ge(gated, LANES * i + u + 2)
                    dve.tensor_tensor(tile_rows(gates, LANES * i + u), k.ps[u][:, 0:32], bias[:, :], ALU.add).then_inc(biased, 1)
            dve.wait_ge(biased, T + 1)
            dve.tensor_copy(fg[:, :, :], gates[:, :, HEADS:32]).then_inc(dn, 1)
            dve.wait_ge(dn, 1)
            dve.tensor_scalar(low[:, :, :], fg[:, :, :], 0.0, None, ALU.min).then_inc(dn, 1)
            dve.scalar_tensor_tensor(out=big[:, :, :], in0=fg[:, :, :], scalar=-1.0, in1=fg[:, :, :], op0=ALU.mult, op1=ALU.max).then_inc(dn, 1)
            dve.wait_ge(logs, 2)
            dve.tensor_tensor(low[:, :, :], low[:, :, :], big[:, :, :], ALU.subtract).then_inc(dn, 1)
            dve.wait_ge(dn, 4)
            dve.sem_inc(dn, 1)
            dve.wait_ge(summed, 1)
            dve.tensor_copy(cum[:, :, :].rearrange("p t h -> p (t h)"), k.ps[LANES][:, 0:D]).then_inc(dn, 1)
            dve.wait_ge(dn, 6)
            dve.tensor_tensor(inp[:, :, :], gates[:, :, 0:HEADS], cum[:, :, :], ALU.subtract).then_inc(dn, 1)


def mlstm_attention(nc, k, cum, inp, centred, var):
    with ExitStack() as ctx:
        def sb(name, shape, dt=F32):
            return ctx.enter_context(nc.sbuf_tensor("ma" + name, shape, dt))
        xs = [sb(f"xs{u}", [P, 2, P]) for u in range(2)]
        cT = [sb(f"cT{u}", [P, 2, P]) for u in range(2)]
        vs = [sb(f"vs{u}", [P, 2, D]) for u in range(2)]
        vd = [sb(f"vd{u}", [P, 2, D]) for u in range(2)]
        kexp = [sb(f"kexp{u}", [P, 2, 2, 8, S]) for u in range(2)]
        diag = [sb(f"diag{u}", [P, HEADS * S]) for u in range(2)]
        sc = [sb(f"sc{u}", [P, HEADS * S]) for u in range(2)]
        pT = [sb(f"pT{u}", [P, 8, P]) for u in range(2)]
        hd = [sb(f"hd{u}", [P, D]) for u in range(2)]
        m = [sb(f"m{u}", [P, 6, HEADS]) for u in range(2)]
        MAX, SUM, CUMMAX, FLOOR, NORM, MEAN = range(6)
        arrived = [nc.alloc_semaphore(f"ma_arrived{u}") for u in range(2)]
        pe_ = lane_steps(nc, "ma", "pe", "DECAY SCORES PT O")
        act_ = lane_steps(nc, "ma", "act", "EXP FLOOR PT")
        dve_ = lane_steps(nc, "ma", "dve", "DIAG KEXP VBD MASK MAX SUB CUMMAX C SUM ABS NORM EPS REC O MEAN MEAN16 CENTRE SQ VAR")
        pool_ = lane_steps(nc, "ma", "pool", "XS")
        bank = [[k.ps[4 * u + n] for n in range(4)] for u in range(2)]
        block = ctx.enter_context(nc.Block("ma_b"))

        @block.sync
        def _(sp):
            def tile(u, i, before, after):
                t = 2 * i + u
                rows = slice(t * P, t * P + P) if isinstance(t, int) else bass.ds(t * P, P)
                if not isinstance(i, int) or i:
                    sp.wait_ge(dve_[u].sem, dve_[u].at(i - 1, "VBD"))
                sp.dma_start(cT[u][:, :, :], k.a["ctxT"].rearrange("(c p) n -> p c n", p=P)[:, :, rows]).then_inc(arrived[u], 16)
                for r in range(2):
                    sp.dma_start(vs[u][row_slice(r), :, :], k.ctx_rows[rows, :].rearrange("(b j) n -> j b n", b=2)).then_inc(arrived[u], 16)

            staggered(sp, tile)

        @block.gpsimd
        def _(pool):
            def tile(u, i, before, after):
                t = 2 * i + u
                rows = slice(t * P, t * P + P) if isinstance(t, int) else bass.ds(t * P, P)
                if not isinstance(i, int) or i:
                    pool.wait_ge(pe_[u].sem, pe_[u].at(i - 1, "SCORES"))
                pool.tensor_copy(xs[u][:, :, :], k.xT[:, :, rows]).then_inc(pool_[u].sem, 1)

            staggered(pool, tile)

        @block.tensor
        def _(pe):
            def finish(u, i):
                pe.wait_ge(dve_[u].sem, dve_[u].at(i, "C"))
                weight_transposes(pe, bank[u][0:2], sc[u], k.ident[:, :]).then_inc(pe_[u].sem, 1)
                pe.wait_ge(act_[u].sem, act_[u].at(i, "PT"))
                value_matmuls(pe, bank[u][2], pT[u], vd[u]).then_inc(pe_[u].sem, 1)

            def tile(u, i, before, after):
                pe.wait_ge(dve_[u].sem, dve_[u].at(i, "DIAG"))
                for c in range(2):
                    mm = pe.matmul(bank[u][c], k.ones64[:, :], diag[u][:, c * 512:(c + 1) * 512], start=True, stop=True)
                mm.then_inc(pe_[u].sem, 1)
                pe.wait_ge(dve_[u].sem, dve_[u].at(i, "KEXP"))
                pe.wait_ge(pool_[u].sem, pool_[u].at(i, "XS"))
                score_matmuls(pe, bank[u][2:4], xs[u], kexp[u]).then_inc(pe_[u].sem, 1)
                if before:
                    finish(*before)

            finish(*staggered(pe, tile))

        @block.scalar
        def _(act):
            act.preload_act_table(ACT.Exp)

            def weights_out(u, i):
                act.wait_ge(pe_[u].sem, pe_[u].at(i, "PT"))
                act.copy(pT[u][:, 0:4, :], bank[u][0].rearrange("p (c n) -> p c n", c=4))
                act.copy(pT[u][:, 4:8, :], bank[u][1].rearrange("p (c n) -> p c n", c=4)).then_inc(act_[u].sem, 1)

            def tile(u, i, before, after):
                if before:
                    weights_out(*before)
                act.wait_ge(dve_[u].sem, dve_[u].at(i, "SUB"))
                act.activation(sc[u][:, :], sc[u][:, :], ACT.Exp).then_inc(act_[u].sem, 1)
                act.wait_ge(dve_[u].sem, dve_[u].at(i, "CUMMAX"))
                act.activation(m[u][:, FLOOR, :], m[u][:, CUMMAX, :], ACT.Exp, scale=-1.0).then_inc(act_[u].sem, 1)

            weights_out(*staggered(act, tile))

        @block.vector
        def _(dve):
            def wait(u, i, step):
                dve.wait_ge(dve_[u].sem, dve_[u].at(i, step))

            def spread(u, i):
                t = 2 * i + u
                dve.wait_ge(dve_[u].sem, dve_[u].turns(i))
                dve.tensor_tensor(heads3(diag[u][:, :]), per_head(tile_rows(inp, t)), over_heads(k.eye64[:, :]), ALU.mult).then_inc(dve_[u].sem, 1)
                dve.wait_ge(arrived[u], 48 * (i + 1))
                spread_keys(dve, kexp[u], cT[u], k.head_mask[:, :]).then_inc(dve_[u].sem, 1)
                values_by_parity(dve, vd[u], vs[u][:, :, :], k.parity[:, :]).then_inc(dve_[u].sem, 1)

            def decays(u, i):
                t = 2 * i + u
                dve.wait_ge(pe_[u].sem, pe_[u].at(i, "DECAY"))
                for c in range(2):
                    ins = dve.tensor_tensor(heads3(sc[u][:, c * 512:(c + 1) * 512]), heads3(bank[u][c]),
                                            over_heads(k.causal[:, :], 8), ALU.add)
                ins.then_inc(dve_[u].sem, 1)
                wait(u, i, "MASK")
                dve.tensor_reduce(m[u][:, MAX, :], heads3(sc[u][:, :]), AX.X, ALU.max).then_inc(dve_[u].sem, 1)
                wait(u, i, "MAX")
                dve.tensor_tensor(heads3(sc[u][:, :]), heads3(sc[u][:, :]), per_head(m[u][:, MAX, :]), ALU.subtract).then_inc(dve_[u].sem, 1)
                dve.tensor_tensor(m[u][:, CUMMAX, :], m[u][:, MAX, :], tile_rows(cum, t), ALU.add).then_inc(dve_[u].sem, 1)

            def weights(u, i):
                dve.wait_ge(pe_[u].sem, pe_[u].at(i, "SCORES"))
                dve.wait_ge(act_[u].sem, act_[u].at(i, "EXP"))
                for c in range(2):
                    half = sc[u][:, c * 512:(c + 1) * 512]
                    ins = dve.scalar_tensor_tensor(out=half, in0=bank[u][2 + c], scalar=HD ** -0.5, in1=half,
                                                   op0=ALU.mult, op1=ALU.mult)
                ins.then_inc(dve_[u].sem, 1)
                wait(u, i, "C")
                dve.tensor_reduce(m[u][:, SUM, :], heads3(sc[u][:, :]), AX.X, ALU.add).then_inc(dve_[u].sem, 1)
                wait(u, i, "SUM")
                dve.scalar_tensor_tensor(out=m[u][:, NORM, :], in0=m[u][:, SUM, :], scalar=-1.0, in1=m[u][:, SUM, :],
                                         op0=ALU.mult, op1=ALU.max).then_inc(dve_[u].sem, 1)
                wait(u, i, "ABS")
                dve.wait_ge(act_[u].sem, act_[u].at(i, "FLOOR"))
                dve.tensor_tensor(m[u][:, NORM, :], m[u][:, NORM, :], m[u][:, FLOOR, :], ALU.max).then_inc(dve_[u].sem, 1)
                wait(u, i, "NORM")
                dve.tensor_scalar(m[u][:, NORM, :], m[u][:, NORM, :], 1e-6, None, ALU.add).then_inc(dve_[u].sem, 1)
                wait(u, i, "EPS")
                dve.reciprocal(m[u][:, NORM, :], m[u][:, NORM, :]).then_inc(dve_[u].sem, 1)

            def outputs(u, i):
                t = 2 * i + u
                h3 = hd[u][:, :].rearrange("p (h d) -> p h d", d=HD)
                ctile = tile_rows(centred, t).rearrange("p (h d) -> p h d", d=HD)
                wait(u, i, "REC")
                dve.wait_ge(pe_[u].sem, pe_[u].at(i, "O"))
                for b in range(2):
                    r = row_slice(b)
                    ins = dve.tensor_tensor(hd[u][r, :].rearrange("p (c h d) -> p c h d", h=2, d=HD), own_batch(bank[u][2], b),
                                            m[u][r, NORM, :].rearrange("p (c h) -> p c h", h=2).unsqueeze(3).to_broadcast([64, 8, 2, HD]),
                                            ALU.mult)
                ins.then_inc(dve_[u].sem, 1)
                wait(u, i, "O")
                dve.tensor_reduce(m[u][:, MEAN, :], h3, AX.X, ALU.add).then_inc(dve_[u].sem, 1)
                wait(u, i, "MEAN")
                dve.tensor_scalar(m[u][:, MEAN, :], m[u][:, MEAN, :], 1.0 / HD, None, ALU.mult).then_inc(dve_[u].sem, 1)
                wait(u, i, "MEAN16")
                dve.tensor_tensor(h3, h3, per_head(m[u][:, MEAN, :], HD), ALU.subtract).then_inc(dve_[u].sem, 1)
                wait(u, i, "CENTRE")
                dve.tensor_copy(ctile, h3)
                dve.tensor_tensor(diag[u][:, 0:D], hd[u][:, :], hd[u][:, :], ALU.mult).then_inc(dve_[u].sem, 1)
                wait(u, i, "SQ")
                dve.tensor_reduce(tile_rows(var, t), diag[u][:, 0:D].rearrange("p (h d) -> p h d", d=HD), AX.X, ALU.add).then_inc(dve_[u].sem, 1)

            def tile(u, i, before, after):
                spread(u, i)
                if before:
                    weights(*before)
                decays(u, i)
                if before:
                    outputs(*before)

            end = staggered(dve, tile)
            weights(*end)
            outputs(*end)


def mlstm_output(nc, k, centred, var):
    with ExitStack() as ctx:
        scale = ctx.enter_context(nc.sbuf_tensor("mo_scale", [P, D], F32))
        loaded, vec, rooted = semaphores(nc, ctx, "mo", "loaded vec rooted")
        chain = [nc.alloc_semaphore(f"mo_chain{u}") for u in range(2)]
        block = ctx.enter_context(nc.Block("mo_b"))

        @block.sync
        def _(sp):
            sp.dma_start(scale[:, :], k.a["L1_xattn_ln_scale"].partition_broadcast(P)).then_inc(loaded, 16)

        @block.scalar
        def _(act):
            act.wait_ge(vec, 1)
            act.activation(var[:, :, :], var[:, :, :], ACT.Sqrt).then_inc(rooted, 1)

        @block.vector
        def _(dve):
            dve.tensor_scalar(var[:, :, :], var[:, :, :], 1.0 / HD, 1e-6, ALU.mult, ALU.add).then_inc(vec, 1)
            dve.wait_ge(vec, 1)
            dve.wait_ge(rooted, 1)
            dve.reciprocal(var[:, :, :], var[:, :, :]).then_inc(vec, 1)
            dve.wait_ge(vec, 2)
            dve.wait_ge(loaded, 16)
            with dve.Fori(0, T // 2) as i:
                for u in range(2):
                    c = tile_rows(centred, 2 * i + u)
                    c3 = c.rearrange("p (h d) -> p h d", d=HD)
                    dve.tensor_tensor(c3, c3, var[:, bass.ds(2 * i + u, 1), :].rearrange("p t h -> p (t h)").unsqueeze(2).to_broadcast([P, HEADS, HD]),
                                      ALU.mult).then_inc(chain[u], 1)
                for u in range(2):
                    c = tile_rows(centred, 2 * i + u)
                    dve.wait_ge(chain[u], 3 * i + 1)
                    dve.tensor_tensor(c, c, scale[:, :], ALU.mult).then_inc(chain[u], 1)
                for u in range(2):
                    c, xt = tile_rows(centred, 2 * i + u), tile_rows(k.x, 2 * i + u)
                    dve.wait_ge(chain[u], 3 * i + 2)
                    dve.tensor_tensor(xt, xt, c, ALU.add).then_inc(chain[u], 1)


def l1_ffn(nc, k):
    with ExitStack() as outer:
        k.combT = outer.enter_context(nc.sbuf_tensor("f1combT", [COMB_ROWS, N], BF16))
        gates = outer.enter_context(nc.sbuf_tensor("f1gates", [P, T, 8], F32))
        w = outer.enter_context(nc.sbuf_tensor("f1wr", [P, 2, 8], F32))
        loaded, = semaphores(nc, outer, "f1", "router_loaded")
        nc.sync.dma_start(w[:, :, :], k.a["L1_wr"].rearrange("(c p) n -> p c n", p=P)).then_inc(loaded, 16)
        moe_route(nc, k, "r1", w, loaded, 8, 2, True, 1.0, rows=gates)
        l1_ffn_scatter(nc, k, gates)


def l1_ffn_scatter(nc, k, gates):
    GT, E = 4 * P, 8
    with ExitStack() as ctx:
        def sb(name, shape, dt=F32):
            return ctx.enter_context(nc.sbuf_tensor("f1" + name, shape, dt))
        w1, w3, w2 = (sb(n, [P, 2, D]) for n in ("w1", "w3", "w2"))
        h1 = sb("h1", [P, 2, GT])
        h2 = sb("h2", [P, 4, D])
        gs = sb("gs", [P, 4, E])
        acc = sb("acc", [E, D])
        accT = sb("accT", [P, 2, E])
        loaded, picked, cleared, first, second, summed, act1, act2, added, turned, copied, projected, final = semaphores(
            nc, ctx, "f1", "loaded picked cleared first second summed act1 act2 added turned copied projected final")
        block = ctx.enter_context(nc.Block("f1_b"))

        @block.sync
        def _(sp):
            for t, n in ((w1, "L1_w1"), (w3, "L1_w3"), (w2, "L1_w2")):
                sp.dma_start(t[:, :, :], k.a[n].rearrange("(c p) n -> p c n", p=P)).then_inc(loaded, 16)

        @block.gpsimd
        def _(pool):
            with pool.Fori(0, N // GT) as i:
                pool.wait_ge(summed, i)
                pool.tensor_copy(gs[:, :, :], gates[:, bass.ds(4 * i, 4), :]).then_inc(picked, 1)

        @block.tensor
        def _(pe):
            pe.wait_ge(loaded, 48)
            with pe.Fori(0, N // GT) as i:
                pe.wait_ge(act1, 2 * i)
                for m in range(2):
                    for c in range(2):
                        mm = pe.matmul(k.ps[m], w1[:, c, m * P:(m + 1) * P], k.xT[:, c, bass.ds(i * GT, GT)],
                                       start=(c == 0), stop=(c == 1))
                    mm.then_inc(first, 1)
                pe.wait_ge(act1, 2 * i + 2)
                pe.wait_ge(act2, 2 * i)
                for t in range(4):
                    for c in range(2):
                        mm = pe.matmul(k.ps[2 + t // 2][:, (t % 2) * D:(t % 2 + 1) * D], h1[:, c, t * P:(t + 1) * P], w3[:, c, :],
                                       start=(c == 0), stop=(c == 1))
                    mm.then_inc(second, 1)
                pe.wait_ge(act2, 2 * i + 2)
                pe.wait_ge(picked, i + 1)
                pe.wait_ge(added, i)
                for t in range(4):
                    mm = pe.matmul(k.ps[4][0:E, 0:D], gs[:, t, :], h2[:, t, :], start=(t == 0), stop=(t == 3))
                mm.then_inc(summed, 1)
            pe.wait_ge(added, N // GT)
            for c in range(2):
                mm = pe.transpose(k.ps[5][:, c * E:(c + 1) * E], acc[:, c * P:(c + 1) * P], k.ident[0:E, 0:E])
            mm.then_inc(turned, 1)
            pe.wait_ge(copied, 1)
            for c in range(2):
                mm = pe.matmul(k.ps[6][0:E, 0:D], accT[:, c, :], w2[:, c, :], start=(c == 0), stop=(c == 1))
            mm.then_inc(projected, 1)

        @block.scalar
        def _(act):
            act.preload_act_table(ACT.Silu)
            with act.Fori(0, N // GT) as i:
                act.wait_ge(second, 4 * i)
                for m in range(2):
                    act.wait_ge(first, 2 * i + m + 1)
                    act.activation(h1[:, m, :], k.ps[m], ACT.Silu).then_inc(act1, 1)
                act.wait_ge(summed, i)
                for m in range(2):
                    act.wait_ge(second, 4 * i + 2 * m + 2)
                    act.activation(h2[:, 2 * m:2 * m + 2, :].rearrange("p t d -> p (t d)"), k.ps[2 + m], ACT.Silu).then_inc(act2, 1)
            act.wait_ge(turned, 1)
            act.copy(accT[:, :, :], k.ps[5][:, 0:2 * E].rearrange("p (c e) -> p c e", c=2)).then_inc(copied, 1)

        @block.vector
        def _(dve):
            dve.memset(acc[:, :], 0.0).then_inc(cleared, 1)
            dve.wait_ge(cleared, 1)
            with dve.Fori(0, N // GT) as i:
                dve.wait_ge(added, i)
                dve.wait_ge(summed, i + 1)
                dve.tensor_tensor(acc[:, :], acc[:, :], k.ps[4][0:E, 0:D], ALU.add).then_inc(added, 1)
            dve.wait_ge(projected, 1)
            dve.tensor_tensor(k.x[0:E, 0, :], k.x[0:E, 0, :], k.ps[6][0:E, 0:D], ALU.add).then_inc(final, 1)


MAGIC = 1.5 * 2.0 ** 23


def l2_attention(nc, k):
    with ExitStack() as outer:
        def sb(name, shape, dt=F32):
            return outer.enter_context(nc.sbuf_tensor("b2" + name, shape, dt))
        wq = {n: sb("q_" + n, [P, c, m], BF16) for n, (c, m) in BIT_WEIGHTS.items()}
        wm = {n: sb("m_" + n, [P, 1]) for n in BIT_WEIGHTS}
        x1 = sb("x1", [P, T, D])
        bit_weights(nc, k, wq, wm)
        rs = sb("rs", [P, T])
        rms_scales(nc, k, "b2n1", k.x, rs)
        bit_attention(nc, k, wq, wm, x1, rs)
        rms_scales(nc, k, "b2n2", x1, rs)
        bit_mlp(nc, k, wq, wm, x1, rs)


BIT_WEIGHTS = {"qkv": (2, 768), "o": (2, 256), "down": (4, 256)}


def bit_weights(nc, k, wq, wm):
    with ExitStack() as ctx:
        def sb(name, shape, dt=F32):
            return ctx.enter_context(nc.sbuf_tensor("bw" + name, shape, dt))
        raw = {n: sb("raw_" + n, [P, c, m]) for n, (c, m) in BIT_WEIGHTS.items()}
        part = {n: sb("part_" + n, [P, 1]) for n in BIT_WEIGHTS}
        inv = {n: sb("inv_" + n, [P, 1]) for n in BIT_WEIGHTS}
        loaded, summed, spread, vec = semaphores(nc, ctx, "bw", "loaded summed spread vec")
        block = ctx.enter_context(nc.Block("bw_b"))

        @block.sync
        def _(sp):
            for n in BIT_WEIGHTS:
                sp.dma_start(raw[n][:, :, :], k.a["L2_" + n].rearrange("(c p) n -> p c n", p=P)).then_inc(loaded, 16)

        @block.tensor
        def _(pe):
            for j, n in enumerate(BIT_WEIGHTS):
                pe.wait_ge(summed, j + 1)
                pe.matmul(k.ps[j][:, 0:1], k.ones[:, :], part[n][:, :], start=True, stop=True).then_inc(spread, 1)

        @block.vector
        def _(dve):
            count = [0]

            def link(ins):
                count[0] += 1
                ins.then_inc(vec, 1)
                dve.wait_ge(vec, count[0])

            dve.wait_ge(loaded, 48)
            for n in BIT_WEIGHTS:
                dve.tensor_reduce(part[n][:, :], raw[n][:, :, :].rearrange("p c n -> p (c n)"), AX.X, ALU.add,
                                  apply_absolute_value=True).then_inc(summed, 1)
            for j, (n, (c, m)) in enumerate(BIT_WEIGHTS.items()):
                flat = raw[n][:, :, :].rearrange("p c n -> p (c n)")
                dve.wait_ge(spread, j + 1)
                link(dve.tensor_scalar(wm[n][:, :], k.ps[j][:, 0:1], 1.0 / (c * P * m), 1e-5, ALU.mult, ALU.max))
                link(dve.reciprocal(inv[n][:, :], wm[n][:, :]))
                link(dve.tensor_scalar(flat, flat, inv[n][:, :], MAGIC, ALU.mult, ALU.add))
                link(dve.tensor_scalar(flat, flat, -MAGIC, -1.0, ALU.add, ALU.max))
                link(dve.tensor_scalar(wq[n][:, :, :].rearrange("p c n -> p (c n)"), flat, 1.0, None, ALU.min))


def rms_scales(nc, k, name, x, rs):
    with ExitStack() as ctx:
        junk = [ctx.enter_context(nc.sbuf_tensor(f"{name}junk{u}", [P, D], F32)) for u in range(2)]
        squared, vec, scaled = semaphores(nc, ctx, name, "squared vec scaled")
        block = ctx.enter_context(nc.Block(name + "_b"))

        @block.scalar
        def _(act):
            act.preload_act_table(ACT.Square)
            with act.Fori(0, T // 2) as i:
                for u in range(2):
                    act.wait_ge(squared, 2 * i)
                    act.activation(junk[u][:, :], tile_rows(x, 2 * i + u), ACT.Square,
                                   accum_out=rs[:, bass.ds(2 * i + u, 1)]).then_inc(squared, 1)

        @block.vector
        def _(dve):
            dve.wait_ge(squared, T)
            dve.tensor_scalar(rs[:, :], rs[:, :], 1.0 / D, 1e-5, ALU.mult, ALU.add).then_inc(vec, 1)

        @block.gpsimd
        def _(pool):
            pool.wait_ge(vec, 1)
            pool.tensor_tensor(rs[:, :], rs[:, :], k.minus_half[:, 0:T], ALU.pow).then_inc(scaled, 1)


QUANT = "AMAX CLAMP REC SCALE ROUND INT DEQ"


def quantise(dve, done, wait, tag, row, width, q, rounded, ints, wscale):
    done(dve.tensor_reduce(q[:, 0:1], row, AX.X, ALU.max, apply_absolute_value=True), tag + "AMAX")
    wait(tag + "AMAX")
    done(dve.tensor_scalar(q[:, 0:1], q[:, 0:1], 1e-5, None, ALU.max), tag + "CLAMP")
    wait(tag + "CLAMP")
    done(dve.reciprocal(q[:, 1:2], q[:, 0:1]), tag + "REC")
    wait(tag + "REC")
    done(dve.tensor_scalar(q[:, 2:3], q[:, 1:2], 127.0, None, ALU.mult), tag + "SCALE")
    wait(tag + "SCALE")
    done(dve.tensor_scalar(rounded, row, q[:, 2:3], MAGIC, ALU.mult, ALU.add), tag + "ROUND")
    wait(tag + "ROUND")
    done(dve.tensor_scalar(ints, rounded, -MAGIC, None, ALU.add), tag + "INT")
    done(dve.tensor_scalar(q[:, 3:4], q[:, 0:1], wscale[:, :], 1.0 / 127.0, ALU.mult, ALU.mult), tag + "DEQ")


def tagged(tag):
    return " ".join(tag + n for n in QUANT.split())


def bit_attention(nc, k, wq, wm, x1, rs):
    with ExitStack() as ctx:
        def sb(name, shape, dt=F32):
            return ctx.enter_context(nc.sbuf_tensor("ba" + name, shape, dt))
        norm_w = sb("norm_w", [P, D])
        identb = sb("identb", [P, P], BF16)
        h = [sb(f"h{u}", [P, D]) for u in range(2)]
        hr = [sb(f"hr{u}", [P, D]) for u in range(2)]
        hi = [sb(f"hi{u}", [P, D], BF16) for u in range(2)]
        hiT = [sb(f"hiT{u}", [P, 2, P], BF16) for u in range(2)]
        qa = [sb(f"qa{u}", [P, 4]) for u in range(2)]
        qo = [sb(f"qo{u}", [P, 4]) for u in range(2)]
        t1 = [sb(f"t1{u}", [P, 512]) for u in range(2)]
        t2 = [sb(f"t2{u}", [P, 512]) for u in range(2)]
        qk = [sb(f"qk{u}", [P, 512]) for u in range(2)]
        v = [sb(f"v{u}", [P, D]) for u in range(2)]
        vd = [sb(f"vd{u}", [P, 2, D]) for u in range(2)]
        qkT = [sb(f"qkT{u}", [P, 4, P]) for u in range(2)]
        kexp = [sb(f"kexp{u}", [P, 2, 2, 8, S]) for u in range(2)]
        sc = [sb(f"sc{u}", [P, HEADS * S]) for u in range(2)]
        pT = [sb(f"pT{u}", [P, 8, P]) for u in range(2)]
        mx = [sb(f"mx{u}", [P, HEADS]) for u in range(2)]
        den = [sb(f"den{u}", [P, HEADS]) for u in range(2)]
        loaded, ready = semaphores(nc, ctx, "ba", "loaded ready")
        pe_ = lane_steps(nc, "ba", "pe", "HT QKV TURNED SCORES PT O OT Y")
        act_ = lane_steps(nc, "ba", "act", "HT V QKT EXP PT OT")
        dve_ = lane_steps(nc, "ba", "dve", "H " + tagged("H") + " COS SIN ROPED VBD KEXP MASK MAX SUB SUM REC O "
                          + tagged("O") + " X1")
        bank = [[k.ps[4 * u + n] for n in range(4)] for u in range(2)]
        block = ctx.enter_context(nc.Block("ba_b"))

        @block.sync
        def _(sp):
            sp.dma_start(norm_w[:, :], k.a["L2_norm1"].partition_broadcast(P)).then_inc(loaded, 16)

        @block.tensor
        def _(pe):
            pe.wait_ge(ready, 1)
            with pe.Fori(0, T // 2) as i:
                for u in range(2):
                    pe.wait_ge(dve_[u].sem, dve_[u].at(i, "HINT"))
                    turned = bank[u][0].bitcast(BF16)
                    for c in range(2):
                        mm = pe.transpose(turned[:, c * P:(c + 1) * P], hi[u][:, c * P:(c + 1) * P], identb[:, :])
                    mm.then_inc(pe_[u].sem, 1)
                for u in range(2):
                    pe.wait_ge(act_[u].sem, act_[u].at(i, "HT"))
                    for o, lo, hi_ in ((bank[u][0], 0, 512), (bank[u][1][:, 0:D], 512, 768)):
                        for c in range(2):
                            mm = pe.matmul(o, hiT[u][:, c, :], wq["qkv"][:, c, lo:hi_], start=(c == 0), stop=(c == 1))
                    mm.then_inc(pe_[u].sem, 1)
                for u in range(2):
                    pe.wait_ge(dve_[u].sem, dve_[u].at(i, "ROPED"))
                    pe.wait_ge(act_[u].sem, act_[u].at(i, "V"))
                    for c in range(4):
                        pe.transpose(bank[u][2][:, c * P:(c + 1) * P], qk[u][:, c * P:(c + 1) * P], k.ident[:, :])
                    for b in range(2):
                        mm = pe.matmul(bank[u][3][:, b * D:(b + 1) * D], k.dup[:, b * P:(b + 1) * P], v[u][:, :], start=True, stop=True)
                    mm.then_inc(pe_[u].sem, 1)
                for u in range(2):
                    pe.wait_ge(dve_[u].sem, dve_[u].at(i, "KEXP"))
                    score_matmuls(pe, bank[u][0:2], qkT[u], kexp[u]).then_inc(pe_[u].sem, 1)
                for u in range(2):
                    pe.wait_ge(act_[u].sem, act_[u].at(i, "EXP"))
                    weight_transposes(pe, bank[u][2:4], sc[u], k.ident[:, :]).then_inc(pe_[u].sem, 1)
                for u in range(2):
                    pe.wait_ge(act_[u].sem, act_[u].at(i, "PT"))
                    value_matmuls(pe, bank[u][0], pT[u], vd[u]).then_inc(pe_[u].sem, 1)
                for u in range(2):
                    pe.wait_ge(dve_[u].sem, dve_[u].at(i, "OINT"))
                    turned = bank[u][1].bitcast(BF16)
                    for c in range(2):
                        mm = pe.transpose(turned[:, c * P:(c + 1) * P], hi[u][:, c * P:(c + 1) * P], identb[:, :])
                    mm.then_inc(pe_[u].sem, 1)
                for u in range(2):
                    pe.wait_ge(act_[u].sem, act_[u].at(i, "OT"))
                    for c in range(2):
                        mm = pe.matmul(bank[u][2][:, 0:D], hiT[u][:, c, :], wq["o"][:, c, :], start=(c == 0), stop=(c == 1))
                    mm.then_inc(pe_[u].sem, 1)

        @block.scalar
        def _(act):
            act.preload_act_table(ACT.Exp)

            with act.Fori(0, T // 2) as i:
                for u in range(2):
                    act.wait_ge(pe_[u].sem, pe_[u].at(i, "HT"))
                    act.copy(hiT[u][:, :, :], bank[u][0].bitcast(BF16)[:, 0:D].rearrange("p (c n) -> p c n", c=2)).then_inc(act_[u].sem, 1)
                for u in range(2):
                    act.wait_ge(pe_[u].sem, pe_[u].at(i, "QKV"))
                    act.wait_ge(dve_[u].sem, dve_[u].at(i, "HDEQ"))
                    act.activation(v[u][:, :], bank[u][1][:, 0:D], ACT.Copy, scale=qa[u][:, 3:4]).then_inc(act_[u].sem, 1)
                for u in range(2):
                    act.wait_ge(pe_[u].sem, pe_[u].at(i, "TURNED"))
                    act.copy(qkT[u][:, :, :], bank[u][2].rearrange("p (c n) -> p c n", c=4)).then_inc(act_[u].sem, 1)
                for u in range(2):
                    act.wait_ge(dve_[u].sem, dve_[u].at(i, "SUB"))
                    act.activation(sc[u][:, :], sc[u][:, :], ACT.Exp).then_inc(act_[u].sem, 1)
                for u in range(2):
                    act.wait_ge(pe_[u].sem, pe_[u].at(i, "PT"))
                    act.copy(pT[u][:, 0:4, :], bank[u][2].rearrange("p (c n) -> p c n", c=4))
                    act.copy(pT[u][:, 4:8, :], bank[u][3].rearrange("p (c n) -> p c n", c=4)).then_inc(act_[u].sem, 1)
                for u in range(2):
                    act.wait_ge(pe_[u].sem, pe_[u].at(i, "OT"))
                    act.copy(hiT[u][:, :, :], bank[u][1].bitcast(BF16)[:, 0:D].rearrange("p (c n) -> p c n", c=2)).then_inc(act_[u].sem, 1)

        @block.vector
        def _(dve):
            dve.tensor_copy(identb[:, :], k.ident[:, :]).then_inc(ready, 1)
            dve.wait_ge(loaded, 16)
            with dve.Fori(0, T // 2) as i:
                def done(ins, step, u):
                    ins.then_inc(dve_[u].sem, 1)

                def wait(step, u):
                    dve.wait_ge(dve_[u].sem, dve_[u].at(i, step))

                for u in range(2):
                    t = 2 * i + u
                    dve.scalar_tensor_tensor(out=h[u][:, :], in0=tile_rows(k.x, t), scalar=rs[:, bass.ds(t, 1)], in1=norm_w[:, :],
                                             op0=ALU.mult, op1=ALU.mult).then_inc(dve_[u].sem, 1)
                    wait("H", u)
                    quantise(dve, lambda ins, s, u=u: done(ins, s, u), lambda s, u=u: wait(s, u), "H", h[u][:, :], D,
                             qa[u], hr[u][:, :], hi[u][:, :], wm["qkv"])
                for u in range(2):
                    dve.wait_ge(pe_[u].sem, pe_[u].at(i, "QKV"))
                    wait("HDEQ", u)
                    for o, table in ((t1, k.cos), (t2, k.sin)):
                        dve.scalar_tensor_tensor(out=by8(o[u][:, :]), in0=by8(bank[u][0]), scalar=qa[u][:, 3:4], in1=angles(table),
                                                 op0=ALU.mult, op1=ALU.mult).then_inc(dve_[u].sem, 1)
                    wait("SIN", u)
                    rope_sums(dve, qk[u][:, :], t1[u][:, :], t2[u][:, :]).then_inc(dve_[u].sem, 1)
                for u in range(2):
                    dve.wait_ge(pe_[u].sem, pe_[u].at(i, "TURNED"))
                    values_by_parity(dve, vd[u], bank[u][3].rearrange("p (b n) -> p b n", b=2), k.parity[:, :]).then_inc(dve_[u].sem, 1)
                    dve.wait_ge(act_[u].sem, act_[u].at(i, "QKT"))
                    spread_keys(dve, kexp[u], qkT[u][:, 2:4, :], k.head_mask[:, :]).then_inc(dve_[u].sem, 1)
                for u in range(2):
                    dve.wait_ge(pe_[u].sem, pe_[u].at(i, "SCORES"))
                    for c in range(2):
                        ins = dve.scalar_tensor_tensor(out=heads3(sc[u][:, c * 512:(c + 1) * 512]), in0=heads3(bank[u][c]),
                                                       scalar=HD ** -0.5, in1=over_heads(k.block_causal[:, :], 8), op0=ALU.mult, op1=ALU.add)
                    ins.then_inc(dve_[u].sem, 1)
                    wait("MASK", u)
                    dve.tensor_reduce(mx[u][:, :], heads3(sc[u][:, :]), AX.X, ALU.max).then_inc(dve_[u].sem, 1)
                    wait("MAX", u)
                    dve.tensor_tensor(heads3(sc[u][:, :]), heads3(sc[u][:, :]), per_head(mx[u][:, :]), ALU.subtract).then_inc(dve_[u].sem, 1)
                for u in range(2):
                    dve.wait_ge(act_[u].sem, act_[u].at(i, "EXP"))
                    dve.tensor_reduce(den[u][:, :], heads3(sc[u][:, :]), AX.X, ALU.add).then_inc(dve_[u].sem, 1)
                    wait("SUM", u)
                    dve.reciprocal(den[u][:, :], den[u][:, :]).then_inc(dve_[u].sem, 1)
                for u in range(2):
                    dve.wait_ge(pe_[u].sem, pe_[u].at(i, "O"))
                    wait("REC", u)
                    for b in range(2):
                        r = row_slice(b)
                        ins = dve.tensor_tensor(h[u][r, :].rearrange("p (c h d) -> p c h d", h=2, d=HD), own_batch(bank[u][0], b),
                                                den[u][r, :].rearrange("p (c h) -> p c h", h=2).unsqueeze(3).to_broadcast([64, 8, 2, HD]),
                                                ALU.mult)
                    ins.then_inc(dve_[u].sem, 1)
                    wait("O", u)
                    quantise(dve, lambda ins, s, u=u: done(ins, s, u), lambda s, u=u: wait(s, u), "O", h[u][:, :], D,
                             qo[u], hr[u][:, :], hi[u][:, :], wm["o"])
                for u in range(2):
                    t = 2 * i + u
                    dve.wait_ge(pe_[u].sem, pe_[u].at(i, "Y"))
                    wait("ODEQ", u)
                    dve.scalar_tensor_tensor(out=tile_rows(x1, t), in0=bank[u][2][:, 0:D], scalar=qo[u][:, 3:4], in1=tile_rows(k.x, t),
                                             op0=ALU.mult, op1=ALU.add).then_inc(dve_[u].sem, 1)


def bit_mlp(nc, k, wq, wm, x1, rs):
    with ExitStack() as ctx:
        def sb(name, shape, dt=F32):
            return ctx.enter_context(nc.sbuf_tensor("bm" + name, shape, dt))
        norm_w = sb("norm_w", [P, D])
        identb = sb("identb", [P, P], BF16)
        up = sb("up", [P, 2, 1024])
        h = [sb(f"h{u}", [P, D]) for u in range(2)]
        hT = [sb(f"hT{u}", [P, 2, P]) for u in range(2)]
        sg = [sb(f"sg{u}", [P, 512]) for u in range(2)]
        gv = [sb(f"gv{u}", [P, 512]) for u in range(2)]
        gi = [sb(f"gi{u}", [P, 512], BF16) for u in range(2)]
        giT = [sb(f"giT{u}", [P, 4, P], BF16) for u in range(2)]
        qa = [sb(f"qa{u}", [P, 4]) for u in range(2)]
        loaded, ready = semaphores(nc, ctx, "bm", "loaded ready")
        pe_ = lane_steps(nc, "bm", "pe", "HT GATE VAL GT Y")
        act_ = lane_steps(nc, "bm", "act", "HT SILU GT")
        dve_ = lane_steps(nc, "bm", "dve", "H X GV " + tagged("G") + " Y")
        bank = [[k.ps[4 * u + n] for n in range(4)] for u in range(2)]
        block = ctx.enter_context(nc.Block("bm_b"))

        @block.sync
        def _(sp):
            sp.dma_start(norm_w[:, :], k.a["L2_norm2"].partition_broadcast(P)).then_inc(loaded, 16)
            sp.dma_start(up[:, :, :], k.a["L2_up"].rearrange("(c p) n -> p c n", p=P)).then_inc(loaded, 16)

        @block.tensor
        def _(pe):
            pe.wait_ge(loaded, 32)
            pe.wait_ge(ready, 1)
            with pe.Fori(0, T // 2) as i:
                for u in range(2):
                    pe.wait_ge(dve_[u].sem, dve_[u].at(i, "H"))
                    for c in range(2):
                        mm = pe.transpose(bank[u][0][:, c * P:(c + 1) * P], h[u][:, c * P:(c + 1) * P], k.ident[:, :])
                    mm.then_inc(pe_[u].sem, 1)
                for u in range(2):
                    pe.wait_ge(act_[u].sem, act_[u].at(i, "HT"))
                    for half in range(2):
                        for c in range(2):
                            mm = pe.matmul(bank[u][1 + half], hT[u][:, c, :], up[:, c, half * 512:(half + 1) * 512],
                                           start=(c == 0), stop=(c == 1))
                        mm.then_inc(pe_[u].sem, 1)
                for u in range(2):
                    pe.wait_ge(dve_[u].sem, dve_[u].at(i, "GINT"))
                    turned = bank[u][3].bitcast(BF16)
                    for c in range(4):
                        mm = pe.transpose(turned[:, c * P:(c + 1) * P], gi[u][:, c * P:(c + 1) * P], identb[:, :])
                    mm.then_inc(pe_[u].sem, 1)
                for u in range(2):
                    pe.wait_ge(act_[u].sem, act_[u].at(i, "GT"))
                    for c in range(4):
                        mm = pe.matmul(bank[u][0][:, 0:D], giT[u][:, c, :], wq["down"][:, c, :], start=(c == 0), stop=(c == 3))
                    mm.then_inc(pe_[u].sem, 1)

        @block.scalar
        def _(act):
            act.preload_act_table(ACT.Silu)
            with act.Fori(0, T // 2) as i:
                for u in range(2):
                    act.wait_ge(pe_[u].sem, pe_[u].at(i, "HT"))
                    act.copy(hT[u][:, :, :], bank[u][0][:, 0:D].rearrange("p (c n) -> p c n", c=2)).then_inc(act_[u].sem, 1)
                for u in range(2):
                    act.wait_ge(pe_[u].sem, pe_[u].at(i, "GATE"))
                    act.activation(sg[u][:, :], bank[u][1], ACT.Silu).then_inc(act_[u].sem, 1)
                for u in range(2):
                    act.wait_ge(pe_[u].sem, pe_[u].at(i, "GT"))
                    act.copy(giT[u][:, :, :], bank[u][3].bitcast(BF16)[:, 0:512].rearrange("p (c n) -> p c n", c=4)).then_inc(act_[u].sem, 1)

        @block.vector
        def _(dve):
            dve.tensor_copy(identb[:, :], k.ident[:, :]).then_inc(ready, 1)
            dve.wait_ge(loaded, 32)
            with dve.Fori(0, T // 2) as i:
                def done(ins, step, u):
                    ins.then_inc(dve_[u].sem, 1)

                def wait(step, u):
                    dve.wait_ge(dve_[u].sem, dve_[u].at(i, step))

                for u in range(2):
                    t = 2 * i + u
                    dve.scalar_tensor_tensor(out=h[u][:, :], in0=tile_rows(x1, t), scalar=rs[:, bass.ds(t, 1)], in1=norm_w[:, :],
                                             op0=ALU.mult, op1=ALU.mult).then_inc(dve_[u].sem, 1)
                    dve.tensor_tensor(tile_rows(k.x, t), tile_rows(k.x, t), tile_rows(x1, t), ALU.add).then_inc(dve_[u].sem, 1)
                for u in range(2):
                    dve.wait_ge(pe_[u].sem, pe_[u].at(i, "VAL"))
                    dve.wait_ge(act_[u].sem, act_[u].at(i, "SILU"))
                    dve.tensor_tensor(gv[u][:, :], sg[u][:, :], bank[u][2], ALU.mult).then_inc(dve_[u].sem, 1)
                    wait("GV", u)
                    quantise(dve, lambda ins, s, u=u: done(ins, s, u), lambda s, u=u: wait(s, u), "G", gv[u][:, :], 512,
                             qa[u], sg[u][:, :], gi[u][:, :], wm["down"])
                for u in range(2):
                    t = 2 * i + u
                    dve.wait_ge(pe_[u].sem, pe_[u].at(i, "Y"))
                    wait("GDEQ", u)
                    dve.scalar_tensor_tensor(out=tile_rows(k.x, t), in0=bank[u][0][:, 0:D], scalar=qa[u][:, 3:4], in1=tile_rows(k.x, t),
                                             op0=ALU.mult, op1=ALU.add).then_inc(dve_[u].sem, 1)


def l2_cross(nc, k):
    with ExitStack() as outer:
        xn = outer.enter_context(nc.sbuf_tensor("c2xn", [P, T, D], F32))
        cn = outer.enter_context(nc.sbuf_tensor("c2cn", [P, T, D], F32))
        cosine_norms(nc, k, xn, cn)
        cosine_attention(nc, k, xn, cn)


def cosine_norms(nc, k, xn, cn):
    with ExitStack() as ctx:
        def sb(name, shape, dt=F32):
            return ctx.enter_context(nc.sbuf_tensor("cn" + name, shape, dt))
        cs = [sb(f"cs{u}", [P, D]) for u in range(2)]
        sq = [sb(f"sq{u}", [P, 512]) for u in range(2)]
        nrm = [sb(f"nrm{u}", [P, 512]) for u in range(2)]
        arrived = [nc.alloc_semaphore(f"cn_arrived{u}") for u in range(2)]
        pe_ = lane_steps(nc, "cn", "pe", "SUMS")
        act_ = lane_steps(nc, "cn", "act", "SQRT")
        dve_ = lane_steps(nc, "cn", "dve", "SQ MAX REC")
        pool_ = lane_steps(nc, "cn", "pool", "XN CN")
        block = ctx.enter_context(nc.Block("cn_b"))

        @block.sync
        def _(sp):
            with sp.Fori(0, T // 2) as i:
                for u in range(2):
                    sp.wait_ge(pool_[u].sem, pool_[u].turns(i))
                    sp.dma_start(cs[u][:, :], k.ctx_rows[bass.ds((2 * i + u) * P, P), :]).then_inc(arrived[u], 16)

        @block.tensor
        def _(pe):
            with pe.Fori(0, T // 2) as i:
                for u in range(2):
                    pe.wait_ge(dve_[u].sem, dve_[u].at(i, "SQ"))
                    pe.matmul(k.ps[u], k.ones8[:, :], sq[u][:, :], start=True, stop=True).then_inc(pe_[u].sem, 1)

        @block.scalar
        def _(act):
            act.preload_act_table(ACT.Sqrt)
            with act.Fori(0, T // 2) as i:
                for u in range(2):
                    act.wait_ge(pe_[u].sem, pe_[u].at(i, "SUMS"))
                    act.activation(nrm[u][:, :], k.ps[u], ACT.Sqrt).then_inc(act_[u].sem, 1)

        @block.vector
        def _(dve):
            with dve.Fori(0, T // 2) as i:
                for u in range(2):
                    xt = k.x[:, bass.ds(2 * i + u, 1), :].rearrange("p t d -> p (t d)")
                    dve.wait_ge(arrived[u], 16 * (i + 1))
                    dve.tensor_tensor(sq[u][:, 0:D], xt, xt, ALU.mult)
                    dve.tensor_tensor(sq[u][:, D:2 * D], cs[u][:, :], cs[u][:, :], ALU.mult).then_inc(dve_[u].sem, 1)
                for u in range(2):
                    dve.wait_ge(act_[u].sem, act_[u].at(i, "SQRT"))
                    dve.tensor_scalar(nrm[u][:, :], nrm[u][:, :], 1e-12, None, ALU.max).then_inc(dve_[u].sem, 1)
                    dve.wait_ge(dve_[u].sem, dve_[u].at(i, "MAX"))
                    dve.reciprocal(nrm[u][:, :], nrm[u][:, :]).then_inc(dve_[u].sem, 1)

        @block.gpsimd
        def _(pool):
            with pool.Fori(0, T // 2) as i:
                for u in range(2):
                    t = bass.ds(2 * i + u, 1)
                    flat = "p t d -> p (t d)"
                    pool.wait_ge(dve_[u].sem, dve_[u].at(i, "REC"))
                    pool.tensor_tensor(xn[:, t, :].rearrange(flat), k.x[:, t, :].rearrange(flat), nrm[u][:, 0:D], ALU.mult).then_inc(pool_[u].sem, 1)
                    pool.tensor_tensor(cn[:, t, :].rearrange(flat), cs[u][:, :], nrm[u][:, D:2 * D], ALU.mult).then_inc(pool_[u].sem, 1)


def cosine_attention(nc, k, xn, cn):
    ALPHA, SYS, HD8 = 5.0, 16, 8
    PAIRS = SYS // 2
    with ExitStack() as ctx:
        def sb(name, shape, dt=F32):
            return ctx.enter_context(nc.sbuf_tensor("ca" + name, shape, dt))
        kn = [sb(f"kn{u}", [P, D]) for u in range(2)]
        cT = [sb(f"cT{u}", [P, 2, P]) for u in range(2)]
        qe = [sb(f"qe{u}", [P, SYS, D]) for u in range(2)]
        v1 = [sb(f"v1{u}", [P, 2, SYS, 32]) for u in range(2)]
        ex = [sb(f"ex{m}", [P, 2, 2 * D]) for m in range(4)]
        osb = sb("osb", [P, 4, D])
        rec = sb("rec", [P, D])
        quotient = sb("quotient", [P, D])
        arrived = [nc.alloc_semaphore(f"ca_arrived{u}") for u in range(2)]
        ones_set, spread, keyed, divided = semaphores(nc, ctx, "ca", "ones_set spread keyed divided")
        valued, scored, exped, attended, o_copied, picked, added = semaphores(
            nc, ctx, "ca", "valued scored exped attended o_copied picked added")
        VALUED, SCORED, EXPED, ATTENDED, O_COPIED, PICKED, ADDED = 2, 1, 2, 4 + PAIRS, 1, 1, 2
        sbank, obank, tbank = [k.psum[:, 0:2, :], k.psum[:, 2:4, :]], k.psum[:, 4:6, :], k.ps[6:8]
        block = ctx.enter_context(nc.Block("ca_b"))

        @block.sync
        def _(sp):
            with sp.Fori(0, T // 2) as i:
                for u in range(2):
                    t = 2 * i + u
                    sp.wait_ge(valued, VALUED + t - 1)
                    sp.dma_start(cT[u][:, :, :], k.a["ctxT"].rearrange("(c p) n -> p c n", p=P)[:, :, bass.ds(t * P, P)]).then_inc(arrived[u], 16)

        @block.gpsimd
        def _(pool):
            pool.sem_inc(valued, VALUED)
            with pool.Fori(0, T // 2) as i:
                for u in range(2):
                    t = 2 * i + u
                    pool.wait_ge(attended, ATTENDED + PAIRS * (t - 1))
                    pool.wait_ge(arrived[u], 16 * (i + 1))
                    pool.tensor_copy(kn[u][:, :], cn[:, bass.ds(t, 1), :]).then_inc(keyed, 1)
                    pool.tensor_copy(v1[u][:, :, :, 0:HD8], cT[u][:, :, :].rearrange("p c (s d) -> p c s d", d=HD8)).then_inc(valued, 1)

        @block.tensor
        def _(pe):
            pe.sem_inc(scored, SCORED)
            pe.sem_inc(attended, ATTENDED)
            pe.sem_inc(picked, PICKED)
            pe.wait_ge(ones_set, 2)

            def scores(u, t, m):
                pe.wait_ge(exped, EXPED + PAIRS * t + m - 1)
                for c in range(2):
                    mm = pe.matmul(sbank[m % 2][:, c, :], kn[u][:, c * P:(c + 1) * P],
                                   qe[u][:, 2 * m:2 * m + 2, :].rearrange("p s d -> p (s d)"), start=True, stop=True)
                mm.then_inc(scored, 1)

            def attend(u, t, m):
                if m == 0:
                    pe.wait_ge(valued, VALUED + t + 1)
                    pe.wait_ge(o_copied, O_COPIED + t)
                pe.wait_ge(exped, EXPED + PAIRS * t + m + 1)
                for s in range(2):
                    sys_ = 2 * m + s
                    row, block_ = sys_ % 4, sys_ // 4
                    for c in range(2):
                        mm = pe.matmul(obank[32 * row:32 * row + 32, block_ // 2, block_ % 2 * D:(block_ % 2 + 1) * D],
                                       v1[u][:, c, sys_, :], ex[m % 4][:, c, s * D:(s + 1) * D], start=(c == 0), stop=(c == 1))
                mm.then_inc(attended, 1)

            def pick(u, t):
                pe.wait_ge(o_copied, O_COPIED + t + 1)
                pe.wait_ge(added, ADDED + t - 1)
                for n in range(2):
                    for block_ in range(4):
                        mm = pe.matmul(tbank[u][32 * block_:32 * block_ + 32, n * D:(n + 1) * D], k.pick[:, 32 * n:32 * n + 32],
                                       osb[:, block_, :], start=True, stop=True)
                mm.then_inc(picked, 1)

            def tile(u, t, first):
                pe.wait_ge(spread, t + 1)
                pe.wait_ge(keyed, t + 1)
                for m in range(PAIRS):
                    scores(u, t, m)
                    if m >= 1:
                        attend(u, t, m - 1)
                    if m == 4 and not first:
                        pick(1 - u, t - 1)
                attend(u, t, PAIRS - 1)

            for t in range(2):
                tile(t, t, t == 0)
            with pe.Fori(1, T // 2) as i:
                for u in range(2):
                    tile(u, 2 * i + u, False)
            pick(1, T - 1)

        @block.scalar
        def _(act):
            act.preload_act_table(ACT.Exp)
            act.sem_inc(exped, EXPED)
            act.sem_inc(o_copied, O_COPIED)

            def outputs(t):
                act.wait_ge(attended, ATTENDED + PAIRS * (t + 1))
                act.wait_ge(picked, PICKED + t)
                act.copy(osb[:, :, :].rearrange("p (b c) d -> p b (c d)", b=2), obank).then_inc(o_copied, 1)

            def tile(t, first):
                for m in range(PAIRS):
                    act.wait_ge(scored, SCORED + PAIRS * t + m + 1)
                    act.wait_ge(attended, ATTENDED + PAIRS * t + m - 3)
                    act.activation(ex[m % 4][:, :, :], sbank[m % 2], ACT.Exp, scale=ALPHA).then_inc(exped, 1)
                    if m == 0 and not first:
                        outputs(t - 1)

            for t in range(2):
                tile(t, t == 0)
            with act.Fori(1, T // 2) as i:
                for u in range(2):
                    tile(2 * i + u, False)
            outputs(T - 1)

        @block.vector
        def _(dve):
            dve.sem_inc(added, ADDED)
            for u in range(2):
                dve.memset(v1[u][:, :, :, HD8:32], 1.0).then_inc(ones_set, 1)

            def spread_queries(u, t):
                at = slice(t, t + 1) if isinstance(t, int) else bass.ds(t, 1)
                dve.tensor_tensor(qe[u][:, :, :], xn[:, at, :].to_broadcast([P, SYS, D]),
                                  k.rows_of_unit[:, :].unsqueeze(2).to_broadcast([P, SYS, D]), ALU.mult).then_inc(spread, 1)

            def divide_add(u, t):
                dve.wait_ge(picked, PICKED + t + 1)
                dve.reciprocal(rec[:, :], tbank[u][:, D:2 * D]).then_inc(divided, 1)
                dve.wait_ge(divided, 2 * t + 1)
                dve.wait_ge(added, ADDED + t)
                dve.tensor_tensor(quotient[:, :], tbank[u][:, 0:D], rec[:, :], ALU.mult).then_inc(divided, 1)
                dve.wait_ge(divided, 2 * t + 2)
                dve.tensor_tensor(tile_rows(k.x, t), tile_rows(k.x, t), quotient[:, :], ALU.add).then_inc(added, 1)

            def tile(u, t, first, last):
                if not first:
                    divide_add(1 - u, t - 1)
                if not last:
                    dve.wait_ge(scored, SCORED + PAIRS * (t + 1))
                    spread_queries(u, t + 2)

            for u in range(2):
                spread_queries(u, u)
            for u in range(2):
                tile(u, u, u == 0, False)
            with dve.Fori(1, T // 2 - 1) as i:
                for u in range(2):
                    tile(u, 2 * i + u, False, False)
            for u in range(2):
                tile(u, T - 2 + u, False, True)
            divide_add(1, T - 1)


def l3_attention(nc, k):
    with ExitStack() as outer:
        def sb(name, shape):
            return outer.enter_context(nc.sbuf_tensor("a3" + name, shape, F32))
        o = sb("o", [P, T, D])
        stats = sb("stats", [P, T, 6])
        diff_attention(nc, k, o, stats)
        group_norm_output(nc, k, o, stats)


def diff_attention(nc, k, o, stats):
    with ExitStack() as ctx:
        def sb(name, shape, dt=F32):
            return ctx.enter_context(nc.sbuf_tensor("d3" + name, shape, dt))
        w = sb("w", [P, 2, 768])
        lams = sb("lams", [P, 4, HD])
        lprod = sb("lprod", [P, 2, HD])
        lsum = sb("lsum", [P, 2])
        lam = sb("lam", [P, 1])
        xs = [sb(f"xs{u}", [P, 2, P]) for u in range(2)]
        t1 = [sb(f"t1{u}", [P, 512]) for u in range(2)]
        t2 = [sb(f"t2{u}", [P, 512]) for u in range(2)]
        qk = [sb(f"qk{u}", [P, 512]) for u in range(2)]
        v = [sb(f"v{u}", [P, D]) for u in range(2)]
        vd = [sb(f"vd{u}", [P, 2, D]) for u in range(2)]
        kT = [sb(f"kT{u}", [P, 2, P]) for u in range(2)]
        qT = [[sb(f"qT{u}{n}", [P, 2, P]) for n in range(2)] for u in range(2)]
        kexp = [sb(f"kexp{u}", [P, 2, 2, 8, S]) for u in range(2)]
        sc = [[sb(f"sc{u}{n}", [P, HEADS * S]) for n in range(2)] for u in range(2)]
        pT = [sb(f"pT{u}", [P, 8, P]) for u in range(2)]
        mx = [[sb(f"mx{u}{n}", [P, HEADS]) for n in range(2)] for u in range(2)]
        den = [[sb(f"den{u}{n}", [P, HEADS]) for n in range(2)] for u in range(2)]
        loaded, vec, lexp = semaphores(nc, ctx, "d3", "loaded vec lexp")
        pe_ = lane_steps(nc, "d3", "pe", "QKV TURNED SCORES0 SCORES1 PT O")
        act_ = lane_steps(nc, "d3", "act", "V QT EXP0 EXP1 PT")
        dve_ = lane_steps(nc, "d3", "dve", "COS SIN ROPED VBD KEXP MASK0 MAX0 MASK1 MAX1 SUB1 REC0 P0 SUM1 REC1 LREC P1 DIFF O STATS")
        pool_ = lane_steps(nc, "d3", "pool", "XS")
        bank = [[k.ps[4 * u + n] for n in range(4)] for u in range(2)]
        block = ctx.enter_context(nc.Block("d3_b"))

        @block.sync
        def _(sp):
            sp.dma_start(w[:, :, :], k.a["L3_qkv"].rearrange("(c p) n -> p c n", p=P)).then_inc(loaded, 16)
            sp.dma_start(lams[:, :, :], k.a["L3_lambdas"].partition_broadcast(P)).then_inc(loaded, 16)

        @block.gpsimd
        def _(pool):
            with pool.Fori(0, T // 2) as i:
                for u in range(2):
                    pool.wait_ge(pe_[u].sem, pe_[u].turns(i))
                    pool.tensor_copy(xs[u][:, :, :], k.xT[:, :, bass.ds((2 * i + u) * P, P)]).then_inc(pool_[u].sem, 1)

        @block.tensor
        def _(pe):
            pe.wait_ge(loaded, 32)

            def project(u, i):
                pe.wait_ge(pool_[u].sem, pool_[u].at(i, "XS"))
                for o_, lo, hi in ((bank[u][0], 0, 512), (bank[u][1][:, 0:D], 512, 768)):
                    for c in range(2):
                        mm = pe.matmul(o_, xs[u][:, c, :], w[:, c, lo:hi], start=(c == 0), stop=(c == 1))
                mm.then_inc(pe_[u].sem, 1)

            def turn(u, i):
                pe.wait_ge(dve_[u].sem, dve_[u].at(i, "ROPED"))
                pe.wait_ge(act_[u].sem, act_[u].at(i, "V"))
                pe.wait_ge(dve_[u].sem, dve_[u].turns(i))
                for c in range(4):
                    pe.transpose(bank[u][2][:, c * P:(c + 1) * P], qk[u][:, c * P:(c + 1) * P], k.ident[:, :])
                for b in range(2):
                    mm = pe.matmul(bank[u][3][:, b * D:(b + 1) * D], k.dup[:, b * P:(b + 1) * P], v[u][:, :], start=True, stop=True)
                mm.then_inc(pe_[u].sem, 1)

            def scores(u, i, n):
                if n == 0:
                    pe.wait_ge(dve_[u].sem, dve_[u].at(i, "KEXP"))
                score_matmuls(pe, bank[u][2 * n:2 * n + 2], qT[u][n], kexp[u]).then_inc(pe_[u].sem, 1)

            def turn_weights(u, i):
                pe.wait_ge(dve_[u].sem, dve_[u].at(i, "DIFF"))
                weight_transposes(pe, bank[u][0:2], sc[u][0], k.ident[:, :]).then_inc(pe_[u].sem, 1)

            def values(u, i):
                pe.wait_ge(act_[u].sem, act_[u].at(i, "PT"))
                value_matmuls(pe, bank[u][2], pT[u], vd[u]).then_inc(pe_[u].sem, 1)

            def tile(u, i, before, after):
                turn(u, i)
                scores(u, i, 0)
                if before:
                    turn_weights(*before)
                scores(u, i, 1)
                if before:
                    values(*before)
                if after:
                    project(*after)

            project(0, 0)
            end = staggered(pe, tile)
            turn_weights(*end)
            values(*end)

        @block.scalar
        def _(act):
            act.preload_act_table(ACT.Exp)
            act.wait_ge(vec, 3)
            act.activation(lsum[:, :], lsum[:, :], ACT.Exp).then_inc(lexp, 1)

            def weights_out(u, i):
                act.wait_ge(pe_[u].sem, pe_[u].at(i, "PT"))
                act.copy(pT[u][:, 0:4, :], bank[u][0].rearrange("p (c n) -> p c n", c=4))
                act.copy(pT[u][:, 4:8, :], bank[u][1].rearrange("p (c n) -> p c n", c=4)).then_inc(act_[u].sem, 1)

            def tile(u, i, before, after):
                act.wait_ge(pe_[u].sem, pe_[u].at(i, "QKV"))
                act.copy(v[u][:, :], bank[u][1][:, 0:D]).then_inc(act_[u].sem, 1)
                act.wait_ge(pe_[u].sem, pe_[u].at(i, "TURNED"))
                act.copy(kT[u][:, :, :], bank[u][2][:, D:2 * D].rearrange("p (c n) -> p c n", c=2))
                for n in range(2):
                    ins = act.activation(qT[u][n][:, :, :], bank[u][2][:, 0:D].rearrange("p (c n) -> p c n", c=2), ACT.Copy,
                                         scale=k.half[:, n:n + 1])
                ins.then_inc(act_[u].sem, 1)
                if before:
                    weights_out(*before)
                act.wait_ge(dve_[u].sem, dve_[u].at(i, "MAX0"))
                exponentials(act, sc[u][0], mx[u][0], den[u][0]).then_inc(act_[u].sem, 1)
                act.wait_ge(dve_[u].sem, dve_[u].at(i, "SUB1"))
                act.activation(sc[u][1][:, :], sc[u][1][:, :], ACT.Exp).then_inc(act_[u].sem, 1)

            weights_out(*staggered(act, tile))

        @block.vector
        def _(dve):
            dve.wait_ge(loaded, 32)
            l4 = lams[:, :, :].rearrange("p (n two) d -> p n two d", two=2)
            dve.tensor_tensor(lprod[:, :, :], l4[:, :, 0, :], l4[:, :, 1, :], ALU.mult).then_inc(vec, 1)
            dve.wait_ge(vec, 1)
            dve.tensor_reduce(lsum[:, :], lprod[:, :, :], AX.X, ALU.add).then_inc(vec, 1)
            dve.wait_ge(vec, 2)
            dve.sem_inc(vec, 1)
            dve.wait_ge(lexp, 1)
            dve.tensor_tensor(lam[:, :], lsum[:, 0:1], lsum[:, 1:2], ALU.subtract).then_inc(vec, 1)
            dve.wait_ge(vec, 4)
            dve.tensor_scalar(lam[:, :], lam[:, :], 0.8, None, ALU.add).then_inc(vec, 1)
            dve.wait_ge(vec, 5)

            def rope(u, i):
                dve.wait_ge(pe_[u].sem, pe_[u].at(i, "QKV"))
                for o_, table in ((t1, k.cos), (t2, k.sin)):
                    dve.tensor_tensor(by8(o_[u][:, :]), by8(bank[u][0]), angles(table), ALU.mult).then_inc(dve_[u].sem, 1)
                dve.wait_ge(dve_[u].sem, dve_[u].at(i, "SIN"))
                rope_sums(dve, qk[u][:, :], t1[u][:, :], t2[u][:, :]).then_inc(dve_[u].sem, 1)

            def spread(u, i):
                dve.wait_ge(pe_[u].sem, pe_[u].at(i, "TURNED"))
                values_by_parity(dve, vd[u], bank[u][3].rearrange("p (b n) -> p b n", b=2), k.parity[:, :]).then_inc(dve_[u].sem, 1)
                dve.wait_ge(act_[u].sem, act_[u].at(i, "QT"))
                spread_keys(dve, kexp[u], kT[u], k.head_mask[:, :]).then_inc(dve_[u].sem, 1)

            def mask(u, i, n):
                dve.wait_ge(pe_[u].sem, pe_[u].at(i, f"SCORES{n}"))
                for c in range(2):
                    ins = dve.scalar_tensor_tensor(out=heads3(sc[u][n][:, c * 512:(c + 1) * 512]), in0=heads3(bank[u][2 * n + c]),
                                                   scalar=HD ** -0.5, in1=over_heads(k.upper[:, :], 8), op0=ALU.mult, op1=ALU.add)
                ins.then_inc(dve_[u].sem, 1)
                dve.wait_ge(dve_[u].sem, dve_[u].at(i, f"MASK{n}"))
                dve.tensor_reduce(mx[u][n][:, :], heads3(sc[u][n][:, :]), AX.X, ALU.max, negate=(n == 0)).then_inc(dve_[u].sem, 1)

            def subtract_maximum(u, i):
                dve.wait_ge(dve_[u].sem, dve_[u].at(i, "MAX1"))
                dve.tensor_tensor(heads3(sc[u][1][:, :]), heads3(sc[u][1][:, :]), per_head(mx[u][1][:, :]), ALU.subtract).then_inc(dve_[u].sem, 1)

            def normalise(u, n):
                dve.tensor_tensor(heads3(sc[u][n][:, :]), heads3(sc[u][n][:, :]), per_head(den[u][n][:, :]),
                                  ALU.mult).then_inc(dve_[u].sem, 1)

            def first_weights(u, i):
                dve.wait_ge(act_[u].sem, act_[u].at(i, "EXP0"))
                dve.reciprocal(den[u][0][:, :], den[u][0][:, :]).then_inc(dve_[u].sem, 1)
                dve.wait_ge(dve_[u].sem, dve_[u].at(i, "REC0"))
                normalise(u, 0)

            def difference(u, i):
                def wait(step):
                    dve.wait_ge(dve_[u].sem, dve_[u].at(i, step))

                dve.wait_ge(act_[u].sem, act_[u].at(i, "EXP1"))
                dve.tensor_reduce(den[u][1][:, :], heads3(sc[u][1][:, :]), AX.X, ALU.add).then_inc(dve_[u].sem, 1)
                wait("SUM1")
                dve.reciprocal(den[u][1][:, :], den[u][1][:, :]).then_inc(dve_[u].sem, 1)
                wait("REC1")
                dve.tensor_scalar(den[u][1][:, :], den[u][1][:, :], lam[:, :], None, ALU.mult).then_inc(dve_[u].sem, 1)
                wait("LREC")
                normalise(u, 1)
                wait("P1")
                dve.tensor_tensor(sc[u][0][:, :], sc[u][0][:, :], sc[u][1][:, :], ALU.subtract).then_inc(dve_[u].sem, 1)

            def outputs(u, i):
                t = 2 * i + u
                dve.wait_ge(pe_[u].sem, pe_[u].at(i, "O"))
                for b in range(2):
                    r = row_slice(b)
                    ins = dve.tensor_copy(tile_rows(o, t)[r, :].rearrange("p (c h d) -> p c h d", h=2, d=HD), own_batch(bank[u][2], b))
                ins.then_inc(dve_[u].sem, 1)
                dve.wait_ge(dve_[u].sem, dve_[u].at(i, "O"))
                dve.bn_stats(tile_rows(stats, t), tile_rows(o, t)).then_inc(dve_[u].sem, 1)

            def tile(u, i, before, after):
                rope(u, i)
                if before:
                    first_weights(*before)
                spread(u, i)
                if before:
                    difference(*before)
                mask(u, i, 0)
                mask(u, i, 1)
                subtract_maximum(u, i)
                if before:
                    outputs(*before)

            end = staggered(dve, tile)
            first_weights(*end)
            difference(*end)
            outputs(*end)


def group_norm_output(nc, k, o, stats):
    with ExitStack() as ctx:
        def sb(name, shape, dt=F32):
            return ctx.enter_context(nc.sbuf_tensor("g3" + name, shape, dt))
        w = sb("w", [P, 2, D])
        gamma, beta = sb("gamma", [P, 4]), sb("beta", [P, 4])
        mom = sb("mom", [P, 4, T])
        pair = sb("pair", [P, 2, T])
        y = [sb(f"y{u}", [P, D]) for u in range(2)]
        yT = [sb(f"yT{u}", [P, 2, P]) for u in range(2)]
        loaded, vec, averaged, rooted = semaphores(nc, ctx, "g3", "loaded vec averaged rooted")
        pe_ = lane_steps(nc, "g3", "pe", "YT OUT")
        act_ = lane_steps(nc, "g3", "act", "YT")
        dve_ = lane_steps(nc, "g3", "dve", "NORM GAMMA BETA X")
        bank = [[k.ps[4 * u + n] for n in range(4)] for u in range(2)]
        block = ctx.enter_context(nc.Block("g3_b"))

        @block.sync
        def _(sp):
            sp.dma_start(w[:, :, :], k.a["L3_wo"].rearrange("(c p) n -> p c n", p=P)).then_inc(loaded, 16)
            for b in range(2):
                sp.dma_start(gamma[row_slice(b), :], k.a["L3_gamma"]).then_inc(loaded, 16)
                sp.dma_start(beta[row_slice(b), :], k.a["L3_beta"]).then_inc(loaded, 16)

        @block.gpsimd
        def _(pool):
            pool.wait_ge(vec, 12)
            pool.tensor_tensor(mom[:, 3, :], mom[:, 2, :], k.minus_half[:, 0:T], ALU.pow).then_inc(rooted, 1)

        @block.tensor
        def _(pe):
            pe.wait_ge(loaded, 80)
            pe.wait_ge(vec, 9)
            pe.matmul(k.ps[7][:, 0:2 * T], k.avg4[:, :], pair[:, :, :].rearrange("p n t -> p (n t)"), start=True, stop=True).then_inc(averaged, 1)
            with pe.Fori(0, T // 2) as i:
                for u in range(2):
                    pe.wait_ge(dve_[u].sem, dve_[u].at(i, "BETA"))
                    for c in range(2):
                        mm = pe.transpose(bank[u][0][:, c * P:(c + 1) * P], y[u][:, c * P:(c + 1) * P], k.ident[:, :])
                    mm.then_inc(pe_[u].sem, 1)
                for u in range(2):
                    pe.wait_ge(act_[u].sem, act_[u].at(i, "YT"))
                    pe.wait_ge(dve_[u].sem, dve_[u].turns(i))
                    for c in range(2):
                        mm = pe.matmul(bank[u][1][:, 0:D], yT[u][:, c, :], w[:, c, :], start=(c == 0), stop=(c == 1))
                    mm.then_inc(pe_[u].sem, 1)

        @block.scalar
        def _(act):
            with act.Fori(0, T // 2) as i:
                for u in range(2):
                    act.wait_ge(pe_[u].sem, pe_[u].at(i, "YT"))
                    act.copy(yT[u][:, :, :], bank[u][0][:, 0:D].rearrange("p (c n) -> p c n", c=2)).then_inc(act_[u].sem, 1)

        @block.vector
        def _(dve):
            count = [0]

            def link(ins):
                count[0] += 1
                ins.then_inc(vec, 1)
                dve.wait_ge(vec, count[0])

            me, mo, ve, vo = stats[:, :, 1], stats[:, :, 4], stats[:, :, 2], stats[:, :, 5]
            link(dve.tensor_tensor(pair[:, 0, :], me, mo, ALU.add))
            link(dve.tensor_scalar(pair[:, 0, :], pair[:, 0, :], 0.5, None, ALU.mult))
            link(dve.tensor_tensor(mom[:, 0, :], me, me, ALU.mult))
            link(dve.tensor_tensor(mom[:, 1, :], mo, mo, ALU.mult))
            link(dve.tensor_tensor(mom[:, 0, :], mom[:, 0, :], mom[:, 1, :], ALU.add))
            link(dve.tensor_scalar(mom[:, 0, :], mom[:, 0, :], 0.5, None, ALU.mult))
            link(dve.tensor_tensor(mom[:, 1, :], ve, vo, ALU.add))
            link(dve.tensor_scalar(mom[:, 1, :], mom[:, 1, :], 1.0 / D, None, ALU.mult))
            link(dve.tensor_tensor(pair[:, 1, :], mom[:, 0, :], mom[:, 1, :], ALU.add))
            dve.wait_ge(averaged, 1)
            link(dve.tensor_copy(pair[:, :, :].rearrange("p n t -> p (n t)"), k.ps[7][:, 0:2 * T]))
            link(dve.tensor_tensor(mom[:, 0, :], pair[:, 0, :], pair[:, 0, :], ALU.mult))
            link(dve.scalar_tensor_tensor(out=mom[:, 2, :], in0=pair[:, 1, :], scalar=1e-5, in1=mom[:, 0, :], op0=ALU.add, op1=ALU.subtract))
            dve.wait_ge(rooted, 1)
            dve.wait_ge(loaded, 80)
            with dve.Fori(0, T // 2) as i:
                for u in range(2):
                    t = 2 * i + u
                    y3 = y[u][:, :].rearrange("p (g d) -> p g d", g=4)
                    dve.tensor_scalar(y[u][:, :], tile_rows(o, t), pair[:, 0, bass.ds(t, 1)], mom[:, 3, bass.ds(t, 1)],
                                      ALU.subtract, ALU.mult).then_inc(dve_[u].sem, 1)
                    dve.wait_ge(dve_[u].sem, dve_[u].at(i, "NORM"))
                    dve.tensor_tensor(y3, y3, gamma[:, :].unsqueeze(2).to_broadcast([P, 4, 64]), ALU.mult).then_inc(dve_[u].sem, 1)
                    dve.wait_ge(dve_[u].sem, dve_[u].at(i, "GAMMA"))
                    dve.tensor_tensor(y3, y3, beta[:, :].unsqueeze(2).to_broadcast([P, 4, 64]), ALU.add).then_inc(dve_[u].sem, 1)
                for u in range(2):
                    xt = tile_rows(k.x, 2 * i + u)
                    dve.wait_ge(pe_[u].sem, pe_[u].at(i, "OUT"))
                    dve.scalar_tensor_tensor(out=xt, in0=bank[u][1][:, 0:D], scalar=1.0 - 0.8, in1=xt, op0=ALU.mult, op1=ALU.add).then_inc(dve_[u].sem, 1)


def l3_cross(nc, k):
    with ExitStack() as ctx:
        def sb(name, shape, dt=F32):
            return ctx.enter_context(nc.sbuf_tensor("c3" + name, shape, dt))
        mk8 = sb("mk8", [P, T, S], mybir.dt.uint8)
        mk = sb("mk", [P, T, S])
        neg = sb("neg", [P, T, S])
        valid = sb("valid", [P, T])
        xs = [sb(f"xs{u}", [P, 2, P]) for u in range(2)]
        cT = [sb(f"cT{u}", [P, 2, P]) for u in range(2)]
        cs = [sb(f"cs{u}", [P, D]) for u in range(2)]
        sc = [sb(f"sc{u}", [P, S]) for u in range(2)]
        nmx = [sb(f"nmx{u}", [P, 1]) for u in range(2)]
        den = [sb(f"den{u}", [P, 1]) for u in range(2)]
        fac = [sb(f"fac{u}", [P, 1]) for u in range(2)]
        pbd = [sb(f"pbd{u}", [P, P]) for u in range(2)]
        pT = [sb(f"pT{u}", [P, P]) for u in range(2)]
        loaded, ready = semaphores(nc, ctx, "c3", "loaded ready")
        arrived = [nc.alloc_semaphore(f"c3_arrived{u}") for u in range(2)]
        pe_ = lane_steps(nc, "c3", "pe", "S PT O")
        act_ = lane_steps(nc, "c3", "act", "EXP PT")
        dve_ = lane_steps(nc, "c3", "dve", "SCALED MASKED MAX REC FAC X")
        pool_ = lane_steps(nc, "c3", "pool", "XS")
        bank = [[k.ps[4 * u + n] for n in range(4)] for u in range(2)]
        block = ctx.enter_context(nc.Block("c3_b"))

        @block.sync
        def _(sp):
            for b in range(2):
                sp.dma_start(mk8[64 * b:64 * b + 64, :, :],
                             k.a["mask"].rearrange("(t b) j -> b t j", b=2)[b].partition_broadcast(64)).then_inc(loaded, 16)
            with sp.Fori(0, T // 2) as i:
                for u in range(2):
                    t = 2 * i + u
                    sp.wait_ge(pe_[u].sem, pe_[u].turns(i))
                    sp.dma_start(cs[u][:, :], k.ctx_rows[bass.ds(t * P, P), :]).then_inc(arrived[u], 16)
                    sp.dma_start(cT[u][:, :, :], k.a["ctxT"].rearrange("(c p) n -> p c n", p=P)[:, :, bass.ds(t * P, P)]).then_inc(arrived[u], 16)

        @block.gpsimd
        def _(pool):
            with pool.Fori(0, T // 2) as i:
                for u in range(2):
                    pool.wait_ge(pe_[u].sem, pe_[u].turns(i))
                    pool.tensor_copy(xs[u][:, :, :], k.xT[:, :, bass.ds((2 * i + u) * P, P)]).then_inc(pool_[u].sem, 1)

        @block.tensor
        def _(pe):
            with pe.Fori(0, T // 2) as i:
                for u in range(2):
                    pe.wait_ge(arrived[u], 32 * (i + 1))
                    pe.wait_ge(pool_[u].sem, pool_[u].at(i, "XS"))
                    pe.wait_ge(dve_[u].sem, dve_[u].turns(i))
                    for c in range(2):
                        mm = pe.matmul(bank[u][0][:, 0:P], xs[u][:, c, :], cT[u][:, c, :], start=(c == 0), stop=(c == 1))
                    mm.then_inc(pe_[u].sem, 1)
                for u in range(2):
                    pe.wait_ge(act_[u].sem, act_[u].at(i, "EXP"))
                    pe.transpose(bank[u][1][:, 0:P], pbd[u][:, :], k.ident[:, :]).then_inc(pe_[u].sem, 1)
                for u in range(2):
                    pe.wait_ge(act_[u].sem, act_[u].at(i, "PT"))
                    pe.matmul(bank[u][2][:, 0:D], pT[u][:, :], cs[u][:, :], start=True, stop=True).then_inc(pe_[u].sem, 1)

        @block.scalar
        def _(act):
            act.preload_act_table(ACT.Exp)
            act.wait_ge(ready, 6)
            with act.Fori(0, T // 2) as i:
                for u in range(2):
                    act.wait_ge(dve_[u].sem, dve_[u].at(i, "MAX"))
                    for b in range(2):
                        r = slice(64 * b, 64 * b + 64)
                        ins = act.activation(pbd[u][r, r], sc[u][r, :], ACT.Exp, bias=nmx[u][r, :], accum_out=den[u][r, :])
                    ins.then_inc(act_[u].sem, 1)
                for u in range(2):
                    act.wait_ge(pe_[u].sem, pe_[u].at(i, "PT"))
                    act.copy(pT[u][:, :], bank[u][1][:, 0:P]).then_inc(act_[u].sem, 1)

        @block.vector
        def _(dve):
            dve.memset(pbd[0][:, :], 0.0).then_inc(ready, 1)
            dve.memset(pbd[1][:, :], 0.0).then_inc(ready, 1)
            dve.wait_ge(loaded, 32)
            dve.tensor_copy(mk[:, :, :], mk8[:, :, :]).then_inc(ready, 1)
            dve.wait_ge(ready, 3)
            dve.tensor_scalar(neg[:, :, :], mk[:, :, :], -1.0, -NEG, ALU.add, ALU.mult).then_inc(ready, 1)
            dve.tensor_reduce(valid[:, :], mk[:, :, :], AX.X, ALU.max).then_inc(ready, 1)
            dve.wait_ge(ready, 5)
            dve.sem_inc(ready, 1)
            with dve.Fori(0, T // 2) as i:
                for u in range(2):
                    def wait(step, u=u):
                        dve.wait_ge(dve_[u].sem, dve_[u].at(i, step))

                    t = bass.ds(2 * i + u, 1)
                    dve.wait_ge(pe_[u].sem, pe_[u].at(i, "S"))
                    for b in range(2):
                        r = slice(64 * b, 64 * b + 64)
                        ins = dve.scalar_tensor_tensor(out=sc[u][r, :], in0=bank[u][0][r, r], scalar=D ** -0.5,
                                                       in1=mk[r, t, :].rearrange("p t j -> p (t j)"), op0=ALU.mult, op1=ALU.mult)
                    ins.then_inc(dve_[u].sem, 1)
                    wait("SCALED")
                    dve.tensor_tensor(sc[u][:, :], sc[u][:, :], neg[:, t, :].rearrange("p t j -> p (t j)"), ALU.add).then_inc(dve_[u].sem, 1)
                    wait("MASKED")
                    dve.tensor_reduce(nmx[u][:, :], sc[u][:, :], AX.X, ALU.max, negate=True).then_inc(dve_[u].sem, 1)
                for u in range(2):
                    t = bass.ds(2 * i + u, 1)
                    dve.wait_ge(act_[u].sem, act_[u].at(i, "EXP"))
                    dve.reciprocal(den[u][:, :], den[u][:, :]).then_inc(dve_[u].sem, 1)
                    dve.wait_ge(dve_[u].sem, dve_[u].at(i, "REC"))
                    dve.tensor_tensor(fac[u][:, :], den[u][:, :], valid[:, t], ALU.mult).then_inc(dve_[u].sem, 1)
                for u in range(2):
                    xt = k.x[:, bass.ds(2 * i + u, 1), :].rearrange("p t d -> p (t d)")
                    dve.wait_ge(pe_[u].sem, pe_[u].at(i, "O"))
                    dve.wait_ge(dve_[u].sem, dve_[u].at(i, "FAC"))
                    dve.scalar_tensor_tensor(out=xt, in0=bank[u][2][:, 0:D], scalar=fac[u][:, :], in1=xt,
                                             op0=ALU.mult, op1=ALU.add).then_inc(dve_[u].sem, 1)


class Shared:
    pass


def build(nc, a, out):
    with ExitStack() as ctx:
        k = Shared()
        k.a = a
        def sb(name, shape, dt=F32):
            return ctx.enter_context(nc.sbuf_tensor(name, shape, dt))
        k.psum = ctx.enter_context(nc.psum_tensor("psum", [P, 8, 512], F32))
        k.ps = [k.psum[:, i, :] for i in range(8)]
        k.x = sb("x", [P, T, D])
        k.xT = sb("xT", [P, 2, N])
        k.consts = {n[2:]: sb(n, list(ap.shape)) for n, ap in a.items() if n.startswith("c_")}
        c = k.consts
        k.ident, k.cos, k.sin, k.head_mask, k.parity = c["ident"], c["cos"], c["sin"], c["head_mask"], c["parity"]
        k.strict, k.causal, k.not_first = c["strict"], c["causal"], c["not_first"]
        k.ones8, k.rows_of_unit = c["ones8"], c["rows_of_unit"]
        k.dup, k.block_causal, k.upper, k.half = c["dup"], c["block_causal"], c["upper"], c["half"]
        k.ones64, k.cumulate, k.eye64, k.avg4, k.ones = c["ones64"], c["cumulate"], c["eye64"], c["avg4"], c["ones"]
        k.minus_half = sb("minus_half", [P, T])
        k.v_scr = nc.dram_tensor("v_scr", (N, D), F32, kind="Internal").ap()
        k.u_scr = nc.dram_tensor("u_scr", (N, D), F32, kind="Internal").ap()
        k.l_scr = nc.dram_tensor("l_scr", (NB, 16, S, S), F32, kind="Internal").ap()
        k.p_scr = nc.dram_tensor("p_scr", (T, P, 1024), F32, kind="Internal").ap()
        k.q_scr = nc.dram_tensor("q_scr", (3, D, N), BF16, kind="Internal").ap()
        k.k_scr = nc.dram_tensor("k_scr", (3, D, KEYS), BF16, kind="Internal").ap()
        k.strip_sum, k.pick = c["strip_sum"], c["pick"]
        k.ctx_rows = a["ctx"]
        load_phase(nc, k)
        for n, phase in list(enumerate(PHASES))[FIRST:LAST + 1]:
            with nc.cleanup_on_exit():
                phase(nc, k)
                layer_norm(nc, k, f"ln{n}")
        store_phase(nc, k, out)


def load_phase(nc, k):
    with ExitStack() as ctx:
        loaded, const, turned, copied = semaphores(nc, ctx, "load", "loaded const turned copied")
        block = ctx.enter_context(nc.Block("load_b"))

        @block.sync
        def _(sp):
            for b in range(2):
                sp.dma_start(k.x[64 * b:64 * b + 64, :, :],
                             k.a["x"].rearrange("(t c) s d -> c s t d", c=2)[b]).then_inc(loaded, 16)
            for n, tile in k.consts.items():
                sp.dma_start(tile[:, :], k.a["c_" + n]).then_inc(loaded, 16)
            sp.wait_ge(loaded, 32 + 16 * len(k.consts))

        @block.gpsimd
        def _(pool):
            pool.memset(k.minus_half[:, :], -0.5).then_inc(const, 1)
            pool.wait_ge(const, 1)

        @block.tensor
        def _(pe):
            pe.wait_ge(loaded, 32 + 16 * len(k.consts))
            for t in range(T):
                if t >= 8:
                    pe.wait_ge(copied, t - 7)
                pe.transpose(k.ps[t % 8][:, 0:128], k.x[:, t, 0:128], k.ident[:, :])
                pe.transpose(k.ps[t % 8][:, 128:256], k.x[:, t, 128:256], k.ident[:, :]).then_inc(turned, 1)

        @block.scalar
        def _(act):
            for t in range(T):
                act.wait_ge(turned, t + 1)
                act.copy(k.xT[:, :, t * P:(t + 1) * P],
                         k.ps[t % 8][:, 0:256].rearrange("p (c n) -> p c n", c=2)).then_inc(copied, 1)


def store_phase(nc, k, out):
    with ExitStack() as ctx:
        stored, = semaphores(nc, ctx, "store", "stored")
        block = ctx.enter_context(nc.Block("store_b"))

        @block.sync
        def _(sp):
            for b in range(2):
                sp.dma_start(out.rearrange("(t c) s d -> c s t d", c=2)[b], k.x[64 * b:64 * b + 64, :, :]).then_inc(stored, 16)
            sp.wait_ge(stored, 32)


PHASES = [l0_attention, l0_cross, l0_ffn] + [l1_attention, l1_cross, l1_ffn, l2_attention, l2_cross, l2_ffn, l3_attention, l3_cross, l3_ffn]


def shape_constants():
    p = np.arange(P)
    s = p % S
    j = np.arange(S)
    ang = s[:, None].astype(np.float32) * (1.0 / 10000.0 ** (np.arange(8) / 8.0)).astype(np.float32)[None]
    f = lambda m: np.ascontiguousarray(m, dtype=np.float32)
    return {
        "ident": f(np.eye(P)),
        "cos": f(np.cos(ang)), "sin": f(np.sin(ang)),
        "head_mask": f(p[:, None] // HD == np.arange(8)[None]),
        "parity": f(p[:, None] // S == np.arange(HEADS)[None] % 2),
        "strict": f(np.where(s[:, None] > j[None], 0, NEG)),
        "causal": f(np.where(s[:, None] >= j[None], 0, NEG)),
        "not_first": f(s[:, None] > 0),
        "pick": f(np.concatenate([(p[:, None] % 32 == n * 8 + np.arange(32)[None] % 8) & (p[:, None] // 32 == np.arange(32)[None] // 8)
                                  for n in range(2)], axis=1)),
        "strip_sum": f(p[:, None] % 32 == np.arange(HD + 1)[None]),
        "dup": f(np.concatenate([p[:, None] == b * S + s[None] for b in range(2)], axis=1)),
        "block_causal": f(np.where((s[:, None] >= j[None]) & (s[:, None] // 8 == j[None] // 8), 0, NEG)),
        "upper": f(j[None] > s[:, None]),
        "half": f(p[:, None] % HD // 8 == np.arange(2)[None]),
        "ones64": f(p[:, None] // S == p[None] // S),
        "cumulate": f((p[:, None] // S == p[None] // S) & (p[:, None] <= p[None])),
        "eye64": f(s[:, None] == j[None]),
        "avg4": f((p[:, None] // 4 == p[None] // 4) * 0.25),
        "ones": f(np.ones((P, P))),
        "ones8": f(p[:, None] // 8 == p[None] // 8),
        "rows_of_unit": f(p[:, None] // 8 == np.arange(16)[None]),
    }


def selection(experts, width, hidden, shared_row=False):
    owner = np.minimum(np.arange(hidden) // width, experts)
    row = np.arange(COMB_ROWS) % 32
    rows = experts + 1 if shared_row else experts
    return ((row[:, None] == owner[None]) & (row[:, None] < rows)).astype(np.float32)


def laid_out(i):
    out = {n: np.ascontiguousarray(i[n]) for n in ("x",)}
    out["L0_attn_W"] = np.concatenate([i["L0_attn_Wq"], i["L0_attn_Wk"], i["L0_attn_Wv"], i["L0_attn_Wb"]], axis=1)
    out["L0_attn_bb"] = np.ascontiguousarray(i["L0_attn_bb"])
    out["L0_attn_Wo"] = np.ascontiguousarray(i["L0_attn_Wo"])
    out["mask"] = i["mask_BxS2_bk0"]
    out["L1_wr"], out["L1_w1"], out["L1_w3"], out["L1_w2"] = (i["L1_ffn_" + n].T for n in ("wr", "w1", "w3", "w2"))
    out["L1_gates"] = np.concatenate([i["L1_xattn_Wi"], i["L1_xattn_Wf"]], axis=1)
    out["L1_gates_b"] = np.concatenate([i["L1_xattn_bi"], i["L1_xattn_bf"]])
    out["L1_xattn_ln_scale"] = i["L1_xattn_ln_scale"]
    out["L2_norm1"], out["L2_norm2"] = i["L2_attn_attn_norm_w"], i["L2_attn_ffn_norm_w"]
    out["L2_qkv"], out["L2_o"], out["L2_up"], out["L2_down"] = (i["L2_attn_" + n + "_w"].T for n in ("qkv", "o", "ffn_up", "ffn_down"))
    out["L3_qkv"], out["L3_wo"] = i["L3_attn_w_qkv"].T, i["L3_attn_wo"].T
    out["L3_lambdas"] = np.stack([i["L3_attn_lambda_" + n] for n in ("q1", "k1", "q2", "k2")])
    out["L3_gamma"], out["L3_beta"] = i["L3_attn_gamma"].reshape(S, 4), i["L3_attn_beta"].reshape(S, 4)
    out["L1_kT"] = i["L1_attn_kv_k"].reshape(-1, D).T
    out["L1_v"] = i["L1_attn_kv_v"].reshape(-1, D)
    out["L1_Wq"], out["L1_Wo"] = i["L1_attn_Wq"].T, i["L1_attn_Wo"].T
    out["ctx"] = i["ctx_2048"].reshape(N, D)
    out["ctxT"] = i["ctx_2048"].reshape(N, D).T
    gu, F = i["L0_ffn_gate_up_weights"], i["L0_ffn_gate_up_weights"].shape[1] // 2
    sgu, FS = i["L0_ffn_shared_gate_up"], i["L0_ffn_shared_gate_up"].shape[0] // 2
    out["L0_router"] = i["L0_ffn_gate_weight"].T
    out["L0_g"] = np.concatenate([gu[:, :F].reshape(-1, D), sgu[:FS]]).T
    out["L0_u"] = np.concatenate([gu[:, F:].reshape(-1, D), sgu[FS:]]).T
    out["L0_d"] = np.concatenate([i["L0_ffn_down_weights"].transpose(0, 2, 1).reshape(-1, D), i["L0_ffn_shared_down"].T])
    out["sel176"] = selection(8, F, 8 * F + FS)
    flat = lambda w: w.transpose(1, 0, 2).reshape(D, -1)
    out["L2_router"] = np.concatenate([i["L2_ffn_gate_w"].T, i["L2_ffn_shgate_w"][:, None]], axis=1)
    out["L2_g"] = np.concatenate([flat(i["L2_ffn_w_gate"]), i["L2_ffn_shw_gate"]], axis=1)
    out["L2_u"] = np.concatenate([flat(i["L2_ffn_w_up"]), i["L2_ffn_shw_up"]], axis=1)
    out["L2_d"] = np.concatenate([i["L2_ffn_w_down"].reshape(-1, D), i["L2_ffn_shw_down"]])
    out["sel176s"] = selection(8, F, 8 * F + FS, shared_row=True)
    out["L3_ffn_w_router"] = i["L3_ffn_w_router"]
    out["L3_g"] = np.concatenate([flat(i["L3_ffn_we1"]), i["L3_ffn_ws1"]], axis=1)
    out["L3_u"] = np.concatenate([flat(i["L3_ffn_we3"]), i["L3_ffn_ws3"]], axis=1)
    out["L3_d"] = np.concatenate([i["L3_ffn_we2"].reshape(-1, D), i["L3_ffn_ws2"]])
    out["sel128"] = selection(16, 128, 16 * 128 + 512)
    return {n: np.ascontiguousarray(a) for n, a in out.items()}


def kernel(**inputs):
    import concourse.bacc as _bacc
    from concourse.bass_utils import run_bass_kernel_spmd as _run

    nc = _bacc.Bacc("TRN2", target_bir_lowering=False, num_devices=1)
    arrays, aps = {}, {}
    given = laid_out({n: np.asarray(a) for n, a in inputs.items()})
    for name, a in {**given, **{"c_" + n: c for n, c in shape_constants().items()}}.items():
        arrays[f"in_{name}_dram"] = a
        aps[name] = nc.dram_tensor(f"in_{name}_dram", a.shape, mybir.dt.from_np(a.dtype), kind="ExternalInput").ap()
    out = nc.dram_tensor("out_0_dram", (NB, S, D), F32, kind="ExternalOutput").ap()
    build(nc, aps, out)
    r = _run(nc, [arrays], core_ids=[0])
    return r.results[0]["out_0_dram"]
```

```python
import numpy as np
from contextlib import ExitStack
import concourse.bass as bass
from concourse import mybir

P, D, S, NB = 128, 256, 64, 32
N = S * NB
T = N // P
G = 4
F32, BF16 = mybir.dt.float32, mybir.dt.bfloat16
ALU, ACT, AX = mybir.AluOpType, mybir.ActivationFunctionType, mybir.AxisListType
LN_EPS = 1e-5
HEADS, HD = 16, 16
KEYS = 4096
NEG = -1e30


def semaphores(nc, ctx, phase, names):
    return [nc.alloc_semaphore(f"{phase}_{n}") for n in names.split()]


def layer_norm(nc, k, name):
    with ExitStack() as ctx:
        def sb(n, shape):
            return ctx.enter_context(nc.sbuf_tensor(name + n, shape, F32))
        LANES = 4
        stats = sb("stats", [P, T, 6])
        MEAN, APART, VAR, APART2, TOTAL, RSTD = range(6)
        mom = sb("mom", [P, 6, T])
        stage = [sb(f"stage{u}", [P, D]) for u in range(LANES)]
        taken, vec, vared, rstd_ready, staged, written, turned, copied = semaphores(
            nc, ctx, name, "taken vec variance rstd staged written turned copied")
        block = ctx.enter_context(nc.Block(name + "_b"))

        @block.vector
        def _(dve):
            with dve.Fori(0, T // LANES) as i:
                for u in range(LANES):
                    dve.bn_stats(stats[:, bass.ds(LANES * i + u, 1), :], k.x[:, bass.ds(LANES * i + u, 1), :]).then_inc(taken, 1)
            dve.wait_ge(taken, T)
            me, mo, ve, vo = stats[:, :, 1], stats[:, :, 4], stats[:, :, 2], stats[:, :, 5]
            dve.tensor_tensor(mom[:, MEAN, :], me, mo, ALU.add).then_inc(vec, 1)
            dve.tensor_tensor(mom[:, APART, :], me, mo, ALU.subtract).then_inc(vec, 1)
            dve.tensor_tensor(mom[:, VAR, :], ve, vo, ALU.add).then_inc(vec, 1)
            dve.wait_ge(vec, 3)
            dve.tensor_tensor(mom[:, APART2, :], mom[:, APART, :], mom[:, APART, :], ALU.mult).then_inc(vec, 1)
            dve.tensor_scalar(mom[:, VAR, :], mom[:, VAR, :], 1.0 / D, LN_EPS, ALU.mult, ALU.add).then_inc(vec, 1)
            dve.tensor_scalar(mom[:, MEAN, :], mom[:, MEAN, :], 0.5, None, ALU.mult).then_inc(vec, 1)
            dve.wait_ge(vec, 6)
            dve.scalar_tensor_tensor(out=mom[:, TOTAL, :], in0=mom[:, APART2, :], scalar=0.25, in1=mom[:, VAR, :],
                                     op0=ALU.mult, op1=ALU.add).then_inc(vared, 1)
            dve.wait_ge(rstd_ready, 1)
            with dve.Fori(0, T // LANES) as i:
                for u in range(LANES):
                    xt, t = k.x[:, bass.ds(LANES * i + u, 1), :], bass.ds(LANES * i + u, 1)
                    dve.wait_ge(turned, LANES * i + u + 1)
                    dve.tensor_scalar(stage[u][:, :], xt, mom[:, MEAN, t], mom[:, RSTD, t], ALU.subtract, ALU.mult).then_inc(staged, 1)
                    dve.tensor_scalar(xt, xt, mom[:, MEAN, t], mom[:, RSTD, t], ALU.subtract, ALU.mult).then_inc(written, 1)

        @block.gpsimd
        def _(pool):
            pool.wait_ge(vared, 1)
            pool.tensor_tensor(mom[:, RSTD, :], mom[:, TOTAL, :], k.minus_half[:, 0:T], ALU.pow).then_inc(rstd_ready, 1)

        @block.tensor
        def _(pe):
            pe.sem_inc(turned, LANES)
            with pe.Fori(0, T // LANES) as i:
                for u in range(LANES):
                    pe.wait_ge(staged, LANES * i + u + 1)
                    pe.wait_ge(copied, LANES * i + u + 1)
                    pe.transpose(k.ps[u][:, 0:128], stage[u][:, 0:128], k.ident[:, :])
                    pe.transpose(k.ps[u][:, 128:256], stage[u][:, 128:256], k.ident[:, :]).then_inc(turned, 1)

        @block.scalar
        def _(act):
            act.sem_inc(copied, LANES)
            with act.Fori(0, T // LANES) as i:
                for u in range(LANES):
                    act.wait_ge(turned, LANES * i + u + 1 + LANES)
                    act.copy(k.xT[:, :, bass.ds((LANES * i + u) * P, P)],
                             k.ps[u][:, 0:256].rearrange("p (c n) -> p c n", c=2)).then_inc(copied, 1)




class Steps:

    def __init__(self, nc, engine, name, steps):
        self.sem = nc.alloc_semaphore(name)
        by = {"pe": nc.tensor, "act": nc.scalar, "dve": nc.vector, "pool": nc.gpsimd}[engine]
        by.sem_inc(self.sem, 1)
        self.names = steps.split()
        self.per = len(self.names)

    def at(self, i, step):
        return self.per * i + self.names.index(step) + 2

    def turns(self, i):
        return self.per * i + 1


def lane_steps(nc, phase, engine, steps, lanes=2):
    return [Steps(nc, engine, f"{phase}_{engine}{u}", steps) for u in range(lanes)]


def heads3(ap):
    return ap.rearrange("p (h j) -> p h j", j=S)


def l0_attention(nc, k):
    with ExitStack() as ctx:
        systems = Systems(nc, ctx, k)
        delta_scores(nc, k, systems)
        delta_solve(nc, k, systems)
    delta_output(nc, k)


class Systems:
    GROUPS = NB * HEADS // P

    def __init__(self, nc, ctx, k):
        self.k = k
        self.l = ctx.enter_context(nc.sbuf_tensor("dsl", [P, self.GROUPS, S, S], F32))
        self.v = ctx.enter_context(nc.sbuf_tensor("dsv", [P, self.GROUPS, S, HD], F32))
        self.arrived = [nc.alloc_semaphore(f"ds_arrived{u}") for u in range(2)]

    def scratch(self, scr, b):
        return scr[b * S:(b + 1) * S, :].rearrange("j (h d) -> h j d", d=HD)

    def load(self, sp, g):
        k = self.k
        sp.dma_start(self.l[:, g, :, :].rearrange("p i j -> p (i j)"),
                     k.l_scr[8 * g:8 * g + 8, :, :, :].rearrange("b h i j -> (b h) (i j)")).then_inc(self.arrived[g % 2], 16)
        for b in range(8):
            sp.dma_start(self.v[16 * b:16 * b + 16, g, :, :], self.scratch(k.v_scr, 8 * g + b)).then_inc(self.arrived[g % 2], 16)


def delta_scores(nc, k, systems):
    SCALE = HD ** -0.5
    with ExitStack() as ctx:
        def sb(name, shape, dt=F32):
            return ctx.enter_context(nc.sbuf_tensor("d0" + name, shape, dt))
        w = sb("w", [P, 2, 784])
        bb = sb("bb", [P, HEADS])
        xs = [sb(f"xs{u}", [P, 2, P]) for u in range(2)]
        qk = [sb(f"qk{u}", [P, 512]) for u in range(2)]
        t1 = [sb(f"t1{u}", [P, 512]) for u in range(2)]
        t2 = [sb(f"t2{u}", [P, 512]) for u in range(2)]
        v = [sb(f"v{u}", [P, D]) for u in range(2)]
        beta = [sb(f"beta{u}", [P, HEADS]) for u in range(2)]
        qkT = [sb(f"qkT{u}", [P, 4, P]) for u in range(2)]
        kexp = [sb(f"kexp{u}", [P, 2, 2, 8, S]) for u in range(2)]
        sc = [[sb(f"sc{u}{n}", [P, HEADS * S]) for n in range(2)] for u in range(2)]
        pT = [sb(f"pT{u}", [P, HEADS * S]) for u in range(2)]
        mx = [[sb(f"mx{u}{n}", [P, HEADS]) for n in range(2)] for u in range(2)]
        den = [[sb(f"den{u}{n}", [P, HEADS]) for n in range(2)] for u in range(2)]
        loaded, = semaphores(nc, ctx, "d0", "loaded")
        stored = [nc.alloc_semaphore(f"d0_stored{u}") for u in range(2)]
        pe_ = lane_steps(nc, "d0", "pe", "QKV TURNED SCORES0 SCORES1 PT")
        act_ = lane_steps(nc, "d0", "act", "V QKT EXP0 EXP1 PT")
        dve_ = lane_steps(nc, "d0", "dve", "COS SIN ROPED BETA KEXP MASK0 MAX0 MASK1 MAX1 SUB1 REC0 FAC0 LROW SUM1 REC1 PROW")
        pool_ = lane_steps(nc, "d0", "pool", "XS KEXP")
        bank = [[k.ps[4 * u + n] for n in range(4)] for u in range(2)]
        masks = [k.strict, k.causal]
        block = ctx.enter_context(nc.Block("d0_b"))

        @block.sync
        def _(sp):
            sp.dma_start(w[:, :, :], k.a["L0_attn_W"].rearrange("(c p) n -> p c n", p=P)).then_inc(loaded, 16)
            sp.dma_start(bb[:, :], k.a["L0_attn_bb"].partition_broadcast(P)).then_inc(loaded, 16)
            for u in range(2):
                sp.sem_inc(stored[u], 1)

            def store_weights(u, i):
                t = 2 * i + u
                tile_at = slice(t, t + 1) if isinstance(t, int) else bass.ds(t, 1)
                sp.wait_ge(dve_[u].sem, dve_[u].at(i, "LROW"))
                for b in range(2):
                    at = slice(2 * t + b, 2 * t + b + 1) if isinstance(t, int) else bass.ds(2 * t + b, 1)
                    sp.dma_start(k.l_scr[at, :, :, :].rearrange("b h i j -> (b i) h j"),
                                 heads3(sc[u][0][64 * b:64 * b + 64, :])).then_inc(stored[u], 16)
                sp.wait_ge(act_[u].sem, act_[u].at(i, "PT"))
                sp.dma_start(k.p_scr[tile_at, :, :].rearrange("t p n -> (t p) n"), pT[u][:, :]).then_inc(stored[u], 16)

            def tile(u, i, before, after):
                t = 2 * i + u
                rows = slice(t * P, t * P + P) if isinstance(t, int) else bass.ds(t * P, P)
                if isinstance(t, int) and t == T - 2:
                    sp.wait_ge(stored[0], 64 * i + 1)
                    sp.wait_ge(stored[1], 64 * (i - 1) + 16 + 1)
                    for g in range(2):
                        systems.load(sp, g)
                sp.wait_ge(act_[u].sem, act_[u].at(i, "V"))
                sp.dma_start(k.v_scr[rows, :], v[u][:, :]).then_inc(stored[u], 16)
                if before:
                    store_weights(*before)

            store_weights(*staggered(sp, tile))
            for u in range(2):
                sp.wait_ge(stored[u], 64 * (T // 2) + 1)

        @block.gpsimd
        def _(pool):
            def stage(u, i):
                t = 2 * i + u
                columns = slice(t * P, t * P + P) if isinstance(t, int) else bass.ds(t * P, P)
                pool.wait_ge(pe_[u].sem, pe_[u].turns(i))
                pool.tensor_copy(xs[u][:, :, :], k.xT[:, :, columns]).then_inc(pool_[u].sem, 1)

            def tile(u, i, before, after):
                pool.wait_ge(act_[u].sem, act_[u].at(i, "QKT"))
                spread_keys(pool, kexp[u], qkT[u][:, 2:4, :], k.head_mask[:, :], (1,)).then_inc(pool_[u].sem, 1)
                if after:
                    stage(*after)

            stage(0, 0)
            staggered(pool, tile)

        @block.tensor
        def _(pe):
            pe.wait_ge(loaded, 32)

            def project(u, i):
                pe.wait_ge(pool_[u].sem, pool_[u].at(i, "XS"))
                pe.wait_ge(act_[u].sem, act_[u].turns(i))
                for o, lo, hi in ((bank[u][0], 0, 512), (bank[u][1][:, 0:272], 512, 784)):
                    for c in range(2):
                        mm = pe.matmul(o, xs[u][:, c, :], w[:, c, lo:hi], start=(c == 0), stop=(c == 1))
                mm.then_inc(pe_[u].sem, 1)

            def turn(u, i):
                pe.wait_ge(dve_[u].sem, dve_[u].at(i, "ROPED"))
                for c in range(4):
                    mm = pe.transpose(bank[u][2][:, c * P:(c + 1) * P], qk[u][:, c * P:(c + 1) * P], k.ident[:, :])
                mm.then_inc(pe_[u].sem, 1)

            def scores(u, i, n):
                if n == 0:
                    pe.wait_ge(act_[u].sem, act_[u].at(i, "QKT"))
                    pe.wait_ge(dve_[u].sem, dve_[u].at(i, "KEXP"))
                    pe.wait_ge(pool_[u].sem, pool_[u].at(i, "KEXP"))
                queries = qkT[u][:, 2:4, :] if n == 0 else qkT[u][:, 0:2, :]
                score_matmuls(pe, bank[u][2 * n:2 * n + 2], queries, kexp[u]).then_inc(pe_[u].sem, 1)

            def turn_weights(u, i):
                pe.wait_ge(dve_[u].sem, dve_[u].at(i, "PROW"))
                weight_transposes(pe, bank[u][0:2], sc[u][1], k.ident[:, :]).then_inc(pe_[u].sem, 1)

            def tile(u, i, before, after):
                turn(u, i)
                scores(u, i, 0)
                if before:
                    turn_weights(*before)
                scores(u, i, 1)
                if after:
                    project(*after)

            project(0, 0)
            turn_weights(*staggered(pe, tile))

        @block.scalar
        def _(act):
            act.preload_act_table(ACT.Exp)

            def weights_out(u, i):
                act.wait_ge(pe_[u].sem, pe_[u].at(i, "PT"))
                act.copy(pT[u][:, 0:512], bank[u][0])
                act.copy(pT[u][:, 512:1024], bank[u][1]).then_inc(act_[u].sem, 1)

            def tile(u, i, before, after):
                act.wait_ge(pe_[u].sem, pe_[u].at(i, "QKV"))
                act.wait_ge(stored[u], 64 * i + 1)
                act.copy(v[u][:, :], bank[u][1][:, 0:D]).then_inc(act_[u].sem, 1)
                act.wait_ge(pe_[u].sem, pe_[u].at(i, "TURNED"))
                act.copy(qkT[u][:, :, :], bank[u][2].rearrange("p (c n) -> p c n", c=4)).then_inc(act_[u].sem, 1)
                if before:
                    weights_out(*before)
                act.wait_ge(dve_[u].sem, dve_[u].at(i, "MAX0"))
                exponentials(act, sc[u][0], mx[u][0], den[u][0]).then_inc(act_[u].sem, 1)
                act.wait_ge(dve_[u].sem, dve_[u].at(i, "SUB1"))
                act.activation(sc[u][1][:, :], sc[u][1][:, :], ACT.Exp).then_inc(act_[u].sem, 1)

            weights_out(*staggered(act, tile))

        @block.vector
        def _(dve):
            def wait(u, i, step):
                dve.wait_ge(dve_[u].sem, dve_[u].at(i, step))

            dve.wait_ge(loaded, 32)

            def rope(u, i):
                dve.wait_ge(pe_[u].sem, pe_[u].at(i, "QKV"))
                for o, table in ((t1, k.cos), (t2, k.sin)):
                    dve.tensor_tensor(by8(o[u][:, :]), by8(bank[u][0]), angles(table), ALU.mult).then_inc(dve_[u].sem, 1)
                wait(u, i, "SIN")
                rope_sums(dve, qk[u][:, :], t1[u][:, :], t2[u][:, :]).then_inc(dve_[u].sem, 1)
                dve.wait_ge(act_[u].sem, act_[u].at(i, "V"))
                dve.tensor_tensor(beta[u][:, :], bank[u][1][:, D:D + HEADS], bb[:, :], ALU.add).then_inc(dve_[u].sem, 1)

            def mask(u, i, n):
                dve.wait_ge(pe_[u].sem, pe_[u].at(i, f"SCORES{n}"))
                for c in range(2):
                    ins = dve.scalar_tensor_tensor(out=heads3(sc[u][n][:, c * 512:(c + 1) * 512]), in0=heads3(bank[u][2 * n + c]),
                                                   scalar=SCALE, in1=over_heads(masks[n][:, :], 8), op0=ALU.mult, op1=ALU.add)
                ins.then_inc(dve_[u].sem, 1)
                wait(u, i, f"MASK{n}")
                dve.tensor_reduce(mx[u][n][:, :], heads3(sc[u][n][:, :]), AX.X, ALU.max, negate=(n == 0)).then_inc(dve_[u].sem, 1)

            def normalise(u, n):
                dve.tensor_tensor(heads3(sc[u][n][:, :]), heads3(sc[u][n][:, :]), per_head(den[u][n][:, :]), ALU.mult).then_inc(dve_[u].sem, 1)

            def finish_keys(u, i):
                dve.wait_ge(act_[u].sem, act_[u].at(i, "EXP0"))
                dve.reciprocal(den[u][0][:, :], den[u][0][:, :]).then_inc(dve_[u].sem, 1)
                wait(u, i, "REC0")
                dve.scalar_tensor_tensor(out=den[u][0][:, :], in0=den[u][0][:, :], scalar=k.not_first[:, :],
                                         in1=beta[u][:, :], op0=ALU.mult, op1=ALU.mult).then_inc(dve_[u].sem, 1)
                wait(u, i, "FAC0")
                normalise(u, 0)

            def finish_queries(u, i):
                dve.wait_ge(act_[u].sem, act_[u].at(i, "EXP1"))
                dve.tensor_reduce(den[u][1][:, :], heads3(sc[u][1][:, :]), AX.X, ALU.add).then_inc(dve_[u].sem, 1)
                wait(u, i, "SUM1")
                dve.reciprocal(den[u][1][:, :], den[u][1][:, :]).then_inc(dve_[u].sem, 1)
                wait(u, i, "REC1")
                normalise(u, 1)

            def tile(u, i, before, after):
                rope(u, i)
                if before:
                    finish_keys(*before)
                dve.wait_ge(act_[u].sem, act_[u].at(i, "QKT"))
                spread_keys(dve, kexp[u], qkT[u][:, 2:4, :], k.head_mask[:, :], (0,)).then_inc(dve_[u].sem, 1)
                if before:
                    finish_queries(*before)
                mask(u, i, 0)
                mask(u, i, 1)
                wait(u, i, "MAX1")
                dve.tensor_tensor(heads3(sc[u][1][:, :]), heads3(sc[u][1][:, :]), per_head(mx[u][1][:, :]), ALU.subtract).then_inc(dve_[u].sem, 1)

            end = staggered(dve, tile)
            finish_keys(*end)
            finish_queries(*end)


def delta_solve(nc, k, systems):
    GROUPS, lm, vs, arrived = systems.GROUPS, systems.l, systems.v, systems.arrived
    with ExitStack() as ctx:
        def sb(name, shape, dt=F32):
            return ctx.enter_context(nc.sbuf_tensor("ds" + name, shape, dt))
        tmp = [sb(f"tmp{u}", [P, S, HD]) for u in range(2)]
        chain = [nc.alloc_semaphore(f"ds_chain{u}") for u in range(2)]
        stored, = semaphores(nc, ctx, "ds", "stored")
        STEPS = 2 * (S - 1)
        block = ctx.enter_context(nc.Block("ds_b"))

        @block.sync
        def _(sp):
            for g in range(2, GROUPS):
                sp.wait_ge(arrived[g % 2], 16 * 9)
                systems.load(sp, g)
            for g in range(GROUPS):
                sp.wait_ge(chain[g % 2], 1 + STEPS * (g // 2 + 1))
                for b in range(8):
                    sp.dma_start(systems.scratch(k.u_scr, 8 * g + b), vs[16 * b:16 * b + 16, g, :, :]).then_inc(stored, 16)
            sp.wait_ge(stored, 16 * 8 * GROUPS)

        @block.vector
        def _(dve):
            for u in range(2):
                dve.sem_inc(chain[u], 1)
            with dve.Fori(0, GROUPS // 2) as i:
                l_, v_ = ([ap[:, bass.ds(2 * i + u, 1), :, :].rearrange("p g i j -> p (g i) j") for u in range(2)] for ap in (lm, vs))
                for u in range(2):
                    dve.wait_ge(arrived[u], 16 * 9 * (i + 1))
                for j in range(S - 1):
                    n = S - 1 - j
                    for u in range(2):
                        dve.wait_ge(chain[u], i * STEPS + 2 * j + 1)
                        dve.tensor_tensor(tmp[u][:, 0:n, :], l_[u][:, j + 1:S, j].unsqueeze(2).to_broadcast([P, n, HD]),
                                          v_[u][:, j, :].unsqueeze(1).to_broadcast([P, n, HD]), ALU.mult).then_inc(chain[u], 1)
                    for u in range(2):
                        dve.wait_ge(chain[u], i * STEPS + 2 * j + 2)
                        dve.tensor_tensor(v_[u][:, j + 1:S, :], v_[u][:, j + 1:S, :], tmp[u][:, 0:n, :],
                                          ALU.subtract).then_inc(chain[u], 1)


def delta_output(nc, k):
    LANES = 4
    with ExitStack() as ctx:
        def sb(name, shape, dt=F32):
            return ctx.enter_context(nc.sbuf_tensor("do" + name, shape, dt))
        w = sb("w", [P, 2, D])
        pT = [sb(f"pT{u}", [P, 8, P]) for u in range(LANES)]
        ud = [sb(f"ud{u}", [P, 2, D]) for u in range(LANES)]
        o = [sb(f"o{u}", [P, D]) for u in range(LANES)]
        oT = [sb(f"oT{u}", [P, 2, P]) for u in range(LANES)]
        loaded, = semaphores(nc, ctx, "do", "loaded")
        arrived = [nc.alloc_semaphore(f"do_arrived{u}") for u in range(LANES)]
        pe_ = lane_steps(nc, "do", "pe", "O OT Y", LANES)
        act_ = lane_steps(nc, "do", "act", "O OT", LANES)
        dve_ = lane_steps(nc, "do", "dve", "UBD Y", LANES)
        bank = [[k.ps[2 * u + n] for n in range(2)] for u in range(LANES)]
        block = ctx.enter_context(nc.Block("do_b"))

        @block.sync
        def _(sp):
            sp.dma_start(w[:, :, :], k.a["L0_attn_Wo"].rearrange("(c p) n -> p c n", p=P)).then_inc(loaded, 16)
            with sp.Fori(0, T // LANES) as i:
                for u in range(LANES):
                    t = LANES * i + u
                    sp.wait_ge(pe_[u].sem, pe_[u].turns(i))
                    sp.dma_start(pT[u][:, :, :].rearrange("p c n -> p (c n)"),
                                 k.p_scr[bass.ds(t, 1), :, :].rearrange("t p n -> (t p) n")).then_inc(arrived[u], 16)
                    for r in range(2):
                        sp.dma_start(ud[u][64 * r:64 * r + 64, :, :],
                                     k.u_scr[bass.ds(t * P, P), :].rearrange("(b j) n -> j b n", b=2)).then_inc(arrived[u], 16)

        @block.vector
        def _(dve):
            with dve.Fori(0, T // LANES) as i:
                for u in range(LANES):
                    dve.wait_ge(arrived[u], 48 * (i + 1))
                    dve.tensor_tensor(ud[u][:, :, :].rearrange("p b (h d) -> p b h d", d=HD),
                                      ud[u][:, :, :].rearrange("p b (h d) -> p b h d", d=HD),
                                      k.parity[:, :].unsqueeze(1).unsqueeze(3).to_broadcast([P, 2, HEADS, HD]),
                                      ALU.mult).then_inc(dve_[u].sem, 1)
                for u in range(LANES):
                    xt = k.x[:, bass.ds(LANES * i + u, 1), :].rearrange("p t d -> p (t d)")
                    dve.wait_ge(pe_[u].sem, pe_[u].at(i, "Y"))
                    dve.tensor_tensor(xt, xt, bank[u][0][:, 0:D], ALU.add).then_inc(dve_[u].sem, 1)

        @block.tensor
        def _(pe):
            pe.wait_ge(loaded, 16)
            with pe.Fori(0, T // LANES) as i:
                for u in range(LANES):
                    pe.wait_ge(dve_[u].sem, dve_[u].at(i, "UBD"))
                    for c in range(8):
                        mm = pe.matmul(bank[u][0][:, 64 * c:64 * c + 64].rearrange("p (b n) -> p b n", b=2), pT[u][:, c, :],
                                       ud[u][:, :, 32 * c:32 * c + 32], start=True, stop=True)
                    mm.then_inc(pe_[u].sem, 1)
                for u in range(LANES):
                    pe.wait_ge(act_[u].sem, act_[u].at(i, "O"))
                    for c in range(2):
                        mm = pe.transpose(bank[u][1][:, c * P:(c + 1) * P], o[u][:, c * P:(c + 1) * P], k.ident[:, :])
                    mm.then_inc(pe_[u].sem, 1)
                for u in range(LANES):
                    pe.wait_ge(act_[u].sem, act_[u].at(i, "OT"))
                    pe.wait_ge(dve_[u].sem, dve_[u].turns(i))
                    for c in range(2):
                        mm = pe.matmul(bank[u][0][:, 0:D], oT[u][:, c, :], w[:, c, :], start=(c == 0), stop=(c == 1))
                    mm.then_inc(pe_[u].sem, 1)

        @block.scalar
        def _(act):
            with act.Fori(0, T // LANES) as i:
                for u in range(LANES):
                    act.wait_ge(pe_[u].sem, pe_[u].at(i, "O"))
                    for b in range(2):
                        r = slice(64 * b, 64 * b + 64)
                        ins = act.copy(o[u][r, :].rearrange("p (c n) -> p c n", c=8),
                                       bank[u][0][r, :].rearrange("p (c b n) -> p c b n", b=2, n=32)[:, :, b, :])
                    ins.then_inc(act_[u].sem, 1)
                for u in range(LANES):
                    act.wait_ge(pe_[u].sem, pe_[u].at(i, "OT"))
                    act.copy(oT[u][:, :, :], bank[u][1][:, 0:D].rearrange("p (c n) -> p c n", c=2)).then_inc(act_[u].sem, 1)


def row_slice(b):
    return slice(64 * b, 64 * b + 64)


def tile_rows(ap, t):
    at = slice(t, t + 1) if isinstance(t, int) else bass.ds(t, 1)
    return ap[:, at, :].rearrange("p t d -> p (t d)")


def over_heads(ap, n=HEADS):
    return ap.unsqueeze(1).to_broadcast([P, n, S])


def per_head(ap, n=S):
    return ap.unsqueeze(2).to_broadcast([P, HEADS, n])


def spread_keys(eng, out, keys, head_mask, halves=(0, 1)):
    for c in halves:
        ins = eng.tensor_tensor(
            out[:, c, :, :, :],
            keys[:, c, :].rearrange("p (b j) -> p b j", b=2).unsqueeze(2).to_broadcast([P, 2, 8, S]),
            head_mask.unsqueeze(1).unsqueeze(3).to_broadcast([P, 2, 8, S]), ALU.mult)
    return ins


def score_matmuls(pe, banks, queries, keys):
    for b in range(2):
        for c in range(2):
            mm = pe.matmul(banks[c][row_slice(b), :], queries[:, c, row_slice(b)], keys[:, c, b, :, :],
                           start=True, stop=True)
    return mm


def weight_transposes(pe, banks, weights, ident):
    for c in range(8):
        mm = pe.transpose(banks[c // 4][:, (c % 4) * P:(c % 4 + 1) * P], weights[:, c * P:(c + 1) * P], ident)
    return mm


def value_matmuls(pe, bank, weights_t, values):
    for c in range(8):
        mm = pe.matmul(bank[:, 64 * c:64 * c + 64].rearrange("p (b n) -> p b n", b=2), weights_t[:, c, :],
                       values[:, :, 32 * c:32 * c + 32], start=True, stop=True)
    return mm


def own_batch(bank, b):
    return bank[row_slice(b), :].rearrange("p (c b h d) -> p c b h d", b=2, h=2, d=HD)[:, :, b, :, :]


def values_by_parity(eng, out, values, parity):
    return eng.tensor_tensor(out[:, :, :].rearrange("p b (h d) -> p b h d", d=HD), values.rearrange("p b (h d) -> p b h d", d=HD),
                             parity.unsqueeze(1).unsqueeze(3).to_broadcast([P, 2, HEADS, HD]), ALU.mult)


def rope_sums(eng, out, by_cos, by_sin):
    c, s, o = (a.rearrange("p (n f d) -> p n f d", f=2, d=8) for a in (by_cos, by_sin, out))
    eng.tensor_tensor(o[:, :, 0, :], c[:, :, 0, :], s[:, :, 1, :], ALU.subtract)
    return eng.tensor_tensor(o[:, :, 1, :], c[:, :, 1, :], s[:, :, 0, :], ALU.add)


def angles(table):
    return table[:, :].unsqueeze(1).to_broadcast([P, 64, 8])


def by8(ap):
    return ap.rearrange("p (n d) -> p n d", d=8)


def exponentials(act, weights, minus_max, sums):
    for h in range(HEADS):
        here = weights[:, h * S:(h + 1) * S]
        ins = act.activation(here, here, ACT.Exp, bias=minus_max[:, h:h + 1], accum_out=sums[:, h:h + 1])
    return ins


def staggered(eng, tile):
    last = T // 2 - 1
    tile(0, 0, None, (1, 0))
    tile(1, 0, (0, 0), (0, 1))
    with eng.Fori(1, last) as i:
        tile(0, i, (1, i - 1), (1, i))
        tile(1, i, (0, i), (0, i + 1))
    tile(0, last, (1, last - 1), (1, last))
    tile(1, last, (0, last), None)
    return 1, last


def l0_cross(nc, k):
    LANES = 4
    with ExitStack() as ctx:
        def sb(name, shape, dt=F32):
            return ctx.enter_context(nc.sbuf_tensor("c0" + name, shape, dt))
        xs = [sb(f"xs{u}", [P, D]) for u in range(LANES)]
        cs = [sb(f"cs{u}", [P, D]) for u in range(LANES)]
        cT = [sb(f"cT{u}", [P, 2, P]) for u in range(LANES)]
        sig = [sb(f"sig{u}", [P, 2, 2, D]) for u in range(LANES)]
        arrived = [nc.alloc_semaphore(f"c0_arrived{u}") for u in range(LANES)]
        pe_ = lane_steps(nc, "c0", "pe", "S0 S1 O", LANES)
        act_ = lane_steps(nc, "c0", "act", "SIG0 SIG1", LANES)
        dve_ = lane_steps(nc, "c0", "dve", "X", LANES)
        pool_ = lane_steps(nc, "c0", "pool", "XS", LANES)
        bank = [[k.ps[2 * u + n] for n in range(2)] for u in range(LANES)]
        block = ctx.enter_context(nc.Block("c0_b"))

        @block.sync
        def _(sp):
            with sp.Fori(0, T // LANES) as i:
                for u in range(LANES):
                    t = LANES * i + u
                    sp.wait_ge(pe_[u].sem, pe_[u].turns(i))
                    sp.dma_start(cs[u][:, :], k.ctx_rows[bass.ds(t * P, P), :]).then_inc(arrived[u], 16)
                    sp.dma_start(cT[u][:, :, :], k.a["ctxT"].rearrange("(c p) n -> p c n", p=P)[:, :, bass.ds(t * P, P)]).then_inc(arrived[u], 16)

        @block.gpsimd
        def _(pool):
            with pool.Fori(0, T // LANES) as i:
                for u in range(LANES):
                    pool.wait_ge(pe_[u].sem, pe_[u].turns(i))
                    pool.tensor_copy(xs[u][:, :], k.x[:, bass.ds(LANES * i + u, 1), :]).then_inc(pool_[u].sem, 1)

        @block.tensor
        def _(pe):
            with pe.Fori(0, T // LANES) as i:
                for u in range(LANES):
                    pe.wait_ge(arrived[u], 32 * (i + 1))
                    pe.wait_ge(pool_[u].sem, pool_[u].at(i, "XS"))
                    for b in range(2):
                        r = slice(64 * b, 64 * b + 64)
                        if b == 0:
                            pe.wait_ge(act_[u].sem, act_[u].turns(i))
                            pe.wait_ge(dve_[u].sem, dve_[u].turns(i))
                        for c in range(2):
                            mm = pe.matmul(bank[u][b][:, c * D:(c + 1) * D], xs[u][r, c * P:(c + 1) * P], cs[u][r, :],
                                           start=True, stop=True)
                        mm.then_inc(pe_[u].sem, 1)
                for u in range(LANES):
                    for b in range(2):
                        pe.wait_ge(act_[u].sem, act_[u].at(i, f"SIG{b}"))
                        for c in range(2):
                            mm = pe.matmul(bank[u][0][64 * b:64 * b + 64, 0:D], cT[u][:, c, 64 * b:64 * b + 64], sig[u][:, b, c, :],
                                           start=(c == 0), stop=(c == 1))
                    mm.then_inc(pe_[u].sem, 1)

        @block.scalar
        def _(act):
            act.preload_act_table(ACT.Sigmoid)
            with act.Fori(0, T // LANES) as i:
                for u in range(LANES):
                    act.wait_ge(pe_[u].sem, pe_[u].turns(i))
                    for b in range(2):
                        act.wait_ge(pe_[u].sem, pe_[u].at(i, f"S{b}"))
                        act.activation(sig[u][:, b, :, :].rearrange("p c m -> p (c m)"), bank[u][b][:, :], ACT.Sigmoid,
                                       scale=S ** -0.5).then_inc(act_[u].sem, 1)

        @block.vector
        def _(dve):
            with dve.Fori(0, T // LANES) as i:
                for u in range(LANES):
                    xt = k.x[:, bass.ds(LANES * i + u, 1), :].rearrange("p t d -> p (t d)")
                    dve.wait_ge(pe_[u].sem, pe_[u].at(i, "O"))
                    dve.tensor_tensor(xt, xt, bank[u][0][:, 0:D], ALU.add).then_inc(dve_[u].sem, 1)


COMB_ROWS = 96


def moe_route(nc, k, name, w, loaded, E, TOP, renorm, times, shared_gate=False, rows=None):
    EC = E + 1 if shared_gate else E
    with ExitStack() as ctx:
        def sb(n, shape, dt=F32):
            return ctx.enter_context(nc.sbuf_tensor(name + n, shape, dt))
        xs = [sb(f"xs{u}", [P, 2, 4 * P]) for u in range(2)]
        pr = [sb(f"pr{u}", [P, 4, EC]) for u in range(2)]
        cb = [sb(f"cb{u}", [P, 4, EC]) for u in range(2)]
        rep = [sb(f"rep{u}", [P, 4, E]) for u in range(2)]
        top = [sb(f"top{u}", [P, 4, 8]) for u in range(2)]
        m4 = [sb(f"m4{u}", [P, 4]) for u in range(2)]
        parts = [sb(f"parts{u}", [P, 4, COMB_ROWS], BF16) for u in range(2)]
        rest = [sb(f"rest{u}", [P, 4, EC]) for u in range(2)]
        identb = sb("identb", [P, P], BF16)
        ready, = semaphores(nc, ctx, name, "ready")
        carrier = sb("carrier", [P, 1])
        pe_ = lane_steps(nc, name, "pe", "LOGITS COMBT")
        act_ = lane_steps(nc, name, "act", "EXP COMBT")
        dve_ = lane_steps(nc, name, "dve", "MAX SUB SUM REC PROBS TOP REST REP COMB" + (" WSUM WREC WNORM" if renorm else "")
                          + (" GATE GATED" if shared_gate else "") + (" ROWS" if rows is not None else "") + " HIGH REST1 MIDDLE REST2 LOW")
        pool_ = lane_steps(nc, name, "pool", "XS")
        bank = [[k.ps[4 * u + n] for n in range(4)] for u in range(2)]
        block = ctx.enter_context(nc.Block(name + "_b"))

        @block.gpsimd
        def _(pool):
            with pool.Fori(0, T // 8) as i:
                for u in range(2):
                    pool.wait_ge(pe_[u].sem, pe_[u].turns(i))
                    pool.tensor_copy(xs[u][:, :, :], k.xT[:, :, bass.ds((2 * i + u) * 4 * P, 4 * P)]).then_inc(pool_[u].sem, 1)

        @block.tensor
        def _(pe):
            pe.wait_ge(loaded, 16)
            pe.wait_ge(ready, 1)
            with pe.Fori(0, T // 8) as i:
                for u in range(2):
                    pe.wait_ge(pool_[u].sem, pool_[u].at(i, "XS"))
                    pe.wait_ge(dve_[u].sem, dve_[u].turns(i))
                    for t in range(4):
                        for c in range(2):
                            mm = pe.matmul(bank[u][0][:, t * EC:(t + 1) * EC], xs[u][:, c, t * P:(t + 1) * P], w[:, c, :],
                                           start=(c == 0), stop=(c == 1))
                    mm.then_inc(pe_[u].sem, 1)
                for u in range(2):
                    pe.wait_ge(dve_[u].sem, dve_[u].turns(i + 1))
                    pe.wait_ge(act_[u].sem, act_[u].turns(i))
                    for t in range(4):
                        mm = pe.transpose(bank[u][1].bitcast(BF16)[0:COMB_ROWS, t * P:(t + 1) * P], parts[u][:, t, :], identb[:, :])
                    mm.then_inc(pe_[u].sem, 1)

        @block.scalar
        def _(act):
            act.preload_act_table(ACT.Exp)
            with act.Fori(0, T // 8) as i:
                for u in range(2):
                    act.wait_ge(dve_[u].sem, dve_[u].at(i, "SUB"))
                    act.activation(pr[u][:, :, :], pr[u][:, :, :], ACT.Exp).then_inc(act_[u].sem, 1)
                for u in range(2):
                    act.wait_ge(pe_[u].sem, pe_[u].at(i, "COMBT"))
                    act.copy(k.combT[:, bass.ds((2 * i + u) * 4 * P, 4 * P)], bank[u][1].bitcast(BF16)[0:COMB_ROWS, 0:4 * P]).then_inc(act_[u].sem, 1)

        @block.vector
        def _(dve):
            dve.tensor_copy(identb[:, :], k.ident[:, :]).then_inc(ready, 1)
            for u in range(2):
                dve.memset(parts[u][:, :, :], 0.0).then_inc(ready, 1)
            dve.wait_ge(ready, 3)
            with dve.Fori(0, T // 8) as i:
                for u in range(2):
                    def wait(step, u=u):
                        dve.wait_ge(dve_[u].sem, dve_[u].at(i, step))

                    lg = bank[u][0][:, 0:4 * EC].rearrange("p (t e) -> p t e", e=EC)
                    probs, comb = pr[u][:, :, 0:E], cb[u][:, :, 0:E]
                    spread = m4[u][:, :].unsqueeze(2).to_broadcast([P, 4, E])
                    dve.wait_ge(pe_[u].sem, pe_[u].at(i, "LOGITS"))
                    dve.tensor_reduce(m4[u][:, :], lg[:, :, 0:E], AX.X, ALU.max).then_inc(dve_[u].sem, 1)
                    wait("MAX")
                    if shared_gate:
                        dve.tensor_scalar(pr[u][:, :, E], lg[:, :, E], -1.0, None, ALU.mult)
                    dve.tensor_tensor(probs, lg[:, :, 0:E], spread, ALU.subtract).then_inc(dve_[u].sem, 1)
                for u in range(2):
                    probs, comb = pr[u][:, :, 0:E], cb[u][:, :, 0:E]
                    spread = m4[u][:, :].unsqueeze(2).to_broadcast([P, 4, E])

                    def wait(step, u=u):
                        dve.wait_ge(dve_[u].sem, dve_[u].at(i, step))

                    dve.wait_ge(act_[u].sem, act_[u].at(i, "EXP"))
                    dve.tensor_reduce(m4[u][:, :], probs, AX.X, ALU.add).then_inc(dve_[u].sem, 1)
                    wait("SUM")
                    dve.reciprocal(m4[u][:, :], m4[u][:, :]).then_inc(dve_[u].sem, 1)
                    wait("REC")
                    dve.tensor_tensor(probs, probs, spread, ALU.mult).then_inc(dve_[u].sem, 1)
                    wait("PROBS")
                    dve.memset(carrier[:, :], 0.0)
                    for t in range(4):
                        ins = dve.max(top[u][:, t, :], pr[u][:, t, 0:E])
                    ins.then_inc(dve_[u].sem, 1)
                    wait("TOP")
                    dve.memset(top[u][:, :, TOP:8], -1.0).then_inc(dve_[u].sem, 1)
                    wait("REST")
                    dve.memset(carrier[:, :], 0.0)
                    for t in range(4):
                        ins = dve.match_replace(out=rep[u][:, t, :], in_to_replace=top[u][:, t, :],
                                                in_values=pr[u][:, t, 0:E], imm_value=0.0)
                    ins.then_inc(dve_[u].sem, 1)
                    wait("REP")
                    dve.tensor_tensor(comb, probs, rep[u][:, :, :], ALU.subtract).then_inc(dve_[u].sem, 1)
                    if renorm:
                        wait("COMB")
                        dve.tensor_reduce(m4[u][:, :], comb, AX.X, ALU.add).then_inc(dve_[u].sem, 1)
                        wait("WSUM")
                        dve.reciprocal(m4[u][:, :], m4[u][:, :]).then_inc(dve_[u].sem, 1)
                        wait("WREC")
                        if times != 1.0:
                            for t in range(4):
                                ins = dve.tensor_scalar(cb[u][:, t, 0:E], cb[u][:, t, 0:E], m4[u][:, t:t + 1], times, ALU.mult, ALU.mult)
                            ins.then_inc(dve_[u].sem, 1)
                        else:
                            dve.tensor_tensor(comb, comb, spread, ALU.mult).then_inc(dve_[u].sem, 1)
                    if rows is not None:
                        wait("WNORM")
                        dve.tensor_copy(rows[:, bass.ds(4 * (2 * i + u), 4), :], comb).then_inc(dve_[u].sem, 1)
                    if shared_gate:
                        wait("WNORM")
                        dve.tensor_scalar(pr[u][:, :, E], pr[u][:, :, E], 1.0, None, ALU.add).then_inc(dve_[u].sem, 1)
                        wait("GATE")
                        dve.reciprocal(cb[u][:, :, E], pr[u][:, :, E]).then_inc(dve_[u].sem, 1)
                    dve.wait_ge(dve_[u].sem, dve_[u].at(i, "HIGH") - 1)
                    high, middle, low = (parts[u][:, :, 32 * n:32 * n + EC] for n in range(3))
                    dve.wait_ge(pe_[u].sem, pe_[u].turns(i))
                    dve.tensor_copy(high, cb[u][:, :, :]).then_inc(dve_[u].sem, 1)
                    wait("HIGH")
                    dve.tensor_tensor(rest[u][:, :, :], cb[u][:, :, :], high, ALU.subtract).then_inc(dve_[u].sem, 1)
                    wait("REST1")
                    dve.tensor_copy(middle, rest[u][:, :, :]).then_inc(dve_[u].sem, 1)
                    wait("MIDDLE")
                    dve.tensor_tensor(rest[u][:, :, :], rest[u][:, :, :], middle, ALU.subtract).then_inc(dve_[u].sem, 1)
                    wait("REST2")
                    dve.tensor_copy(low, rest[u][:, :, :]).then_inc(dve_[u].sem, 1)


class Experts:

    def __init__(self, nc, ctx, k, name, weights, n_exp, n_shared):
        gname, uname, dname, sname = weights
        self.n_exp = n_exp
        self.widths = [P] * n_exp + list(n_shared)
        self.chunks = len(self.widths)
        self.starts = [sum(self.widths[:c]) for c in range(self.chunks)]
        hidden = sum(self.widths)

        def sb(n, shape):
            return ctx.enter_context(nc.sbuf_tensor(name + n, shape, F32))
        self.gate, self.up = sb("wg", [P, 2, hidden]), sb("wu", [P, 2, hidden])
        self.down = sb("wd", [P, self.chunks, D])
        self.sel = sb("sel", [COMB_ROWS, hidden])
        self.selb = ctx.enter_context(nc.sbuf_tensor(name + "selb", [COMB_ROWS, hidden], BF16))
        self.loaded = nc.alloc_semaphore(name + "_loaded")
        halves = "(c p) n -> p c n"
        nc.sync.dma_start(self.gate[:, :, :], k.a[gname].rearrange(halves, p=P)).then_inc(self.loaded, 16)
        nc.sync.dma_start(self.up[:, :, :], k.a[uname].rearrange(halves, p=P)).then_inc(self.loaded, 16)
        self.sel_loaded, self.sel_ready = semaphores(nc, ctx, name, "sel_loaded sel_ready")
        nc.sync.dma_start(self.sel[:, :], k.a[sname]).then_inc(self.sel_loaded, 16)
        full = self.widths.count(P)
        nc.sync.dma_start(self.down[:, 0:full, :], k.a[dname][0:full * P, :].rearrange(halves, p=P)).then_inc(self.loaded, 16)
        for c in range(full, self.chunks):
            rows = slice(self.starts[c], self.starts[c] + self.widths[c])
            nc.sync.dma_start(self.down[0:self.widths[c], c, :], k.a[dname][rows, :]).then_inc(self.loaded, 16)
        self.loads = 16 * (3 + self.chunks - full)


def moe_experts(nc, k, name, experts, shared_by_row, shared_times):
    widths, starts, NC = experts.widths, experts.starts, experts.chunks
    wg, wu, wd, sel = experts.gate, experts.up, experts.down, experts.selb
    scaled = [c < experts.n_exp or shared_by_row for c in range(NC)]
    GT = 4 * P
    with ExitStack() as ctx:
        def sb(n, shape, dt=F32):
            return ctx.enter_context(nc.sbuf_tensor(name + n, shape, dt))
        h = sb("h", [P, NC, GT])
        sg = [sb(f"sg{u}", [P, GT]) for u in range(2)]
        gated, upped, silu_done, product = semaphores(nc, ctx, name, "gated upped silu_done product")
        h_done, down_done, x_added = semaphores(nc, ctx, name, "h_done down_done x_added")
        gbank, ubank, cbank, ybank = k.ps[0:2], k.ps[2:4], k.ps[4:6], k.ps[6:8]
        n_scaled = sum(scaled)
        block = ctx.enter_context(nc.Block(name + "_b"))

        @block.tensor
        def _(pe):
            pe.sem_inc(down_done, 1)
            pe.wait_ge(experts.loaded, experts.loads)
            pe.wait_ge(experts.sel_ready, 1)
            with pe.Fori(0, N // GT) as i:
                xg = [k.xT[:, c, bass.ds(i * GT, GT)] for c in range(2)]
                cg = k.combT[:, bass.ds(i * GT, GT)]
                for c in range(NC):
                    w_, s_, u = widths[c], starts[c], c % 2
                    pe.wait_ge(h_done, NC * i + max(c - 1, 0) + 1)
                    for kk in range(2):
                        mm = pe.matmul(gbank[u][0:w_, :], wg[:, kk, s_:s_ + w_], xg[kk], start=(kk == 0), stop=(kk == 1))
                    mm.then_inc(gated, 1)
                    for kk in range(2):
                        mm = pe.matmul(ubank[u][0:w_, :], wu[:, kk, s_:s_ + w_], xg[kk], start=(kk == 0), stop=(kk == 1))
                    if scaled[c]:
                        mm = pe.matmul(cbank[u][0:w_, :], sel[:, s_:s_ + w_], cg, start=True, stop=True)
                    mm.then_inc(upped, 1)
                for t in range(4):
                    pe.wait_ge(x_added, 4 * i + max(t - 1, 0) + 1)
                    for c in range(NC):
                        if t == 0:
                            pe.wait_ge(h_done, NC * i + c + 2)
                        mm = pe.matmul(ybank[t % 2][:, 0:D], h[0:widths[c], c, t * P:(t + 1) * P], wd[0:widths[c], c, :],
                                       start=(c == 0), stop=(c == NC - 1))
                    mm.then_inc(down_done, 1)

        @block.scalar
        def _(act):
            act.preload_act_table(ACT.Silu)
            act.wait_ge(experts.sel_loaded, 16)
            act.copy(experts.selb[:, :], experts.sel[:, :]).then_inc(experts.sel_ready, 1)
            with act.Fori(0, N // GT) as i:
                for c in range(NC):
                    act.wait_ge(gated, NC * i + c + 1)
                    act.wait_ge(h_done, NC * i + max(c - 1, 0) + 1)
                    act.activation(sg[c % 2][0:widths[c], :], gbank[c % 2][0:widths[c], :], ACT.Silu).then_inc(silu_done, 1)

        @block.vector
        def _(dve):
            dve.sem_inc(h_done, 1)
            dve.sem_inc(x_added, 1)
            with dve.Fori(0, N // GT) as i:
                dve.wait_ge(down_done, 4 * i + 1)
                for c in range(NC):
                    w_, u = widths[c], c % 2
                    dve.wait_ge(silu_done, NC * i + c + 1)
                    dve.wait_ge(upped, NC * i + c + 1)
                    if scaled[c]:
                        dve.tensor_tensor(sg[u][0:w_, :], sg[u][0:w_, :], ubank[u][0:w_, :], ALU.mult).then_inc(product, 1)
                        dve.wait_ge(product, n_scaled * i + sum(scaled[:c]) + 1)
                        dve.tensor_tensor(h[0:w_, c, :], sg[u][0:w_, :], cbank[u][0:w_, :], ALU.mult).then_inc(h_done, 1)
                    else:
                        dve.scalar_tensor_tensor(out=h[0:w_, c, :], in0=sg[u][0:w_, :], scalar=shared_times, in1=ubank[u][0:w_, :],
                                                 op0=ALU.mult, op1=ALU.mult).then_inc(h_done, 1)
                for t in range(4):
                    xt = k.x[:, bass.ds(4 * i + t, 1), :].rearrange("p t d -> p (t d)")
                    dve.wait_ge(down_done, 4 * i + t + 2)
                    dve.tensor_tensor(xt, xt, ybank[t % 2][:, 0:D], ALU.add).then_inc(x_added, 1)


def feed_forward(nc, k, name, router, E, TOP, renorm, times, weights, n_exp, n_shared, shared_gate=False, shared_times=1.0):
    rows = E + 1 if shared_gate else E
    with ExitStack() as ctx:
        k.combT = ctx.enter_context(nc.sbuf_tensor(name + "combT", [COMB_ROWS, N], BF16))
        w = ctx.enter_context(nc.sbuf_tensor(name + "wr", [P, 2, rows], F32))
        loaded, = semaphores(nc, ctx, name, "router_loaded")
        nc.sync.dma_start(w[:, :, :], k.a[router].rearrange("(c p) n -> p c n", p=P)).then_inc(loaded, 16)
        experts = Experts(nc, ctx, k, name, weights, n_exp, n_shared)
        moe_route(nc, k, "r" + name, w, loaded, E, TOP, renorm, times, shared_gate=shared_gate)
        moe_experts(nc, k, name, experts, shared_gate, shared_times)


def l0_ffn(nc, k):
    feed_forward(nc, k, "f0", "L0_router", 8, 2, False, 1.0, ("L0_g", "L0_u", "L0_d", "sel176"), 11, (128, 128, 96))


def l2_ffn(nc, k):
    feed_forward(nc, k, "f2", "L2_router", 8, 2, True, 1.0, ("L2_g", "L2_u", "L2_d", "sel176s"), 11, (128, 128, 96), shared_gate=True)


def l3_ffn(nc, k):
    TOP = 4
    feed_forward(nc, k, "f3", "L3_ffn_w_router", 16, TOP, True, TOP / (TOP + 1), ("L3_g", "L3_u", "L3_d", "sel128"), 16, (128,) * 4,
                 shared_times=1.0 / (TOP + 1))


KT = KEYS // P
QG = 4 * P
STACK = 6 * HD


def l1_attention(nc, k):
    split_to_dram(nc, k)
    with nc.sbuf_tensor("a1o", [P, T, D], F32) as o:
        key_attention(nc, k, o)
        project_add(nc, k, "a1p", o, "L1_Wo")


def split_to_dram(nc, k):
    with ExitStack() as ctx:
        def sb(name, shape, dt=F32):
            return ctx.enter_context(nc.sbuf_tensor("s1" + name, shape, dt))
        CH = 1024
        LANES = range(4)
        w = sb("w", [P, 2, D])
        raw = [sb(f"raw{n}", [P, CH]) for n in LANES]
        part = [[sb(f"part{n}{m}", [P, CH], BF16) for m in range(3)] for n in LANES]
        loaded, = semaphores(nc, ctx, "s1", "loaded")
        arrived = [nc.alloc_semaphore(f"s1_arrived{n}") for n in LANES]
        stored = [nc.alloc_semaphore(f"s1_stored{n}") for n in LANES]
        pe_ = lane_steps(nc, "s1", "pe", "Q", 4)
        act_ = lane_steps(nc, "s1", "act", "HIGH LOW", 4)
        dve_ = lane_steps(nc, "s1", "dve", "REST1 MIDDLE REST2", 4)
        qbank = [k.psum[:, 2 * n:2 * n + 2, :] for n in LANES]
        q = [b.rearrange("p c n -> p (c n)") for b in qbank]
        block = ctx.enter_context(nc.Block("s1_b"))
        NK, NQ = KEYS // CH // 2, N // CH // 2

        def chunk(n, i):
            return bass.ds((2 * i + n // 2) * CH, CH)

        def features(n):
            return slice(n % 2 * P, n % 2 * P + P)

        def store(eng, i, turn, scr):
            for n in LANES:
                for m in range(3):
                    into = scr[m, features(n), chunk(n, i)]
                    eng.wait_ge(act_[n].sem, act_[n].at(turn, "LOW"))
                    eng.dma_start(into, part[n][m][:, :]).then_inc(stored[n], 16)

        @block.sync
        def _(sp):
            sp.dma_start(w[:, :, :], k.a["L1_Wq"].rearrange("(c p) n -> p c n", p=P)).then_inc(loaded, 16)

            def load(n, i):
                sp.dma_start(raw[n][:, :], k.a["L1_kT"][features(n), chunk(n, i)]).then_inc(arrived[n], 16)

            for n in LANES:
                load(n, 0)
            for i in range(NK):
                store(sp, i, i, k.k_scr)
                if i + 1 < NK:
                    for n in LANES:
                        load(n, i + 1)
            for i in range(NQ):
                store(sp, i, i + NK, k.q_scr)
            for n in LANES:
                sp.wait_ge(stored[n], 16 * 3 * (NK + NQ))

        @block.tensor
        def _(pe):
            pe.wait_ge(loaded, 16)
            for i in range(NQ):
                for n in LANES:
                    if i:
                        pe.wait_ge(dve_[n].sem, dve_[n].turns(i + NK))
                    for half in range(2):
                        lo = (2 * i + n // 2) * CH + half * 512
                        for c in range(2):
                            mm = pe.matmul(qbank[n][:, half, :], w[:, c, features(n)], k.xT[:, c, lo:lo + 512],
                                           start=(c == 0), stop=(c == 1))
                    mm.then_inc(pe_[n].sem, 1)

        @block.scalar
        def _(act):
            for i in range(NK + NQ):
                for n in LANES:
                    if i < NK:
                        act.wait_ge(arrived[n], 16 * (i + 1))
                    else:
                        act.wait_ge(pe_[n].sem, pe_[n].at(i - NK, "Q"))
                    if i:
                        act.wait_ge(stored[n], 16 * 3 * i)
                    act.copy(part[n][0][:, :], raw[n][:, :] if i < NK else q[n]).then_inc(act_[n].sem, 1)
                for n in LANES:
                    act.wait_ge(dve_[n].sem, dve_[n].at(i, "REST2"))
                    act.copy(part[n][2][:, :], raw[n][:, :]).then_inc(act_[n].sem, 1)

        @block.vector
        def _(dve):
            for i in range(NK + NQ):
                for n in LANES:
                    dve.wait_ge(act_[n].sem, act_[n].at(i, "HIGH"))
                    dve.tensor_tensor(raw[n][:, :], raw[n][:, :] if i < NK else q[n], part[n][0][:, :], ALU.subtract).then_inc(dve_[n].sem, 1)
                    dve.wait_ge(dve_[n].sem, dve_[n].at(i, "REST1"))
                    dve.tensor_copy(part[n][1][:, :], raw[n][:, :]).then_inc(dve_[n].sem, 1)
                    dve.wait_ge(dve_[n].sem, dve_[n].at(i, "MIDDLE"))
                    dve.tensor_tensor(raw[n][:, :], raw[n][:, :], part[n][1][:, :], ALU.subtract).then_inc(dve_[n].sem, 1)


def key_attention(nc, k, o):
    RING = 4
    AM = 4 * (KEYS // QG)
    LAG = 4
    SUMS_AT, ROWS_AT = 8, 18
    SPLITS = 6
    BODIES = 4 * HEADS
    with ExitStack() as ctx:
        def sb(name, shape, dt=F32):
            return ctx.enter_context(nc.sbuf_tensor("k1" + name, shape, dt))
        identb = sb("identb", [P, P], BF16)
        kst = [sb(f"kst{r}", [STACK + 3, KEYS], BF16) for r in range(RING)]
        qst = [sb(f"qst{r}", [STACK + 3, N], BF16) for r in range(RING)]
        v = sb("v", [P, KT, D])
        vst = [sb(f"vst{u}", [P, KT, 32]) for u in range(2)]
        ex = [sb(f"ex{m}", [P, QG]) for m in range(8)]
        osb = sb("osb", [P, QG])
        pm = sb("pm", [P, 4, KEYS // QG])
        nm = sb("nm", [P, 4])
        rest = sb("rest", [P, 4])
        nm3 = sb("nm3", [P, 4, 3], BF16)
        rec = sb("rec", [P, 4])
        v_loaded, ready, valued, released = semaphores(nc, ctx, "k1", "v_loaded ready valued released")
        stacked = [nc.alloc_semaphore(f"k1_stacked{r}") for r in range(RING)]
        scored, exped, attended, a_scored, a_reduced, reciprocal = semaphores(
            nc, ctx, "k1", "scored exped attended a_scored a_reduced reciprocal")
        o_copied, summed, normed, split, rows_scored, rows_copied = semaphores(
            nc, ctx, "k1", "o_copied summed normed split rows_scored rows_copied")
        abank, sbank = k.ps[0:3], k.ps[3:6]
        obank, mbank = k.ps[6], k.ps[7]
        LOADS = 12 * 16
        EX, SB, AB = 8, 3, 3

        def bank_free(n, a):
            return KT * n + a + (2 if a < KT % 3 else 1)

        block = ctx.enter_context(nc.Block("k1_b"))

        def all_heads(eng, head):
            head(0, 0, True, False)
            with eng.Fori(0, HEADS // RING - 1) as i:
                for u in range(1, RING + 1):
                    head(RING * i + u, u % RING, False, False)
            for h in range(HEADS - RING + 1, HEADS):
                head(h, h % RING, False, h == HEADS - 1)

        def bodies(eng, h, body):
            body(4 * h, 0)
            with eng.Fori(1, 4) as qg:
                body(4 * h + qg, qg)

        def heads_attended(heads):
            return 4 * KT * heads + EX

        def opening(qg):
            return isinstance(qg, int)

        @block.sync
        def _(sp):
            sp.dma_start(v[:, :, :], k.a["L1_v"].rearrange("(t p) d -> p t d", p=P)).then_inc(v_loaded, 16)

            def load(r, h):
                parts = ((0, 0), (1, 0), (2, 0), (0, 1), (1, 1), (0, 2))
                here = slice(h * HD, h * HD + HD) if isinstance(h, int) else bass.ds(h * HD, HD)
                for row, (k_part, q_part) in enumerate(parts):
                    at = slice(HD * row, HD * row + HD)
                    sp.dma_start(kst[r][at, :], k.k_scr[k_part, here, :]).then_inc(stacked[r], 16)
                    sp.dma_start(qst[r][at, :], k.q_scr[q_part, here, :]).then_inc(stacked[r], 16)

            for h in range(RING):
                load(h, h)
            with sp.Fori(0, HEADS // RING - 1) as i:
                for u in range(1, RING + 1):
                    sp.wait_ge(attended, heads_attended(RING * i + u))
                    sp.sem_inc(released, 1)
                    load((u + 3) % RING, RING * i + u + 3)

        @block.gpsimd
        def _(pool):
            for u in range(2):
                pool.memset(vst[u][:, :, HD:HD + 1], 1.0)
                pool.memset(vst[u][:, :, HD + 1:32], 0.0)
            pool.wait_ge(v_loaded, 16)
            for h in range(2):
                pool.tensor_copy(vst[h][:, :, 0:HD], v[:, :, h * HD:(h + 1) * HD]).then_inc(valued, 1)
            with pool.Fori(1, HEADS // 2) as i:
                for u in range(2):
                    h = 2 * i + u
                    pool.wait_ge(attended, heads_attended(h - 1))
                    pool.tensor_copy(vst[u][:, :, 0:HD], v[:, :, bass.ds(h * HD, HD)]).then_inc(valued, 1)

        @block.tensor
        def _(pe):
            pe.sem_inc(attended, EX)
            pe.sem_inc(summed, 1)
            pe.sem_inc(rows_scored, 1)
            pe.wait_ge(ready, 2)

            def maximum_product(r, qg, n, a):
                tile, group = divmod(a, KEYS // QG)
                pe.wait_ge(a_reduced, bank_free(n, a))
                pe.matmul(abank[a % 3], qst[r][0:STACK, bass.ds(qg * QG + tile * P, P)], kst[r][0:STACK, group * QG:(group + 1) * QG],
                          start=True, stop=True).then_inc(a_scored, 1)

            def maximum_rows(n):
                pe.wait_ge(split, SPLITS * (n + 1) + 1)
                for tile in range(4):
                    mm = pe.matmul(mbank[STACK:STACK + 3, tile * P:(tile + 1) * P], nm3[:, tile, :], identb[:, :], start=True, stop=True)
                mm.then_inc(rows_scored, 1)

            def attend(u, n, p):
                pe.wait_ge(exped, KT * n + p + 1 + SB)
                strip = slice(32 * (p % 4), 32 * (p % 4) + 32)
                pe.matmul(obank[strip, :], vst[u % 2][:, p, :], ex[p % EX][:, :],
                          start=(p < 4), stop=(p >= KT - 4)).then_inc(attended, 1)

            def sums(n):
                pe.wait_ge(o_copied, n + 2)
                for tile in range(4):
                    mm = pe.matmul(mbank[:, tile * 17:tile * 17 + 17], osb[:, tile * P:(tile + 1) * P], k.strip_sum[:, :],
                                   start=True, stop=True)
                mm.then_inc(summed, 1)

            pe.wait_ge(stacked[0], LOADS)
            with pe.Fori(0, 4) as qg:
                for a in range(AM):
                    maximum_product(0, qg, qg, a)
                pe.wait_ge(rows_copied, qg + 1)
                maximum_rows(qg)

            def head(h, u, first, last):
                nxt = (u + 1) % RING

                def body(n, qg):
                    started = first and opening(qg)
                    ending = (u - 1) % RING if opening(qg) else u
                    for p in range(KT):
                        if p == SUMS_AT and not started:
                            if last and not opening(qg):
                                pe.wait_ge(normed, n)
                                pe.wait_ge(rows_copied, BODIES + 1)
                            else:
                                pe.wait_ge(rows_copied, n + 4)
                            sums(n - 1)
                        if p == ROWS_AT and not started and not (last and not opening(qg)):
                            pe.wait_ge(normed, n + 1)
                            maximum_rows(n + 3)
                        if p == 0:
                            pe.wait_ge(rows_copied, n + 2)
                        pe.wait_ge(exped, bank_free(n, p))
                        pe.matmul(sbank[p % 3], kst[u][:, p * P:(p + 1) * P], qst[u][:, bass.ds(qg * QG, QG)],
                                  start=True, stop=True).then_inc(scored, 1)
                        if not last:
                            if p == 0 and opening(qg):
                                pe.wait_ge(stacked[nxt], LOADS * ((h + 1 - nxt) // RING + 1) if isinstance(h, int)
                                           else turn_loads(h, u))
                            maximum_product(nxt, qg, n + 4, p)
                        if p >= LAG:
                            if p == LAG:
                                if opening(qg):
                                    pe.wait_ge(valued, h + 1)
                                pe.wait_ge(o_copied, n + 1)
                            attend(u, n, p - LAG)
                        elif not started:
                            attend(ending, n - 1, KT - LAG + p)

                bodies(pe, h, body)

            def turn_loads(h, u):
                following = u + 1 if u else RING + 1
                return (h - (u or RING)) // RING * LOADS + LOADS * (1 + following // RING)

            all_heads(pe, head)
            last = (HEADS - 1) % RING
            for p in range(KT - LAG, KT):
                attend(last, BODIES - 1, p)
            pe.wait_ge(normed, BODIES)
            sums(BODIES - 1)

        @block.scalar
        def _(act):
            act.preload_act_table(ACT.Exp)
            act.sem_inc(exped, SB)
            act.sem_inc(o_copied, 1)
            act.sem_inc(rows_copied, 1)

            def rows(r, qg, n):
                act.wait_ge(rows_scored, n + 2)
                act.copy(qst[r][STACK:STACK + 3, bass.ds(qg * QG, QG)], mbank[STACK:STACK + 3, :]).then_inc(rows_copied, 1)

            def strips(n):
                act.wait_ge(attended, KT * (n + 1) + EX)
                act.wait_ge(summed, n + 1)
                act.copy(osb[:, :], obank).then_inc(o_copied, 1)

            with act.Fori(0, 4) as qg:
                rows(0, qg, qg)

            def head(h, u, first, last):
                def body(n, qg):
                    started = first and opening(qg)
                    for p in range(KT):
                        if p == LAG and not started:
                            strips(n - 1)
                        if p == ROWS_AT + 1 and not started:
                            if opening(qg):
                                rows(u, 3, n + 3)
                            elif not last:
                                rows((u + 1) % RING, qg - 1, n + 3)
                        act.wait_ge(scored, KT * n + p + 1)
                        act.wait_ge(attended, KT * n + p + 1)
                        act.activation(ex[p % EX][:, :], sbank[p % 3], ACT.Exp, scale=HD ** -0.5).then_inc(exped, 1)

                bodies(act, h, body)

            all_heads(act, head)
            strips(BODIES - 1)

        @block.vector
        def _(dve):
            dve.tensor_copy(identb[:, :], k.ident[:, :]).then_inc(ready, 1)
            for r in range(RING):
                ins = dve.memset(kst[r][STACK:STACK + 3, :], 1.0)
            ins.then_inc(ready, 1)
            dve.sem_inc(a_reduced, AB)
            dve.sem_inc(normed, 1)
            dve.sem_inc(split, 1)

            def reduce(n, a):
                tile, group = divmod(a, KEYS // QG)
                if a == 0:
                    dve.wait_ge(split, SPLITS * n + 1)
                dve.wait_ge(a_scored, AM * n + a + 1)
                dve.tensor_reduce(pm[:, tile, group:group + 1], abank[a % 3], AX.X, ALU.max).then_inc(a_reduced, 1)

            def split_maxima(n):
                dve.wait_ge(a_reduced, AM * (n + 1) + AB)
                dve.tensor_reduce(nm[:, :], pm[:, :, :], AX.X, ALU.max, negate=True).then_inc(split, 1)
                dve.wait_ge(rows_scored, n + 1)
                dve.wait_ge(split, SPLITS * n + 2)
                dve.tensor_copy(nm3[:, :, 0], nm[:, :]).then_inc(split, 1)
                dve.wait_ge(split, SPLITS * n + 3)
                dve.tensor_tensor(rest[:, :], nm[:, :], nm3[:, :, 0], ALU.subtract).then_inc(split, 1)
                dve.wait_ge(split, SPLITS * n + 4)
                dve.tensor_copy(nm3[:, :, 1], rest[:, :]).then_inc(split, 1)
                dve.wait_ge(split, SPLITS * n + 5)
                dve.tensor_tensor(rest[:, :], rest[:, :], nm3[:, :, 1], ALU.subtract).then_inc(split, 1)
                dve.wait_ge(split, SPLITS * n + 6)
                dve.tensor_copy(nm3[:, :, 2], rest[:, :]).then_inc(split, 1)

            def divide(n, h, quarter):
                sums = mbank[:, 0:68].rearrange("p (t d) -> p t d", d=17)
                dve.wait_ge(summed, n + 2)
                dve.wait_ge(normed, n + 1)
                dve.reciprocal(rec[:, :], sums[:, :, HD]).then_inc(reciprocal, 1)
                dve.wait_ge(reciprocal, n + 1)
                dve.tensor_tensor(o[:, bass.ds(4 * quarter, 4), bass.ds(h * HD, HD)], sums[:, :, 0:HD],
                                  rec[:, :].unsqueeze(2).to_broadcast([P, 4, HD]), ALU.mult).then_inc(normed, 1)

            with dve.Fori(0, 4) as qg:
                for a in range(AM):
                    reduce(qg, a)
                split_maxima(qg)

            def head(h, u, first, last):
                def body(n, qg):
                    divide_at = SUMS_AT + 2
                    for a in range(AM):
                        if a == divide_at and not (first and opening(qg)):
                            divide(n - 1, h - 1 if opening(qg) else h, 3 if opening(qg) else qg - 1)
                        if not last:
                            reduce(n + 4, a)
                    if not last:
                        split_maxima(n + 4)

                bodies(dve, h, body)

            all_heads(dve, head)
            divide(BODIES - 1, HEADS - 1, 3)


def project_add(nc, k, name, o, weight):
    LANES = 4
    with ExitStack() as ctx:
        def sb(n, shape, dt=F32):
            return ctx.enter_context(nc.sbuf_tensor(name + n, shape, dt))
        w = sb("w", [P, 2, D])
        os = [sb(f"os{u}", [P, D]) for u in range(LANES)]
        oT = [sb(f"oT{u}", [P, 2, P]) for u in range(LANES)]
        loaded, = semaphores(nc, ctx, name, "loaded")
        pe_ = lane_steps(nc, name, "pe", "OT Y", LANES)
        act_ = lane_steps(nc, name, "act", "OT", LANES)
        dve_ = lane_steps(nc, name, "dve", "PICK X", LANES)
        bank = [[k.ps[2 * u + n] for n in range(2)] for u in range(LANES)]
        block = ctx.enter_context(nc.Block(name + "_b"))

        @block.sync
        def _(sp):
            sp.dma_start(w[:, :, :], k.a[weight].rearrange("(c p) n -> p c n", p=P)).then_inc(loaded, 16)

        @block.tensor
        def _(pe):
            pe.wait_ge(loaded, 16)
            with pe.Fori(0, T // LANES) as i:
                for u in range(LANES):
                    pe.wait_ge(dve_[u].sem, dve_[u].at(i, "PICK"))
                    for c in range(2):
                        mm = pe.transpose(bank[u][0][:, c * P:(c + 1) * P], os[u][:, c * P:(c + 1) * P], k.ident[:, :])
                    mm.then_inc(pe_[u].sem, 1)
                for u in range(LANES):
                    pe.wait_ge(act_[u].sem, act_[u].at(i, "OT"))
                    for c in range(2):
                        mm = pe.matmul(bank[u][1][:, 0:D], oT[u][:, c, :], w[:, c, :], start=(c == 0), stop=(c == 1))
                    mm.then_inc(pe_[u].sem, 1)

        @block.scalar
        def _(act):
            with act.Fori(0, T // LANES) as i:
                for u in range(LANES):
                    act.wait_ge(pe_[u].sem, pe_[u].at(i, "OT"))
                    act.copy(oT[u][:, :, :], bank[u][0][:, 0:D].rearrange("p (c n) -> p c n", c=2)).then_inc(act_[u].sem, 1)

        @block.vector
        def _(dve):
            with dve.Fori(0, T // LANES) as i:
                for u in range(LANES):
                    dve.tensor_copy(os[u][:, :], tile_rows(o, LANES * i + u)).then_inc(dve_[u].sem, 1)
                for u in range(LANES):
                    xt = tile_rows(k.x, LANES * i + u)
                    dve.wait_ge(pe_[u].sem, pe_[u].at(i, "Y"))
                    dve.tensor_tensor(xt, xt, bank[u][1][:, 0:D], ALU.add).then_inc(dve_[u].sem, 1)


def l1_cross(nc, k):
    with ExitStack() as outer:
        def sb(name, shape):
            return outer.enter_context(nc.sbuf_tensor("m1" + name, shape, F32))
        cum = sb("cum", [P, T, HEADS])
        inp = sb("inp", [P, T, HEADS])
        centred = sb("centred", [P, T, D])
        var = sb("var", [P, T, HEADS])
        mlstm_gates(nc, k, cum, inp)
        mlstm_attention(nc, k, cum, inp, centred, var)
        mlstm_output(nc, k, centred, var)


def mlstm_gates(nc, k, cum, inp):
    with ExitStack() as ctx:
        def sb(name, shape, dt=F32):
            return ctx.enter_context(nc.sbuf_tensor("mg" + name, shape, dt))
        LANES = 4
        w = sb("w", [P, 6, 32])
        bias = sb("bias", [P, 32])
        xs = [sb(f"xs{u}", [P, 2, P]) for u in range(LANES)]
        cT = [sb(f"cT{u}", [P, 2, P]) for u in range(LANES)]
        gates = sb("gates", [P, T, 32])
        fg = sb("fg", [P, T, HEADS])
        low = sb("low", [P, T, HEADS])
        big = sb("big", [P, T, HEADS])
        loaded, gated, biased, logs, summed, dn = semaphores(nc, ctx, "mg", "loaded gated biased logs summed vec")
        arrived = [nc.alloc_semaphore(f"mg_arrived{u}") for u in range(LANES)]
        copied, = semaphores(nc, ctx, "mg", "copied")
        block = ctx.enter_context(nc.Block("mg_b"))

        @block.sync
        def _(sp):
            sp.dma_start(w[:, :, :], k.a["L1_gates"].rearrange("(c p) n -> p c n", p=P)).then_inc(loaded, 16)
            sp.dma_start(bias[:, :], k.a["L1_gates_b"].partition_broadcast(P)).then_inc(loaded, 16)
            with sp.Fori(0, T // LANES) as i:
                for u in range(LANES):
                    sp.wait_ge(gated, LANES * i + 1)
                    sp.dma_start(cT[u][:, :, :], k.a["ctxT"].rearrange("(c p) n -> p c n", p=P)[:, :, bass.ds((LANES * i + u) * P, P)]).then_inc(arrived[u], 16)

        @block.gpsimd
        def _(pool):
            with pool.Fori(0, T // LANES) as i:
                for u in range(LANES):
                    pool.wait_ge(gated, LANES * i + 1)
                    pool.tensor_copy(xs[u][:, :, :], k.xT[:, :, bass.ds((LANES * i + u) * P, P)]).then_inc(copied, 1)

        @block.tensor
        def _(pe):
            pe.sem_inc(gated, 1)
            pe.wait_ge(loaded, 32)
            with pe.Fori(0, T // LANES) as i:
                for u in range(LANES):
                    pe.wait_ge(arrived[u], 16 * (i + 1))
                    pe.wait_ge(copied, LANES * i + u + 1)
                    pe.wait_ge(biased, LANES * i + 1)
                    for c in range(6):
                        lhs = xs[u] if c < 2 else cT[u]
                        mm = pe.matmul(k.ps[u][:, 0:32], lhs[:, c % 2, :], w[:, c, :], start=(c == 0), stop=(c == 5))
                    mm.then_inc(gated, 1)
            pe.wait_ge(dn, 5)
            pe.matmul(k.ps[LANES][:, 0:D], k.cumulate[:, :], low[:, :, :].rearrange("p t h -> p (t h)"),
                      start=True, stop=True).then_inc(summed, 1)

        @block.scalar
        def _(act):
            act.preload_act_table_set("natural_log_exp_and_others")
            act.wait_ge(dn, 3)
            act.activation(big[:, :, :], big[:, :, :], ACT.Exp, scale=-1.0).then_inc(logs, 1)
            act.wait_ge(logs, 1)
            act.activation(big[:, :, :], big[:, :, :], ACT.Ln, bias=1.0).then_inc(logs, 1)

        @block.vector
        def _(dve):
            dve.sem_inc(biased, 1)
            with dve.Fori(0, T // LANES) as i:
                for u in range(LANES):
                    dve.wait_ge(gated, LANES * i + u + 2)
                    dve.tensor_tensor(tile_rows(gates, LANES * i + u), k.ps[u][:, 0:32], bias[:, :], ALU.add).then_inc(biased, 1)
            dve.wait_ge(biased, T + 1)
            dve.tensor_copy(fg[:, :, :], gates[:, :, HEADS:32]).then_inc(dn, 1)
            dve.wait_ge(dn, 1)
            dve.tensor_scalar(low[:, :, :], fg[:, :, :], 0.0, None, ALU.min).then_inc(dn, 1)
            dve.scalar_tensor_tensor(out=big[:, :, :], in0=fg[:, :, :], scalar=-1.0, in1=fg[:, :, :], op0=ALU.mult, op1=ALU.max).then_inc(dn, 1)
            dve.wait_ge(logs, 2)
            dve.tensor_tensor(low[:, :, :], low[:, :, :], big[:, :, :], ALU.subtract).then_inc(dn, 1)
            dve.wait_ge(dn, 4)
            dve.sem_inc(dn, 1)
            dve.wait_ge(summed, 1)
            dve.tensor_copy(cum[:, :, :].rearrange("p t h -> p (t h)"), k.ps[LANES][:, 0:D]).then_inc(dn, 1)
            dve.wait_ge(dn, 6)
            dve.tensor_tensor(inp[:, :, :], gates[:, :, 0:HEADS], cum[:, :, :], ALU.subtract).then_inc(dn, 1)


def mlstm_attention(nc, k, cum, inp, centred, var):
    with ExitStack() as ctx:
        def sb(name, shape, dt=F32):
            return ctx.enter_context(nc.sbuf_tensor("ma" + name, shape, dt))
        xs = [sb(f"xs{u}", [P, 2, P]) for u in range(2)]
        cT = [sb(f"cT{u}", [P, 2, P]) for u in range(2)]
        vs = [sb(f"vs{u}", [P, 2, D]) for u in range(2)]
        vd = [sb(f"vd{u}", [P, 2, D]) for u in range(2)]
        kexp = [sb(f"kexp{u}", [P, 2, 2, 8, S]) for u in range(2)]
        diag = [sb(f"diag{u}", [P, HEADS * S]) for u in range(2)]
        sc = [sb(f"sc{u}", [P, HEADS * S]) for u in range(2)]
        pT = [sb(f"pT{u}", [P, 8, P]) for u in range(2)]
        hd = [sb(f"hd{u}", [P, D]) for u in range(2)]
        m = [sb(f"m{u}", [P, 6, HEADS]) for u in range(2)]
        MAX, SUM, CUMMAX, FLOOR, NORM, MEAN = range(6)
        arrived = [nc.alloc_semaphore(f"ma_arrived{u}") for u in range(2)]
        pe_ = lane_steps(nc, "ma", "pe", "DECAY SCORES PT O")
        act_ = lane_steps(nc, "ma", "act", "EXP FLOOR PT")
        dve_ = lane_steps(nc, "ma", "dve", "DIAG KEXP VBD MASK MAX SUB CUMMAX C SUM ABS NORM EPS REC O MEAN MEAN16 CENTRE SQ VAR")
        pool_ = lane_steps(nc, "ma", "pool", "XS KEXP")
        bank = [[k.ps[4 * u + n] for n in range(4)] for u in range(2)]
        block = ctx.enter_context(nc.Block("ma_b"))

        @block.sync
        def _(sp):
            def tile(u, i, before, after):
                t = 2 * i + u
                rows = slice(t * P, t * P + P) if isinstance(t, int) else bass.ds(t * P, P)
                if not isinstance(i, int) or i:
                    sp.wait_ge(dve_[u].sem, dve_[u].at(i - 1, "VBD"))
                    sp.wait_ge(pool_[u].sem, pool_[u].at(i - 1, "KEXP"))
                sp.dma_start(cT[u][:, :, :], k.a["ctxT"].rearrange("(c p) n -> p c n", p=P)[:, :, rows]).then_inc(arrived[u], 16)
                for r in range(2):
                    sp.dma_start(vs[u][row_slice(r), :, :], k.ctx_rows[rows, :].rearrange("(b j) n -> j b n", b=2)).then_inc(arrived[u], 16)

            staggered(sp, tile)

        @block.gpsimd
        def _(pool):
            def tile(u, i, before, after):
                t = 2 * i + u
                rows = slice(t * P, t * P + P) if isinstance(t, int) else bass.ds(t * P, P)
                if not isinstance(i, int) or i:
                    pool.wait_ge(pe_[u].sem, pe_[u].at(i - 1, "SCORES"))
                pool.tensor_copy(xs[u][:, :, :], k.xT[:, :, rows]).then_inc(pool_[u].sem, 1)
                pool.wait_ge(arrived[u], 48 * (i + 1))
                spread_keys(pool, kexp[u], cT[u], k.head_mask[:, :], (1,)).then_inc(pool_[u].sem, 1)

            staggered(pool, tile)

        @block.tensor
        def _(pe):
            def finish(u, i):
                pe.wait_ge(dve_[u].sem, dve_[u].at(i, "C"))
                weight_transposes(pe, bank[u][0:2], sc[u], k.ident[:, :]).then_inc(pe_[u].sem, 1)
                pe.wait_ge(act_[u].sem, act_[u].at(i, "PT"))
                value_matmuls(pe, bank[u][2], pT[u], vd[u]).then_inc(pe_[u].sem, 1)

            def tile(u, i, before, after):
                pe.wait_ge(dve_[u].sem, dve_[u].at(i, "DIAG"))
                for c in range(2):
                    mm = pe.matmul(bank[u][c], k.ones64[:, :], diag[u][:, c * 512:(c + 1) * 512], start=True, stop=True)
                mm.then_inc(pe_[u].sem, 1)
                pe.wait_ge(dve_[u].sem, dve_[u].at(i, "KEXP"))
                pe.wait_ge(pool_[u].sem, pool_[u].at(i, "KEXP"))
                score_matmuls(pe, bank[u][2:4], xs[u], kexp[u]).then_inc(pe_[u].sem, 1)
                if before:
                    finish(*before)

            finish(*staggered(pe, tile))

        @block.scalar
        def _(act):
            act.preload_act_table(ACT.Exp)

            def weights_out(u, i):
                act.wait_ge(pe_[u].sem, pe_[u].at(i, "PT"))
                act.copy(pT[u][:, 0:4, :], bank[u][0].rearrange("p (c n) -> p c n", c=4))
                act.copy(pT[u][:, 4:8, :], bank[u][1].rearrange("p (c n) -> p c n", c=4)).then_inc(act_[u].sem, 1)

            def tile(u, i, before, after):
                if before:
                    weights_out(*before)
                act.wait_ge(dve_[u].sem, dve_[u].at(i, "SUB"))
                act.activation(sc[u][:, :], sc[u][:, :], ACT.Exp).then_inc(act_[u].sem, 1)
                act.wait_ge(dve_[u].sem, dve_[u].at(i, "CUMMAX"))
                act.activation(m[u][:, FLOOR, :], m[u][:, CUMMAX, :], ACT.Exp, scale=-1.0).then_inc(act_[u].sem, 1)

            weights_out(*staggered(act, tile))

        @block.vector
        def _(dve):
            def wait(u, i, step):
                dve.wait_ge(dve_[u].sem, dve_[u].at(i, step))

            def spread(u, i):
                t = 2 * i + u
                dve.wait_ge(dve_[u].sem, dve_[u].turns(i))
                dve.tensor_tensor(heads3(diag[u][:, :]), per_head(tile_rows(inp, t)), over_heads(k.eye64[:, :]), ALU.mult).then_inc(dve_[u].sem, 1)
                dve.wait_ge(arrived[u], 48 * (i + 1))
                spread_keys(dve, kexp[u], cT[u], k.head_mask[:, :], (0,)).then_inc(dve_[u].sem, 1)
                values_by_parity(dve, vd[u], vs[u][:, :, :], k.parity[:, :]).then_inc(dve_[u].sem, 1)

            def decays(u, i):
                t = 2 * i + u
                dve.wait_ge(pe_[u].sem, pe_[u].at(i, "DECAY"))
                for c in range(2):
                    ins = dve.tensor_tensor(heads3(sc[u][:, c * 512:(c + 1) * 512]), heads3(bank[u][c]),
                                            over_heads(k.causal[:, :], 8), ALU.add)
                ins.then_inc(dve_[u].sem, 1)
                wait(u, i, "MASK")
                dve.tensor_reduce(m[u][:, MAX, :], heads3(sc[u][:, :]), AX.X, ALU.max).then_inc(dve_[u].sem, 1)
                wait(u, i, "MAX")
                dve.tensor_tensor(heads3(sc[u][:, :]), heads3(sc[u][:, :]), per_head(m[u][:, MAX, :]), ALU.subtract).then_inc(dve_[u].sem, 1)
                dve.tensor_tensor(m[u][:, CUMMAX, :], m[u][:, MAX, :], tile_rows(cum, t), ALU.add).then_inc(dve_[u].sem, 1)

            def weights(u, i):
                dve.wait_ge(pe_[u].sem, pe_[u].at(i, "SCORES"))
                dve.wait_ge(act_[u].sem, act_[u].at(i, "EXP"))
                for c in range(2):
                    half = sc[u][:, c * 512:(c + 1) * 512]
                    ins = dve.scalar_tensor_tensor(out=half, in0=bank[u][2 + c], scalar=HD ** -0.5, in1=half,
                                                   op0=ALU.mult, op1=ALU.mult)
                ins.then_inc(dve_[u].sem, 1)
                wait(u, i, "C")
                dve.tensor_reduce(m[u][:, SUM, :], heads3(sc[u][:, :]), AX.X, ALU.add).then_inc(dve_[u].sem, 1)
                wait(u, i, "SUM")
                dve.scalar_tensor_tensor(out=m[u][:, NORM, :], in0=m[u][:, SUM, :], scalar=-1.0, in1=m[u][:, SUM, :],
                                         op0=ALU.mult, op1=ALU.max).then_inc(dve_[u].sem, 1)
                wait(u, i, "ABS")
                dve.wait_ge(act_[u].sem, act_[u].at(i, "FLOOR"))
                dve.tensor_tensor(m[u][:, NORM, :], m[u][:, NORM, :], m[u][:, FLOOR, :], ALU.max).then_inc(dve_[u].sem, 1)
                wait(u, i, "NORM")
                dve.tensor_scalar(m[u][:, NORM, :], m[u][:, NORM, :], 1e-6, None, ALU.add).then_inc(dve_[u].sem, 1)
                wait(u, i, "EPS")
                dve.reciprocal(m[u][:, NORM, :], m[u][:, NORM, :]).then_inc(dve_[u].sem, 1)

            def outputs(u, i):
                t = 2 * i + u
                h3 = hd[u][:, :].rearrange("p (h d) -> p h d", d=HD)
                ctile = tile_rows(centred, t).rearrange("p (h d) -> p h d", d=HD)
                wait(u, i, "REC")
                dve.wait_ge(pe_[u].sem, pe_[u].at(i, "O"))
                for b in range(2):
                    r = row_slice(b)
                    ins = dve.tensor_tensor(hd[u][r, :].rearrange("p (c h d) -> p c h d", h=2, d=HD), own_batch(bank[u][2], b),
                                            m[u][r, NORM, :].rearrange("p (c h) -> p c h", h=2).unsqueeze(3).to_broadcast([64, 8, 2, HD]),
                                            ALU.mult)
                ins.then_inc(dve_[u].sem, 1)
                wait(u, i, "O")
                dve.tensor_reduce(m[u][:, MEAN, :], h3, AX.X, ALU.add).then_inc(dve_[u].sem, 1)
                wait(u, i, "MEAN")
                dve.tensor_scalar(m[u][:, MEAN, :], m[u][:, MEAN, :], 1.0 / HD, None, ALU.mult).then_inc(dve_[u].sem, 1)
                wait(u, i, "MEAN16")
                dve.tensor_tensor(h3, h3, per_head(m[u][:, MEAN, :], HD), ALU.subtract).then_inc(dve_[u].sem, 1)
                wait(u, i, "CENTRE")
                dve.tensor_copy(ctile, h3)
                dve.tensor_tensor(diag[u][:, 0:D], hd[u][:, :], hd[u][:, :], ALU.mult).then_inc(dve_[u].sem, 1)
                wait(u, i, "SQ")
                dve.tensor_reduce(tile_rows(var, t), diag[u][:, 0:D].rearrange("p (h d) -> p h d", d=HD), AX.X, ALU.add).then_inc(dve_[u].sem, 1)

            def tile(u, i, before, after):
                spread(u, i)
                if before:
                    weights(*before)
                decays(u, i)
                if before:
                    outputs(*before)

            end = staggered(dve, tile)
            weights(*end)
            outputs(*end)


def mlstm_output(nc, k, centred, var):
    with ExitStack() as ctx:
        scale = ctx.enter_context(nc.sbuf_tensor("mo_scale", [P, D], F32))
        loaded, vec, rooted = semaphores(nc, ctx, "mo", "loaded vec rooted")
        chain = [nc.alloc_semaphore(f"mo_chain{u}") for u in range(2)]
        block = ctx.enter_context(nc.Block("mo_b"))

        @block.sync
        def _(sp):
            sp.dma_start(scale[:, :], k.a["L1_xattn_ln_scale"].partition_broadcast(P)).then_inc(loaded, 16)

        @block.scalar
        def _(act):
            act.wait_ge(vec, 1)
            act.activation(var[:, :, :], var[:, :, :], ACT.Sqrt).then_inc(rooted, 1)

        @block.vector
        def _(dve):
            dve.tensor_scalar(var[:, :, :], var[:, :, :], 1.0 / HD, 1e-6, ALU.mult, ALU.add).then_inc(vec, 1)
            dve.wait_ge(vec, 1)
            dve.wait_ge(rooted, 1)
            dve.reciprocal(var[:, :, :], var[:, :, :]).then_inc(vec, 1)
            dve.wait_ge(vec, 2)
            dve.wait_ge(loaded, 16)
            with dve.Fori(0, T // 2) as i:
                for u in range(2):
                    c = tile_rows(centred, 2 * i + u)
                    c3 = c.rearrange("p (h d) -> p h d", d=HD)
                    dve.tensor_tensor(c3, c3, var[:, bass.ds(2 * i + u, 1), :].rearrange("p t h -> p (t h)").unsqueeze(2).to_broadcast([P, HEADS, HD]),
                                      ALU.mult).then_inc(chain[u], 1)
                for u in range(2):
                    c = tile_rows(centred, 2 * i + u)
                    dve.wait_ge(chain[u], 3 * i + 1)
                    dve.tensor_tensor(c, c, scale[:, :], ALU.mult).then_inc(chain[u], 1)
                for u in range(2):
                    c, xt = tile_rows(centred, 2 * i + u), tile_rows(k.x, 2 * i + u)
                    dve.wait_ge(chain[u], 3 * i + 2)
                    dve.tensor_tensor(xt, xt, c, ALU.add).then_inc(chain[u], 1)


def l1_ffn(nc, k):
    with ExitStack() as outer:
        k.combT = outer.enter_context(nc.sbuf_tensor("f1combT", [COMB_ROWS, N], BF16))
        gates = outer.enter_context(nc.sbuf_tensor("f1gates", [P, T, 8], F32))
        w = outer.enter_context(nc.sbuf_tensor("f1wr", [P, 2, 8], F32))
        loaded, = semaphores(nc, outer, "f1", "router_loaded")
        nc.sync.dma_start(w[:, :, :], k.a["L1_wr"].rearrange("(c p) n -> p c n", p=P)).then_inc(loaded, 16)
        moe_route(nc, k, "r1", w, loaded, 8, 2, True, 1.0, rows=gates)
        l1_ffn_scatter(nc, k, gates)


def l1_ffn_scatter(nc, k, gates):
    GT, E = 4 * P, 8
    with ExitStack() as ctx:
        def sb(name, shape, dt=F32):
            return ctx.enter_context(nc.sbuf_tensor("f1" + name, shape, dt))
        w1, w3, w2 = (sb(n, [P, 2, D]) for n in ("w1", "w3", "w2"))
        h1 = sb("h1", [P, 2, GT])
        h2 = sb("h2", [P, 4, D])
        gs = sb("gs", [P, 4, E])
        acc = sb("acc", [E, D])
        accT = sb("accT", [P, 2, E])
        loaded, picked, cleared, first, turned, copied, projected, final = semaphores(
            nc, ctx, "f1", "loaded picked cleared first turned copied projected final")
        second, summed, act1, act2, added = semaphores(nc, ctx, "f1", "second summed act1 act2 added")
        block = ctx.enter_context(nc.Block("f1_b"))

        @block.sync
        def _(sp):
            for t, n in ((w1, "L1_w1"), (w3, "L1_w3"), (w2, "L1_w2")):
                sp.dma_start(t[:, :, :], k.a[n].rearrange("(c p) n -> p c n", p=P)).then_inc(loaded, 16)

        @block.gpsimd
        def _(pool):
            with pool.Fori(0, N // GT) as i:
                pool.wait_ge(summed, i + 1)
                pool.tensor_copy(gs[:, :, :], gates[:, bass.ds(4 * i, 4), :]).then_inc(picked, 1)

        @block.tensor
        def _(pe):
            pe.sem_inc(second, 1)
            pe.sem_inc(summed, 1)
            pe.wait_ge(loaded, 48)
            with pe.Fori(0, N // GT) as i:
                pe.wait_ge(act1, 2 * i + 1)
                for m in range(2):
                    for c in range(2):
                        mm = pe.matmul(k.ps[m], w1[:, c, m * P:(m + 1) * P], k.xT[:, c, bass.ds(i * GT, GT)],
                                       start=(c == 0), stop=(c == 1))
                    mm.then_inc(first, 1)
                pe.wait_ge(act1, 2 * i + 3)
                pe.wait_ge(act2, 2 * i + 1)
                for t in range(4):
                    for c in range(2):
                        mm = pe.matmul(k.ps[2 + t // 2][:, (t % 2) * D:(t % 2 + 1) * D], h1[:, c, t * P:(t + 1) * P], w3[:, c, :],
                                       start=(c == 0), stop=(c == 1))
                    mm.then_inc(second, 1)
                pe.wait_ge(act2, 2 * i + 3)
                pe.wait_ge(picked, i + 1)
                pe.wait_ge(added, i + 1)
                for t in range(4):
                    mm = pe.matmul(k.ps[4][0:E, 0:D], gs[:, t, :], h2[:, t, :], start=(t == 0), stop=(t == 3))
                mm.then_inc(summed, 1)
            pe.wait_ge(added, N // GT + 1)
            for c in range(2):
                mm = pe.transpose(k.ps[5][:, c * E:(c + 1) * E], acc[:, c * P:(c + 1) * P], k.ident[0:E, 0:E])
            mm.then_inc(turned, 1)
            pe.wait_ge(copied, 1)
            for c in range(2):
                mm = pe.matmul(k.ps[6][0:E, 0:D], accT[:, c, :], w2[:, c, :], start=(c == 0), stop=(c == 1))
            mm.then_inc(projected, 1)

        @block.scalar
        def _(act):
            act.preload_act_table(ACT.Silu)
            act.sem_inc(act1, 1)
            act.sem_inc(act2, 1)
            with act.Fori(0, N // GT) as i:
                act.wait_ge(second, 4 * i + 1)
                for m in range(2):
                    act.wait_ge(first, 2 * i + m + 1)
                    act.activation(h1[:, m, :], k.ps[m], ACT.Silu).then_inc(act1, 1)
                act.wait_ge(summed, i + 1)
                for m in range(2):
                    act.wait_ge(second, 4 * i + 2 * m + 3)
                    act.activation(h2[:, 2 * m:2 * m + 2, :].rearrange("p t d -> p (t d)"), k.ps[2 + m], ACT.Silu).then_inc(act2, 1)
            act.wait_ge(turned, 1)
            act.copy(accT[:, :, :], k.ps[5][:, 0:2 * E].rearrange("p (c e) -> p c e", c=2)).then_inc(copied, 1)

        @block.vector
        def _(dve):
            dve.sem_inc(added, 1)
            dve.memset(acc[:, :], 0.0).then_inc(cleared, 1)
            dve.wait_ge(cleared, 1)
            with dve.Fori(0, N // GT) as i:
                dve.wait_ge(added, i + 1)
                dve.wait_ge(summed, i + 2)
                dve.tensor_tensor(acc[:, :], acc[:, :], k.ps[4][0:E, 0:D], ALU.add).then_inc(added, 1)
            dve.wait_ge(projected, 1)
            dve.tensor_tensor(k.x[0:E, 0, :], k.x[0:E, 0, :], k.ps[6][0:E, 0:D], ALU.add).then_inc(final, 1)


MAGIC = 1.5 * 2.0 ** 23


def l2_attention(nc, k):
    with ExitStack() as outer:
        def sb(name, shape, dt=F32):
            return outer.enter_context(nc.sbuf_tensor("b2" + name, shape, dt))
        wq = {n: sb("q_" + n, [P, c, m], BF16) for n, (c, m) in BIT_WEIGHTS.items()}
        wm = {n: sb("m_" + n, [P, 1]) for n in BIT_WEIGHTS}
        x1 = sb("x1", [P, T, D])
        bit_weights(nc, k, wq, wm)
        rs = sb("rs", [P, T])
        rms_scales(nc, k, "b2n1", k.x, rs)
        bit_attention(nc, k, wq, wm, x1, rs)
        rms_scales(nc, k, "b2n2", x1, rs)
        bit_mlp(nc, k, wq, wm, x1, rs)


BIT_WEIGHTS = {"qkv": (2, 768), "o": (2, 256), "down": (4, 256)}


def bit_weights(nc, k, wq, wm):
    with ExitStack() as ctx:
        def sb(name, shape, dt=F32):
            return ctx.enter_context(nc.sbuf_tensor("bw" + name, shape, dt))
        raw = {n: sb("raw_" + n, [P, c, m]) for n, (c, m) in BIT_WEIGHTS.items()}
        part = {n: sb("part_" + n, [P, 1]) for n in BIT_WEIGHTS}
        inv = {n: sb("inv_" + n, [P, 1]) for n in BIT_WEIGHTS}
        loaded, summed, spread, vec = semaphores(nc, ctx, "bw", "loaded summed spread vec")
        block = ctx.enter_context(nc.Block("bw_b"))

        @block.sync
        def _(sp):
            for n in BIT_WEIGHTS:
                sp.dma_start(raw[n][:, :, :], k.a["L2_" + n].rearrange("(c p) n -> p c n", p=P)).then_inc(loaded, 16)

        @block.tensor
        def _(pe):
            for j, n in enumerate(BIT_WEIGHTS):
                pe.wait_ge(summed, j + 1)
                pe.matmul(k.ps[j][:, 0:1], k.ones[:, :], part[n][:, :], start=True, stop=True).then_inc(spread, 1)

        @block.vector
        def _(dve):
            count = [0]

            def link(ins):
                count[0] += 1
                ins.then_inc(vec, 1)
                dve.wait_ge(vec, count[0])

            dve.wait_ge(loaded, 48)
            for n in BIT_WEIGHTS:
                dve.tensor_reduce(part[n][:, :], raw[n][:, :, :].rearrange("p c n -> p (c n)"), AX.X, ALU.add,
                                  apply_absolute_value=True).then_inc(summed, 1)
            for j, (n, (c, m)) in enumerate(BIT_WEIGHTS.items()):
                flat = raw[n][:, :, :].rearrange("p c n -> p (c n)")
                dve.wait_ge(spread, j + 1)
                link(dve.tensor_scalar(wm[n][:, :], k.ps[j][:, 0:1], 1.0 / (c * P * m), 1e-5, ALU.mult, ALU.max))
                link(dve.reciprocal(inv[n][:, :], wm[n][:, :]))
                link(dve.tensor_scalar(flat, flat, inv[n][:, :], MAGIC, ALU.mult, ALU.add))
                link(dve.tensor_scalar(flat, flat, -MAGIC, -1.0, ALU.add, ALU.max))
                link(dve.tensor_scalar(wq[n][:, :, :].rearrange("p c n -> p (c n)"), flat, 1.0, None, ALU.min))


def rms_scales(nc, k, name, x, rs):
    with ExitStack() as ctx:
        junk = [ctx.enter_context(nc.sbuf_tensor(f"{name}junk{u}", [P, D], F32)) for u in range(2)]
        squared, vec, scaled = semaphores(nc, ctx, name, "squared vec scaled")
        block = ctx.enter_context(nc.Block(name + "_b"))

        @block.scalar
        def _(act):
            act.preload_act_table(ACT.Square)
            act.sem_inc(squared, 1)
            with act.Fori(0, T // 2) as i:
                for u in range(2):
                    act.wait_ge(squared, 2 * i + 1)
                    act.activation(junk[u][:, :], tile_rows(x, 2 * i + u), ACT.Square,
                                   accum_out=rs[:, bass.ds(2 * i + u, 1)]).then_inc(squared, 1)

        @block.vector
        def _(dve):
            dve.wait_ge(squared, T + 1)
            dve.tensor_scalar(rs[:, :], rs[:, :], 1.0 / D, 1e-5, ALU.mult, ALU.add).then_inc(vec, 1)

        @block.gpsimd
        def _(pool):
            pool.wait_ge(vec, 1)
            pool.tensor_tensor(rs[:, :], rs[:, :], k.minus_half[:, 0:T], ALU.pow).then_inc(scaled, 1)


QUANT = "AMAX CLAMP REC SCALE ROUND INT DEQ"


def quantise(dve, done, wait, tag, row, width, q, rounded, ints, wscale):
    done(dve.tensor_reduce(q[:, 0:1], row, AX.X, ALU.max, apply_absolute_value=True), tag + "AMAX")
    wait(tag + "AMAX")
    done(dve.tensor_scalar(q[:, 0:1], q[:, 0:1], 1e-5, None, ALU.max), tag + "CLAMP")
    wait(tag + "CLAMP")
    done(dve.reciprocal(q[:, 1:2], q[:, 0:1]), tag + "REC")
    wait(tag + "REC")
    done(dve.tensor_scalar(q[:, 2:3], q[:, 1:2], 127.0, None, ALU.mult), tag + "SCALE")
    wait(tag + "SCALE")
    done(dve.tensor_scalar(rounded, row, q[:, 2:3], MAGIC, ALU.mult, ALU.add), tag + "ROUND")
    wait(tag + "ROUND")
    done(dve.tensor_scalar(ints, rounded, -MAGIC, None, ALU.add), tag + "INT")
    done(dve.tensor_scalar(q[:, 3:4], q[:, 0:1], wscale[:, :], 1.0 / 127.0, ALU.mult, ALU.mult), tag + "DEQ")


def tagged(tag):
    return " ".join(tag + n for n in QUANT.split())


def bit_attention(nc, k, wq, wm, x1, rs):
    with ExitStack() as ctx:
        def sb(name, shape, dt=F32):
            return ctx.enter_context(nc.sbuf_tensor("ba" + name, shape, dt))
        norm_w = sb("norm_w", [P, D])
        identb = sb("identb", [P, P], BF16)
        h = [sb(f"h{u}", [P, D]) for u in range(2)]
        hr = [sb(f"hr{u}", [P, D]) for u in range(2)]
        hi = [sb(f"hi{u}", [P, D], BF16) for u in range(2)]
        hiT = [sb(f"hiT{u}", [P, 2, P], BF16) for u in range(2)]
        qa = [sb(f"qa{u}", [P, 4]) for u in range(2)]
        qo = [sb(f"qo{u}", [P, 4]) for u in range(2)]
        t1 = [sb(f"t1{u}", [P, 512]) for u in range(2)]
        t2 = [sb(f"t2{u}", [P, 512]) for u in range(2)]
        qk = [sb(f"qk{u}", [P, 512]) for u in range(2)]
        v = [sb(f"v{u}", [P, D]) for u in range(2)]
        vd = [sb(f"vd{u}", [P, 2, D]) for u in range(2)]
        qkT = [sb(f"qkT{u}", [P, 4, P]) for u in range(2)]
        kexp = [sb(f"kexp{u}", [P, 2, 2, 8, S]) for u in range(2)]
        sc = [sb(f"sc{u}", [P, HEADS * S]) for u in range(2)]
        pT = [sb(f"pT{u}", [P, 8, P]) for u in range(2)]
        mx = [sb(f"mx{u}", [P, HEADS]) for u in range(2)]
        den = [sb(f"den{u}", [P, HEADS]) for u in range(2)]
        loaded, ready = semaphores(nc, ctx, "ba", "loaded ready")
        pe_ = lane_steps(nc, "ba", "pe", "HT QKV TURNED SCORES PT O OT Y")
        act_ = lane_steps(nc, "ba", "act", "HT V QKT EXP PT OT")
        dve_ = lane_steps(nc, "ba", "dve", "H " + tagged("H") + " COS SIN ROPED VBD KEXP MASK MAX SUB SUM REC O "
                          + tagged("O") + " X1")
        pool_ = lane_steps(nc, "ba", "pool", "KEXP")
        bank = [[k.ps[4 * u + n] for n in range(4)] for u in range(2)]
        block = ctx.enter_context(nc.Block("ba_b"))

        @block.gpsimd
        def _(pool):
            with pool.Fori(0, T // 2) as i:
                for u in range(2):
                    pool.wait_ge(act_[u].sem, act_[u].at(i, "QKT"))
                    spread_keys(pool, kexp[u], qkT[u][:, 2:4, :], k.head_mask[:, :], (1,)).then_inc(pool_[u].sem, 1)

        @block.sync
        def _(sp):
            sp.dma_start(norm_w[:, :], k.a["L2_norm1"].partition_broadcast(P)).then_inc(loaded, 16)

        @block.tensor
        def _(pe):
            pe.wait_ge(ready, 1)
            with pe.Fori(0, T // 2) as i:
                for u in range(2):
                    pe.wait_ge(dve_[u].sem, dve_[u].at(i, "HINT"))
                    turned = bank[u][0].bitcast(BF16)
                    for c in range(2):
                        mm = pe.transpose(turned[:, c * P:(c + 1) * P], hi[u][:, c * P:(c + 1) * P], identb[:, :])
                    mm.then_inc(pe_[u].sem, 1)
                for u in range(2):
                    pe.wait_ge(act_[u].sem, act_[u].at(i, "HT"))
                    for o, lo, hi_ in ((bank[u][0], 0, 512), (bank[u][1][:, 0:D], 512, 768)):
                        for c in range(2):
                            mm = pe.matmul(o, hiT[u][:, c, :], wq["qkv"][:, c, lo:hi_], start=(c == 0), stop=(c == 1))
                    mm.then_inc(pe_[u].sem, 1)
                for u in range(2):
                    pe.wait_ge(dve_[u].sem, dve_[u].at(i, "ROPED"))
                    pe.wait_ge(act_[u].sem, act_[u].at(i, "V"))
                    for c in range(4):
                        pe.transpose(bank[u][2][:, c * P:(c + 1) * P], qk[u][:, c * P:(c + 1) * P], k.ident[:, :])
                    for b in range(2):
                        mm = pe.matmul(bank[u][3][:, b * D:(b + 1) * D], k.dup[:, b * P:(b + 1) * P], v[u][:, :], start=True, stop=True)
                    mm.then_inc(pe_[u].sem, 1)
                for u in range(2):
                    pe.wait_ge(dve_[u].sem, dve_[u].at(i, "KEXP"))
                    pe.wait_ge(pool_[u].sem, pool_[u].at(i, "KEXP"))
                    score_matmuls(pe, bank[u][0:2], qkT[u], kexp[u]).then_inc(pe_[u].sem, 1)
                for u in range(2):
                    pe.wait_ge(act_[u].sem, act_[u].at(i, "EXP"))
                    weight_transposes(pe, bank[u][2:4], sc[u], k.ident[:, :]).then_inc(pe_[u].sem, 1)
                for u in range(2):
                    pe.wait_ge(act_[u].sem, act_[u].at(i, "PT"))
                    value_matmuls(pe, bank[u][0], pT[u], vd[u]).then_inc(pe_[u].sem, 1)
                for u in range(2):
                    pe.wait_ge(dve_[u].sem, dve_[u].at(i, "OINT"))
                    turned = bank[u][1].bitcast(BF16)
                    for c in range(2):
                        mm = pe.transpose(turned[:, c * P:(c + 1) * P], hi[u][:, c * P:(c + 1) * P], identb[:, :])
                    mm.then_inc(pe_[u].sem, 1)
                for u in range(2):
                    pe.wait_ge(act_[u].sem, act_[u].at(i, "OT"))
                    for c in range(2):
                        mm = pe.matmul(bank[u][2][:, 0:D], hiT[u][:, c, :], wq["o"][:, c, :], start=(c == 0), stop=(c == 1))
                    mm.then_inc(pe_[u].sem, 1)

        @block.scalar
        def _(act):
            act.preload_act_table(ACT.Exp)

            with act.Fori(0, T // 2) as i:
                for u in range(2):
                    act.wait_ge(pe_[u].sem, pe_[u].at(i, "HT"))
                    act.copy(hiT[u][:, :, :], bank[u][0].bitcast(BF16)[:, 0:D].rearrange("p (c n) -> p c n", c=2)).then_inc(act_[u].sem, 1)
                for u in range(2):
                    act.wait_ge(pe_[u].sem, pe_[u].at(i, "QKV"))
                    act.wait_ge(dve_[u].sem, dve_[u].at(i, "HDEQ"))
                    act.activation(v[u][:, :], bank[u][1][:, 0:D], ACT.Copy, scale=qa[u][:, 3:4]).then_inc(act_[u].sem, 1)
                for u in range(2):
                    act.wait_ge(pe_[u].sem, pe_[u].at(i, "TURNED"))
                    act.copy(qkT[u][:, :, :], bank[u][2].rearrange("p (c n) -> p c n", c=4)).then_inc(act_[u].sem, 1)
                for u in range(2):
                    act.wait_ge(dve_[u].sem, dve_[u].at(i, "SUB"))
                    act.activation(sc[u][:, :], sc[u][:, :], ACT.Exp).then_inc(act_[u].sem, 1)
                for u in range(2):
                    act.wait_ge(pe_[u].sem, pe_[u].at(i, "PT"))
                    act.copy(pT[u][:, 0:4, :], bank[u][2].rearrange("p (c n) -> p c n", c=4))
                    act.copy(pT[u][:, 4:8, :], bank[u][3].rearrange("p (c n) -> p c n", c=4)).then_inc(act_[u].sem, 1)
                for u in range(2):
                    act.wait_ge(pe_[u].sem, pe_[u].at(i, "OT"))
                    act.copy(hiT[u][:, :, :], bank[u][1].bitcast(BF16)[:, 0:D].rearrange("p (c n) -> p c n", c=2)).then_inc(act_[u].sem, 1)

        @block.vector
        def _(dve):
            dve.tensor_copy(identb[:, :], k.ident[:, :]).then_inc(ready, 1)
            dve.wait_ge(loaded, 16)
            with dve.Fori(0, T // 2) as i:
                def done(ins, step, u):
                    ins.then_inc(dve_[u].sem, 1)

                def wait(step, u):
                    dve.wait_ge(dve_[u].sem, dve_[u].at(i, step))

                for u in range(2):
                    t = 2 * i + u
                    dve.scalar_tensor_tensor(out=h[u][:, :], in0=tile_rows(k.x, t), scalar=rs[:, bass.ds(t, 1)], in1=norm_w[:, :],
                                             op0=ALU.mult, op1=ALU.mult).then_inc(dve_[u].sem, 1)
                    wait("H", u)
                    quantise(dve, lambda ins, s, u=u: done(ins, s, u), lambda s, u=u: wait(s, u), "H", h[u][:, :], D,
                             qa[u], hr[u][:, :], hi[u][:, :], wm["qkv"])
                for u in range(2):
                    dve.wait_ge(pe_[u].sem, pe_[u].at(i, "QKV"))
                    wait("HDEQ", u)
                    for o, table in ((t1, k.cos), (t2, k.sin)):
                        dve.scalar_tensor_tensor(out=by8(o[u][:, :]), in0=by8(bank[u][0]), scalar=qa[u][:, 3:4], in1=angles(table),
                                                 op0=ALU.mult, op1=ALU.mult).then_inc(dve_[u].sem, 1)
                    wait("SIN", u)
                    rope_sums(dve, qk[u][:, :], t1[u][:, :], t2[u][:, :]).then_inc(dve_[u].sem, 1)
                for u in range(2):
                    dve.wait_ge(pe_[u].sem, pe_[u].at(i, "TURNED"))
                    values_by_parity(dve, vd[u], bank[u][3].rearrange("p (b n) -> p b n", b=2), k.parity[:, :]).then_inc(dve_[u].sem, 1)
                    dve.wait_ge(act_[u].sem, act_[u].at(i, "QKT"))
                    spread_keys(dve, kexp[u], qkT[u][:, 2:4, :], k.head_mask[:, :], (0,)).then_inc(dve_[u].sem, 1)
                for u in range(2):
                    dve.wait_ge(pe_[u].sem, pe_[u].at(i, "SCORES"))
                    for c in range(2):
                        ins = dve.scalar_tensor_tensor(out=heads3(sc[u][:, c * 512:(c + 1) * 512]), in0=heads3(bank[u][c]),
                                                       scalar=HD ** -0.5, in1=over_heads(k.block_causal[:, :], 8), op0=ALU.mult, op1=ALU.add)
                    ins.then_inc(dve_[u].sem, 1)
                    wait("MASK", u)
                    dve.tensor_reduce(mx[u][:, :], heads3(sc[u][:, :]), AX.X, ALU.max).then_inc(dve_[u].sem, 1)
                    wait("MAX", u)
                    dve.tensor_tensor(heads3(sc[u][:, :]), heads3(sc[u][:, :]), per_head(mx[u][:, :]), ALU.subtract).then_inc(dve_[u].sem, 1)
                for u in range(2):
                    dve.wait_ge(act_[u].sem, act_[u].at(i, "EXP"))
                    dve.tensor_reduce(den[u][:, :], heads3(sc[u][:, :]), AX.X, ALU.add).then_inc(dve_[u].sem, 1)
                    wait("SUM", u)
                    dve.reciprocal(den[u][:, :], den[u][:, :]).then_inc(dve_[u].sem, 1)
                for u in range(2):
                    dve.wait_ge(pe_[u].sem, pe_[u].at(i, "O"))
                    wait("REC", u)
                    for b in range(2):
                        r = row_slice(b)
                        ins = dve.tensor_tensor(h[u][r, :].rearrange("p (c h d) -> p c h d", h=2, d=HD), own_batch(bank[u][0], b),
                                                den[u][r, :].rearrange("p (c h) -> p c h", h=2).unsqueeze(3).to_broadcast([64, 8, 2, HD]),
                                                ALU.mult)
                    ins.then_inc(dve_[u].sem, 1)
                    wait("O", u)
                    quantise(dve, lambda ins, s, u=u: done(ins, s, u), lambda s, u=u: wait(s, u), "O", h[u][:, :], D,
                             qo[u], hr[u][:, :], hi[u][:, :], wm["o"])
                for u in range(2):
                    t = 2 * i + u
                    dve.wait_ge(pe_[u].sem, pe_[u].at(i, "Y"))
                    wait("ODEQ", u)
                    dve.scalar_tensor_tensor(out=tile_rows(x1, t), in0=bank[u][2][:, 0:D], scalar=qo[u][:, 3:4], in1=tile_rows(k.x, t),
                                             op0=ALU.mult, op1=ALU.add).then_inc(dve_[u].sem, 1)


def bit_mlp(nc, k, wq, wm, x1, rs):
    LANES = 4
    with ExitStack() as ctx:
        def sb(name, shape, dt=F32):
            return ctx.enter_context(nc.sbuf_tensor("bm" + name, shape, dt))
        norm_w = sb("norm_w", [P, D])
        identb = sb("identb", [P, P], BF16)
        up = sb("up", [P, 2, 1024])
        h = [sb(f"h{u}", [P, D]) for u in range(LANES)]
        hT = [sb(f"hT{u}", [P, 2, P]) for u in range(LANES)]
        sg = [sb(f"sg{u}", [P, 512]) for u in range(LANES)]
        gv = [sb(f"gv{u}", [P, 512]) for u in range(LANES)]
        gi = [sb(f"gi{u}", [P, 512], BF16) for u in range(LANES)]
        giT = [sb(f"giT{u}", [P, 4, P], BF16) for u in range(LANES)]
        qa = [sb(f"qa{u}", [P, 4]) for u in range(LANES)]
        loaded, ready = semaphores(nc, ctx, "bm", "loaded ready")
        pe_ = lane_steps(nc, "bm", "pe", "HT GATE VAL GT Y", LANES)
        act_ = lane_steps(nc, "bm", "act", "HT SILU GT", LANES)
        dve_ = lane_steps(nc, "bm", "dve", "H X GV " + tagged("G") + " Y", LANES)
        bank = [[k.ps[2 * u + n] for n in range(2)] for u in range(LANES)]
        block = ctx.enter_context(nc.Block("bm_b"))

        @block.sync
        def _(sp):
            sp.dma_start(norm_w[:, :], k.a["L2_norm2"].partition_broadcast(P)).then_inc(loaded, 16)
            sp.dma_start(up[:, :, :], k.a["L2_up"].rearrange("(c p) n -> p c n", p=P)).then_inc(loaded, 16)

        @block.tensor
        def _(pe):
            pe.wait_ge(loaded, 32)
            pe.wait_ge(ready, 1)
            with pe.Fori(0, T // LANES) as i:
                for u in range(LANES):
                    pe.wait_ge(dve_[u].sem, dve_[u].at(i, "H"))
                    for c in range(2):
                        mm = pe.transpose(bank[u][0][:, c * P:(c + 1) * P], h[u][:, c * P:(c + 1) * P], k.ident[:, :])
                    mm.then_inc(pe_[u].sem, 1)
                for u in range(LANES):
                    pe.wait_ge(act_[u].sem, act_[u].at(i, "HT"))
                    for half in range(2):
                        for c in range(2):
                            mm = pe.matmul(bank[u][half], hT[u][:, c, :], up[:, c, half * 512:(half + 1) * 512],
                                           start=(c == 0), stop=(c == 1))
                        mm.then_inc(pe_[u].sem, 1)
                for u in range(LANES):
                    pe.wait_ge(dve_[u].sem, dve_[u].at(i, "GINT"))
                    turned = bank[u][0].bitcast(BF16)
                    for c in range(4):
                        mm = pe.transpose(turned[:, c * P:(c + 1) * P], gi[u][:, c * P:(c + 1) * P], identb[:, :])
                    mm.then_inc(pe_[u].sem, 1)
                for u in range(LANES):
                    pe.wait_ge(act_[u].sem, act_[u].at(i, "GT"))
                    for c in range(4):
                        mm = pe.matmul(bank[u][1][:, 0:D], giT[u][:, c, :], wq["down"][:, c, :], start=(c == 0), stop=(c == 3))
                    mm.then_inc(pe_[u].sem, 1)

        @block.scalar
        def _(act):
            act.preload_act_table(ACT.Silu)
            with act.Fori(0, T // LANES) as i:
                for u in range(LANES):
                    act.wait_ge(pe_[u].sem, pe_[u].at(i, "HT"))
                    act.copy(hT[u][:, :, :], bank[u][0][:, 0:D].rearrange("p (c n) -> p c n", c=2)).then_inc(act_[u].sem, 1)
                for u in range(LANES):
                    act.wait_ge(pe_[u].sem, pe_[u].at(i, "GATE"))
                    act.activation(sg[u][:, :], bank[u][0], ACT.Silu).then_inc(act_[u].sem, 1)
                for u in range(LANES):
                    act.wait_ge(pe_[u].sem, pe_[u].at(i, "GT"))
                    act.copy(giT[u][:, :, :], bank[u][0].bitcast(BF16)[:, 0:512].rearrange("p (c n) -> p c n", c=4)).then_inc(act_[u].sem, 1)

        @block.vector
        def _(dve):
            dve.tensor_copy(identb[:, :], k.ident[:, :]).then_inc(ready, 1)
            dve.wait_ge(loaded, 32)
            with dve.Fori(0, T // LANES) as i:
                def done(ins, step, u):
                    ins.then_inc(dve_[u].sem, 1)

                def wait(step, u):
                    dve.wait_ge(dve_[u].sem, dve_[u].at(i, step))

                for u in range(LANES):
                    t = LANES * i + u
                    dve.scalar_tensor_tensor(out=h[u][:, :], in0=tile_rows(x1, t), scalar=rs[:, bass.ds(t, 1)], in1=norm_w[:, :],
                                             op0=ALU.mult, op1=ALU.mult).then_inc(dve_[u].sem, 1)
                    dve.tensor_tensor(tile_rows(k.x, t), tile_rows(k.x, t), tile_rows(x1, t), ALU.add).then_inc(dve_[u].sem, 1)
                for u in range(LANES):
                    dve.wait_ge(pe_[u].sem, pe_[u].at(i, "VAL"))
                    dve.wait_ge(act_[u].sem, act_[u].at(i, "SILU"))
                    dve.tensor_tensor(gv[u][:, :], sg[u][:, :], bank[u][1], ALU.mult).then_inc(dve_[u].sem, 1)
                    wait("GV", u)
                    quantise(dve, lambda ins, s, u=u: done(ins, s, u), lambda s, u=u: wait(s, u), "G", gv[u][:, :], 512,
                             qa[u], sg[u][:, :], gi[u][:, :], wm["down"])
                for u in range(LANES):
                    t = LANES * i + u
                    dve.wait_ge(pe_[u].sem, pe_[u].at(i, "Y"))
                    wait("GDEQ", u)
                    dve.scalar_tensor_tensor(out=tile_rows(k.x, t), in0=bank[u][1][:, 0:D], scalar=qa[u][:, 3:4], in1=tile_rows(k.x, t),
                                             op0=ALU.mult, op1=ALU.add).then_inc(dve_[u].sem, 1)


def l2_cross(nc, k):
    cosine_norms(nc, k)
    cosine_attention(nc, k)


def cosine_norms(nc, k):
    LANES = 4
    with ExitStack() as ctx:
        def sb(name, shape, dt=F32):
            return ctx.enter_context(nc.sbuf_tensor("cn" + name, shape, dt))
        cs = [sb(f"cs{u}", [P, D]) for u in range(LANES)]
        sq = [sb(f"sq{u}", [P, 2 * D]) for u in range(LANES)]
        nrm = [sb(f"nrm{u}", [P, 2 * D]) for u in range(LANES)]
        xc = [sb(f"xc{u}", [P, 2 * D]) for u in range(LANES)]
        part = [[sb(f"part{u}{n}", [P, 2 * D], BF16) for n in range(3)] for u in range(LANES)]
        arrived = [nc.alloc_semaphore(f"cn_arrived{u}") for u in range(LANES)]
        stored = [nc.alloc_semaphore(f"cn_stored{u}") for u in range(LANES)]
        pe_ = lane_steps(nc, "cn", "pe", "SUMS", LANES)
        act_ = lane_steps(nc, "cn", "act", "SQRT HIGH MIDDLE LOW", LANES)
        dve_ = lane_steps(nc, "cn", "dve", "SQ MAX REC REST1 REST2", LANES)
        pool_ = lane_steps(nc, "cn", "pool", "XN CN", LANES)
        block = ctx.enter_context(nc.Block("cn_b"))

        @block.sync
        def _(sp):
            for u in range(LANES):
                sp.sem_inc(stored[u], 1)
            with sp.Fori(0, T // LANES) as i:
                for u in range(LANES):
                    sp.wait_ge(pool_[u].sem, pool_[u].turns(i))
                    sp.dma_start(cs[u][:, :], k.ctx_rows[bass.ds((LANES * i + u) * P, P), :]).then_inc(arrived[u], 16)
            for u in range(LANES):
                sp.wait_ge(stored[u], 48 * (T // LANES) + 1)

        @block.tensor
        def _(pe):
            with pe.Fori(0, T // LANES) as i:
                for u in range(LANES):
                    pe.wait_ge(dve_[u].sem, dve_[u].at(i, "SQ"))
                    pe.matmul(k.ps[u], k.ones8[:, :], sq[u][:, :], start=True, stop=True).then_inc(pe_[u].sem, 1)

        @block.scalar
        def _(act):
            act.preload_act_table(ACT.Sqrt)
            with act.Fori(0, T // LANES) as i:
                for u in range(LANES):
                    act.wait_ge(pe_[u].sem, pe_[u].at(i, "SUMS"))
                    act.activation(nrm[u][:, :], k.ps[u], ACT.Sqrt).then_inc(act_[u].sem, 1)
                for u in range(LANES):
                    act.wait_ge(pool_[u].sem, pool_[u].at(i, "CN"))
                    act.wait_ge(stored[u], 48 * i + 1)
                    act.copy(part[u][0][:, :], xc[u][:, :]).then_inc(act_[u].sem, 1)
                for n, (rest, step) in enumerate((("REST1", "MIDDLE"), ("REST2", "LOW"))):
                    for u in range(LANES):
                        act.wait_ge(dve_[u].sem, dve_[u].at(i, rest))
                        act.copy(part[u][n + 1][:, :], xc[u][:, :]).then_inc(act_[u].sem, 1)
                for u in range(LANES):
                    for n, step in enumerate(("HIGH", "MIDDLE", "LOW")):
                        act.wait_ge(act_[u].sem, act_[u].at(i, step))
                        act.dma_start(k.n_scr[n, bass.ds((LANES * i + u) * P, P), :], part[u][n][:, :]).then_inc(stored[u], 16)

        @block.gpsimd
        def _(pool):
            with pool.Fori(0, T // LANES) as i:
                for u in range(LANES):
                    pool.wait_ge(dve_[u].sem, dve_[u].at(i, "REC"))
                    pool.wait_ge(act_[u].sem, act_[u].turns(i))
                    pool.tensor_tensor(xc[u][:, 0:D], tile_rows(k.x, LANES * i + u), nrm[u][:, 0:D], ALU.mult).then_inc(pool_[u].sem, 1)
                    pool.tensor_tensor(xc[u][:, D:2 * D], cs[u][:, :], nrm[u][:, D:2 * D], ALU.mult).then_inc(pool_[u].sem, 1)

        @block.vector
        def _(dve):
            with dve.Fori(0, T // LANES) as i:
                for u in range(LANES):
                    xt = tile_rows(k.x, LANES * i + u)
                    dve.wait_ge(arrived[u], 16 * (i + 1))
                    dve.tensor_tensor(sq[u][:, 0:D], xt, xt, ALU.mult)
                    dve.tensor_tensor(sq[u][:, D:2 * D], cs[u][:, :], cs[u][:, :], ALU.mult).then_inc(dve_[u].sem, 1)
                for u in range(LANES):
                    dve.wait_ge(act_[u].sem, act_[u].at(i, "SQRT"))
                    dve.tensor_scalar(nrm[u][:, :], nrm[u][:, :], 1e-12, None, ALU.max).then_inc(dve_[u].sem, 1)
                    dve.wait_ge(dve_[u].sem, dve_[u].at(i, "MAX"))
                    dve.reciprocal(nrm[u][:, :], nrm[u][:, :]).then_inc(dve_[u].sem, 1)
                for n, (taken, rest) in enumerate((("HIGH", "REST1"), ("MIDDLE", "REST2"))):
                    for u in range(LANES):
                        dve.wait_ge(act_[u].sem, act_[u].at(i, taken))
                        dve.tensor_tensor(xc[u][:, :], xc[u][:, :], part[u][n][:, :], ALU.subtract).then_inc(dve_[u].sem, 1)


def cosine_attention(nc, k):
    ALPHA, SYS, HD8 = 5.0, 16, 8
    PAIRS, GROUPS = SYS // 2, SYS // 4
    with ExitStack() as ctx:
        def sb(name, shape, dt=F32):
            return ctx.enter_context(nc.sbuf_tensor("ca" + name, shape, dt))
        PARTS = ((0, 0), (1, 0), (2, 0), (0, 1), (1, 1), (0, 2))
        stacks = [sb(f"stacks{u}", [HD8 * len(PARTS), SYS, 2 * D], BF16) for u in range(2)]
        cT = [sb(f"cT{u}", [P, 2, P]) for u in range(2)]
        v1 = [sb(f"v1{u}", [P, 2, SYS, 32]) for u in range(2)]
        ex = [sb(f"ex{m}", [P, 2, 2 * D]) for m in range(4)]
        osb = sb("osb", [P, 4, D])
        rec = sb("rec", [P, D])
        quotient = sb("quotient", [P, D])
        arrived = [nc.alloc_semaphore(f"ca_arrived{u}") for u in range(2)]
        ones_set, divided = semaphores(nc, ctx, "ca", "ones_set divided")
        LOADS = 16 * (1 + 2 * len(PARTS))
        valued, scored, exped, attended, o_copied, picked, added = semaphores(
            nc, ctx, "ca", "valued scored exped attended o_copied picked added")
        VALUED, SCORED, EXPED, ATTENDED, O_COPIED, PICKED, ADDED = 2, 1, 2, 4 + PAIRS, 1, 1, 2
        sbank, obank, tbank = [k.psum[:, 0:2, :], k.psum[:, 2:4, :]], k.psum[:, 4:6, :], k.ps[6:8]
        block = ctx.enter_context(nc.Block("ca_b"))

        @block.sync
        def _(sp):
            with sp.Fori(0, T // 2) as i:
                for u in range(2):
                    t = 2 * i + u
                    sp.wait_ge(valued, VALUED + t - 1)
                    sp.wait_ge(attended, ATTENDED + PAIRS * (t - 1))
                    sp.dma_start(cT[u][:, :, :], k.a["ctxT"].rearrange("(c p) n -> p c n", p=P)[:, :, bass.ds(t * P, P)]).then_inc(arrived[u], 16)
                    for row, parts in enumerate(PARTS):
                        for side, part in enumerate(parts):
                            columns = slice((1 - side) * D, (2 - side) * D)
                            sp.dma_start(stacks[u][HD8 * row:HD8 * row + HD8, :, side * D:(side + 1) * D],
                                         k.n_scr[part, bass.ds(t * P, P), columns].rearrange("(s d) f -> d s f", d=HD8)).then_inc(arrived[u], 16)

        @block.gpsimd
        def _(pool):
            pool.sem_inc(valued, VALUED)
            pool.wait_ge(ones_set, 2)
            with pool.Fori(0, T // 2) as i:
                for u in range(2):
                    t = 2 * i + u
                    pool.wait_ge(arrived[u], LOADS * (i + 1))
                    pool.tensor_tensor(v1[u][:, :, :, 0:HD8], cT[u][:, :, :].rearrange("p c (s d) -> p c s d", d=HD8),
                                       v1[u][:, :, :, HD8:2 * HD8], ALU.mult).then_inc(valued, 1)

        @block.tensor
        def _(pe):
            pe.sem_inc(scored, SCORED)
            pe.sem_inc(attended, ATTENDED)
            pe.sem_inc(picked, PICKED)
            pe.wait_ge(ones_set, 2)

            def scores(u, t, m):
                pe.wait_ge(exped, EXPED + PAIRS * t + m - 1)
                for s in range(2):
                    for c in range(2):
                        mm = pe.matmul(sbank[m % 2][:, c, s * D:(s + 1) * D], stacks[u][:, 2 * m + s, c * P:(c + 1) * P],
                                       stacks[u][:, 2 * m + s, D:2 * D], start=True, stop=True)
                mm.then_inc(scored, 1)

            def attend(u, t, g):
                if g == 0:
                    pe.wait_ge(valued, VALUED + t + 1)
                    pe.wait_ge(o_copied, O_COPIED + t)
                pe.wait_ge(exped, EXPED + PAIRS * t + 2 * g + 2)
                for c in range(2):
                    for row in range(4):
                        m, s = 2 * g + row // 2, row % 2
                        mm = pe.matmul(obank[32 * row:32 * row + 32, g // 2, g % 2 * D:(g % 2 + 1) * D],
                                       v1[u][:, c, 4 * g + row, :], ex[m % 4][:, c, s * D:(s + 1) * D], start=(c == 0), stop=(c == 1))
                mm.then_inc(attended, 2)

            def pick(u, t):
                pe.wait_ge(o_copied, O_COPIED + t + 1)
                pe.wait_ge(added, ADDED + t - 1)
                for n in range(2):
                    for block_ in range(4):
                        mm = pe.matmul(tbank[u][32 * block_:32 * block_ + 32, n * D:(n + 1) * D], k.pick[:, 32 * n:32 * n + 32],
                                       osb[:, block_, :], start=True, stop=True)
                mm.then_inc(picked, 1)

            def tile(u, t, turn, first):
                pe.wait_ge(arrived[u], LOADS * (turn + 1))
                for m in range(PAIRS):
                    scores(u, t, m)
                    if m == 1 and not first:
                        attend(1 - u, t - 1, GROUPS - 1)
                    if m >= 2 and m % 2 == 0:
                        attend(u, t, m // 2 - 1)
                    if m == 4 and not first:
                        pick(1 - u, t - 1)

            for t in range(2):
                tile(t, t, 0, t == 0)
            with pe.Fori(1, T // 2) as i:
                for u in range(2):
                    tile(u, 2 * i + u, i, False)
            attend(1, T - 1, GROUPS - 1)
            pick(1, T - 1)

        @block.scalar
        def _(act):
            act.preload_act_table(ACT.Exp)
            act.sem_inc(exped, EXPED)
            act.sem_inc(o_copied, O_COPIED)

            def outputs(t):
                act.wait_ge(attended, ATTENDED + PAIRS * (t + 1))
                act.wait_ge(picked, PICKED + t)
                act.copy(osb[:, :, :].rearrange("p (b c) d -> p b (c d)", b=2), obank).then_inc(o_copied, 1)

            def tile(t, first):
                for m in range(PAIRS):
                    act.wait_ge(scored, SCORED + PAIRS * t + m + 1)
                    act.wait_ge(attended, ATTENDED + PAIRS * t + m - 3)
                    act.activation(ex[m % 4][:, :, :], sbank[m % 2], ACT.Exp, scale=ALPHA).then_inc(exped, 1)
                    if m == 1 and not first:
                        outputs(t - 1)

            for t in range(2):
                tile(t, t == 0)
            with act.Fori(1, T // 2) as i:
                for u in range(2):
                    tile(2 * i + u, False)
            outputs(T - 1)

        @block.vector
        def _(dve):
            dve.sem_inc(added, ADDED)
            for u in range(2):
                dve.memset(v1[u][:, :, :, HD8:32], 1.0).then_inc(ones_set, 1)

            def divide_add(u, t):
                dve.wait_ge(picked, PICKED + t + 1)
                dve.reciprocal(rec[:, :], tbank[u][:, D:2 * D]).then_inc(divided, 1)
                dve.wait_ge(divided, 2 * t + 1)
                dve.wait_ge(added, ADDED + t)
                dve.tensor_tensor(quotient[:, :], tbank[u][:, 0:D], rec[:, :], ALU.mult).then_inc(divided, 1)
                dve.wait_ge(divided, 2 * t + 2)
                dve.tensor_tensor(tile_rows(k.x, t), tile_rows(k.x, t), quotient[:, :], ALU.add).then_inc(added, 1)

            with dve.Fori(0, T // 2) as i:
                for u in range(2):
                    divide_add(u, 2 * i + u)


def l3_attention(nc, k):
    with ExitStack() as outer:
        def sb(name, shape):
            return outer.enter_context(nc.sbuf_tensor("a3" + name, shape, F32))
        o = sb("o", [P, T, D])
        stats = sb("stats", [P, T, 6])
        diff_attention(nc, k, o, stats)
        group_norm_output(nc, k, o, stats)


def diff_attention(nc, k, o, stats):
    with ExitStack() as ctx:
        def sb(name, shape, dt=F32):
            return ctx.enter_context(nc.sbuf_tensor("d3" + name, shape, dt))
        w = sb("w", [P, 2, 768])
        lams = sb("lams", [P, 4, HD])
        lprod = sb("lprod", [P, 2, HD])
        lsum = sb("lsum", [P, 2])
        lam = sb("lam", [P, 1])
        xs = [sb(f"xs{u}", [P, 2, P]) for u in range(2)]
        t1 = [sb(f"t1{u}", [P, 512]) for u in range(2)]
        t2 = [sb(f"t2{u}", [P, 512]) for u in range(2)]
        qk = [sb(f"qk{u}", [P, 512]) for u in range(2)]
        v = [sb(f"v{u}", [P, D]) for u in range(2)]
        vd = [sb(f"vd{u}", [P, 2, D]) for u in range(2)]
        kT = [sb(f"kT{u}", [P, 2, P]) for u in range(2)]
        qT = [[sb(f"qT{u}{n}", [P, 2, P]) for n in range(2)] for u in range(2)]
        kexp = [sb(f"kexp{u}", [P, 2, 2, 8, S]) for u in range(2)]
        sc = [[sb(f"sc{u}{n}", [P, HEADS * S]) for n in range(2)] for u in range(2)]
        pT = [sb(f"pT{u}", [P, 8, P]) for u in range(2)]
        mx = [[sb(f"mx{u}{n}", [P, HEADS]) for n in range(2)] for u in range(2)]
        den = [[sb(f"den{u}{n}", [P, HEADS]) for n in range(2)] for u in range(2)]
        loaded, vec, lexp = semaphores(nc, ctx, "d3", "loaded vec lexp")
        pe_ = lane_steps(nc, "d3", "pe", "QKV TURNED SCORES0 SCORES1 PT O")
        act_ = lane_steps(nc, "d3", "act", "V QT EXP0 EXP1 PT")
        dve_ = lane_steps(nc, "d3", "dve", "COS SIN ROPED VBD KEXP MASK0 MAX0 MASK1 MAX1 SUB1 REC0 P0 SUM1 REC1 LREC P1 DIFF O STATS")
        pool_ = lane_steps(nc, "d3", "pool", "XS KEXP")
        bank = [[k.ps[4 * u + n] for n in range(4)] for u in range(2)]
        block = ctx.enter_context(nc.Block("d3_b"))

        @block.sync
        def _(sp):
            sp.dma_start(w[:, :, :], k.a["L3_qkv"].rearrange("(c p) n -> p c n", p=P)).then_inc(loaded, 16)
            sp.dma_start(lams[:, :, :], k.a["L3_lambdas"].partition_broadcast(P)).then_inc(loaded, 16)

        @block.gpsimd
        def _(pool):
            def stage(u, i):
                t = 2 * i + u
                columns = slice(t * P, t * P + P) if isinstance(t, int) else bass.ds(t * P, P)
                pool.wait_ge(pe_[u].sem, pe_[u].turns(i))
                pool.tensor_copy(xs[u][:, :, :], k.xT[:, :, columns]).then_inc(pool_[u].sem, 1)

            def tile(u, i, before, after):
                pool.wait_ge(act_[u].sem, act_[u].at(i, "QT"))
                spread_keys(pool, kexp[u], kT[u], k.head_mask[:, :], (1,)).then_inc(pool_[u].sem, 1)
                if after:
                    stage(*after)

            stage(0, 0)
            staggered(pool, tile)

        @block.tensor
        def _(pe):
            pe.wait_ge(loaded, 32)

            def project(u, i):
                pe.wait_ge(pool_[u].sem, pool_[u].at(i, "XS"))
                for o_, lo, hi in ((bank[u][0], 0, 512), (bank[u][1][:, 0:D], 512, 768)):
                    for c in range(2):
                        mm = pe.matmul(o_, xs[u][:, c, :], w[:, c, lo:hi], start=(c == 0), stop=(c == 1))
                mm.then_inc(pe_[u].sem, 1)

            def turn(u, i):
                pe.wait_ge(dve_[u].sem, dve_[u].at(i, "ROPED"))
                pe.wait_ge(act_[u].sem, act_[u].at(i, "V"))
                pe.wait_ge(dve_[u].sem, dve_[u].turns(i))
                for c in range(4):
                    pe.transpose(bank[u][2][:, c * P:(c + 1) * P], qk[u][:, c * P:(c + 1) * P], k.ident[:, :])
                for b in range(2):
                    mm = pe.matmul(bank[u][3][:, b * D:(b + 1) * D], k.dup[:, b * P:(b + 1) * P], v[u][:, :], start=True, stop=True)
                mm.then_inc(pe_[u].sem, 1)

            def scores(u, i, n):
                if n == 0:
                    pe.wait_ge(dve_[u].sem, dve_[u].at(i, "KEXP"))
                    pe.wait_ge(pool_[u].sem, pool_[u].at(i, "KEXP"))
                score_matmuls(pe, bank[u][2 * n:2 * n + 2], qT[u][n], kexp[u]).then_inc(pe_[u].sem, 1)

            def turn_weights(u, i):
                pe.wait_ge(dve_[u].sem, dve_[u].at(i, "DIFF"))
                weight_transposes(pe, bank[u][0:2], sc[u][0], k.ident[:, :]).then_inc(pe_[u].sem, 1)

            def values(u, i):
                pe.wait_ge(act_[u].sem, act_[u].at(i, "PT"))
                value_matmuls(pe, bank[u][2], pT[u], vd[u]).then_inc(pe_[u].sem, 1)

            def tile(u, i, before, after):
                turn(u, i)
                scores(u, i, 0)
                if before:
                    turn_weights(*before)
                scores(u, i, 1)
                if before:
                    values(*before)
                if after:
                    project(*after)

            project(0, 0)
            end = staggered(pe, tile)
            turn_weights(*end)
            values(*end)

        @block.scalar
        def _(act):
            act.preload_act_table(ACT.Exp)
            act.wait_ge(vec, 3)
            act.activation(lsum[:, :], lsum[:, :], ACT.Exp).then_inc(lexp, 1)

            def weights_out(u, i):
                act.wait_ge(pe_[u].sem, pe_[u].at(i, "PT"))
                act.copy(pT[u][:, 0:4, :], bank[u][0].rearrange("p (c n) -> p c n", c=4))
                act.copy(pT[u][:, 4:8, :], bank[u][1].rearrange("p (c n) -> p c n", c=4)).then_inc(act_[u].sem, 1)

            def tile(u, i, before, after):
                act.wait_ge(pe_[u].sem, pe_[u].at(i, "QKV"))
                act.copy(v[u][:, :], bank[u][1][:, 0:D]).then_inc(act_[u].sem, 1)
                act.wait_ge(pe_[u].sem, pe_[u].at(i, "TURNED"))
                act.copy(kT[u][:, :, :], bank[u][2][:, D:2 * D].rearrange("p (c n) -> p c n", c=2))
                for n in range(2):
                    ins = act.activation(qT[u][n][:, :, :], bank[u][2][:, 0:D].rearrange("p (c n) -> p c n", c=2), ACT.Copy,
                                         scale=k.half[:, n:n + 1])
                ins.then_inc(act_[u].sem, 1)
                if before:
                    weights_out(*before)
                act.wait_ge(dve_[u].sem, dve_[u].at(i, "MAX0"))
                exponentials(act, sc[u][0], mx[u][0], den[u][0]).then_inc(act_[u].sem, 1)
                act.wait_ge(dve_[u].sem, dve_[u].at(i, "SUB1"))
                act.activation(sc[u][1][:, :], sc[u][1][:, :], ACT.Exp).then_inc(act_[u].sem, 1)

            weights_out(*staggered(act, tile))

        @block.vector
        def _(dve):
            dve.wait_ge(loaded, 32)
            l4 = lams[:, :, :].rearrange("p (n two) d -> p n two d", two=2)
            dve.tensor_tensor(lprod[:, :, :], l4[:, :, 0, :], l4[:, :, 1, :], ALU.mult).then_inc(vec, 1)
            dve.wait_ge(vec, 1)
            dve.tensor_reduce(lsum[:, :], lprod[:, :, :], AX.X, ALU.add).then_inc(vec, 1)
            dve.wait_ge(vec, 2)
            dve.sem_inc(vec, 1)
            dve.wait_ge(lexp, 1)
            dve.tensor_tensor(lam[:, :], lsum[:, 0:1], lsum[:, 1:2], ALU.subtract).then_inc(vec, 1)
            dve.wait_ge(vec, 4)
            dve.tensor_scalar(lam[:, :], lam[:, :], 0.8, None, ALU.add).then_inc(vec, 1)
            dve.wait_ge(vec, 5)

            def rope(u, i):
                dve.wait_ge(pe_[u].sem, pe_[u].at(i, "QKV"))
                for o_, table in ((t1, k.cos), (t2, k.sin)):
                    dve.tensor_tensor(by8(o_[u][:, :]), by8(bank[u][0]), angles(table), ALU.mult).then_inc(dve_[u].sem, 1)
                dve.wait_ge(dve_[u].sem, dve_[u].at(i, "SIN"))
                rope_sums(dve, qk[u][:, :], t1[u][:, :], t2[u][:, :]).then_inc(dve_[u].sem, 1)

            def spread(u, i):
                dve.wait_ge(pe_[u].sem, pe_[u].at(i, "TURNED"))
                values_by_parity(dve, vd[u], bank[u][3].rearrange("p (b n) -> p b n", b=2), k.parity[:, :]).then_inc(dve_[u].sem, 1)
                dve.wait_ge(act_[u].sem, act_[u].at(i, "QT"))
                spread_keys(dve, kexp[u], kT[u], k.head_mask[:, :], (0,)).then_inc(dve_[u].sem, 1)

            def mask(u, i, n):
                dve.wait_ge(pe_[u].sem, pe_[u].at(i, f"SCORES{n}"))
                for c in range(2):
                    ins = dve.scalar_tensor_tensor(out=heads3(sc[u][n][:, c * 512:(c + 1) * 512]), in0=heads3(bank[u][2 * n + c]),
                                                   scalar=HD ** -0.5, in1=over_heads(k.upper[:, :], 8), op0=ALU.mult, op1=ALU.add)
                ins.then_inc(dve_[u].sem, 1)
                dve.wait_ge(dve_[u].sem, dve_[u].at(i, f"MASK{n}"))
                dve.tensor_reduce(mx[u][n][:, :], heads3(sc[u][n][:, :]), AX.X, ALU.max, negate=(n == 0)).then_inc(dve_[u].sem, 1)

            def subtract_maximum(u, i):
                dve.wait_ge(dve_[u].sem, dve_[u].at(i, "MAX1"))
                dve.tensor_tensor(heads3(sc[u][1][:, :]), heads3(sc[u][1][:, :]), per_head(mx[u][1][:, :]), ALU.subtract).then_inc(dve_[u].sem, 1)

            def normalise(u, n):
                dve.tensor_tensor(heads3(sc[u][n][:, :]), heads3(sc[u][n][:, :]), per_head(den[u][n][:, :]),
                                  ALU.mult).then_inc(dve_[u].sem, 1)

            def first_weights(u, i):
                dve.wait_ge(act_[u].sem, act_[u].at(i, "EXP0"))
                dve.reciprocal(den[u][0][:, :], den[u][0][:, :]).then_inc(dve_[u].sem, 1)
                dve.wait_ge(dve_[u].sem, dve_[u].at(i, "REC0"))
                normalise(u, 0)

            def difference(u, i):
                def wait(step):
                    dve.wait_ge(dve_[u].sem, dve_[u].at(i, step))

                dve.wait_ge(act_[u].sem, act_[u].at(i, "EXP1"))
                dve.tensor_reduce(den[u][1][:, :], heads3(sc[u][1][:, :]), AX.X, ALU.add).then_inc(dve_[u].sem, 1)
                wait("SUM1")
                dve.reciprocal(den[u][1][:, :], den[u][1][:, :]).then_inc(dve_[u].sem, 1)
                wait("REC1")
                dve.tensor_scalar(den[u][1][:, :], den[u][1][:, :], lam[:, :], None, ALU.mult).then_inc(dve_[u].sem, 1)
                wait("LREC")
                normalise(u, 1)
                wait("P1")
                dve.tensor_tensor(sc[u][0][:, :], sc[u][0][:, :], sc[u][1][:, :], ALU.subtract).then_inc(dve_[u].sem, 1)

            def outputs(u, i):
                t = 2 * i + u
                dve.wait_ge(pe_[u].sem, pe_[u].at(i, "O"))
                for b in range(2):
                    r = row_slice(b)
                    ins = dve.tensor_copy(tile_rows(o, t)[r, :].rearrange("p (c h d) -> p c h d", h=2, d=HD), own_batch(bank[u][2], b))
                ins.then_inc(dve_[u].sem, 1)
                dve.wait_ge(dve_[u].sem, dve_[u].at(i, "O"))
                dve.bn_stats(tile_rows(stats, t), tile_rows(o, t)).then_inc(dve_[u].sem, 1)

            def tile(u, i, before, after):
                rope(u, i)
                if before:
                    first_weights(*before)
                spread(u, i)
                if before:
                    difference(*before)
                mask(u, i, 0)
                mask(u, i, 1)
                subtract_maximum(u, i)
                if before:
                    outputs(*before)

            end = staggered(dve, tile)
            first_weights(*end)
            difference(*end)
            outputs(*end)


def group_norm_output(nc, k, o, stats):
    LANES = 4
    with ExitStack() as ctx:
        def sb(name, shape, dt=F32):
            return ctx.enter_context(nc.sbuf_tensor("g3" + name, shape, dt))
        w = sb("w", [P, 2, D])
        gamma, beta = sb("gamma", [P, 4]), sb("beta", [P, 4])
        mom = sb("mom", [P, 4, T])
        pair = sb("pair", [P, 2, T])
        y = [sb(f"y{u}", [P, D]) for u in range(LANES)]
        yT = [sb(f"yT{u}", [P, 2, P]) for u in range(LANES)]
        loaded, vec, averaged, rooted = semaphores(nc, ctx, "g3", "loaded vec averaged rooted")
        pe_ = lane_steps(nc, "g3", "pe", "YT OUT", LANES)
        act_ = lane_steps(nc, "g3", "act", "YT", LANES)
        dve_ = lane_steps(nc, "g3", "dve", "NORM GAMMA BETA X", LANES)
        bank = [[k.ps[2 * u + n] for n in range(2)] for u in range(LANES)]
        block = ctx.enter_context(nc.Block("g3_b"))

        @block.sync
        def _(sp):
            sp.dma_start(w[:, :, :], k.a["L3_wo"].rearrange("(c p) n -> p c n", p=P)).then_inc(loaded, 16)
            for b in range(2):
                sp.dma_start(gamma[row_slice(b), :], k.a["L3_gamma"]).then_inc(loaded, 16)
                sp.dma_start(beta[row_slice(b), :], k.a["L3_beta"]).then_inc(loaded, 16)

        @block.gpsimd
        def _(pool):
            pool.wait_ge(vec, 12)
            pool.tensor_tensor(mom[:, 3, :], mom[:, 2, :], k.minus_half[:, 0:T], ALU.pow).then_inc(rooted, 1)

        @block.tensor
        def _(pe):
            pe.wait_ge(loaded, 80)
            pe.wait_ge(vec, 9)
            pe.matmul(k.ps[7][:, 0:2 * T], k.avg4[:, :], pair[:, :, :].rearrange("p n t -> p (n t)"), start=True, stop=True).then_inc(averaged, 1)
            with pe.Fori(0, T // LANES) as i:
                for u in range(LANES):
                    pe.wait_ge(dve_[u].sem, dve_[u].at(i, "BETA"))
                    for c in range(2):
                        mm = pe.transpose(bank[u][0][:, c * P:(c + 1) * P], y[u][:, c * P:(c + 1) * P], k.ident[:, :])
                    mm.then_inc(pe_[u].sem, 1)
                for u in range(LANES):
                    pe.wait_ge(act_[u].sem, act_[u].at(i, "YT"))
                    pe.wait_ge(dve_[u].sem, dve_[u].turns(i))
                    for c in range(2):
                        mm = pe.matmul(bank[u][1][:, 0:D], yT[u][:, c, :], w[:, c, :], start=(c == 0), stop=(c == 1))
                    mm.then_inc(pe_[u].sem, 1)

        @block.scalar
        def _(act):
            with act.Fori(0, T // LANES) as i:
                for u in range(LANES):
                    act.wait_ge(pe_[u].sem, pe_[u].at(i, "YT"))
                    act.copy(yT[u][:, :, :], bank[u][0][:, 0:D].rearrange("p (c n) -> p c n", c=2)).then_inc(act_[u].sem, 1)

        @block.vector
        def _(dve):
            count = [0]

            def link(ins):
                count[0] += 1
                ins.then_inc(vec, 1)
                dve.wait_ge(vec, count[0])

            me, mo, ve, vo = stats[:, :, 1], stats[:, :, 4], stats[:, :, 2], stats[:, :, 5]
            link(dve.tensor_tensor(pair[:, 0, :], me, mo, ALU.add))
            link(dve.tensor_scalar(pair[:, 0, :], pair[:, 0, :], 0.5, None, ALU.mult))
            link(dve.tensor_tensor(mom[:, 0, :], me, me, ALU.mult))
            link(dve.tensor_tensor(mom[:, 1, :], mo, mo, ALU.mult))
            link(dve.tensor_tensor(mom[:, 0, :], mom[:, 0, :], mom[:, 1, :], ALU.add))
            link(dve.tensor_scalar(mom[:, 0, :], mom[:, 0, :], 0.5, None, ALU.mult))
            link(dve.tensor_tensor(mom[:, 1, :], ve, vo, ALU.add))
            link(dve.tensor_scalar(mom[:, 1, :], mom[:, 1, :], 1.0 / D, None, ALU.mult))
            link(dve.tensor_tensor(pair[:, 1, :], mom[:, 0, :], mom[:, 1, :], ALU.add))
            dve.wait_ge(averaged, 1)
            link(dve.tensor_copy(pair[:, :, :].rearrange("p n t -> p (n t)"), k.ps[7][:, 0:2 * T]))
            link(dve.tensor_tensor(mom[:, 0, :], pair[:, 0, :], pair[:, 0, :], ALU.mult))
            link(dve.scalar_tensor_tensor(out=mom[:, 2, :], in0=pair[:, 1, :], scalar=1e-5, in1=mom[:, 0, :], op0=ALU.add, op1=ALU.subtract))
            dve.wait_ge(rooted, 1)
            dve.wait_ge(loaded, 80)
            with dve.Fori(0, T // LANES) as i:
                for u in range(LANES):
                    t = LANES * i + u
                    y3 = y[u][:, :].rearrange("p (g d) -> p g d", g=4)
                    dve.tensor_scalar(y[u][:, :], tile_rows(o, t), pair[:, 0, bass.ds(t, 1)], mom[:, 3, bass.ds(t, 1)],
                                      ALU.subtract, ALU.mult).then_inc(dve_[u].sem, 1)
                    dve.wait_ge(dve_[u].sem, dve_[u].at(i, "NORM"))
                    dve.tensor_tensor(y3, y3, gamma[:, :].unsqueeze(2).to_broadcast([P, 4, 64]), ALU.mult).then_inc(dve_[u].sem, 1)
                    dve.wait_ge(dve_[u].sem, dve_[u].at(i, "GAMMA"))
                    dve.tensor_tensor(y3, y3, beta[:, :].unsqueeze(2).to_broadcast([P, 4, 64]), ALU.add).then_inc(dve_[u].sem, 1)
                for u in range(LANES):
                    xt = tile_rows(k.x, LANES * i + u)
                    dve.wait_ge(pe_[u].sem, pe_[u].at(i, "OUT"))
                    dve.scalar_tensor_tensor(out=xt, in0=bank[u][1][:, 0:D], scalar=1.0 - 0.8, in1=xt, op0=ALU.mult, op1=ALU.add).then_inc(dve_[u].sem, 1)


def l3_cross(nc, k):
    LANES = 4
    with ExitStack() as ctx:
        def sb(name, shape, dt=F32):
            return ctx.enter_context(nc.sbuf_tensor("c3" + name, shape, dt))
        mk8 = sb("mk8", [P, T, S], mybir.dt.uint8)
        mk = sb("mk", [P, T, S])
        neg = sb("neg", [P, T, S])
        valid = sb("valid", [P, T])
        xs = [sb(f"xs{u}", [P, 2, P]) for u in range(LANES)]
        cT = [sb(f"cT{u}", [P, 2, P]) for u in range(LANES)]
        cs = [sb(f"cs{u}", [P, D]) for u in range(LANES)]
        sc = [sb(f"sc{u}", [P, S]) for u in range(LANES)]
        nmx = [sb(f"nmx{u}", [P, 1]) for u in range(LANES)]
        den = [sb(f"den{u}", [P, 1]) for u in range(LANES)]
        fac = [sb(f"fac{u}", [P, 1]) for u in range(LANES)]
        pbd = [sb(f"pbd{u}", [P, P]) for u in range(LANES)]
        pT = [sb(f"pT{u}", [P, P]) for u in range(LANES)]
        loaded, ready = semaphores(nc, ctx, "c3", "loaded ready")
        arrived = [nc.alloc_semaphore(f"c3_arrived{u}") for u in range(LANES)]
        pe_ = lane_steps(nc, "c3", "pe", "S PT O", LANES)
        act_ = lane_steps(nc, "c3", "act", "EXP PT", LANES)
        dve_ = lane_steps(nc, "c3", "dve", "SCALED MASKED MAX REC FAC X", LANES)
        pool_ = lane_steps(nc, "c3", "pool", "XS", LANES)
        bank = [[k.ps[2 * u + n] for n in range(2)] for u in range(LANES)]
        block = ctx.enter_context(nc.Block("c3_b"))

        @block.sync
        def _(sp):
            for b in range(2):
                sp.dma_start(mk8[64 * b:64 * b + 64, :, :],
                             k.a["mask"].rearrange("(t b) j -> b t j", b=2)[b].partition_broadcast(64)).then_inc(loaded, 16)
            with sp.Fori(0, T // LANES) as i:
                for u in range(LANES):
                    t = LANES * i + u
                    sp.wait_ge(pe_[u].sem, pe_[u].turns(i))
                    sp.dma_start(cs[u][:, :], k.ctx_rows[bass.ds(t * P, P), :]).then_inc(arrived[u], 16)
                    sp.dma_start(cT[u][:, :, :], k.a["ctxT"].rearrange("(c p) n -> p c n", p=P)[:, :, bass.ds(t * P, P)]).then_inc(arrived[u], 16)

        @block.gpsimd
        def _(pool):
            with pool.Fori(0, T // LANES) as i:
                for u in range(LANES):
                    pool.wait_ge(pe_[u].sem, pe_[u].turns(i))
                    pool.tensor_copy(xs[u][:, :, :], k.xT[:, :, bass.ds((LANES * i + u) * P, P)]).then_inc(pool_[u].sem, 1)

        @block.tensor
        def _(pe):
            with pe.Fori(0, T // LANES) as i:
                for u in range(LANES):
                    pe.wait_ge(arrived[u], 32 * (i + 1))
                    pe.wait_ge(pool_[u].sem, pool_[u].at(i, "XS"))
                    pe.wait_ge(dve_[u].sem, dve_[u].turns(i))
                    for c in range(2):
                        mm = pe.matmul(bank[u][0][:, 0:P], xs[u][:, c, :], cT[u][:, c, :], start=(c == 0), stop=(c == 1))
                    mm.then_inc(pe_[u].sem, 1)
                for u in range(LANES):
                    pe.wait_ge(act_[u].sem, act_[u].at(i, "EXP"))
                    pe.transpose(bank[u][1][:, 0:P], pbd[u][:, :], k.ident[:, :]).then_inc(pe_[u].sem, 1)
                for u in range(LANES):
                    pe.wait_ge(act_[u].sem, act_[u].at(i, "PT"))
                    pe.matmul(bank[u][0][:, 0:D], pT[u][:, :], cs[u][:, :], start=True, stop=True).then_inc(pe_[u].sem, 1)

        @block.scalar
        def _(act):
            act.preload_act_table(ACT.Exp)
            act.wait_ge(ready, LANES + 4)
            with act.Fori(0, T // LANES) as i:
                for u in range(LANES):
                    act.wait_ge(dve_[u].sem, dve_[u].at(i, "MAX"))
                    for b in range(2):
                        r = slice(64 * b, 64 * b + 64)
                        ins = act.activation(pbd[u][r, r], sc[u][r, :], ACT.Exp, bias=nmx[u][r, :], accum_out=den[u][r, :])
                    ins.then_inc(act_[u].sem, 1)
                for u in range(LANES):
                    act.wait_ge(pe_[u].sem, pe_[u].at(i, "PT"))
                    act.copy(pT[u][:, :], bank[u][1][:, 0:P]).then_inc(act_[u].sem, 1)

        @block.vector
        def _(dve):
            for u in range(LANES):
                dve.memset(pbd[u][:, :], 0.0).then_inc(ready, 1)
            dve.wait_ge(loaded, 32)
            dve.tensor_copy(mk[:, :, :], mk8[:, :, :]).then_inc(ready, 1)
            dve.wait_ge(ready, LANES + 1)
            dve.tensor_scalar(neg[:, :, :], mk[:, :, :], -1.0, -NEG, ALU.add, ALU.mult).then_inc(ready, 1)
            dve.tensor_reduce(valid[:, :], mk[:, :, :], AX.X, ALU.max).then_inc(ready, 1)
            dve.wait_ge(ready, LANES + 3)
            dve.sem_inc(ready, 1)
            with dve.Fori(0, T // LANES) as i:
                for u in range(LANES):
                    def wait(step, u=u):
                        dve.wait_ge(dve_[u].sem, dve_[u].at(i, step))

                    t = bass.ds(LANES * i + u, 1)
                    dve.wait_ge(pe_[u].sem, pe_[u].at(i, "S"))
                    for b in range(2):
                        r = slice(64 * b, 64 * b + 64)
                        ins = dve.scalar_tensor_tensor(out=sc[u][r, :], in0=bank[u][0][r, r], scalar=D ** -0.5,
                                                       in1=mk[r, t, :].rearrange("p t j -> p (t j)"), op0=ALU.mult, op1=ALU.mult)
                    ins.then_inc(dve_[u].sem, 1)
                    wait("SCALED")
                    dve.tensor_tensor(sc[u][:, :], sc[u][:, :], neg[:, t, :].rearrange("p t j -> p (t j)"), ALU.add).then_inc(dve_[u].sem, 1)
                    wait("MASKED")
                    dve.tensor_reduce(nmx[u][:, :], sc[u][:, :], AX.X, ALU.max, negate=True).then_inc(dve_[u].sem, 1)
                for u in range(LANES):
                    t = bass.ds(LANES * i + u, 1)
                    dve.wait_ge(act_[u].sem, act_[u].at(i, "EXP"))
                    dve.reciprocal(den[u][:, :], den[u][:, :]).then_inc(dve_[u].sem, 1)
                    dve.wait_ge(dve_[u].sem, dve_[u].at(i, "REC"))
                    dve.tensor_tensor(fac[u][:, :], den[u][:, :], valid[:, t], ALU.mult).then_inc(dve_[u].sem, 1)
                for u in range(LANES):
                    xt = k.x[:, bass.ds(LANES * i + u, 1), :].rearrange("p t d -> p (t d)")
                    dve.wait_ge(pe_[u].sem, pe_[u].at(i, "O"))
                    dve.wait_ge(dve_[u].sem, dve_[u].at(i, "FAC"))
                    dve.scalar_tensor_tensor(out=xt, in0=bank[u][0][:, 0:D], scalar=fac[u][:, :], in1=xt,
                                             op0=ALU.mult, op1=ALU.add).then_inc(dve_[u].sem, 1)


class Shared:
    pass


def build(nc, a, out):
    with ExitStack() as ctx:
        k = Shared()
        k.a = a
        def sb(name, shape, dt=F32):
            return ctx.enter_context(nc.sbuf_tensor(name, shape, dt))
        k.psum = ctx.enter_context(nc.psum_tensor("psum", [P, 8, 512], F32))
        k.ps = [k.psum[:, i, :] for i in range(8)]
        k.x = sb("x", [P, T, D])
        k.xT = sb("xT", [P, 2, N])
        k.consts = {n[2:]: sb(n, list(ap.shape)) for n, ap in a.items() if n.startswith("c_")}
        c = k.consts
        k.ident, k.cos, k.sin, k.head_mask, k.parity = c["ident"], c["cos"], c["sin"], c["head_mask"], c["parity"]
        k.strict, k.causal, k.not_first = c["strict"], c["causal"], c["not_first"]
        k.ones8, k.rows_of_unit = c["ones8"], c["rows_of_unit"]
        k.dup, k.block_causal, k.upper, k.half = c["dup"], c["block_causal"], c["upper"], c["half"]
        k.ones64, k.cumulate, k.eye64, k.avg4, k.ones = c["ones64"], c["cumulate"], c["eye64"], c["avg4"], c["ones"]
        k.minus_half = sb("minus_half", [P, T])
        k.v_scr = nc.dram_tensor("v_scr", (N, D), F32, kind="Internal").ap()
        k.u_scr = nc.dram_tensor("u_scr", (N, D), F32, kind="Internal").ap()
        k.l_scr = nc.dram_tensor("l_scr", (NB, 16, S, S), F32, kind="Internal").ap()
        k.p_scr = nc.dram_tensor("p_scr", (T, P, 1024), F32, kind="Internal").ap()
        k.q_scr = nc.dram_tensor("q_scr", (3, D, N), BF16, kind="Internal").ap()
        k.k_scr = nc.dram_tensor("k_scr", (3, D, KEYS), BF16, kind="Internal").ap()
        k.n_scr = nc.dram_tensor("n_scr", (3, N, 2 * D), BF16, kind="Internal").ap()
        k.strip_sum, k.pick = c["strip_sum"], c["pick"]
        k.ctx_rows = a["ctx"]
        load_phase(nc, k)
        for n, phase in enumerate(PHASES):
            with nc.cleanup_on_exit():
                phase(nc, k)
                layer_norm(nc, k, f"ln{n}")
        store_phase(nc, k, out)


def load_phase(nc, k):
    with ExitStack() as ctx:
        loaded, const, turned, copied = semaphores(nc, ctx, "load", "loaded const turned copied")
        block = ctx.enter_context(nc.Block("load_b"))

        @block.sync
        def _(sp):
            for b in range(2):
                sp.dma_start(k.x[64 * b:64 * b + 64, :, :],
                             k.a["x"].rearrange("(t c) s d -> c s t d", c=2)[b]).then_inc(loaded, 16)
            for n, tile in k.consts.items():
                sp.dma_start(tile[:, :], k.a["c_" + n]).then_inc(loaded, 16)
            sp.wait_ge(loaded, 32 + 16 * len(k.consts))

        @block.gpsimd
        def _(pool):
            pool.memset(k.minus_half[:, :], -0.5).then_inc(const, 1)
            pool.wait_ge(const, 1)

        @block.tensor
        def _(pe):
            pe.wait_ge(loaded, 32 + 16 * len(k.consts))
            for t in range(T):
                if t >= 8:
                    pe.wait_ge(copied, t - 7)
                pe.transpose(k.ps[t % 8][:, 0:128], k.x[:, t, 0:128], k.ident[:, :])
                pe.transpose(k.ps[t % 8][:, 128:256], k.x[:, t, 128:256], k.ident[:, :]).then_inc(turned, 1)

        @block.scalar
        def _(act):
            for t in range(T):
                act.wait_ge(turned, t + 1)
                act.copy(k.xT[:, :, t * P:(t + 1) * P],
                         k.ps[t % 8][:, 0:256].rearrange("p (c n) -> p c n", c=2)).then_inc(copied, 1)


def store_phase(nc, k, out):
    with ExitStack() as ctx:
        stored, = semaphores(nc, ctx, "store", "stored")
        block = ctx.enter_context(nc.Block("store_b"))

        @block.sync
        def _(sp):
            for b in range(2):
                sp.dma_start(out.rearrange("(t c) s d -> c s t d", c=2)[b], k.x[64 * b:64 * b + 64, :, :]).then_inc(stored, 16)
            sp.wait_ge(stored, 32)


PHASES = [l0_attention, l0_cross, l0_ffn] + [l1_attention, l1_cross, l1_ffn, l2_attention, l2_cross, l2_ffn, l3_attention, l3_cross, l3_ffn]


def shape_constants():
    p = np.arange(P)
    s = p % S
    j = np.arange(S)
    ang = s[:, None].astype(np.float32) * (1.0 / 10000.0 ** (np.arange(8) / 8.0)).astype(np.float32)[None]
    f = lambda m: np.ascontiguousarray(m, dtype=np.float32)
    return {
        "ident": f(np.eye(P)),
        "cos": f(np.cos(ang)), "sin": f(np.sin(ang)),
        "head_mask": f(p[:, None] // HD == np.arange(8)[None]),
        "parity": f(p[:, None] // S == np.arange(HEADS)[None] % 2),
        "strict": f(np.where(s[:, None] > j[None], 0, NEG)),
        "causal": f(np.where(s[:, None] >= j[None], 0, NEG)),
        "not_first": f(s[:, None] > 0),
        "pick": f(np.concatenate([(p[:, None] % 32 == n * 8 + np.arange(32)[None] % 8) & (p[:, None] // 32 == np.arange(32)[None] // 8)
                                  for n in range(2)], axis=1)),
        "strip_sum": f(p[:, None] % 32 == np.arange(HD + 1)[None]),
        "dup": f(np.concatenate([p[:, None] == b * S + s[None] for b in range(2)], axis=1)),
        "block_causal": f(np.where((s[:, None] >= j[None]) & (s[:, None] // 8 == j[None] // 8), 0, NEG)),
        "upper": f(j[None] > s[:, None]),
        "half": f(p[:, None] % HD // 8 == np.arange(2)[None]),
        "ones64": f(p[:, None] // S == p[None] // S),
        "cumulate": f((p[:, None] // S == p[None] // S) & (p[:, None] <= p[None])),
        "eye64": f(s[:, None] == j[None]),
        "avg4": f((p[:, None] // 4 == p[None] // 4) * 0.25),
        "ones": f(np.ones((P, P))),
        "ones8": f(p[:, None] // 8 == p[None] // 8),
        "rows_of_unit": f(p[:, None] // 8 == np.arange(16)[None]),
    }


def selection(experts, width, hidden, shared_row=False):
    owner = np.minimum(np.arange(hidden) // width, experts)
    row = np.arange(COMB_ROWS) % 32
    rows = experts + 1 if shared_row else experts
    return ((row[:, None] == owner[None]) & (row[:, None] < rows)).astype(np.float32)


def laid_out(i):
    out = {n: np.ascontiguousarray(i[n]) for n in ("x",)}
    out["L0_attn_W"] = np.concatenate([i["L0_attn_Wq"], i["L0_attn_Wk"], i["L0_attn_Wv"], i["L0_attn_Wb"]], axis=1)
    out["L0_attn_bb"] = np.ascontiguousarray(i["L0_attn_bb"])
    out["L0_attn_Wo"] = np.ascontiguousarray(i["L0_attn_Wo"])
    out["mask"] = i["mask_BxS2_bk0"]
    out["L1_wr"], out["L1_w1"], out["L1_w3"], out["L1_w2"] = (i["L1_ffn_" + n].T for n in ("wr", "w1", "w3", "w2"))
    out["L1_gates"] = np.concatenate([i["L1_xattn_Wi"], i["L1_xattn_Wf"]], axis=1)
    out["L1_gates_b"] = np.concatenate([i["L1_xattn_bi"], i["L1_xattn_bf"]])
    out["L1_xattn_ln_scale"] = i["L1_xattn_ln_scale"]
    out["L2_norm1"], out["L2_norm2"] = i["L2_attn_attn_norm_w"], i["L2_attn_ffn_norm_w"]
    out["L2_qkv"], out["L2_o"], out["L2_up"], out["L2_down"] = (i["L2_attn_" + n + "_w"].T for n in ("qkv", "o", "ffn_up", "ffn_down"))
    out["L3_qkv"], out["L3_wo"] = i["L3_attn_w_qkv"].T, i["L3_attn_wo"].T
    out["L3_lambdas"] = np.stack([i["L3_attn_lambda_" + n] for n in ("q1", "k1", "q2", "k2")])
    out["L3_gamma"], out["L3_beta"] = i["L3_attn_gamma"].reshape(S, 4), i["L3_attn_beta"].reshape(S, 4)
    out["L1_kT"] = i["L1_attn_kv_k"].reshape(-1, D).T
    out["L1_v"] = i["L1_attn_kv_v"].reshape(-1, D)
    out["L1_Wq"], out["L1_Wo"] = i["L1_attn_Wq"].T, i["L1_attn_Wo"].T
    out["ctx"] = i["ctx_2048"].reshape(N, D)
    out["ctxT"] = i["ctx_2048"].reshape(N, D).T
    gu, F = i["L0_ffn_gate_up_weights"], i["L0_ffn_gate_up_weights"].shape[1] // 2
    sgu, FS = i["L0_ffn_shared_gate_up"], i["L0_ffn_shared_gate_up"].shape[0] // 2
    out["L0_router"] = i["L0_ffn_gate_weight"].T
    out["L0_g"] = np.concatenate([gu[:, :F].reshape(-1, D), sgu[:FS]]).T
    out["L0_u"] = np.concatenate([gu[:, F:].reshape(-1, D), sgu[FS:]]).T
    out["L0_d"] = np.concatenate([i["L0_ffn_down_weights"].transpose(0, 2, 1).reshape(-1, D), i["L0_ffn_shared_down"].T])
    out["sel176"] = selection(8, F, 8 * F + FS)
    flat = lambda w: w.transpose(1, 0, 2).reshape(D, -1)
    out["L2_router"] = np.concatenate([i["L2_ffn_gate_w"].T, i["L2_ffn_shgate_w"][:, None]], axis=1)
    out["L2_g"] = np.concatenate([flat(i["L2_ffn_w_gate"]), i["L2_ffn_shw_gate"]], axis=1)
    out["L2_u"] = np.concatenate([flat(i["L2_ffn_w_up"]), i["L2_ffn_shw_up"]], axis=1)
    out["L2_d"] = np.concatenate([i["L2_ffn_w_down"].reshape(-1, D), i["L2_ffn_shw_down"]])
    out["sel176s"] = selection(8, F, 8 * F + FS, shared_row=True)
    out["L3_ffn_w_router"] = i["L3_ffn_w_router"]
    out["L3_g"] = np.concatenate([flat(i["L3_ffn_we1"]), i["L3_ffn_ws1"]], axis=1)
    out["L3_u"] = np.concatenate([flat(i["L3_ffn_we3"]), i["L3_ffn_ws3"]], axis=1)
    out["L3_d"] = np.concatenate([i["L3_ffn_we2"].reshape(-1, D), i["L3_ffn_ws2"]])
    out["sel128"] = selection(16, 128, 16 * 128 + 512)
    return {n: np.ascontiguousarray(a) for n, a in out.items()}


def kernel(**inputs):
    import concourse.bacc as _bacc
    from concourse.bass_utils import run_bass_kernel_spmd as _run

    nc = _bacc.Bacc("TRN2", target_bir_lowering=False, num_devices=1)
    arrays, aps = {}, {}
    given = laid_out({n: np.asarray(a) for n, a in inputs.items()})
    for name, a in {**given, **{"c_" + n: c for n, c in shape_constants().items()}}.items():
        arrays[f"in_{name}_dram"] = a
        aps[name] = nc.dram_tensor(f"in_{name}_dram", a.shape, mybir.dt.from_np(a.dtype), kind="ExternalInput").ap()
    out = nc.dram_tensor("out_0_dram", (NB, S, D), F32, kind="ExternalOutput").ap()
    build(nc, aps, out)
    r = _run(nc, [arrays], core_ids=[0])
    return r.results[0]["out_0_dram"]
```
